# Optimizing a Trainium2 kernel written in Bass

```python
import numpy as np
import jax
import jax.numpy as jnp

def _softmax(x, axis=-1):
    return jax.nn.softmax(x, axis=axis)

def _gelu(x):
    return jax.nn.gelu(x, approximate=True)

def _silu(x):
    return jax.nn.silu(x)

def _sigmoid(x):
    return jax.nn.sigmoid(x)

def _layernorm(x, axis=-1, eps=1e-05):
    m = jnp.mean(x, axis=axis, keepdims=True)
    v = jnp.var(x, axis=axis, keepdims=True)
    return (x - m) / jnp.sqrt(v + eps)

def _scatter_add(tgt, idx, src, axis=0):
    return tgt.at[idx].add(src)

def _segment_sum(src, seg, n):
    return jax.ops.segment_sum(src, seg, n)
kernel_name = 'mk_gnn_ffn_d2_gnn_r32_b9714c'

def setup_inputs(seed: int=0):
    np.random.seed(seed)
    _w = jnp.asarray

    def _rec_inputs():
        import jax
        import jax.numpy as jnp
        _gk = jax.random.key(seed)
        x = -0.0002117 + 1 * jax.random.normal(jax.random.fold_in(_gk, 1), (3125, 256), jnp.float32)
        _s = jax.random.randint(jax.random.fold_in(_gk, 2), (25000,), 0, 3125, jnp.int32)
        _d = jax.random.randint(jax.random.fold_in(_gk, 3), (25000,), 0, 3125, jnp.int32)
        _loop = jnp.arange(3125, dtype=jnp.int32)
        src = jnp.concatenate([_s, _d, _loop])
        dst = jnp.concatenate([_d, _s, _loop])
        _o = jnp.argsort(dst, stable=True)
        src = src[_o]
        dst = dst[_o]
        edge_weight = jax.random.uniform(jax.random.fold_in(_gk, 13), (53125,), jnp.float32, 0.0, 1)
        node_vec = jax.random.uniform(jax.random.fold_in(_gk, 14), (3125,), jnp.float32, 0.0, 0.999833)
        return (x, src, dst, edge_weight, node_vec)
    x, src, dst, edge_weight, node_vec = _rec_inputs()

    def _L0_gnn_setup():
        import jax, jax.numpy as jnp
        import numpy as np
        N_NODES = 3125
        N_EDGES = 100000
        D = 256
        key = jax.random.key(seed)
        k1, k2, k3, k4, k5, k6 = jax.random.split(key, 6)
        x = jax.random.normal(k1, (N_NODES, D), dtype=jnp.float32)
        edge_row = jax.random.randint(k2, (N_EDGES,), 0, N_NODES, dtype=jnp.int32)
        edge_col = jax.random.randint(k3, (N_EDGES,), 0, N_NODES, dtype=jnp.int32)
        edge_val = jax.random.uniform(k4, (N_EDGES,), dtype=jnp.float32)
        stdv = 1.0 / np.sqrt(D)
        weight = jax.random.uniform(k5, (D, D), dtype=jnp.float32, minval=-stdv, maxval=stdv)
        b = jax.random.uniform(k6, (D,), dtype=jnp.float32, minval=-stdv, maxval=stdv)
        return {'x': x, 'edge_row': edge_row, 'edge_col': edge_col, 'edge_val': edge_val, 'weight': weight, 'b': b}
    _L0_gnn_all = _L0_gnn_setup()
    _L0_gnn_in = {k: v for k, v in _L0_gnn_all.items() if k in ('weight', 'b')}
    del _L0_gnn_all

    def _L0_ffn_setup():
        import jax, jax.numpy as jnp
        import numpy as np
        C = 256
        HID = 1024
        E = 8
        TEMP = 1.0
        key = jax.random.key(seed)
        ks = jax.random.split(key, 7)
        x = jax.random.normal(ks[0], (8, 512, C), dtype=jnp.float32)
        W1 = jax.random.normal(ks[1], (C, HID), dtype=jnp.float32) * 0.02
        b1 = jnp.zeros((HID,), dtype=jnp.float32)
        Wg = jax.random.normal(ks[2], (HID, E), dtype=jnp.float32) * 0.02
        bg = jnp.zeros((E,), dtype=jnp.float32)
        Wd = jax.random.normal(ks[3], (E, HID, C), dtype=jnp.float32) * 0.02
        bd = jnp.zeros((E, C), dtype=jnp.float32)
        return {'x': x, 'W1': W1, 'b1': b1, 'Wg': Wg, 'bg': bg, 'Wd': Wd, 'bd': bd}
    _L0_ffn_all = _L0_ffn_setup()
    _L0_ffn_in = {k: v for k, v in _L0_ffn_all.items() if k in ('W1', 'b1', 'Wg', 'bg', 'Wd', 'bd')}
    del _L0_ffn_all

    def _L1_gnn_setup():
        import jax, jax.numpy as jnp
        import numpy as np
        from jax import lax
        N, E, D = (256, 8192, 256)
        NH, FOUT = (4, 64)
        D_STATE, D_CONV, DT_RANK = (16, 4, 16)

        def _layer_norm(x, g, b, eps=1e-05):
            mu = jnp.mean(x, -1, keepdims=True)
            var = jnp.var(x, -1, keepdims=True)
            return (x - mu) * lax.rsqrt(var + eps) * g + b

        def _mamba(xs, in_proj_w, conv_w, conv_b, x_proj_w, dt_proj_w, dt_proj_b, A_log, D_param, out_proj_w):
            n = xs.shape[0]
            xz = xs @ in_proj_w.T
            xc, z = jnp.split(xz, 2, axis=-1)
            K = conv_w.shape[1]
            xp = jnp.pad(xc, ((K - 1, 0), (0, 0)))
            xc = sum((xp[k:k + n] * conv_w[:, k] for k in range(K))) + conv_b
            xc = jax.nn.silu(xc)
            dbc = xc @ x_proj_w.T
            dt = jax.nn.softplus(dbc[:, :DT_RANK] @ dt_proj_w.T + dt_proj_b)
            Bm = dbc[:, DT_RANK:DT_RANK + D_STATE]
            Cm = dbc[:, DT_RANK + D_STATE:]
            A = -jnp.exp(A_log)
            dA = jnp.exp(dt[:, :, None] * A)
            dBx = (dt * xc)[:, :, None] * Bm[:, None, :]

            def step(h, t):
                dA_t, dBx_t, C_t = t
                h = dA_t * h + dBx_t
                return (h, h @ C_t)
            _, y = lax.scan(step, jnp.zeros((xc.shape[1], D_STATE), xs.dtype), (dA, dBx, Cm))
            y = y + xc * D_param
            y = y * jax.nn.silu(z)
            return y @ out_proj_w.T

        def _forward(x, edge_index, deg_noise, gat_w, gat_a_src, gat_a_tgt, gat_b, ln_local_g, ln_local_b, ln_global_g, ln_global_b, ln2_g, ln2_b, in_proj_w, conv_w, conv_b, x_proj_w, dt_proj_w, dt_proj_b, A_log, D_param, out_proj_w, wl, wg, ff1_w, ff1_b, ff2_w, ff2_b):
            n = x.shape[0]
            src, tgt = (edge_index[0], edge_index[1])
            proj = (x @ gat_w.T).reshape(n, NH, FOUT)
            s_src = jnp.sum(proj * gat_a_src, -1)
            s_tgt = jnp.sum(proj * gat_a_tgt, -1)
            e = jax.nn.leaky_relu(s_src[src] + s_tgt[tgt], 0.2)
            exp_e = jnp.exp(e - jnp.max(e))
            denom = jax.ops.segment_sum(exp_e, tgt, num_segments=n)
            attn = exp_e / (denom[tgt] + 1e-16)
            agg = jax.ops.segment_sum(proj[src] * attn[:, :, None], tgt, num_segments=n)
            h_local = jax.nn.elu((agg + x.reshape(n, NH, FOUT)).reshape(n, NH * FOUT) + gat_b)
            h_local = _layer_norm(h_local, ln_local_g, ln_local_b)
            deg = jax.ops.segment_sum(jnp.ones((src.shape[0],), x.dtype), src, num_segments=n)
            perm = jnp.argsort(deg + deg_noise, stable=True)
            inv = jnp.argsort(perm)
            y = _mamba(x[perm], in_proj_w, conv_w, conv_b, x_proj_w, dt_proj_w, dt_proj_b, A_log, D_param, out_proj_w)
            h_attn = _layer_norm(x + y[inv], ln_global_g, ln_global_b)
            gate = jax.nn.sigmoid(h_local @ wl.T + h_attn @ wg.T)
            h = gate * h_local + (1.0 - gate) * h_attn
            ff = jax.nn.relu(h @ ff1_w.T + ff1_b) @ ff2_w.T + ff2_b
            return _layer_norm(h + ff, ln2_g, ln2_b)
        key = jax.random.key(seed)
        ks = jax.random.split(key, 24)
        w = lambda i, shape, s=0.05: jax.random.normal(ks[i], shape, dtype=jnp.float32) * s
        return {'x': jax.random.normal(ks[0], (N, D), dtype=jnp.float32), 'edge_index': jax.random.randint(ks[1], (2, E), 0, N, dtype=jnp.int32), 'edge_prob': jax.random.uniform(ks[2], (E,), dtype=jnp.float32), 'deg_noise': jax.random.uniform(ks[3], (N,), dtype=jnp.float32), 'gat_w': w(4, (NH * FOUT, D)), 'gat_a_src': w(5, (NH, FOUT)), 'gat_a_tgt': w(6, (NH, FOUT)), 'gat_b': jnp.zeros((NH * FOUT,), jnp.float32), 'ln_local_g': jnp.ones((D,), jnp.float32), 'ln_local_b': jnp.zeros((D,), jnp.float32), 'ln_global_g': jnp.ones((D,), jnp.float32), 'ln_global_b': jnp.zeros((D,), jnp.float32), 'ln2_g': jnp.ones((D,), jnp.float32), 'ln2_b': jnp.zeros((D,), jnp.float32), 'in_proj_w': w(7, (2 * D, D)), 'conv_w': w(8, (D, D_CONV), 0.2), 'conv_b': jnp.zeros((D,), jnp.float32), 'x_proj_w': w(9, (DT_RANK + 2 * D_STATE, D)), 'dt_proj_w': w(10, (D, DT_RANK)), 'dt_proj_b': w(11, (D,), 0.1) - 4.0, 'A_log': jnp.log(jnp.tile(jnp.arange(1, D_STATE + 1, dtype=jnp.float32), (D, 1))), 'D_param': jnp.ones((D,), jnp.float32), 'out_proj_w': w(12, (D, D)), 'wl': w(13, (D, D)), 'wg': w(14, (D, D)), 'ff1_w': w(15, (2 * D, D)), 'ff1_b': jnp.zeros((2 * D,), jnp.float32), 'ff2_w': w(16, (D, 2 * D)), 'ff2_b': jnp.zeros((D,), jnp.float32)}
    _L1_gnn_all = _L1_gnn_setup()
    _L1_gnn_in = {k: v for k, v in _L1_gnn_all.items() if k in ('gat_w', 'gat_a_src', 'gat_a_tgt', 'gat_b', 'ln_local_g', 'ln_local_b', 'ln_global_g', 'ln_global_b', 'ln2_g', 'ln2_b', 'in_proj_w', 'conv_w', 'conv_b', 'x_proj_w', 'dt_proj_w', 'dt_proj_b', 'A_log', 'D_param', 'out_proj_w', 'wl', 'wg', 'ff1_w', 'ff1_b', 'ff2_w', 'ff2_b')}
    del _L1_gnn_all

    def _L1_ffn_setup():
        import math
        import jax, jax.numpy as jnp
        import numpy as np
        CAPACITY_FACTOR = 1.25
        key = jax.random.key(seed)
        ks = jax.random.split(key, 5)
        B, L, D, F, E = (8, 256, 256, 1024, 8)
        h = jax.random.normal(ks[0], (B, L, D), dtype=jnp.float32)
        gate_w = jax.random.normal(ks[1], (D, E), dtype=jnp.float32) * 0.02
        gate_b = jnp.zeros((E,), dtype=jnp.float32)
        w1 = jax.random.normal(ks[2], (E, D, F), dtype=jnp.float32) * (1.0 / math.sqrt(D))
        b1 = jnp.zeros((E, F), dtype=jnp.float32)
        w2 = jax.random.normal(ks[3], (E, F, D), dtype=jnp.float32) * (1.0 / math.sqrt(F))
        b2 = jnp.zeros((E, D), dtype=jnp.float32)
        return {'h': h, 'gate_w': gate_w, 'gate_b': gate_b, 'w1': w1, 'b1': b1, 'w2': w2, 'b2': b2}
    _L1_ffn_all = _L1_ffn_setup()
    _L1_ffn_in = {k: v for k, v in _L1_ffn_all.items() if k in ('gate_w', 'gate_b', 'w1', 'b1', 'w2', 'b2')}
    del _L1_ffn_all
    return {'x': x, 'src': src, 'dst': dst, 'edge_weight': edge_weight, 'node_vec': node_vec, 'L0_gnn_weight': _L0_gnn_in['weight'], 'L0_gnn_b': _L0_gnn_in['b'], 'L0_ffn_W1': _L0_ffn_in['W1'], 'L0_ffn_b1': _L0_ffn_in['b1'], 'L0_ffn_Wg': _L0_ffn_in['Wg'], 'L0_ffn_bg': _L0_ffn_in['bg'], 'L0_ffn_Wd': _L0_ffn_in['Wd'], 'L0_ffn_bd': _L0_ffn_in['bd'], 'L1_gnn_gat_w': _L1_gnn_in['gat_w'], 'L1_gnn_gat_a_src': _L1_gnn_in['gat_a_src'], 'L1_gnn_gat_a_tgt': _L1_gnn_in['gat_a_tgt'], 'L1_gnn_gat_b': _L1_gnn_in['gat_b'], 'L1_gnn_ln_local_g': _L1_gnn_in['ln_local_g'], 'L1_gnn_ln_local_b': _L1_gnn_in['ln_local_b'], 'L1_gnn_ln_global_g': _L1_gnn_in['ln_global_g'], 'L1_gnn_ln_global_b': _L1_gnn_in['ln_global_b'], 'L1_gnn_ln2_g': _L1_gnn_in['ln2_g'], 'L1_gnn_ln2_b': _L1_gnn_in['ln2_b'], 'L1_gnn_in_proj_w': _L1_gnn_in['in_proj_w'], 'L1_gnn_conv_w': _L1_gnn_in['conv_w'], 'L1_gnn_conv_b': _L1_gnn_in['conv_b'], 'L1_gnn_x_proj_w': _L1_gnn_in['x_proj_w'], 'L1_gnn_dt_proj_w': _L1_gnn_in['dt_proj_w'], 'L1_gnn_dt_proj_b': _L1_gnn_in['dt_proj_b'], 'L1_gnn_A_log': _L1_gnn_in['A_log'], 'L1_gnn_D_param': _L1_gnn_in['D_param'], 'L1_gnn_out_proj_w': _L1_gnn_in['out_proj_w'], 'L1_gnn_wl': _L1_gnn_in['wl'], 'L1_gnn_wg': _L1_gnn_in['wg'], 'L1_gnn_ff1_w': _L1_gnn_in['ff1_w'], 'L1_gnn_ff1_b': _L1_gnn_in['ff1_b'], 'L1_gnn_ff2_w': _L1_gnn_in['ff2_w'], 'L1_gnn_ff2_b': _L1_gnn_in['ff2_b'], 'L1_ffn_gate_w': _L1_ffn_in['gate_w'], 'L1_ffn_gate_b': _L1_ffn_in['gate_b'], 'L1_ffn_w1': _L1_ffn_in['w1'], 'L1_ffn_b1': _L1_ffn_in['b1'], 'L1_ffn_w2': _L1_ffn_in['w2'], 'L1_ffn_b2': _L1_ffn_in['b2']}

def reference(x, src, dst, edge_weight, node_vec, L0_gnn_weight, L0_gnn_b, L0_ffn_W1, L0_ffn_b1, L0_ffn_Wg, L0_ffn_bg, L0_ffn_Wd, L0_ffn_bd, L1_gnn_gat_w, L1_gnn_gat_a_src, L1_gnn_gat_a_tgt, L1_gnn_gat_b, L1_gnn_ln_local_g, L1_gnn_ln_local_b, L1_gnn_ln_global_g, L1_gnn_ln_global_b, L1_gnn_ln2_g, L1_gnn_ln2_b, L1_gnn_in_proj_w, L1_gnn_conv_w, L1_gnn_conv_b, L1_gnn_x_proj_w, L1_gnn_dt_proj_w, L1_gnn_dt_proj_b, L1_gnn_A_log, L1_gnn_D_param, L1_gnn_out_proj_w, L1_gnn_wl, L1_gnn_wg, L1_gnn_ff1_w, L1_gnn_ff1_b, L1_gnn_ff2_w, L1_gnn_ff2_b, L1_ffn_gate_w, L1_ffn_gate_b, L1_ffn_w1, L1_ffn_b1, L1_ffn_w2, L1_ffn_b2):
    import jax
    import jax.numpy as jnp

    def _L0_gnn_ref(x, edge_row, edge_col, edge_val, weight, b):
        import jax, jax.numpy as jnp
        import numpy as np
        N_NODES = 3125
        N_EDGES = 100000
        D = 256
        support = x @ weight
        msgs = support[edge_col] * edge_val[:, None]
        out = jax.ops.segment_sum(msgs, edge_row, num_segments=N_NODES)
        return out + b

    def _L0_ffn_ref(x, W1, b1, Wg, bg, Wd, bd):
        import jax, jax.numpy as jnp
        import numpy as np
        C = 256
        HID = 1024
        E = 8
        TEMP = 1.0
        orig_shape = x.shape
        xf = x.reshape(-1, orig_shape[-1])
        H = jax.nn.gelu(xf @ W1 + b1, approximate=False)
        probs = jax.nn.softmax((H @ Wg + bg) / TEMP, axis=-1)
        assign = jnp.argmax(probs, axis=-1)
        out = jnp.zeros_like(xf)
        for e in range(Wd.shape[0]):
            y = H @ Wd[e] + bd[e]
            sel = (assign == e)[:, None]
            out = out + jnp.where(sel, probs[:, e:e + 1] * y, 0.0)
        return out.reshape(orig_shape)

    def _L1_gnn_ref(x, edge_index, edge_prob, deg_noise, gat_w, gat_a_src, gat_a_tgt, gat_b, ln_local_g, ln_local_b, ln_global_g, ln_global_b, ln2_g, ln2_b, in_proj_w, conv_w, conv_b, x_proj_w, dt_proj_w, dt_proj_b, A_log, D_param, out_proj_w, wl, wg, ff1_w, ff1_b, ff2_w, ff2_b):
        import jax, jax.numpy as jnp
        import numpy as np
        from jax import lax
        N, E, D = (256, 8192, 256)
        NH, FOUT = (4, 64)
        D_STATE, D_CONV, DT_RANK = (16, 4, 16)

        def _layer_norm(x, g, b, eps=1e-05):
            mu = jnp.mean(x, -1, keepdims=True)
            var = jnp.var(x, -1, keepdims=True)
            return (x - mu) * lax.rsqrt(var + eps) * g + b

        def _mamba(xs, in_proj_w, conv_w, conv_b, x_proj_w, dt_proj_w, dt_proj_b, A_log, D_param, out_proj_w):
            n = xs.shape[0]
            xz = xs @ in_proj_w.T
            xc, z = jnp.split(xz, 2, axis=-1)
            K = conv_w.shape[1]
            xp = jnp.pad(xc, ((K - 1, 0), (0, 0)))
            xc = sum((xp[k:k + n] * conv_w[:, k] for k in range(K))) + conv_b
            xc = jax.nn.silu(xc)
            dbc = xc @ x_proj_w.T
            dt = jax.nn.softplus(dbc[:, :DT_RANK] @ dt_proj_w.T + dt_proj_b)
            Bm = dbc[:, DT_RANK:DT_RANK + D_STATE]
            Cm = dbc[:, DT_RANK + D_STATE:]
            A = -jnp.exp(A_log)
            dA = jnp.exp(dt[:, :, None] * A)
            dBx = (dt * xc)[:, :, None] * Bm[:, None, :]

            def step(h, t):
                dA_t, dBx_t, C_t = t
                h = dA_t * h + dBx_t
                return (h, h @ C_t)
            _, y = lax.scan(step, jnp.zeros((xc.shape[1], D_STATE), xs.dtype), (dA, dBx, Cm))
            y = y + xc * D_param
            y = y * jax.nn.silu(z)
            return y @ out_proj_w.T

        def _forward(x, edge_index, deg_noise, gat_w, gat_a_src, gat_a_tgt, gat_b, ln_local_g, ln_local_b, ln_global_g, ln_global_b, ln2_g, ln2_b, in_proj_w, conv_w, conv_b, x_proj_w, dt_proj_w, dt_proj_b, A_log, D_param, out_proj_w, wl, wg, ff1_w, ff1_b, ff2_w, ff2_b):
            n = x.shape[0]
            src, tgt = (edge_index[0], edge_index[1])
            proj = (x @ gat_w.T).reshape(n, NH, FOUT)
            s_src = jnp.sum(proj * gat_a_src, -1)
            s_tgt = jnp.sum(proj * gat_a_tgt, -1)
            e = jax.nn.leaky_relu(s_src[src] + s_tgt[tgt], 0.2)
            exp_e = jnp.exp(e - jnp.max(e))
            denom = jax.ops.segment_sum(exp_e, tgt, num_segments=n)
            attn = exp_e / (denom[tgt] + 1e-16)
            agg = jax.ops.segment_sum(proj[src] * attn[:, :, None], tgt, num_segments=n)
            h_local = jax.nn.elu((agg + x.reshape(n, NH, FOUT)).reshape(n, NH * FOUT) + gat_b)
            h_local = _layer_norm(h_local, ln_local_g, ln_local_b)
            deg = jax.ops.segment_sum(jnp.ones((src.shape[0],), x.dtype), src, num_segments=n)
            perm = jnp.argsort(deg + deg_noise, stable=True)
            inv = jnp.argsort(perm)
            y = _mamba(x[perm], in_proj_w, conv_w, conv_b, x_proj_w, dt_proj_w, dt_proj_b, A_log, D_param, out_proj_w)
            h_attn = _layer_norm(x + y[inv], ln_global_g, ln_global_b)
            gate = jax.nn.sigmoid(h_local @ wl.T + h_attn @ wg.T)
            h = gate * h_local + (1.0 - gate) * h_attn
            ff = jax.nn.relu(h @ ff1_w.T + ff1_b) @ ff2_w.T + ff2_b
            return _layer_norm(h + ff, ln2_g, ln2_b)
        return _forward(x, edge_index, deg_noise, gat_w, gat_a_src, gat_a_tgt, gat_b, ln_local_g, ln_local_b, ln_global_g, ln_global_b, ln2_g, ln2_b, in_proj_w, conv_w, conv_b, x_proj_w, dt_proj_w, dt_proj_b, A_log, D_param, out_proj_w, wl, wg, ff1_w, ff1_b, ff2_w, ff2_b)

    def _L1_ffn_ref(h, gate_w, gate_b, w1, b1, w2, b2):
        import math
        import jax, jax.numpy as jnp
        import numpy as np
        CAPACITY_FACTOR = 1.25
        B, L, D = h.shape
        E = gate_w.shape[1]
        T = B * L
        C = max(1, math.ceil(CAPACITY_FACTOR * T / E))
        x = h.reshape(T, D)
        logits = x @ gate_w + gate_b
        probs = jax.nn.softmax(logits, axis=-1)
        idx = jnp.argmax(probs, axis=-1)
        prb = jnp.take_along_axis(probs, idx[:, None], axis=1)[:, 0]
        one_hot = jax.nn.one_hot(idx, E, dtype=jnp.float32)
        pos = (jnp.cumsum(one_hot, axis=0) * one_hot).sum(-1).astype(jnp.int32) - 1
        kept = pos < C
        pos_safe = jnp.where(kept, pos, C)
        buf = jnp.zeros((E, C, D), dtype=h.dtype).at[idx, pos_safe].set(x, mode='drop')
        hmid = jax.nn.relu(jnp.einsum('ecd,edf->ecf', buf, w1) + b1[:, None, :])
        ybuf = jnp.einsum('ecf,efd->ecd', hmid, w2) + b2[:, None, :]
        pos_g = jnp.minimum(pos, C - 1)
        y_tok = ybuf[idx, pos_g] * (prb * kept)[:, None]
        y = y_tok.reshape(B, L, D)
        y = jnp.nan_to_num(y, nan=0.0, posinf=10000.0, neginf=-10000.0)
        return y
    edge_index = jnp.stack([src, dst])
    x = x + _L0_gnn_ref(_layernorm(x, axis=-1), src, dst, edge_weight, L0_gnn_weight, L0_gnn_b)
    x = x + _L0_ffn_ref(_layernorm(x, axis=-1)[None], L0_ffn_W1, L0_ffn_b1, L0_ffn_Wg, L0_ffn_bg, L0_ffn_Wd, L0_ffn_bd)[0]
    x = x + _L1_gnn_ref(_layernorm(x, axis=-1), edge_index, edge_weight, node_vec, L1_gnn_gat_w, L1_gnn_gat_a_src, L1_gnn_gat_a_tgt, L1_gnn_gat_b, L1_gnn_ln_local_g, L1_gnn_ln_local_b, L1_gnn_ln_global_g, L1_gnn_ln_global_b, L1_gnn_ln2_g, L1_gnn_ln2_b, L1_gnn_in_proj_w, L1_gnn_conv_w, L1_gnn_conv_b, L1_gnn_x_proj_w, L1_gnn_dt_proj_w, L1_gnn_dt_proj_b, L1_gnn_A_log, L1_gnn_D_param, L1_gnn_out_proj_w, L1_gnn_wl, L1_gnn_wg, L1_gnn_ff1_w, L1_gnn_ff1_b, L1_gnn_ff2_w, L1_gnn_ff2_b)
    x = x + _L1_ffn_ref(_layernorm(x, axis=-1)[None], L1_ffn_gate_w, L1_ffn_gate_b, L1_ffn_w1, L1_ffn_b1, L1_ffn_w2, L1_ffn_b2)[0]
    return x

_drawn_inputs = setup_inputs


def setup_inputs(seed=0):
    import zlib

    import numpy as np

    out = dict(_drawn_inputs(seed))
    spreads = {'L0_ffn_b1': (0.0, 0.8),
     'L0_ffn_bg': (0.0, 0.591),
     'L0_ffn_bd': (0.0, 0.8),
     'L1_gnn_gat_b': (0.0, 0.387),
     'L1_gnn_ln_local_g': (1.0, 0.2),
     'L1_gnn_ln_local_b': (0.0, 0.332),
     'L1_gnn_ln_global_g': (1.0, 0.2),
     'L1_gnn_ln_global_b': (0.0, 0.382),
     'L1_gnn_ln2_g': (1.0, 0.2),
     'L1_gnn_ln2_b': (0.0, 0.1),
     'L1_gnn_conv_b': (0.0, 0.8),
     'L1_gnn_D_param': (1.0, 0.6),
     'L1_gnn_ff1_b': (0.0, 0.303),
     'L1_gnn_ff2_b': (0.0, 0.268),
     'L1_ffn_gate_b': (0.0, 0.294),
     'L1_ffn_b1': (0.0, 2.0),
     'L1_ffn_b2': (0.0, 0.8)}
    factors = {'node_vec': 4.328,
     'L0_ffn_W1': 4.225,
     'L0_ffn_Wg': 4.493,
     'L0_ffn_Wd': 5.185,
     'L1_gnn_gat_a_src': 2.914,
     'L1_gnn_gat_a_tgt': 22.542,
     'L1_gnn_in_proj_w': 3.56,
     'L1_gnn_conv_w': 3.813,
     'L1_gnn_x_proj_w': 8.0,
     'L1_gnn_dt_proj_w': 8.0,
     'L1_gnn_dt_proj_b': 8.0,
     'L1_gnn_A_log': 8.0,
     'L1_gnn_out_proj_w': 3.518}
    for name, (base, spread) in spreads.items():
        noise = np.random.default_rng([zlib.crc32(name.encode()), seed]).standard_normal(out[name].shape)
        drawn = base * np.exp(spread * noise) if base else spread * noise
        out[name] = jnp.asarray(drawn.astype(out[name].dtype))
    for name, factor in factors.items():
        out[name] = (out[name] * factor).astype(out[name].dtype)
    return out
```

```python
from contextlib import ExitStack

import concourse.bass as bass
from concourse import mybir

F32 = mybir.dt.float32
I32 = mybir.dt.int32
ALU = mybir.AluOpType
ACT = mybir.ActivationFunctionType
AX = mybir.AxisListType.X

P = 128
NODES, D = 3125, 256
T = -(-NODES // P)
NP = T * P
LAST = NODES - (T - 1) * P
SLOTS = 5
GROUPS = T // SLOTS
EDGES = 53125
C = 416
EP = C * P
ER, EC = 104, 512
PADNODE = NP - 1
ROW = D + 4
TABLES = 4
TROWS = NP + P
HEADS, HD = 4, 64
EPS = 1e-5
assert T == SLOTS * GROUPS and ER * EC == EP and (ER - 1) * EC < EDGES <= EP


def rounds(engine, n, body):
    body(0, True)
    with engine.Fori(1, n) as g:
        body(g, False)


def after_earlier(engine, sem, first, value):
    if not first:
        engine.wait_ge(sem, value)


def row_view(ap, n):
    return ap.rearrange("(a n) -> a n", a=1)


def setup_stage(nc, k):
    with nc.Block() as block:
        filled, loaded, rows_in = k.sem("setup_filled"), k.sem("setup_loaded"), k.sem("setup_rows_in")
        floats, rows_out = k.sem("setup_floats"), k.sem("setup_rows_out")
        turned, cols = k.sem("setup_turned"), k.sem("setup_cols")
        built, dumps = k.sem("setup_built"), k.sem("setup_dumps")
        src_i = k.stage_sb("setup_src_i", [ER, EC], I32)
        dst_i = k.stage_sb("setup_dst_i", [ER, EC], I32)
        src_r = k.stage_sb("src_r", [ER, EC], F32)
        dst_r = k.stage_sb("dst_r", [ER, EC], F32)
        w_r = k.stage_sb("w_r", [ER, EC], F32)
        dump_i = k.stage_sb("dump_i", [P, 1], I32)
        lane_i, lane_p = k.stage_sb("lane_i", [P, 32], I32), k.stage_sb("lane_p", [P, 1], I32)
        low_i = k.stage_sb("low_i", [ER, 2, EC], I32)
        low_r = k.stage_sb("low_r", [ER, 2, EC], F32)
        high_i = k.stage_sb("high_i", [P, 2, C], I32)
        tail = EDGES - (ER - 1) * EC

        @block.sync
        def _(sp):
            sp.wait_ge(filled, 5)
            sp.dma_start(k.x[:, 0:T - 1, :], k.io["x"][0:(T - 1) * P, :].rearrange("(t p) d -> p t d", p=P)).then_inc(loaded, 16)
            sp.dma_start(k.x[0:LAST, T - 1, :], k.io["x"][(T - 1) * P:NODES, :]).then_inc(loaded, 16)
            for tile, dram in ((src_i, k.io["src"]), (dst_i, k.io["dst"]), (w_r, k.io["edge_weight"])):
                sp.dma_start(tile[0:ER - 1, :], dram[0:(ER - 1) * EC].rearrange("(r c) -> r c", c=EC)).then_inc(rows_in, 16)
                sp.dma_start(tile[ER - 1:ER, 0:tail], row_view(dram[(ER - 1) * EC:EDGES], tail)).then_inc(rows_in, 16)
            sp.wait_ge(floats, 2)
            sp.dma_start(k.src_row.rearrange("(r c) -> r c", c=EC), src_r[:, :]).then_inc(rows_out, 16)
            sp.dma_start(k.dst_row.rearrange("(r c) -> r c", c=EC), dst_r[:, :]).then_inc(rows_out, 16)
            sp.wait_ge(floats, 3)
            for a in range(2):
                sp.dma_start(k.low_row[a].rearrange("(r c) -> r c", c=EC), low_r[:, a, :]).then_inc(rows_out, 16)
            with nc.allow_non_contiguous_dma(reason="12 KB as columns"):
                sp.dma_start(k.noise[:, 0:T - 1], k.io["node_vec"][0:(T - 1) * P].rearrange("(t p) -> p t", p=P)).then_inc(loaded, 16)
                sp.dma_start(k.noise[0:LAST, T - 1:T], k.io["node_vec"][(T - 1) * P:NODES].rearrange("(p a) -> p a", a=1)).then_inc(loaded, 16)
            sp.wait_ge(loaded, 64)
            sp.wait_ge(rows_out, 64)

        @block.gpsimd
        def _(pool):
            pool.memset(k.ident[:, :], 0.0).then_inc(built, 1)
            pool.memset(k.below[:, :], 1.0).then_inc(built, 1)
            pool.iota(dump_i[:, :], [[1, 1]], base=NP, channel_multiplier=1).then_inc(dumps, 1)
            pool.iota(lane_p[:, :], [[1, 1]], base=0, channel_multiplier=1).then_inc(dumps, 1)
            pool.iota(lane_i[:, :], [[1, 32]], base=0, channel_multiplier=0).then_inc(dumps, 1)
            pool.memset(k.before[:, :], 1.0).then_inc(built, 1)
            pool.wait_ge(built, 3)
            pool.affine_select(out=k.ident[:, :], in_=k.ident[:, :], compare_op=ALU.not_equal, fill=1.0, base=0,
                               pattern=[[-1, P]], channel_multiplier=1).then_inc(built, 1)
            pool.affine_select(out=k.below[:, :], in_=k.below[:, :], compare_op=ALU.is_gt, fill=0.0, base=0,
                               pattern=[[-1, P]], channel_multiplier=1).then_inc(built, 1)
            pool.affine_select(out=k.before[:, :], in_=k.before[:, :], compare_op=ALU.is_gt, fill=0.0, base=0,
                               pattern=[[1, P]], channel_multiplier=-1).then_inc(built, 1)

        @block.vector
        def _(dve):
            dve.memset(k.x[:, T - 1, :], 0.0).then_inc(filled, 1)
            dve.memset(src_i[:, :], PADNODE).then_inc(filled, 1)
            dve.memset(dst_i[:, :], PADNODE).then_inc(filled, 1)
            dve.memset(w_r[:, :], 0.0).then_inc(filled, 1)
            dve.memset(k.eps[:, :], EPS)
            dve.memset(k.dst_i[:, C:C + 8], 0)
            dve.memset(k.src_i[:, C:C + 8], 0)
            dve.memset(k.zero[:, :], 0.0)
            dve.memset(k.ones[:, :], 1.0)
            dve.memset(k.noise[:, :], 0.0).then_inc(filled, 1)
            dve.wait_ge(dumps, 3)
            dve.tensor_copy(k.own[:, :], lane_p[:, :])
            dve.tensor_copy(k.dump[:, :], dump_i[:, :])
            dve.tensor_copy(k.lane8[:, :], lane_i[:, 0:EXPERTS])
            dve.tensor_copy(k.lane32[:, :], lane_i[:, :])
            dve.wait_ge(rows_in, 96)
            dve.tensor_copy(src_r[:, :], src_i[:, :]).then_inc(floats, 1)
            dve.tensor_copy(dst_r[:, :], dst_i[:, :]).then_inc(floats, 1)
            dve.tensor_scalar(low_i[:, 0, :], src_i[:, :], P - 1, None, ALU.bitwise_and)
            dve.tensor_scalar(low_i[:, 1, :], dst_i[:, :], P - 1, None, ALU.bitwise_and)
            dve.drain()
            dve.tensor_copy(low_r[:, :, :], low_i[:, :, :]).then_inc(floats, 1)
            for a, col in enumerate((k.src_col, k.dst_col, k.w_col)):
                dve.wait_ge(turned, a + 1)
                by_row = col[:, 0:C].rearrange("p (r q) -> p q r", q=EC // P)
                dve.tensor_copy(by_row, k.ps[a][:, 0:EC // P * ER].rearrange("p (q r) -> p q r", r=ER)).then_inc(cols, 1)
            dve.drain()
            dve.tensor_copy(k.src_i[:, 0:C], k.src_col[:, 0:C])
            dve.tensor_copy(k.dst_i[:, 0:C], k.dst_col[:, 0:C])
            dve.drain()
            dve.tensor_scalar(high_i[:, 0, :], k.src_i[:, 0:C], 7, None, ALU.arith_shift_right)
            dve.tensor_scalar(high_i[:, 1, :], k.dst_i[:, 0:C], 7, None, ALU.arith_shift_right)
            dve.drain()
            dve.tensor_copy(k.high[:, :, :], high_i[:, :, :])
            dve.tensor_scalar(k.src_off[:, :], k.src_col[:, :], -1.0, k.dump[:, :], ALU.mult, ALU.add)
            dve.tensor_scalar(k.dst_off[:, :], k.dst_col[:, :], -1.0, k.dump[:, :], ALU.mult, ALU.add)

        @block.tensor
        def _(pe):
            pe.wait_ge(built, 6)
            pe.wait_ge(floats, 2)
            for a, rows in enumerate((src_r, dst_r, w_r)):
                for q in range(EC // P):
                    last = pe.transpose(k.ps[a][:, q * ER:(q + 1) * ER], rows[:, q * P:(q + 1) * P], k.ident[0:ER, 0:ER])
                last.then_inc(turned, 1)
    k.end_stage()


def norm_stats(nc, k, dve, src, sums, inv, wait_sqrt, need_sqrt):
    st = k.stats
    with dve.Fori(0, T) as t:
        dve.bn_stats(st[:, bass.ds(t * 6, 6)], src[:, t, :])
    dve.drain()
    s = st[:, :].rearrange("p (t s) -> p s t", s=6)
    dve.tensor_tensor(sums[:, 0, :], s[:, 1, :], s[:, 4, :], ALU.add)
    dve.tensor_tensor(sums[:, 1, :], s[:, 1, :], s[:, 4, :], ALU.subtract)
    dve.tensor_tensor(sums[:, 2, :], s[:, 2, :], s[:, 5, :], ALU.add)
    dve.drain()
    dve.tensor_scalar(sums[:, 0, :], sums[:, 0, :], 0.5, None, ALU.mult)
    dve.tensor_tensor(sums[:, 1, :], sums[:, 1, :], sums[:, 1, :], ALU.mult)
    dve.tensor_scalar(sums[:, 2, :], sums[:, 2, :], 1.0 / D, None, ALU.mult)
    dve.drain()
    dve.scalar_tensor_tensor(out=sums[:, 3, :], in0=sums[:, 1, :], scalar=0.25, in1=sums[:, 2, :],
                             op0=ALU.mult, op1=ALU.add).then_inc(need_sqrt, 1)
    dve.wait_ge(wait_sqrt, 1)
    dve.reciprocal(inv[:, :], sums[:, 4, :])
    dve.drain()


def support_stage(nc, k):
    with nc.Block() as block:
        weights, var_ready, dev_ready = k.sem("l0_weights"), k.sem("l0_var_ready"), k.sem("l0_dev_ready")
        normed, turned, turned_sb = k.sem("l0_normed"), k.sem("l0_turned"), k.sem("l0_turned_sb")
        multiplied, out_ready = k.sem("l0_multiplied"), k.sem("l0_out_ready")
        stored = [k.sem(f"l0_stored{j}") for j in range(SLOTS)]
        zeroed = k.sem("l0_zero_tile")
        w = k.stage_sb("l0_w", [P, 2, D], F32)
        sums = k.stage_sb("l0_sums", [P, 5, T], F32)
        inv = k.stage_sb("l0_inv", [P, T], F32)
        xn = k.stage_sb("l0_xn", [P, SLOTS, D], F32)
        xt = k.stage_sb("l0_xt", [P, SLOTS, 2, P], F32)
        out = k.stage_sb("l0_out", [P, SLOTS, D], F32)
        zeros = k.stage_sb("l0_zeros", [P, TROWS // P * ROW], F32)

        @block.sync
        def _(sp):
            sp.dma_start(w[:, :, :], k.io["L0_gnn_weight"].rearrange("(c p) n -> p c n", p=P)).then_inc(weights, 16)

            def store(g, first):
                for j in range(SLOTS):
                    sp.wait_ge(out_ready, g * SLOTS + (j + 1))
                    sp.dma_start(k.nodes_dram[bass.ds((g * SLOTS + j) * P, P), 0:D], out[:, j, :]).then_inc(stored[j], 16)

            rounds(sp, GROUPS, store)
            for j in range(SLOTS):
                sp.wait_ge(stored[j], 16 * GROUPS)

        @block.gpsimd
        def _(pool):
            pool.wait_ge(zeroed, 1)
            for a in range(TABLES):
                pool.dma_start(k.tables[0][a].rearrange("(p r) c -> p (r c)", p=P), zeros[:, :]).then_inc(k.all_scattered[0][a], 16)
            for a in range(TABLES):
                pool.wait_ge(k.all_scattered[0][a], 16)

        @block.vector
        def _(dve):
            dve.memset(zeros[:, :], 0.0).then_inc(zeroed, 1)
            norm_stats(nc, k, dve, k.x, sums, inv, dev_ready, var_ready)

            def tiles(g, first):
                for j in range(SLOTS):
                    t = g * SLOTS + j
                    after_earlier(dve, turned, first, t - (SLOTS - 1))
                    dve.tensor_scalar(xn[:, j, :], k.x[:, t, :], sums[:, 0, bass.ds(t, 1)], inv[:, bass.ds(t, 1)],
                                      ALU.subtract, ALU.mult).then_inc(normed, 1)
                for j in range(SLOTS):
                    t = g * SLOTS + j
                    dve.wait_ge(multiplied, t + 1)
                    after_earlier(dve, stored[j], first, g * 16)
                    dve.tensor_copy(out[:, j, :], k.ps[j][:, D:2 * D]).then_inc(out_ready, 1)

            rounds(dve, GROUPS, tiles)

        @block.scalar
        def _(act):
            act.preload_act_table(ACT.Sqrt)
            act.wait_ge(var_ready, 1)
            act.activation(sums[:, 4, :], sums[:, 3, :], ACT.Sqrt, bias=k.eps[:, :]).then_inc(dev_ready, 1)

            def tiles(g, first):
                for j in range(SLOTS):
                    act.wait_ge(turned, g * SLOTS + (j + 1))
                    act.activation(xt[:, j, :, :], k.ps[j][:, 0:D].rearrange("p (c n) -> p c n", c=2), ACT.Copy).then_inc(turned_sb, 1)

            rounds(act, GROUPS, tiles)

        @block.tensor
        def _(pe):
            pe.wait_ge(weights, 16)

            def tiles(g, first):
                for j in range(SLOTS):
                    t = g * SLOTS + j
                    pe.wait_ge(normed, t + 1)
                    pe.transpose(k.ps[j][:, 0:P], xn[:, j, 0:P], k.ident[:, :])
                    pe.transpose(k.ps[j][:, P:D], xn[:, j, P:D], k.ident[:, :]).then_inc(turned, 1)
                for j in range(SLOTS):
                    t = g * SLOTS + j
                    pe.wait_ge(turned_sb, t + 1)
                    for c in range(2):
                        mm = pe.matmul(k.ps[j][:, D:2 * D], xt[:, j, c, :], w[:, c, :], start=c == 0, stop=c == 1)
                    mm.then_inc(multiplied, 1)

            rounds(pe, GROUPS, tiles)
    k.end_stage()


UNROLL = 2 * TABLES
ROUNDS = C // UNROLL


def edges_stage(nc, k, name, layer, key_row, key_col, key_off, other_i, scale, ranks, scatter_i):
    H = TABLES
    table, scattered = k.tables[layer], k.all_scattered[layer]
    with nc.Block() as block:
        keys_in = [k.sem(f"{name}_keys_in{h}") for h in range(2)]
        gathered = [k.sem(f"{name}_gathered{s}") for s in range(H)]
        gather_i_ready, scatter_i_ready = k.sem(f"{name}_gather_i"), k.sem(f"{name}_scatter_i")
        scaled, summed, out_ready = k.sem(f"{name}_scaled"), k.sem(f"{name}_summed"), k.sem(f"{name}_out_ready")
        pool_step = k.sem(f"{name}_pool_step")
        half_scattered = k.sem(f"{name}_half_scattered")
        lists = [r[0] for r in ranks] or [key_row]
        keys = k.stage_sb(f"{name}_keys", [P, 2, len(lists), H * P], F32)
        gi = k.stage_sb(f"{name}_gi", [P, 2, H], I32)
        si = k.stage_sb(f"{name}_si", [P, 2, H], I32)
        rank = k.stage_sb(f"{name}_rank", [P, len(lists), H], F32)
        shift = k.stage_sb(f"{name}_shift", [P, len(lists), H], F32)
        junk = k.stage_sb(f"{name}_junk", [P, len(lists), H, P], F32)
        same = k.stage_sb(f"{name}_same", [P, H, P], F32)
        rows = k.stage_sb(f"{name}_rows", [P, H, D], F32)
        vals = k.stage_sb(f"{name}_vals", [P, H, ROW], F32)
        out = k.stage_sb(f"{name}_out", [P, H, ROW], F32)

        @block.sync
        def _(sp):
            def load(g, h, first):
                if not first:
                    sp.wait_ge(scaled, g * UNROLL + (h * H + H - UNROLL))
                for a, row in enumerate(lists):
                    sp.dma_start(keys[:, h, a, :], row[bass.ds(g * UNROLL * P + h * H * P, H * P)].partition_broadcast(P)).then_inc(keys_in[h], 16)

            rounds(sp, ROUNDS, lambda g, first: (load(g, 0, first), load(g, 1, first)))

        @block.gpsimd
        def _(pool):
            def gather(h, s):
                pool.indirect_dma_start(out=rows[:, s, :], out_offset=None, in_=k.nodes_dram,
                                        in_offset=bass.IndirectOffsetOnAxis(ap=gi[:, h, s:s + 1], axis=0)).then_inc(gathered[s], 16)

            def body(g, last):
                for h in range(2):
                    for s in range(H):
                        pool.wait_ge(out_ready, g * UNROLL + (h * H + s + 1))
                        pool.wait_ge(scattered[s], g * 32 + (h * 16 + 16))
                        pool.sem_inc(pool_step, 1)
                        pool.indirect_dma_start(out=table[s], out_offset=bass.IndirectOffsetOnAxis(ap=si[:, h, s:s + 1], axis=0),
                                                in_=out[:, s, :], in_offset=None, compute_op=ALU.add).then_inc(scattered[s], 16)
                        if s == H - 1:
                            pool.sem_inc(half_scattered, 1)
                        if not (last and h == 1):
                            pool.wait_ge(scaled, g * UNROLL + (h * H + s + 1))
                            pool.wait_ge(gather_i_ready, g * 2 + (h + 2))
                            pool.sem_inc(pool_step, 1)
                            gather(1 - h, s)

            pool.wait_ge(gather_i_ready, 1)
            for s in range(H):
                gather(0, s)
            with pool.Fori(0, ROUNDS - 1) as g:
                body(g, False)
            body(ROUNDS - 1, True)
            for s in range(H):
                pool.wait_ge(scattered[s], (2 * ROUNDS + 1) * 16)

        @block.vector
        def _(dve):
            def indices(g, h):
                dve.tensor_scalar(gi[:, h, :], other_i[:, bass.ds(g * UNROLL + h * H, H)], 0.0, None, ALU.add).then_inc(gather_i_ready, 1)

            for s in range(H):
                scale(dve, vals[:, s, :], None, None)
            dve.drain()
            indices(0, 0)

            def body(g, first):
                for h in range(2):
                    at = g * UNROLL + h * H
                    dve.wait_ge(keys_in[h], (g + 1) * (16 * len(lists)))
                    for a, (row, col, off, idx) in enumerate(ranks):
                        for s in range(H):
                            dve.scalar_tensor_tensor(out=junk[:, a, s, :], in0=keys[:, h, a, s * P:(s + 1) * P], scalar=col[:, bass.ds(at + s, 1)],
                                                     in1=k.below[:, :], op0=ALU.is_equal, op1=ALU.mult, accum_out=rank[:, a, s:s + 1])
                    if ranks:
                        dve.drain()
                        for a, (row, col, off, idx) in enumerate(ranks):
                            dve.scalar_tensor_tensor(out=shift[:, a, :], in0=rank[:, a, :], scalar=0.0, in1=off[:, bass.ds(at, H)],
                                                     op0=ALU.is_gt, op1=ALU.mult)
                        dve.drain()
                        for a, (row, col, off, idx) in enumerate(ranks):
                            dve.tensor_tensor(idx[:, bass.ds(at, H)], shift[:, a, :], col[:, bass.ds(at, H)], ALU.add)
                        dve.drain()
                    if not first:
                        dve.wait_ge(half_scattered, g * 2 + h)
                    dve.tensor_scalar(si[:, h, :], scatter_i[:, bass.ds(at, H)], 0.0, None, ALU.add).then_inc(scatter_i_ready, 1)
                    indices(g + h, 1 - h)
                    for s in range(H):
                        if not (first and h == 0):
                            dve.wait_ge(summed, at + (s + 1 - H))
                        dve.tensor_scalar(same[:, s, :], keys[:, h, 0, s * P:(s + 1) * P], key_col[:, bass.ds(at + s, 1)], None, ALU.is_equal)
                        dve.wait_ge(gathered[s], g * 32 + (h * 16 + 16))
                        scale(dve, vals[:, s, :], rows[:, s, :], at + s).then_inc(scaled, 1)

            rounds(dve, ROUNDS, body)

        @block.tensor
        def _(pe):
            def body(g, first):
                for h in range(2):
                    for s in range(H):
                        n = g * UNROLL + (h * H + s + 1)
                        pe.wait_ge(scaled, n)
                        if not (first and h == 0):
                            pe.wait_ge(out_ready, n - H)
                        pe.matmul(k.ps[s][:, 0:ROW], same[:, s, :], vals[:, s, :], start=True, stop=True).then_inc(summed, 1)

            rounds(pe, ROUNDS, body)

        @block.scalar
        def _(act):
            def body(g, first):
                for h in range(2):
                    for s in range(H):
                        if not (first and h == 0):
                            act.wait_ge(scattered[s], g * 32 + (h * 16 + 16))
                        act.wait_ge(summed, g * UNROLL + (h * H + s + 1))
                        act.activation(out[:, s, :], k.ps[s][:, 0:ROW], ACT.Copy).then_inc(out_ready, 1)

            act.wait_ge(scatter_i_ready, 1)
            act.preload_act_table(ACT.Copy)
            rounds(act, ROUNDS, body)
    k.end_stage()


def scale_by_weight(k):
    def scale(dve, vals, rows, chunk):
        if rows is None:
            dve.memset(vals[:, D + 1:ROW], 0.0)
            return dve.memset(vals[:, D:D + 1], 1.0)
        return dve.tensor_scalar(vals[:, 0:D], rows, k.w_col[:, bass.ds(chunk, 1)], None, ALU.mult)
    return scale


def combine_stage(nc, k):
    with nc.Block() as block:
        bias_in, summed, folded = k.sem("c0_bias_in"), k.sem("c0_summed"), k.sem("c0_folded")
        tables_in = [k.sem(f"c0_tables_in{h}") for h in range(2)]
        part = k.stage_sb("c0_part", [P, 2, TABLES, SLOTS, ROW], F32)
        bias = k.stage_sb("c0_bias", [P, D], F32)

        @block.sync
        def _(sp):
            sp.dma_start(bias[:, :], k.io["L0_gnn_b"].partition_broadcast(P)).then_inc(bias_in, 16)
            for g in range(GROUPS):
                if g >= 2:
                    sp.wait_ge(summed, g - 1)
                for a in range(TABLES):
                    rows = k.tables[0][a][g * SLOTS * P:(g + 1) * SLOTS * P, :].rearrange("(j p) c -> p j c", p=P)
                    sp.dma_start(part[:, g % 2, a, :, :], rows).then_inc(tables_in[g % 2], 16)

        @block.vector
        def _(dve):
            dve.wait_ge(bias_in, 16)
            for g in range(GROUPS):
                t, pt = part[:, g % 2, :, :, :], slice(g * SLOTS, (g + 1) * SLOTS)
                dve.wait_ge(tables_in[g % 2], 16 * TABLES * (g // 2 + 1))
                dve.tensor_tensor(t[:, 0:2, :, :], t[:, 0:2, :, :], t[:, 2:4, :, :], ALU.add)
                dve.tensor_tensor(k.x[:, pt, :], k.x[:, pt, :], bias[:, :].unsqueeze(1).to_broadcast([P, SLOTS, D]), ALU.add)
                dve.drain()
                dve.tensor_tensor(t[:, 0, :, :], t[:, 0, :, :], t[:, 1, :, :], ALU.add)
                dve.drain()
                dve.tensor_tensor(k.x[:, pt, :], k.x[:, pt, :], t[:, 0, :, 0:D], ALU.add)
                dve.tensor_copy(k.degree[:, pt], t[:, 0, :, D]).then_inc(summed, 1)
    k.end_stage()


EXPERTS, HID = 8, 1024
CAPACITY = -(-5 * NODES // (4 * EXPERTS))
BUF = 512
HC = HID // P
SORTED = T + EXPERTS - 1
QUAD = 4
assert SORTED % QUAD == 0


def transposer(nc, k, name, normed, turned, turned_sb, xn, xt):
    def on_pe(pe, g):
        for j in range(SLOTS):
            pe.wait_ge(normed, g * SLOTS + (j + 1))
            pe.transpose(k.ps[j][:, 0:P], xn[:, j, 0:P], k.ident[:, :])
            pe.transpose(k.ps[j][:, P:D], xn[:, j, P:D], k.ident[:, :]).then_inc(turned, 1)

    def on_act(act, g):
        for j in range(SLOTS):
            act.wait_ge(turned, g * SLOTS + (j + 1))
            act.activation(xt[:, :, j * P:(j + 1) * P], k.ps[j][:, 0:D].rearrange("p (c n) -> p c n", c=2), ACT.Copy).then_inc(turned_sb, 1)

    return on_pe, on_act


def route(nc, k, dve, name, logits, exp_ready, exp_done, mask_ready, counted, padded):
    def tile3(n):
        return k.stage_sb(f"{name}_{n}", [P, T, EXPERTS], F32)

    def tile2(n):
        return k.stage_sb(f"{name}_{n}", [P, T], F32)

    over = lambda a: a[:, :].unsqueeze(2).to_broadcast([P, T, EXPERTS])
    lane = k.lane8[:, :].unsqueeze(1).to_broadcast([P, T, EXPERTS])
    top, total, inv, first = tile2("top"), tile2("total"), tile2("total_inv"), tile2("first")
    prob, tie, hot, place = k.prob_of[name], tile3("tie"), k.hot, tile3("place")
    dve.tensor_reduce(top[:, :], logits[:, :, :], AX, ALU.max)
    dve.drain()
    dve.tensor_tensor(prob[:, :, :], logits[:, :, :], over(top), ALU.subtract).then_inc(exp_ready, 1)
    dve.wait_ge(exp_done, 1)
    dve.tensor_reduce(total[:, :], prob[:, :, :], AX, ALU.add)
    dve.drain()
    dve.reciprocal(inv[:, :], total[:, :])
    dve.drain()
    dve.tensor_tensor(prob[:, :, :], prob[:, :, :], over(inv), ALU.mult)
    dve.drain()
    dve.tensor_reduce(k.prb[:, :], prob[:, :, :], AX, ALU.max)
    dve.drain()
    dve.tensor_tensor(tie[:, :, :], prob[:, :, :], over(k.prb), ALU.is_lt)
    dve.drain()
    dve.scalar_tensor_tensor(out=tie[:, :, :], in0=tie[:, :, :], scalar=float(EXPERTS), in1=lane, op0=ALU.mult, op1=ALU.add)
    dve.drain()
    dve.tensor_reduce(first[:, :], tie[:, :, :], AX, ALU.min)
    dve.drain()
    dve.tensor_tensor(hot[:, :, :], lane, over(first), ALU.is_equal).then_inc(mask_ready, 1)
    n = T * EXPERTS
    dve.wait_ge(counted, 1)
    total8 = tile3("total8")
    run = tile3("run")
    dve.tensor_copy(total8[:, :, :], k.ps[0][:, n:2 * n].rearrange("p (t e) -> p t e", e=EXPERTS))
    dve.drain()
    for e in range(EXPERTS):
        dve.tensor_tensor_scan(run[:, :, e], total8[:, :, e], k.zero[:, :].to_broadcast([P, T]), 0.0, ALU.add, ALU.add)
    dve.drain()
    dve.tensor_tensor(place[:, :, :], run[:, :, :], total8[:, :, :], ALU.subtract)
    dve.drain()
    dve.tensor_tensor(place[:, :, :], place[:, :, :], k.ps[0][:, 0:n].rearrange("p (t e) -> p t e", e=EXPERTS), ALU.add)
    counts = run[:, T - 1, :]
    start = k.stage_sb(f"{name}_start", [P, EXPERTS], F32)
    if padded:
        tiles_i = k.stage_sb(f"{name}_tiles_i", [P, EXPERTS], I32)
        tiles_f = k.stage_sb(f"{name}_tiles_f", [P, EXPERTS], F32)
        ends = k.stage_sb(f"{name}_ends", [P, EXPERTS], F32)
        past = k.stage_sb(f"{name}_past", [P, SORTED, EXPERTS - 1], F32)
        owner = k.stage_sb(f"{name}_owner", [P, SORTED], F32)
        dve.tensor_scalar(tiles_i[:, :], counts, float(P - 1), None, ALU.add)
        dve.drain()
        dve.tensor_scalar(tiles_i[:, :], tiles_i[:, :], 7, None, ALU.arith_shift_right)
        dve.drain()
        dve.tensor_copy(tiles_f[:, :], tiles_i[:, :])
        dve.drain()
        dve.tensor_tensor_scan(ends[:, :], tiles_f[:, :], k.zero[:, :].to_broadcast([P, EXPERTS]), 0.0, ALU.add, ALU.add)
        dve.drain()
        dve.tensor_tensor(start[:, :], ends[:, :], tiles_f[:, :], ALU.subtract)
        dve.tensor_tensor(past[:, :, :], k.lane32[:, 0:SORTED].unsqueeze(2).to_broadcast([P, SORTED, EXPERTS - 1]),
                          ends[:, 0:EXPERTS - 1].unsqueeze(1).to_broadcast([P, SORTED, EXPERTS - 1]), ALU.is_ge)
        dve.drain()
        dve.tensor_scalar(start[:, :], start[:, :], float(P), None, ALU.mult)
        dve.tensor_reduce(owner[:, :], past[:, :, :], AX, ALU.add)
        dve.drain()
        dve.tensor_copy(k.owner_i[:, :], owner[:, :])
    else:
        cap = k.stage_sb(f"{name}_cap", [P, T], F32)
        dve.drain()
        dve.tensor_tensor(tie[:, :, :], place[:, :, :], hot[:, :, :], ALU.mult)
        dve.drain()
        dve.tensor_reduce(cap[:, :], tie[:, :, :], AX, ALU.add)
        dve.drain()
        dve.tensor_scalar(cap[:, :], cap[:, :], float(CAPACITY), None, ALU.is_lt)
        dve.tensor_scalar(place[:, :, :], place[:, :, :], float(CAPACITY - 1), None, ALU.min)
        dve.tensor_scalar(start[:, :], k.lane8[:, :], float(BUF), None, ALU.mult)
        dve.drain()
        dve.tensor_tensor(k.prb[:, :], k.prb[:, :], cap[:, :], ALU.mult)
    dve.drain()
    dve.tensor_tensor(place[:, :, :], place[:, :, :], start[:, :].unsqueeze(1).to_broadcast([P, T, EXPERTS]), ALU.add)
    dve.drain()
    dve.tensor_tensor(place[:, :, :], place[:, :, :], hot[:, :, :], ALU.mult)
    dve.drain()
    dve.tensor_reduce(first[:, :], place[:, :, :], AX, ALU.add)
    dve.drain()
    dve.tensor_copy(k.place_i[:, :], first[:, :])
    if padded:
        dve.tensor_copy(k.send_i[:, :], first[:, :])
    else:
        dve.tensor_scalar(cap[:, :], cap[:, :], -float(1 << 20), float(1 << 20), ALU.mult, ALU.add)
        dve.drain()
        dve.tensor_tensor(k.send_i[:, :], cap[:, :], first[:, :], ALU.add)
    dve.drain()
    return prob


def count_tokens(k, pe):
    n = T * EXPERTS
    hot = k.hot[:, :, :].rearrange("p t e -> p (t e)")
    pe.matmul(k.ps[0][:, 0:n], k.before[:, :], hot, start=True, stop=True)
    return pe.matmul(k.ps[0][:, n:2 * n], k.ones[:, :], hot, start=True, stop=True)


def ffn0_route_stage(nc, k):
    with nc.Block() as block:
        weights, var_ready, dev_ready = k.sem("f0_weights"), k.sem("f0_var_ready"), k.sem("f0_dev_ready")
        normed, turned, turned_sb = k.sem("f0_normed"), k.sem("f0_turned"), k.sem("f0_turned_sb")
        hidden, hidden_sb, gated, logit_ready = k.sem("f0_hidden"), k.sem("f0_hidden_sb"), k.sem("f0_gated"), k.sem("f0_logit_ready")
        exp_ready, exp_done, mask_ready, counted = (k.sem(f"f0_{n}") for n in ("exp_ready", "exp_done", "mask_ready", "counted"))
        placed, sent, zero_sent = k.sem("f0_placed"), k.sem("f0_sent"), k.sem("f0_zero_sent")
        w1 = k.stage_sb("f0_w1", [P, 2, HID], F32)
        wg = k.stage_sb("f0_wg", [P, HC, EXPERTS], F32)
        b1 = k.stage_sb("f0_b1", [P, HC], F32)
        bg = k.stage_sb("f0_bg", [P, EXPERTS], F32)
        sums = k.stage_sb("f0_sums", [P, 5, T], F32)
        inv = k.stage_sb("f0_inv", [P, T], F32)
        xn = k.stage_sb("f0_xn", [P, T, D], F32)
        xs = k.stage_sb("f0_xs", [P, SLOTS, D], F32)
        xt = k.stage_sb("f0_xt", [P, 2, SLOTS * P], F32)
        ht = k.stage_sb("f0_ht", [P, HC, SLOTS * P], F32)
        logits = k.stage_sb("f0_logits", [P, T, EXPERTS], F32)
        half = SLOTS * P // 2
        pe_turn, act_turn = transposer(nc, k, "f0", normed, turned, turned_sb, xs, xt)
        hbank = [k.ps[5], k.ps[6]]
        k.prob_of = {"f0": k.stage_sb("f0_prob", [P, T, EXPERTS], F32)}

        @block.sync
        def _(sp):
            sp.dma_start(w1[:, :, :], k.io["L0_ffn_W1"].rearrange("(c p) n -> p c n", p=P)).then_inc(weights, 16)
            sp.dma_start(wg[:, :, :], k.io["L0_ffn_Wg"].rearrange("(f p) e -> p f e", p=P)).then_inc(weights, 16)
            with nc.allow_non_contiguous_dma(reason="a bias of 4 KB as columns"):
                sp.dma_start(b1[:, :], k.io["L0_ffn_b1"].rearrange("(f p) -> p f", p=P)).then_inc(weights, 16)
            sp.dma_start(bg[:, :], k.io["L0_ffn_bg"].partition_broadcast(P)).then_inc(weights, 16)

        @block.vector
        def _(dve):
            norm_stats(nc, k, dve, k.x, sums, inv, dev_ready, var_ready)
            dve.wait_ge(weights, 64)

            def tiles(g, first):
                for j in range(SLOTS):
                    t = g * SLOTS + j
                    after_earlier(dve, turned, first, t - (SLOTS - 1))
                    dve.tensor_scalar(xn[:, t, :], k.x[:, t, :], sums[:, 0, bass.ds(t, 1)], inv[:, bass.ds(t, 1)], ALU.subtract, ALU.mult)
                    dve.tensor_scalar(xs[:, j, :], k.x[:, t, :], sums[:, 0, bass.ds(t, 1)], inv[:, bass.ds(t, 1)],
                                      ALU.subtract, ALU.mult).then_inc(normed, 1)
                dve.wait_ge(gated, g + 1)
                dve.tensor_tensor(logits[:, bass.ds(g * SLOTS, SLOTS), :], k.ps[7][:, 0:SLOTS * EXPERTS].rearrange("p (j e) -> p j e", e=EXPERTS),
                                  bg[:, :].unsqueeze(1).to_broadcast([P, SLOTS, EXPERTS]), ALU.add).then_inc(logit_ready, 1)

            rounds(dve, GROUPS, tiles)
            dve.drain()
            route(nc, k, dve, "f0", logits, exp_ready, exp_done, mask_ready, counted, True)
            dve.sem_inc(placed, 1)

        @block.tensor
        def _(pe):
            pe.wait_ge(weights, 64)

            def tiles(g, first):
                pe_turn(pe, g)
                pe.wait_ge(turned_sb, (g + 1) * SLOTS)
                for f in range(HC):
                    for h in range(2):
                        n = 2 * f + h
                        if not (first and n < 2):
                            pe.wait_ge(hidden_sb, g * (2 * HC) + (n - 1))
                        for c in range(2):
                            mm = pe.matmul(hbank[h][:, 0:half], w1[:, c, f * P:(f + 1) * P], xt[:, c, h * half:(h + 1) * half], start=c == 0, stop=c == 1)
                        mm.then_inc(hidden, 1)
                pe.wait_ge(hidden_sb, (g + 1) * (2 * HC))
                after_earlier(pe, logit_ready, first, g)
                for j in range(SLOTS):
                    for f in range(HC):
                        mm = pe.matmul(k.ps[7][:, j * EXPERTS:(j + 1) * EXPERTS], ht[:, f, j * P:(j + 1) * P], wg[:, f, :], start=f == 0, stop=f == HC - 1)
                mm.then_inc(gated, 1)

            rounds(pe, GROUPS, tiles)
            pe.wait_ge(mask_ready, 1)
            count_tokens(k, pe).then_inc(counted, 1)

        @block.scalar
        def _(act):
            act.preload_act_table(ACT.Sqrt)
            act.wait_ge(var_ready, 1)
            act.activation(sums[:, 4, :], sums[:, 3, :], ACT.Sqrt, bias=k.eps[:, :]).then_inc(dev_ready, 1)
            act.wait_ge(weights, 64)
            act.preload_act_table(ACT.Gelu)

            def tiles(g, first):
                act_turn(act, g)
                after_earlier(act, gated, first, g)
                for f in range(HC):
                    for h in range(2):
                        act.wait_ge(hidden, g * (2 * HC) + (2 * f + h + 1))
                        act.activation(ht[:, f, h * half:(h + 1) * half], hbank[h][:, 0:half], ACT.Gelu, bias=b1[:, f:f + 1]).then_inc(hidden_sb, 1)

            rounds(act, GROUPS, tiles)
            act.wait_ge(exp_ready, 1)
            act.activation(k.prob_of["f0"][:, :, :], k.prob_of["f0"][:, :, :], ACT.Exp).then_inc(exp_done, 1)

        @block.gpsimd
        def _(pool):
            rows = k.sorted_dram.rearrange("(p r) d -> p r d", p=P)
            per = k.sorted_dram.shape[0] // P
            pool.wait_ge(normed, 1)
            pool.memset(k.wide_zero[:, :], 0.0).then_inc(zero_sent, 1)
            pool.wait_ge(zero_sent, 1)
            pool.dma_start(rows, k.wide_zero[:, 0:D].unsqueeze(1).to_broadcast([P, per, D])).then_inc(sent, 16)
            for a in range(TABLES):
                pool.dma_start(k.tables[1][a].rearrange("(p r) c -> p r c", p=P), k.wide_zero[:, :].unsqueeze(1).to_broadcast([P, TROWS // P, ROW]))\
                    .then_inc(k.all_scattered[1][a], 16)
            pool.wait_ge(sent, 16)
            pool.wait_ge(placed, 1)
            for t in range(T):
                pool.indirect_dma_start(out=k.sorted_dram, out_offset=bass.IndirectOffsetOnAxis(ap=k.send_i[:, t:t + 1], axis=0),
                                        in_=xn[:, t, :], in_offset=None).then_inc(sent, 16)
            pool.wait_ge(sent, 16 * (T + 1))
    k.end_stage()


def ffn0_experts_stage(nc, k):
    with nc.Block() as block:
        weights, rows_in = k.sem("x0_weights"), k.sem("x0_rows_in")
        turned, turned_sb, hidden, hidden_sb = (k.sem(f"x0_{n}") for n in ("turned", "turned_sb", "hidden", "hidden_sb"))
        product, out_ready = k.sem("x0_product"), k.sem("x0_out_ready")
        stored = [k.sem(f"x0_stored{j}") for j in range(QUAD)]
        w1 = k.stage_sb("x0_w1", [P, 2, HID], F32)
        b1 = k.stage_sb("x0_b1", [P, HC], F32)
        wd = k.stage_sb("x0_wd", [P, EXPERTS, HC, D], F32)
        bd = k.stage_sb("x0_bd", [1, EXPERTS, D], F32)
        xs = k.stage_sb("x0_xs", [P, QUAD, D], F32)
        xt = k.stage_sb("x0_xt", [P, 2, QUAD * P], F32)
        ht = k.stage_sb("x0_ht", [P, HC, QUAD * P], F32)
        out = k.stage_sb("x0_out", [P, QUAD, D], F32)
        n_rounds = SORTED // QUAD

        @block.sync
        def _(sp):
            sp.dma_start(w1[:, :, :], k.io["L0_ffn_W1"].rearrange("(c p) n -> p c n", p=P)).then_inc(weights, 16)
            with nc.allow_non_contiguous_dma(reason="a bias of 4 KB as columns"):
                sp.dma_start(b1[:, :], k.io["L0_ffn_b1"].rearrange("(f p) -> p f", p=P)).then_inc(weights, 16)
            sp.dma_start(bd[:, :, :], k.io["L0_ffn_bd"].unsqueeze(0)).then_inc(weights, 16)
            for e in range(EXPERTS):
                sp.dma_start(wd[:, e, :, :], k.io["L0_ffn_Wd"][e].rearrange("(f p) n -> p f n", p=P)).then_inc(weights, 16)

            def tiles(g, first):
                after_earlier(sp, turned, first, g * QUAD)
                sp.dma_start(xs[:, :, :], k.sorted_dram[bass.ds(g * QUAD * P, QUAD * P), :].rearrange("(j p) d -> p j d", p=P)).then_inc(rows_in, 16)
                for j in range(QUAD):
                    sp.wait_ge(out_ready, g * QUAD + (j + 1))
                    sp.dma_start(k.result_dram[bass.ds((g * QUAD + j) * P, P), :], out[:, j, :]).then_inc(stored[j], 16)

            rounds(sp, n_rounds, tiles)
            for j in range(QUAD):
                sp.wait_ge(stored[j], 16 * n_rounds)

        @block.tensor
        def _(pe):
            pe.wait_ge(weights, (3 + EXPERTS) * 16)

            def tiles(g, first):
                pe.wait_ge(rows_in, g * 16 + 16)
                for j in range(QUAD):
                    pe.transpose(k.ps[j][:, 0:P], xs[:, j, 0:P], k.ident[:, :])
                    pe.transpose(k.ps[j][:, P:D], xs[:, j, P:D], k.ident[:, :]).then_inc(turned, 1)
                pe.wait_ge(turned_sb, g * QUAD + QUAD)
                for f in range(HC):
                    if not (first and f < 2):
                        pe.wait_ge(hidden_sb, g * HC + (f - 1))
                    for c in range(2):
                        mm = pe.matmul(k.ps[4 + f % 2][:, :], w1[:, c, f * P:(f + 1) * P], xt[:, c, :], start=c == 0, stop=c == 1)
                    mm.then_inc(hidden, 1)
                pe.wait_ge(hidden_sb, g * HC + HC)
                for j in range(QUAD):
                    e = pe.value_load(k.owner_i[0:1, bass.ds(g * QUAD + j, 1)], min_val=0, max_val=EXPERTS - 1)
                    if not (first and j < 2):
                        pe.wait_ge(out_ready, g * QUAD + (j - 1))
                    bank = k.ps[6 + j % 2]
                    for f in range(HC):
                        pe.matmul(bank[:, 0:D], ht[:, f, j * P:(j + 1) * P], wd[:, bass.ds(e, 1), f, :].rearrange("p a n -> p (a n)"), start=f == 0, stop=False)
                    pe.matmul(bank[:, 0:D], k.ones[0:1, :], bd[0:1, bass.ds(e, 1), :].rearrange("p a n -> p (a n)"), start=False, stop=True).then_inc(product, 1)

            rounds(pe, n_rounds, tiles)

        @block.scalar
        def _(act):
            act.wait_ge(weights, (3 + EXPERTS) * 16)
            act.preload_act_table(ACT.Gelu)

            def tiles(g, first):
                for j in range(QUAD):
                    act.wait_ge(turned, g * QUAD + (j + 1))
                    act.activation(xt[:, :, j * P:(j + 1) * P], k.ps[j][:, 0:D].rearrange("p (c n) -> p c n", c=2), ACT.Copy).then_inc(turned_sb, 1)
                after_earlier(act, product, first, g * QUAD)
                for f in range(HC):
                    act.wait_ge(hidden, g * HC + (f + 1))
                    act.activation(ht[:, f, :], k.ps[4 + f % 2][:, :], ACT.Gelu, bias=b1[:, f:f + 1]).then_inc(hidden_sb, 1)

            rounds(act, n_rounds, tiles)

        @block.vector
        def _(dve):
            def tiles(g, first):
                for j in range(QUAD):
                    after_earlier(dve, stored[j], first, g * 16)
                    dve.wait_ge(product, g * QUAD + (j + 1))
                    dve.tensor_copy(out[:, j, :], k.ps[6 + j % 2][:, 0:D]).then_inc(out_ready, 1)

            rounds(dve, n_rounds, tiles)
    k.end_stage()


def ffn0_return_stage(nc, k):
    with nc.Block() as block:
        back = [k.sem(f"r0_back{j}") for j in range(T)]
        rows = k.stage_sb("r0_rows", [P, T, D], F32)

        @block.gpsimd
        def _(pool):
            for t in range(T):
                pool.indirect_dma_start(out=rows[:, t, :], out_offset=None, in_=k.result_dram,
                                        in_offset=bass.IndirectOffsetOnAxis(ap=k.place_i[:, t:t + 1], axis=0)).then_inc(back[t], 16)

        @block.vector
        def _(dve):
            for t in range(T):
                dve.wait_ge(back[t], 16)
                dve.scalar_tensor_tensor(out=k.x[:, t, :], in0=rows[:, t, :], scalar=k.prb[:, t:t + 1], in1=k.x[:, t, :], op0=ALU.mult, op1=ALU.add)
    k.end_stage()


def by_tile(big):
    return big[:, :, :].rearrange("p c n -> p (c n)").rearrange("p (t d) -> p t d", d=D)


def l1_pre_stage(nc, k):
    with nc.Block() as block:
        weights, var_ready, dev_ready = k.sem("p1_weights"), k.sem("p1_var_ready"), k.sem("p1_dev_ready")
        normed, turned, turned_sb = k.sem("p1_normed"), k.sem("p1_turned"), k.sem("p1_turned_sb")
        product, out_ready = k.sem("p1_product"), k.sem("p1_out_ready")
        zeroed, spread, folded, folded_sb = (k.sem(f"p1_{n}") for n in ("zeroed", "spread", "folded", "folded_sb"))
        keyed, masked, key_turned, key_sb, key_out, key_in = (k.sem(f"p1_{n}") for n in ("keyed", "masked", "key_turned", "key_sb", "key_out", "key_in"))
        ranked, sent = k.sem("p1_ranked"), k.sem("p1_sent")
        stored = [k.sem(f"p1_stored{j}") for j in range(SLOTS)]
        wn = k.stage_sb("p1_wn", [P, 2, D], F32)
        w = k.stage_sb("p1_w", [P, 2, D + 2 * HEADS], F32)
        acol = k.stage_sb("p1_acol", [P, 2, 2], F32)
        amat = k.stage_sb("p1_amat", [P, 2, 2 * HEADS], F32)
        sums = k.stage_sb("p1_sums", [P, 5, T], F32)
        inv = k.stage_sb("p1_inv", [P, T], F32)
        xn = k.stage_sb("p1_xn", [P, T, D], F32)
        xs = k.stage_sb("p1_xs", [P, SLOTS, D], F32)
        xt = k.stage_sb("p1_xt", [P, 2, SLOTS * P], F32)
        out = k.stage_sb("p1_out", [P, SLOTS, D], F32)
        key = k.stage_sb("p1_key", [P, T], F32)
        key_t = k.stage_sb("p1_key_t", [T, P], F32)
        keys = k.stage_sb("p1_keys", [P, NP], F32)
        junk = k.stage_sb("p1_junk", [P, NP], F32)
        count = k.stage_sb("p1_count", [P, 4, T], F32)
        rank = k.stage_sb("p1_rank", [P, T], F32)
        pe_turn, act_turn = transposer(nc, k, "p1", normed, turned, turned_sb, xs, xt)

        @block.sync
        def _(sp):
            sp.dma_start(wn[:, :, :], k.io["gat_w"].rearrange("(c p) n -> p c n", p=P)).then_inc(weights, 16)
            sp.dma_start(w[:, :, 0:D], k.io["gat_w_t"].rearrange("(c p) n -> p c n", p=P)).then_inc(weights, 16)
            with nc.allow_non_contiguous_dma(reason="2 KB as columns"):
                for a, v in enumerate((k.io["L1_gnn_gat_a_src"], k.io["L1_gnn_gat_a_tgt"])):
                    sp.dma_start(acol[:, a, :], v.rearrange("h f -> (h f)").rearrange("(c p) -> p c", p=P)).then_inc(weights, 16)
            sp.wait_ge(key_sb, 1)
            sp.dma_start(k.order_row.rearrange("(t p) -> t p", p=P), key_t[:, :]).then_inc(key_out, 16)
            sp.wait_ge(key_out, 16)
            sp.dma_start(keys[:, :], k.order_row.partition_broadcast(P)).then_inc(key_in, 16)

            def store(g, first):
                for j in range(SLOTS):
                    sp.wait_ge(out_ready, g * SLOTS + (j + 1))
                    sp.dma_start(k.nodes_dram[bass.ds((g * SLOTS + j) * P, P), :], out[:, j, :]).then_inc(stored[j], 16)

            rounds(sp, GROUPS, store)
            for j in range(SLOTS):
                sp.wait_ge(stored[j], 16 * GROUPS)

        @block.gpsimd
        def _(pool):
            pool.wait_ge(keyed, 1)
            pool.affine_select(out=key[:, :], in_=key[:, :], compare_op=ALU.is_ge, fill=1e30, base=NODES - 1,
                               pattern=[[-P, T]], channel_multiplier=-1).then_inc(masked, 1)
            pool.wait_ge(ranked, 1)
            for t in range(T):
                pool.indirect_dma_start(out=k.by_rank_dram, out_offset=bass.IndirectOffsetOnAxis(ap=k.rank_i[:, t:t + 1], axis=0),
                                        in_=xn[:, t, :], in_offset=None).then_inc(sent, 16)
            pool.wait_ge(sent, 16 * T)

        @block.vector
        def _(dve):
            dve.memset(amat[:, :, :], 0.0)
            dve.tensor_tensor(key[:, :], k.degree[:, :], k.noise[:, :], ALU.add).then_inc(keyed, 1)
            dve.drain()
            dve.wait_ge(weights, 64)
            for a in range(2):
                for c in range(2):
                    for b in range(2):
                        lanes = slice(b * HD, (b + 1) * HD)
                        last = dve.tensor_copy(amat[lanes, c, a * HEADS + 2 * c + b:a * HEADS + 2 * c + b + 1], acol[lanes, a, c:c + 1])
            last.then_inc(spread, 1)
            dve.wait_ge(folded, 1)
            dve.tensor_copy(w[:, :, D:D + 2 * HEADS], k.ps[7][:, 0:4 * HEADS].rearrange("p (c a) -> p c a", c=2)).then_inc(folded_sb, 1)
            norm_stats(nc, k, dve, k.x, sums, inv, dev_ready, var_ready)

            def tiles(g, first):
                for j in range(SLOTS):
                    t = g * SLOTS + j
                    after_earlier(dve, turned, first, t - (SLOTS - 1))
                    dve.tensor_scalar(xn[:, t, :], k.x[:, t, :], sums[:, 0, bass.ds(t, 1)], inv[:, bass.ds(t, 1)], ALU.subtract, ALU.mult)
                    dve.tensor_scalar(xs[:, j, :], k.x[:, t, :], sums[:, 0, bass.ds(t, 1)], inv[:, bass.ds(t, 1)],
                                      ALU.subtract, ALU.mult).then_inc(normed, 1)
                for j in range(SLOTS):
                    t = g * SLOTS + j
                    bank = k.ps[5 + j % 3]
                    dve.wait_ge(product, t + 1)
                    after_earlier(dve, stored[j], first, g * 16)
                    dve.tensor_scalar(k.score[:, bass.ds(t, 1), :], bank[:, D:D + 2 * HEADS].unsqueeze(1), 0.0, None, ALU.add)
                    dve.tensor_copy(out[:, j, :], bank[:, 0:D]).then_inc(out_ready, 1)

            rounds(dve, GROUPS, tiles)
            dve.wait_ge(key_in, 16)
            dve.memset(count[:, :, :], 0.0)
            for t in range(T):
                own, end = key[:, t:t + 1], (t + 1) * P
                dve.drain()
                if t > 0:
                    dve.tensor_scalar(junk[:, 0:t * P], keys[:, 0:t * P], own, 0.0, ALU.is_le, ALU.add, accum_out=count[:, 0, t:t + 1])
                dve.tensor_scalar(junk[:, t * P:NP], keys[:, t * P:NP], own, 0.0, ALU.is_lt, ALU.add, accum_out=count[:, 1, t:t + 1])
                dve.drain()
                dve.scalar_tensor_tensor(out=junk[:, 0:P], in0=keys[:, t * P:end], scalar=own, in1=k.below[:, :],
                                         op0=ALU.is_equal, op1=ALU.mult, accum_out=count[:, 2, t:t + 1])
            dve.drain()
            dve.tensor_tensor(rank[:, :], count[:, 0, :], count[:, 1, :], ALU.add)
            dve.drain()
            dve.tensor_tensor(k.rank_i[:, :], rank[:, :], count[:, 2, :], ALU.add).then_inc(ranked, 1)

        @block.tensor
        def _(pe):
            pe.wait_ge(masked, 1)
            pe.transpose(k.ps[0][0:T, 0:P], key[:, :], k.ident[:, :]).then_inc(key_turned, 1)
            pe.wait_ge(weights, 64)
            pe.wait_ge(spread, 1)
            for ci in range(2):
                for c in range(2):
                    mm = pe.matmul(k.ps[7][:, ci * 2 * HEADS:(ci + 1) * 2 * HEADS], wn[:, c, ci * P:(ci + 1) * P], amat[:, c, :], start=c == 0, stop=c == 1)
            mm.then_inc(folded, 1)
            pe.wait_ge(folded_sb, 1)
            pe.wait_ge(key_sb, 1)

            def tiles(g, first):
                pe_turn(pe, g)
                pe.wait_ge(turned_sb, (g + 1) * SLOTS)
                for j in range(SLOTS):
                    if not (first and j < 2):
                        pe.wait_ge(out_ready, g * SLOTS + (j - 1))
                    for c in range(2):
                        mm = pe.matmul(k.ps[5 + j % 3][:, 0:D + 2 * HEADS], xt[:, c, j * P:(j + 1) * P], w[:, c, :], start=c == 0, stop=c == 1)
                    mm.then_inc(product, 1)

            rounds(pe, GROUPS, tiles)

        @block.scalar
        def _(act):
            act.preload_act_table(ACT.Sqrt)
            act.wait_ge(key_turned, 1)
            act.activation(key_t[:, :], k.ps[0][0:T, 0:P], ACT.Copy).then_inc(key_sb, 1)
            act.wait_ge(var_ready, 1)
            act.activation(sums[:, 4, :], sums[:, 3, :], ACT.Sqrt, bias=k.eps[:, :]).then_inc(dev_ready, 1)
            rounds(act, GROUPS, lambda g, first: act_turn(act, g))
    k.end_stage()


def attention_stage(nc, k):
    H = 4
    with nc.Block() as block:
        lows_in = [k.sem(f"a1_lows_in{h}") for h in range(2)]
        split, hot_ready, picked, taken = (k.sem(f"a1_{n}") for n in ("split", "hot_ready", "picked", "taken"))
        whole, masked, own_max, all_max, max_ready, done = (k.sem(f"a1_{n}") for n in ("whole", "masked", "own_max", "all_max", "max_ready", "done"))
        lows = k.stage_sb("a1_lows", [P, 2, 2, H * P], F32)
        hot = k.stage_sb("a1_hot", [P, 2, 2, H * P], F32)
        table = k.stage_sb("a1_table", [P, 2, T, HEADS], F32)
        tile = k.stage_sb("a1_tile", [P, 2, H, T], F32)
        part = k.stage_sb("a1_part", [P, 2, H, HEADS, T], F32)
        both = k.stage_sb("a1_both", [P, 2, H, HEADS], F32)
        scaled = k.stage_sb("a1_scaled", [P, C, HEADS], F32)
        top = k.stage_sb("a1_top", [P, 1], F32)
        top_all = k.stage_sb("a1_top_all", [P, 1], F32)
        minus = k.stage_sb("a1_minus", [P, 1], F32)

        @block.sync
        def _(sp):
            def load(g, first):
                for h in range(2):
                    after_earlier(sp, hot_ready, first, g * 2 + (h - 1))
                    for a in range(2):
                        sp.dma_start(lows[:, h, a, :], k.low_row[a][bass.ds(g * UNROLL * P + h * H * P, H * P)].partition_broadcast(P)).then_inc(lows_in[h], 16)

            rounds(sp, ROUNDS, load)

        @block.vector
        def _(dve):
            for a in range(2):
                last = dve.tensor_copy(table[:, a, :, :], k.score[:, :, a * HEADS:(a + 1) * HEADS])
            last.then_inc(split, 1)
            lane = k.lane32[:, 0:T].unsqueeze(1).to_broadcast([P, H, T])

            def body(g, first):
                for h in range(2):
                    dve.wait_ge(lows_in[h], (g + 1) * 32)
                    if not first:
                        dve.wait_ge(picked, g * 2 + (h - 1))
                    dve.tensor_scalar(hot[:, h, :, :], lows[:, h, :, :], k.own[:, :], None, ALU.is_equal).then_inc(hot_ready, 1)
                for h in range(2):
                    at = g * UNROLL + h * H
                    for a in range(2):
                        dve.tensor_tensor(tile[:, a, :, :], k.high[:, a, bass.ds(at, H)].unsqueeze(2).to_broadcast([P, H, T]), lane, ALU.is_equal)
                    dve.drain()
                    dve.wait_ge(picked, g * 2 + (h + 1))
                    for a in range(2):
                        got = k.ps[2 * h + a][:, 0:H * T * HEADS].rearrange("p (c a h) -> p c h a", c=H, a=T)
                        last = dve.tensor_tensor(part[:, a, :, :, :], got, tile[:, a, :, :].unsqueeze(2).to_broadcast([P, H, HEADS, T]), ALU.mult)
                    last.then_inc(taken, 1)
                    dve.drain()
                    dve.tensor_reduce(both[:, :, :, :], part[:, :, :, :, :], AX, ALU.add)
                    dve.drain()
                    dve.tensor_tensor(k.attn[:, bass.ds(at, H), :], both[:, 0, :, :], both[:, 1, :, :], ALU.add)

            rounds(dve, ROUNDS, body)
            dve.drain()
            dve.scalar_tensor_tensor(out=k.attn[:, :, :], in0=k.attn[:, :, :], scalar=0.2, in1=k.attn[:, :, :], op0=ALU.mult, op1=ALU.max)\
               .then_inc(whole, 1)
            dve.wait_ge(masked, 1)
            dve.tensor_reduce(top[:, :], k.attn[:, :, :].rearrange("p c h -> p (c h)"), AX, ALU.max).then_inc(own_max, 1)
            dve.wait_ge(all_max, 1)
            dve.tensor_scalar(minus[:, :], top_all[:, :], -1.0, None, ALU.mult).then_inc(max_ready, 1)

        @block.tensor
        def _(pe):
            pe.wait_ge(split, 1)

            def body(g, first):
                for h in range(2):
                    pe.wait_ge(hot_ready, g * 2 + (h + 1))
                    after_earlier(pe, taken, first, g * 2 + (h - 1))
                    for a in range(2):
                        for c in range(H):
                            mm = pe.matmul(k.ps[2 * h + a][:, c * T * HEADS:(c + 1) * T * HEADS], hot[:, h, a, c * P:(c + 1) * P],
                                           table[:, a, :, :].rearrange("p t h -> p (t h)"), start=True, stop=True)
                    mm.then_inc(picked, 1)

            rounds(pe, ROUNDS, body)

        @block.gpsimd
        def _(pool):
            pool.wait_ge(whole, 1)
            pool.affine_select(out=k.attn[:, C - 1, :], in_=k.attn[:, C - 1, :], compare_op=ALU.is_ge, fill=-1e30,
                               base=EDGES - (C - 1) * P - 1, pattern=[[0, HEADS]], channel_multiplier=-1).then_inc(masked, 1)
            pool.wait_ge(own_max, 1)
            pool.partition_all_reduce(top_all[:, :], top[:, :], P, bass.bass_isa.ReduceOp.max).then_inc(all_max, 1)

        @block.scalar
        def _(act):
            act.wait_ge(max_ready, 1)
            act.activation(k.attn[:, :, :], k.attn[:, :, :], ACT.Exp, bias=minus[:, :]).then_inc(done, 1)
            act.wait_ge(done, 1)
    k.end_stage()


def scale_by_attention(k):
    def scale(dve, vals, rows, chunk):
        if rows is None:
            return None
        own = k.attn[:, bass.ds(chunk, 1), :].rearrange("p a h -> p (a h)")
        dve.tensor_tensor(vals[:, 0:D].rearrange("p (h f) -> p h f", f=HD), rows.rearrange("p (h f) -> p h f", f=HD),
                          own.unsqueeze(2).to_broadcast([P, HEADS, HD]), ALU.mult)
        return dve.tensor_scalar(vals[:, D:ROW], own, 0.0, None, ALU.add)
    return scale


STATES, DT_RANK, TAPS = 16, 16, 4
HALF = SLOTS * P // 2
LOG1P = (1.0, -0.4999990463256836, 0.33330005407333374, -0.24954558908939362, 0.19678117334842682, -0.15311862528324127,
         0.10614264756441116, -0.057064201682806015, 0.019907161593437195, -0.003256378462538123)


def mamba_in_stage(nc, k):
    with nc.Block() as block:
        weights = k.sem("m1_weights")
        rows_in, turned, turned_sb = k.sem("m1_rows_in"), k.sem("m1_turned"), k.sem("m1_turned_sb")
        product, evicted, edge = k.sem("m1_product"), k.sem("m1_evicted"), k.sem("m1_edge")
        convolved, gated = k.sem("m1_convolved"), k.sem("m1_gated")
        low_rank, low_sb, low_out, stepped, step_sb = (k.sem(f"m1_{n}") for n in ("low_rank", "low_sb", "low_out", "stepped", "step_sb"))
        small, logged, done = k.sem("m1_small"), k.sem("m1_logged"), k.sem("m1_done")
        wi = k.stage_sb("m1_wi", [P, 2, 2 * D], F32)
        wx = k.stage_sb("m1_wx", [P, 2, DT_RANK + 2 * STATES], F32)
        wdt = k.stage_sb("m1_wdt", [DT_RANK, D], F32)
        cw = k.stage_sb("m1_cw", [P, 2, TAPS], F32)
        cb = k.stage_sb("m1_cb", [P, 2], F32)
        db = k.stage_sb("m1_db", [P, 2], F32)
        xs = k.stage_sb("m1_xs", [P, SLOTS, D], F32)
        xt = k.stage_sb("m1_xt", [P, 2, SLOTS * P], F32)
        xc = k.stage_sb("m1_xc", [P, 2, NP + TAPS - 1], F32)
        low = k.stage_sb("m1_low", [DT_RANK + 2 * STATES, SLOTS * P], F32)
        bank = [k.ps[5], k.ps[6]]
        pe_turn, act_turn = transposer(nc, k, "m1", rows_in, turned, turned_sb, xs, xt)

        @block.sync
        def _(sp):
            sp.dma_start(wi[:, :, :], k.io["in_proj_w_t"].rearrange("(c p) n -> p c n", p=P)).then_inc(weights, 16)
            sp.dma_start(wx[:, :, :], k.io["x_proj_w_t"].rearrange("(c p) n -> p c n", p=P)).then_inc(weights, 16)
            sp.dma_start(wdt[:, :], k.io["dt_proj_w_t"]).then_inc(weights, 16)
            sp.dma_start(cw[:, :, :], k.io["L1_gnn_conv_w"].rearrange("(c p) n -> p c n", p=P)).then_inc(weights, 16)
            with nc.allow_non_contiguous_dma(reason="biases of 1 KB as columns"):
                sp.dma_start(cb[:, :], k.io["L1_gnn_conv_b"].rearrange("(c p) -> p c", p=P)).then_inc(weights, 16)
                sp.dma_start(db[:, :], k.io["L1_gnn_dt_proj_b"].rearrange("(c p) -> p c", p=P)).then_inc(weights, 16)
                sp.dma_start(k.d_col[:, :], k.io["L1_gnn_D_param"].rearrange("(c p) -> p c", p=P)).then_inc(weights, 16)
            sp.dma_start(k.a_mat[:, :, :], k.io["L1_gnn_A_log"].rearrange("(c p) n -> p c n", p=P)).then_inc(weights, 16)

            def load(g, first):
                after_earlier(sp, turned, first, g * SLOTS)
                sp.dma_start(xs[:, :, :], k.by_rank_dram[bass.ds(g * SLOTS * P, SLOTS * P), :].rearrange("(j p) d -> p j d", p=P)).then_inc(rows_in, 16)

            rounds(sp, GROUPS, load)

            def store(g, first):
                sp.wait_ge(low_sb, g * 2 + 2)
                sp.dma_start(k.bc_dram[:, bass.ds(g * SLOTS * P, SLOTS * P)], low[DT_RANK:, :]).then_inc(low_out, 16)

            rounds(sp, GROUPS, store)
            sp.wait_ge(low_out, 16 * GROUPS)

        @block.tensor
        def _(pe):
            pe.wait_ge(weights, 128)

            def project(g, first):
                pe.wait_ge(rows_in, (g + 1) * 16)
                for j in range(SLOTS):
                    pe.transpose(k.ps[j][:, 0:P], xs[:, j, 0:P], k.ident[:, :])
                    pe.transpose(k.ps[j][:, P:D], xs[:, j, P:D], k.ident[:, :]).then_inc(turned, 1)
                pe.wait_ge(turned_sb, (g + 1) * SLOTS)
                for o in range(4):
                    for h in range(2):
                        n = 2 * o + h
                        if not (first and n < 2):
                            pe.wait_ge(evicted, g * 8 + (n - 1))
                        for c in range(2):
                            mm = pe.matmul(bank[h][:, 0:HALF], wi[:, c, o * P:(o + 1) * P], xt[:, c, h * HALF:(h + 1) * HALF], start=c == 0, stop=c == 1)
                        mm.then_inc(product, 1)

            rounds(pe, GROUPS, project)
            pe.wait_ge(gated, 2)

            def steps(g, first):
                for h in range(2):
                    at = g * (SLOTS * P) + h * HALF
                    after_earlier(pe, low_sb, first, g * 2 + (h - 1))
                    for c in range(2):
                        mm = pe.matmul(k.ps[h][0:DT_RANK + 2 * STATES, 0:HALF], wx[:, c, :], k.u[:, c, bass.ds(at, HALF)], start=c == 0, stop=c == 1)
                    mm.then_inc(low_rank, 1)
                for h in range(2):
                    pe.wait_ge(low_sb, g * 2 + (h + 1))
                    after_earlier(pe, step_sb, first, g * 4 + (2 * h - 2))
                    for o in range(2):
                        pe.matmul(k.ps[2 + 2 * h + o][:, 0:HALF], wdt[:, o * P:(o + 1) * P], low[0:DT_RANK, h * HALF:(h + 1) * HALF], start=True, stop=True)\
                          .then_inc(stepped, 1)

            rounds(pe, GROUPS, steps)

        @block.scalar
        def _(act):
            act.wait_ge(weights, 128)
            act.activation(k.a_mat[:, :, :], k.a_mat[:, :, :], ACT.Exp)
            act.preload_act_table(ACT.Silu)

            def project(g, first):
                for j in range(SLOTS):
                    act.wait_ge(turned, g * SLOTS + (j + 1))
                    act.activation(xt[:, :, j * P:(j + 1) * P], k.ps[j][:, 0:D].rearrange("p (c n) -> p c n", c=2), ACT.Copy).then_inc(turned_sb, 1)
                for o in range(4):
                    for h in range(2):
                        at = g * (SLOTS * P) + h * HALF
                        act.wait_ge(product, g * 8 + (2 * o + h + 1))
                        if o < 2:
                            act.activation(xc[:, o, bass.ds(at + (TAPS - 1), HALF)], bank[h][:, 0:HALF], ACT.Copy).then_inc(evicted, 1)
                        else:
                            act.activation(k.zs[:, o - 2, bass.ds(at, HALF)], bank[h][:, 0:HALF], ACT.Silu).then_inc(evicted, 1)

            rounds(act, GROUPS, project)
            for c in range(2):
                act.wait_ge(convolved, c + 1)
                act.activation(k.u[:, c, :], k.u[:, c, :], ACT.Silu, bias=cb[:, c:c + 1]).then_inc(gated, 1)

            def steps(g, first):
                for h in range(2):
                    act.wait_ge(low_rank, g * 2 + (h + 1))
                    after_earlier(act, low_out, first, g * 16)
                    after_earlier(act, stepped, first, g * 4)
                    act.activation(low[:, h * HALF:(h + 1) * HALF], k.ps[h][0:DT_RANK + 2 * STATES, 0:HALF], ACT.Copy).then_inc(low_sb, 1)
                for h in range(2):
                    at = g * (SLOTS * P) + h * HALF
                    for o in range(2):
                        act.wait_ge(stepped, g * 4 + (2 * h + o + 1))
                        act.activation(k.dt[:, o, bass.ds(at, HALF)], k.ps[2 + 2 * h + o][:, 0:HALF], ACT.Identity, bias=db[:, o:o + 1]).then_inc(step_sb, 1)

            rounds(act, GROUPS, steps)
            act.drain()
            for c in range(2):
                act.activation(k.dtx[:, c, :], k.dt[:, c, :], ACT.Abs)
            act.drain()
            for c in range(2):
                act.activation(k.dtx[:, c, :], k.dtx[:, c, :], ACT.Exp, scale=-1.0).then_inc(small, 1)

        @block.vector
        def _(dve):
            dve.memset(xc[:, :, 0:TAPS - 1], 0.0)
            dve.drain()
            dve.wait_ge(weights, 128)
            dve.wait_ge(evicted, 8 * GROUPS)
            for tap in range(TAPS):
                for c in range(2):
                    if tap == 0:
                        last = dve.tensor_scalar(k.u[:, c, :], xc[:, c, 0:NP], cw[:, c, 0:1], None, ALU.mult)
                    else:
                        last = dve.scalar_tensor_tensor(out=k.u[:, c, :], in0=xc[:, c, tap:tap + NP], scalar=cw[:, c, tap:tap + 1], in1=k.u[:, c, :],
                                                        op0=ALU.mult, op1=ALU.add)
                    if tap == TAPS - 1:
                        last.then_inc(convolved, 1)
                dve.drain()
            poly = xc[:, :, 0:NP]
            for c in range(2):
                dve.wait_ge(small, c + 1)
                dve.tensor_scalar(poly[:, c, :], k.dtx[:, c, :], LOG1P[-1], None, ALU.mult)
            for coef in LOG1P[-2::-1]:
                dve.drain()
                for c in range(2):
                    dve.scalar_tensor_tensor(out=poly[:, c, :], in0=poly[:, c, :], scalar=coef, in1=k.dtx[:, c, :], op0=ALU.add, op1=ALU.mult)
            dve.drain()
            for c in range(2):
                dve.scalar_tensor_tensor(out=k.dt[:, c, :], in0=k.dt[:, c, :], scalar=0.0, in1=poly[:, c, :], op0=ALU.max, op1=ALU.add)
            dve.drain()
            for c in range(2):
                dve.tensor_tensor(k.dtx[:, c, :], k.dt[:, c, :], k.u[:, c, :], ALU.mult)
            dve.tensor_scalar(k.a_mat[:, :, :], k.a_mat[:, :, :], -1.0, None, ALU.mult)
            for c in range(2):
                dve.tensor_scalar(k.d_mat[:, c, :], k.ident[:, :], k.d_col[:, c:c + 1], None, ALU.mult)
    k.end_stage()


SPAN = 640
SPANS = NP // SPAN
SBANK = SPAN // 2


def scan_stage(nc, k):
    with nc.Block() as block:
        bc_in = [k.sem(f"s1_bc_in{b}") for b in range(2)]
        decayed, fed, scanned, weighed, summed = (k.sem(f"s1_{n}") for n in ("decayed", "fed", "scanned", "weighed", "summed"))
        read_out = k.sem("s1_read_out")
        bc = k.stage_sb("s1_bc", [P, 2, 2, SPAN], F32)
        decay = k.stage_sb("s1_decay", [P, 2, 2, SPAN], F32)
        feed = k.stage_sb("s1_feed", [P, 2, 2, SPAN], F32)
        state = k.stage_sb("s1_state", [P, 2, 2, SPAN], F32)
        weigh = k.stage_sb("s1_weigh", [P, 2, 2, SPAN], F32)
        carry = k.stage_sb("s1_carry", [P, 2, STATES], F32)
        PAIRS = STATES // 2

        @block.sync
        def _(sp):
            def load(q, m, first):
                for b in range(2):
                    n = q * STATES + m * 2 + b
                    if not first:
                        sp.wait_ge(weighed, n * 2 - 2)
                    for a in range(2):
                        row = k.bc_dram[bass.ds(m * 2 + (a * STATES + b), 1), q * SPAN:(q + 1) * SPAN].rearrange("a n -> (a n)")
                        sp.dma_start(bc[:, b, a, :], row.partition_broadcast(P)).then_inc(bc_in[b], 16)

            for q in range(SPANS):
                load(q, 0, q == 0)
                with sp.Fori(1, PAIRS) as m:
                    load(q, m, False)

        @block.scalar
        def _(act):
            act.preload_act_table(ACT.Exp)

            def step(q, m, first):
                for b in range(2):
                    for c in range(2):
                        n = (q * STATES + m * 2 + b) * 2 + c
                        if not first:
                            act.wait_ge(scanned, n - 3)
                        act.activation(decay[:, b, c, :], k.dt[:, c, q * SPAN:(q + 1) * SPAN], ACT.Exp,
                                       scale=k.a_mat[:, c, bass.ds(m * 2 + b, 1)]).then_inc(decayed, 1)

            for q in range(SPANS):
                step(q, 0, q == 0)
                with act.Fori(1, PAIRS) as m:
                    step(q, m, False)

        @block.vector
        def _(dve):
            dve.memset(carry[:, :, :], 0.0)
            dve.drain()

            def step(q, m, first):
                for b in range(2):
                    dve.wait_ge(bc_in[b], (q * PAIRS + m) * 32 + 32)
                    for c in range(2):
                        n = (q * STATES + m * 2 + b) * 2 + c
                        dve.tensor_tensor(feed[:, b, c, :], k.dtx[:, c, q * SPAN:(q + 1) * SPAN], bc[:, b, 0, :], ALU.mult)
                    dve.drain()
                    for c in range(2):
                        n = (q * STATES + m * 2 + b) * 2 + c
                        dve.wait_ge(decayed, n + 1)
                        if not first:
                            dve.wait_ge(weighed, n - 3)
                        dve.tensor_tensor_scan(state[:, b, c, :], decay[:, b, c, :], feed[:, b, c, :], carry[:, c, bass.ds(m * 2 + b, 1)],
                                               ALU.mult, ALU.add).then_inc(scanned, 1)
                    dve.drain()
                    for c in range(2):
                        dve.tensor_scalar(carry[:, c, bass.ds(m * 2 + b, 1)], state[:, b, c, SPAN - 1:SPAN], 0.0, None, ALU.add)

            for q in range(SPANS):
                step(q, 0, q == 0)
                with dve.Fori(1, PAIRS) as m:
                    step(q, m, False)
                for c in range(2):
                    for b in range(2):
                        dve.wait_ge(summed, (q + 1) * 2 * STATES)
                        at = q * SPAN + b * SBANK
                        dve.tensor_tensor(k.zs[:, c, at:at + SBANK], k.zs[:, c, at:at + SBANK], k.ps[2 * c + b][:, 0:SBANK], ALU.mult).then_inc(read_out, 1)
                dve.drain()

        @block.gpsimd
        def _(pool):
            def step(q, m, first):
                for b in range(2):
                    for c in range(2):
                        n = (q * STATES + m * 2 + b) * 2 + c
                        pool.wait_ge(scanned, n + 1)
                        if not first:
                            pool.wait_ge(summed, n - 3)
                        pool.tensor_tensor(weigh[:, b, c, :], state[:, b, c, :], bc[:, b, 1, :], ALU.mult).then_inc(weighed, 1)

            for q in range(SPANS):
                step(q, 0, q == 0)
                with pool.Fori(1, PAIRS) as m:
                    step(q, m, False)

        @block.tensor
        def _(pe):
            def step(q, m, last):
                for b in range(2):
                    for c in range(2):
                        n = (q * STATES + m * 2 + b) * 2 + c
                        pe.wait_ge(weighed, n + 1)
                        for a in range(2):
                            mm = pe.matmul(k.ps[2 * c + a][:, 0:SBANK], k.ident[:, :], weigh[:, b, c, a * SBANK:(a + 1) * SBANK],
                                           start=False, stop=last and b == 1)
                        mm.then_inc(summed, 1)

            for q in range(SPANS):
                if q > 0:
                    pe.wait_ge(read_out, 4 * q)
                for c in range(2):
                    for a in range(2):
                        at = q * SPAN + a * SBANK
                        pe.matmul(k.ps[2 * c + a][:, 0:SBANK], k.d_mat[:, c, :], k.u[:, c, at:at + SBANK], start=True, stop=False)
                with pe.Fori(0, PAIRS - 1) as m:
                    step(q, m, False)
                step(q, PAIRS - 1, True)
    k.end_stage()


def mamba_out_stage(nc, k):
    with nc.Block() as block:
        weights, copied, product, out_ready = (k.sem(f"o1_{n}") for n in ("weights", "copied", "product", "out_ready"))
        stored = [k.sem(f"o1_stored{j}") for j in range(SLOTS)]
        all_stored, back = k.sem("o1_all_stored"), k.sem("o1_back")
        w = k.stage_sb("o1_w", [P, 2, D], F32)
        yg = k.stage_sb("o1_yg", [P, 2, SLOTS * P], F32)
        out = k.stage_sb("o1_out", [P, SLOTS, D], F32)

        @block.sync
        def _(sp):
            sp.dma_start(w[:, :, :], k.io["out_proj_w_t"].rearrange("(c p) n -> p c n", p=P)).then_inc(weights, 16)

            def store(g, first):
                for j in range(SLOTS):
                    sp.wait_ge(out_ready, g * SLOTS + (j + 1))
                    sp.dma_start(k.scan_dram[bass.ds((g * SLOTS + j) * P, P), :], out[:, j, :]).then_inc(stored[j], 16)

            rounds(sp, GROUPS, store)
            for j in range(SLOTS):
                sp.wait_ge(stored[j], 16 * GROUPS)
            sp.sem_inc(all_stored, 1)

        @block.gpsimd
        def _(pool):
            pool.wait_ge(all_stored, 1)
            for t in range(T):
                pool.indirect_dma_start(out=k.ha[:, t, :], out_offset=None, in_=k.scan_dram,
                                        in_offset=bass.IndirectOffsetOnAxis(ap=k.rank_i[:, t:t + 1], axis=0)).then_inc(back, 16)
            pool.wait_ge(back, 16 * T)

        @block.scalar
        def _(act):
            act.preload_act_table(ACT.Copy)

            def copy(g, first):
                after_earlier(act, product, first, g * SLOTS)
                act.activation(yg[:, :, :], k.zs[:, :, bass.ds(g * SLOTS * P, SLOTS * P)], ACT.Copy).then_inc(copied, 1)

            rounds(act, GROUPS, copy)

        @block.tensor
        def _(pe):
            pe.wait_ge(weights, 16)

            def tiles(g, first):
                pe.wait_ge(copied, g + 1)
                for j in range(SLOTS):
                    after_earlier(pe, out_ready, first, g * SLOTS + (j + 1 - SLOTS))
                    for c in range(2):
                        mm = pe.matmul(k.ps[j][:, 0:D], yg[:, c, j * P:(j + 1) * P], w[:, c, :], start=c == 0, stop=c == 1)
                    mm.then_inc(product, 1)

            rounds(pe, GROUPS, tiles)

        @block.vector
        def _(dve):
            def tiles(g, first):
                for j in range(SLOTS):
                    after_earlier(dve, stored[j], first, g * 16)
                    dve.wait_ge(product, g * SLOTS + (j + 1))
                    dve.tensor_copy(out[:, j, :], k.ps[j][:, 0:D]).then_inc(out_ready, 1)

            rounds(dve, GROUPS, tiles)
    k.end_stage()


def l1_post_stage(nc, k):
    with nc.Block() as block:
        weights, tables_in, folded = k.sem("q1_weights"), k.sem("q1_tables_in"), k.sem("q1_folded")
        var = [k.sem(f"q1_var{i}") for i in range(4)]
        dev = [k.sem(f"q1_dev{i}") for i in range(4)]
        raw, expd = k.sem("q1_raw"), k.sem("q1_expd")
        normed, turned, turned_sb, gate_mm, gated = (k.sem(f"q1_{n}") for n in ("normed", "turned", "turned_sb", "gate_mm", "gated"))
        mixed, h_turned, h_turned_sb, hidden, hidden_sb, ff_mm = (k.sem(f"q1_{n}") for n in ("mixed", "h_turned", "h_turned_sb", "hidden", "hidden_sb", "ff_mm"))
        FF = 2 * D
        FC = FF // P
        wl, wg = k.stage_sb("q1_wl", [P, 2, D], F32), k.stage_sb("q1_wg", [P, 2, D], F32)
        f1w, f2w = k.stage_sb("q1_f1w", [P, 2, FF], F32), k.stage_sb("q1_f2w", [P, FC, D], F32)
        f1b, f2b = k.stage_sb("q1_f1b", [P, FC], F32), k.stage_sb("q1_f2b", [1, D], F32)
        gat_b = k.stage_sb("q1_gat_b", [P, D], F32)
        gains = k.stage_sb("q1_gains", [P, 3, D], F32)
        shifts = k.stage_sb("q1_shifts", [P, 3, D], F32)
        part = k.stage_sb("q1_part", [P, TABLES, SLOTS, ROW], F32)
        total = k.stage_sb("q1_total", [P, SLOTS, ROW], F32)
        den = k.stage_sb("q1_den", [P, SLOTS, HEADS], F32)
        sums = [k.stage_sb(f"q1_sums{i}", [P, 5, T], F32) for i in range(4)]
        inv = [k.stage_sb(f"q1_inv{i}", [P, T], F32) for i in range(4)]
        xg = k.stage_sb("q1_xg", [P, SLOTS, D], F32)
        ls, gs = k.stage_sb("q1_ls", [P, SLOTS, D], F32), k.stage_sb("q1_gs", [P, SLOTS, D], F32)
        gate = k.stage_sb("q1_gate", [P, SLOTS, D], F32)
        both_t = k.stage_sb("q1_both_t", [P, 4, SLOTS * P], F32)
        h_t = k.stage_sb("q1_h_t", [P, 2, SLOTS * P], F32)
        f1 = k.stage_sb("q1_f1", [P, FC, SLOTS * P], F32)
        over = lambda a: a.unsqueeze(1).to_broadcast([P, SLOTS, D])
        heads = lambda a: a.rearrange("p j (h f) -> p j h f", f=HD)

        @block.sync
        def _(sp):
            for dst, src in ((wl, k.io["wl_t"]), (wg, k.io["wg_t"]), (f1w, k.io["ff1_w_t"]), (f2w, k.io["ff2_w_t"])):
                sp.dma_start(dst[:, :, :], src.rearrange("(c p) n -> p c n", p=P)).then_inc(weights, 16)
            with nc.allow_non_contiguous_dma(reason="a bias of 2 KB as columns"):
                sp.dma_start(f1b[:, :], k.io["L1_gnn_ff1_b"].rearrange("(c p) -> p c", p=P)).then_inc(weights, 16)
            sp.dma_start(f2b[:, :], row_view(k.io["L1_gnn_ff2_b"], D)).then_inc(weights, 16)
            sp.dma_start(gat_b[:, :], k.io["L1_gnn_gat_b"].partition_broadcast(P)).then_inc(weights, 16)
            for i, (g, b) in enumerate(((k.io["L1_gnn_ln_local_g"], k.io["L1_gnn_ln_local_b"]), (k.io["L1_gnn_ln_global_g"], k.io["L1_gnn_ln_global_b"]),
                                        (k.io["L1_gnn_ln2_g"], k.io["L1_gnn_ln2_b"]))):
                sp.dma_start(gains[:, i, :], g.partition_broadcast(P)).then_inc(weights, 16)
                sp.dma_start(shifts[:, i, :], b.partition_broadcast(P)).then_inc(weights, 16)

            def load(g, first):
                after_earlier(sp, folded, first, g)
                for a in range(TABLES):
                    rows = k.tables[1][a][bass.ds(g * SLOTS * P, SLOTS * P), :].rearrange("(j p) c -> p j c", p=P)
                    sp.dma_start(part[:, a, :, :], rows).then_inc(tables_in, 16)

            rounds(sp, GROUPS, load)

        @block.vector
        def _(dve):
            norm_stats(nc, k, dve, k.x, sums[0], inv[0], dev[0], var[0])
            dve.wait_ge(weights, 13 * 16)

            def branches(g, first):
                here = bass.ds(g * SLOTS, SLOTS)
                dve.wait_ge(tables_in, (g + 1) * (16 * TABLES))
                dve.tensor_tensor(part[:, 0:2, :, :], part[:, 0:2, :, :], part[:, 2:4, :, :], ALU.add)
                for j in range(SLOTS):
                    t = g * SLOTS + j
                    dve.tensor_scalar(xg[:, j, :], k.x[:, t, :], sums[0][:, 0, bass.ds(t, 1)], inv[0][:, bass.ds(t, 1)], ALU.subtract, ALU.mult)
                dve.drain()
                dve.tensor_tensor(total[:, :, :], part[:, 0, :, :], part[:, 1, :, :], ALU.add).then_inc(folded, 1)
                dve.tensor_tensor(k.ha[:, here, :], k.ha[:, here, :], xg[:, :, :], ALU.add)
                dve.drain()
                dve.tensor_tensor(xg[:, :, :], xg[:, :, :], over(gat_b[:, :]), ALU.add)
                dve.tensor_scalar(den[:, :, :], total[:, :, D:ROW], 1e-16, None, ALU.add)
                dve.drain()
                dve.reciprocal(den[:, :, :], den[:, :, :])
                dve.drain()
                dve.tensor_tensor(heads(total[:, :, 0:D]), heads(total[:, :, 0:D]), den[:, :, :].unsqueeze(3).to_broadcast([P, SLOTS, HEADS, HD]), ALU.mult)
                dve.drain()
                dve.tensor_tensor(xg[:, :, :], xg[:, :, :], total[:, :, 0:D], ALU.add)
                dve.drain()
                dve.tensor_scalar(gate[:, :, :], xg[:, :, :], 0.0, None, ALU.min).then_inc(raw, 1)
                dve.wait_ge(expd, g + 1)
                dve.scalar_tensor_tensor(out=xg[:, :, :], in0=xg[:, :, :], scalar=0.0, in1=gate[:, :, :], op0=ALU.max, op1=ALU.add)
                dve.drain()
                dve.tensor_scalar(k.hl[:, here, :], xg[:, :, :], -1.0, None, ALU.add)
                dve.drain()

            rounds(dve, GROUPS, branches)
            norm_stats(nc, k, dve, k.hl, sums[1], inv[1], dev[1], var[1])
            norm_stats(nc, k, dve, k.ha, sums[2], inv[2], dev[2], var[2])

            def mix(g, first):
                here = bass.ds(g * SLOTS, SLOTS)
                for j in range(SLOTS):
                    t = g * SLOTS + j
                    for i, (dst, src) in enumerate(((ls, k.hl), (gs, k.ha))):
                        dve.tensor_scalar(dst[:, j, :], src[:, t, :], sums[1 + i][:, 0, bass.ds(t, 1)], inv[1 + i][:, bass.ds(t, 1)], ALU.subtract, ALU.mult)
                dve.drain()
                for i, dst in enumerate((ls, gs)):
                    dve.tensor_tensor(dst[:, :, :], dst[:, :, :], over(gains[:, i, :]), ALU.mult)
                dve.drain()
                for i, dst in enumerate((ls, gs)):
                    last = dve.tensor_tensor(dst[:, :, :], dst[:, :, :], over(shifts[:, i, :]), ALU.add)
                last.then_inc(normed, 1)
                dve.drain()
                dve.wait_ge(turned, (g + 1) * SLOTS)
                dve.tensor_tensor(ls[:, :, :], ls[:, :, :], gs[:, :, :], ALU.subtract)
                dve.drain()
                dve.wait_ge(gated, (g + 1) * SLOTS)
                dve.tensor_tensor(ls[:, :, :], ls[:, :, :], gate[:, :, :], ALU.mult)
                dve.drain()
                dve.tensor_tensor(gs[:, :, :], gs[:, :, :], ls[:, :, :], ALU.add).then_inc(mixed, 1)
                for j in range(SLOTS):
                    dve.wait_ge(ff_mm, g * SLOTS + (j + 1))
                    dve.tensor_tensor(k.hl[:, bass.ds(g * SLOTS + j, 1), :], gs[:, j:j + 1, :], k.ps[j][:, 0:D].unsqueeze(1), ALU.add)
                dve.drain()

            rounds(dve, GROUPS, mix)
            norm_stats(nc, k, dve, k.hl, sums[3], inv[3], dev[3], var[3])

            def add(g, first):
                here = bass.ds(g * SLOTS, SLOTS)
                for j in range(SLOTS):
                    t = g * SLOTS + j
                    dve.tensor_scalar(ls[:, j, :], k.hl[:, t, :], sums[3][:, 0, bass.ds(t, 1)], inv[3][:, bass.ds(t, 1)], ALU.subtract, ALU.mult)
                dve.drain()
                dve.tensor_tensor(ls[:, :, :], ls[:, :, :], over(gains[:, 2, :]), ALU.mult)
                dve.tensor_tensor(k.x[:, here, :], k.x[:, here, :], over(shifts[:, 2, :]), ALU.add)
                dve.drain()
                dve.tensor_tensor(k.x[:, here, :], k.x[:, here, :], ls[:, :, :], ALU.add)
                dve.drain()

            rounds(dve, GROUPS, add)

        @block.scalar
        def _(act):
            def root(i):
                act.wait_ge(var[i], 1)
                act.activation(sums[i][:, 4, :], sums[i][:, 3, :], ACT.Sqrt, bias=k.eps[:, :]).then_inc(dev[i], 1)

            act.preload_act_table(ACT.Sqrt)
            root(0)
            act.preload_act_table(ACT.Exp)

            def branches(g, first):
                act.wait_ge(raw, g + 1)
                act.activation(gate[:, :, :], gate[:, :, :], ACT.Exp).then_inc(expd, 1)

            rounds(act, GROUPS, branches)
            act.preload_act_table(ACT.Sqrt)
            root(1)
            root(2)
            act.wait_ge(weights, 13 * 16)
            act.preload_act_table(ACT.Sigmoid)

            def mix(g, first):
                for j in range(SLOTS):
                    act.wait_ge(turned, g * SLOTS + (j + 1))
                    act.activation(both_t[:, :, j * P:(j + 1) * P], k.ps[j][:, :].rearrange("p (c n) -> p c n", c=4), ACT.Copy).then_inc(turned_sb, 1)
                for j in range(SLOTS):
                    act.wait_ge(gate_mm, g * SLOTS + (j + 1))
                    act.activation(gate[:, j, :], k.ps[5 + j % 3][:, 0:D], ACT.Sigmoid).then_inc(gated, 1)
                for j in range(SLOTS):
                    act.wait_ge(h_turned, g * SLOTS + (j + 1))
                    act.activation(h_t[:, :, j * P:(j + 1) * P], k.ps[j][:, 0:D].rearrange("p (c n) -> p c n", c=2), ACT.Copy).then_inc(h_turned_sb, 1)
                for f in range(FC):
                    for h in range(2):
                        act.wait_ge(hidden, g * (2 * FC) + (2 * f + h + 1))
                        act.activation(f1[:, f, h * HALF:(h + 1) * HALF], k.ps[5 + h][:, 0:HALF], ACT.Relu, bias=f1b[:, f:f + 1]).then_inc(hidden_sb, 1)

            rounds(act, GROUPS, mix)
            act.preload_act_table(ACT.Sqrt)
            root(3)

        @block.tensor
        def _(pe):
            pe.wait_ge(weights, 13 * 16)

            def mix(g, first):
                pe.wait_ge(normed, g + 1)
                for j in range(SLOTS):
                    for c in range(4):
                        mm = pe.transpose(k.ps[j][:, c * P:(c + 1) * P], (ls, gs)[c // 2][:, j, (c % 2) * P:(c % 2 + 1) * P], k.ident[:, :])
                    mm.then_inc(turned, 1)
                for j in range(SLOTS):
                    pe.wait_ge(turned_sb, g * SLOTS + (j + 1))
                    if j >= 3:
                        pe.wait_ge(gated, g * SLOTS + (j - 2))
                    for c in range(4):
                        mm = pe.matmul(k.ps[5 + j % 3][:, 0:D], both_t[:, c, j * P:(j + 1) * P], (wl, wg)[c // 2][:, c % 2, :], start=c == 0, stop=c == 3)
                    mm.then_inc(gate_mm, 1)
                pe.wait_ge(mixed, g + 1)
                for j in range(SLOTS):
                    pe.transpose(k.ps[j][:, 0:P], gs[:, j, 0:P], k.ident[:, :])
                    pe.transpose(k.ps[j][:, P:D], gs[:, j, P:D], k.ident[:, :]).then_inc(h_turned, 1)
                pe.wait_ge(h_turned_sb, (g + 1) * SLOTS)
                for f in range(FC):
                    for h in range(2):
                        n = 2 * f + h
                        if n >= 2:
                            pe.wait_ge(hidden_sb, g * (2 * FC) + (n - 1))
                        for c in range(2):
                            mm = pe.matmul(k.ps[5 + h][:, 0:HALF], f1w[:, c, f * P:(f + 1) * P], h_t[:, c, h * HALF:(h + 1) * HALF], start=c == 0, stop=c == 1)
                        mm.then_inc(hidden, 1)
                pe.wait_ge(hidden_sb, (g + 1) * (2 * FC))
                for j in range(SLOTS):
                    for f in range(FC):
                        pe.matmul(k.ps[j][:, 0:D], f1[:, f, j * P:(j + 1) * P], f2w[:, f, :], start=f == 0, stop=False)
                    pe.matmul(k.ps[j][:, 0:D], k.ones[0:1, :], f2b[0:1, :], start=False, stop=True).then_inc(ff_mm, 1)

            rounds(pe, GROUPS, mix)
    k.end_stage()


def ffn1_route_stage(nc, k):
    with nc.Block() as block:
        weights, var_ready, dev_ready = k.sem("g1_weights"), k.sem("g1_var_ready"), k.sem("g1_dev_ready")
        normed, turned, turned_sb = k.sem("g1_normed"), k.sem("g1_turned"), k.sem("g1_turned_sb")
        gated, logit_ready = k.sem("g1_gated"), k.sem("g1_logit_ready")
        exp_ready, exp_done, mask_ready, counted = (k.sem(f"g1_{n}") for n in ("exp_ready", "exp_done", "mask_ready", "counted"))
        placed, sent = k.sem("g1_placed"), k.sem("g1_sent")
        wg = k.stage_sb("g1_wg", [P, 2, EXPERTS], F32)
        bg = k.stage_sb("g1_bg", [P, EXPERTS], F32)
        sums = k.stage_sb("g1_sums", [P, 5, T], F32)
        inv = k.stage_sb("g1_inv", [P, T], F32)
        xn = k.stage_sb("g1_xn", [P, T, D], F32)
        xs = k.stage_sb("g1_xs", [P, SLOTS, D], F32)
        xt = k.stage_sb("g1_xt", [P, 2, SLOTS * P], F32)
        logits = k.stage_sb("g1_logits", [P, T, EXPERTS], F32)
        pe_turn, act_turn = transposer(nc, k, "g1", normed, turned, turned_sb, xs, xt)
        k.prob_of["g1"] = k.stage_sb("g1_prob", [P, T, EXPERTS], F32)

        @block.sync
        def _(sp):
            sp.dma_start(wg[:, :, :], k.io["L1_ffn_gate_w"].rearrange("(c p) e -> p c e", p=P)).then_inc(weights, 16)
            sp.dma_start(bg[:, :], k.io["L1_ffn_gate_b"].partition_broadcast(P)).then_inc(weights, 16)

        @block.vector
        def _(dve):
            norm_stats(nc, k, dve, k.x, sums, inv, dev_ready, var_ready)
            dve.wait_ge(weights, 32)

            def tiles(g, first):
                for j in range(SLOTS):
                    t = g * SLOTS + j
                    after_earlier(dve, turned, first, t - (SLOTS - 1))
                    dve.tensor_scalar(xn[:, t, :], k.x[:, t, :], sums[:, 0, bass.ds(t, 1)], inv[:, bass.ds(t, 1)], ALU.subtract, ALU.mult)
                    dve.tensor_scalar(xs[:, j, :], k.x[:, t, :], sums[:, 0, bass.ds(t, 1)], inv[:, bass.ds(t, 1)],
                                      ALU.subtract, ALU.mult).then_inc(normed, 1)
                dve.wait_ge(gated, g + 1)
                dve.tensor_tensor(logits[:, bass.ds(g * SLOTS, SLOTS), :], k.ps[7][:, 0:SLOTS * EXPERTS].rearrange("p (j e) -> p j e", e=EXPERTS),
                                  bg[:, :].unsqueeze(1).to_broadcast([P, SLOTS, EXPERTS]), ALU.add).then_inc(logit_ready, 1)

            rounds(dve, GROUPS, tiles)
            dve.drain()
            route(nc, k, dve, "g1", logits, exp_ready, exp_done, mask_ready, counted, False)
            dve.sem_inc(placed, 1)

        @block.tensor
        def _(pe):
            pe.wait_ge(weights, 32)

            def tiles(g, first):
                pe_turn(pe, g)
                pe.wait_ge(turned_sb, (g + 1) * SLOTS)
                after_earlier(pe, logit_ready, first, g)
                for j in range(SLOTS):
                    for c in range(2):
                        mm = pe.matmul(k.ps[7][:, j * EXPERTS:(j + 1) * EXPERTS], xt[:, c, j * P:(j + 1) * P], wg[:, c, :], start=c == 0, stop=c == 1)
                mm.then_inc(gated, 1)

            rounds(pe, GROUPS, tiles)
            pe.wait_ge(mask_ready, 1)
            count_tokens(k, pe).then_inc(counted, 1)

        @block.scalar
        def _(act):
            act.preload_act_table(ACT.Sqrt)
            act.wait_ge(var_ready, 1)
            act.activation(sums[:, 4, :], sums[:, 3, :], ACT.Sqrt, bias=k.eps[:, :]).then_inc(dev_ready, 1)

            def tiles(g, first):
                after_earlier(act, gated, first, g)
                act_turn(act, g)

            rounds(act, GROUPS, tiles)
            act.wait_ge(exp_ready, 1)
            act.activation(k.prob_of["g1"][:, :, :], k.prob_of["g1"][:, :, :], ACT.Exp).then_inc(exp_done, 1)

        @block.gpsimd
        def _(pool):
            rows = k.sorted_dram.rearrange("(p r) d -> p r d", p=P)
            per = k.sorted_dram.shape[0] // P
            pool.dma_start(rows, k.wide_zero[:, 0:D].unsqueeze(1).to_broadcast([P, per, D])).then_inc(sent, 16)
            pool.wait_ge(sent, 16)
            pool.wait_ge(placed, 1)
            for t in range(T):
                pool.indirect_dma_start(out=k.sorted_dram, out_offset=bass.IndirectOffsetOnAxis(ap=k.send_i[:, t:t + 1], axis=0),
                                        in_=xn[:, t, :], in_offset=None, bounds_check=EXPERTS * BUF - 1, oob_is_err=False).then_inc(sent, 16)
            pool.wait_ge(sent, 16 * (T + 1))
    k.end_stage()


BT = BUF // P
assert EXPERTS * BUF == SORTED * P and CAPACITY <= BUF


def ffn1_experts_stage(nc, k):
    with nc.Block() as block:
        loaded = [k.sem(f"y1_loaded{s}") for s in range(2)]
        turned, turned_sb, hidden, hidden_sb = (k.sem(f"y1_{n}") for n in ("turned", "turned_sb", "hidden", "hidden_sb"))
        product, out_ready = k.sem("y1_product"), k.sem("y1_out_ready")
        stored = [k.sem(f"y1_stored{j}") for j in range(BT)]
        w1 = k.stage_sb("y1_w1", [P, 2, 2, HID], F32)
        w2 = k.stage_sb("y1_w2", [P, 2, HC, D], F32)
        b1, b2 = k.stage_sb("y1_b1", [P, 2, HC], F32), k.stage_sb("y1_b2", [1, 2, D], F32)
        xs = k.stage_sb("y1_xs", [P, 2, BT, D], F32)
        xt = k.stage_sb("y1_xt", [P, 2, BUF], F32)
        ht = k.stage_sb("y1_ht", [P, HC, BUF], F32)
        out = k.stage_sb("y1_out", [P, BT, D], F32)
        n_rounds = EXPERTS // 2

        @block.sync
        def _(sp):
            def load(r, s, first):
                e = r * 2 + s
                after_earlier(sp, product, first, e * BT - BT)
                sp.dma_start(xs[:, s, :, :], k.sorted_dram[bass.ds(e * BUF, BUF), :].rearrange("(j p) d -> p j d", p=P)).then_inc(loaded[s], 16)
                sp.dma_start(w1[:, s, :, :], k.io["L1_ffn_w1"][bass.ds(e, 1)].rearrange("a (c p) n -> p (a c) n", p=P)).then_inc(loaded[s], 16)
                sp.dma_start(w2[:, s, :, :], k.io["L1_ffn_w2"][bass.ds(e, 1)].rearrange("a (f p) n -> p (a f) n", p=P)).then_inc(loaded[s], 16)
                with nc.allow_non_contiguous_dma(reason="a bias of 4 KB as columns"):
                    sp.dma_start(b1[:, s, :], k.io["L1_ffn_b1"][bass.ds(e, 1)].rearrange("a (f p) -> p (a f)", p=P)).then_inc(loaded[s], 16)
                sp.dma_start(b2[:, s, :], k.io["L1_ffn_b2"][bass.ds(e, 1)]).then_inc(loaded[s], 16)

            load(0, 0, True)

            def tiles(r, last):
                load(r, 1, isinstance(r, int))
                for s in range(2):
                    e = r * 2 + s
                    for j in range(BT):
                        sp.wait_ge(out_ready, e * BT + (j + 1))
                        sp.dma_start(k.result_dram[bass.ds(e * BUF + j * P, P), :], out[:, j, :]).then_inc(stored[j], 16)
                    if s == 0 and not last:
                        load(r + 1, 0, False)

            tiles(0, False)
            with sp.Fori(1, n_rounds - 1) as r:
                tiles(r, False)
            tiles(n_rounds - 1, True)
            for j in range(BT):
                sp.wait_ge(stored[j], 16 * EXPERTS)

        @block.tensor
        def _(pe):
            def tiles(r, first):
                for s in range(2):
                    e = r * 2 + s
                    pe.wait_ge(loaded[s], (r + 1) * (5 * 16))
                    for j in range(BT):
                        pe.transpose(k.ps[j][:, 0:P], xs[:, s, j, 0:P], k.ident[:, :])
                        pe.transpose(k.ps[j][:, P:D], xs[:, s, j, P:D], k.ident[:, :]).then_inc(turned, 1)
                    pe.wait_ge(turned_sb, e * BT + BT)
                    for f in range(HC):
                        if not (first and s == 0 and f < 2):
                            pe.wait_ge(hidden_sb, e * HC + (f - 1))
                        for c in range(2):
                            mm = pe.matmul(k.ps[4 + f % 2][:, :], w1[:, s, c, f * P:(f + 1) * P], xt[:, c, :], start=c == 0, stop=c == 1)
                        mm.then_inc(hidden, 1)
                    pe.wait_ge(hidden_sb, e * HC + HC)
                    for j in range(BT):
                        if not (first and s == 0 and j < 2):
                            pe.wait_ge(out_ready, e * BT + (j - 1))
                        bank = k.ps[6 + j % 2]
                        for f in range(HC):
                            pe.matmul(bank[:, 0:D], ht[:, f, j * P:(j + 1) * P], w2[:, s, f, :], start=f == 0, stop=False)
                        pe.matmul(bank[:, 0:D], k.ones[0:1, :], b2[0:1, s, :], start=False, stop=True).then_inc(product, 1)

            rounds(pe, n_rounds, tiles)

        @block.scalar
        def _(act):
            act.preload_act_table(ACT.Relu)

            def tiles(r, first):
                for s in range(2):
                    e = r * 2 + s
                    act.wait_ge(loaded[s], (r + 1) * (5 * 16))
                    for j in range(BT):
                        act.wait_ge(turned, e * BT + (j + 1))
                        act.activation(xt[:, :, j * P:(j + 1) * P], k.ps[j][:, 0:D].rearrange("p (c n) -> p c n", c=2), ACT.Copy).then_inc(turned_sb, 1)
                    if not (first and s == 0):
                        act.wait_ge(product, e * BT)
                    for f in range(HC):
                        act.wait_ge(hidden, e * HC + (f + 1))
                        act.activation(ht[:, f, :], k.ps[4 + f % 2][:, :], ACT.Relu, bias=b1[:, s, f:f + 1]).then_inc(hidden_sb, 1)

            rounds(act, n_rounds, tiles)

        @block.vector
        def _(dve):
            def tiles(r, first):
                for s in range(2):
                    e = r * 2 + s
                    for j in range(BT):
                        if not (first and s == 0):
                            dve.wait_ge(stored[j], e * 16)
                        dve.wait_ge(product, e * BT + (j + 1))
                        dve.tensor_copy(out[:, j, :], k.ps[6 + j % 2][:, 0:D]).then_inc(out_ready, 1)

            rounds(dve, n_rounds, tiles)
    k.end_stage()


BIG = 3.4028234663852886e38


def ffn1_return_stage(nc, k, out):
    with nc.Block() as block:
        back = [k.sem(f"z1_back{g}") for g in range(GROUPS)]
        summed, stored = k.sem("z1_summed"), k.sem("z1_stored")
        rows = k.stage_sb("z1_rows", [P, T, D], F32)
        clamped = k.stage_sb("z1_clamped", [P, SLOTS, D], F32)
        clean = k.stage_sb("z1_clean", [P, SLOTS, D], F32)
        number = k.stage_sb("z1_number", [P, SLOTS, D], I32)
        finite = k.stage_sb("z1_finite", [P, SLOTS, D], I32)

        @block.gpsimd
        def _(pool):
            for t in range(T):
                pool.indirect_dma_start(out=rows[:, t, :], out_offset=None, in_=k.result_dram,
                                        in_offset=bass.IndirectOffsetOnAxis(ap=k.place_i[:, t:t + 1], axis=0)).then_inc(back[t // SLOTS], 16)

        @block.vector
        def _(dve):
            for g in range(GROUPS):
                here = slice(g * SLOTS, (g + 1) * SLOTS)
                z = rows[:, here, :]
                dve.wait_ge(back[g], 16 * SLOTS)
                dve.memset(clean[:, :, :], 0.0)
                dve.tensor_tensor(z, z, k.prb[:, here].unsqueeze(2).to_broadcast([P, SLOTS, D]), ALU.mult)
                dve.drain()
                dve.tensor_scalar(clamped[:, :, :], z, -1e4, 1e4, ALU.max, ALU.min)
                dve.tensor_tensor(number[:, :, :], z, z, ALU.is_equal)
                dve.tensor_scalar(finite[:, :, :], z, 0.0, 0.0, ALU.mult, ALU.is_equal)
                dve.drain()
                dve.copy_predicated(clean[:, :, :], number[:, :, :], clamped[:, :, :])
                dve.drain()
                dve.copy_predicated(clean[:, :, :], finite[:, :, :], z)
                dve.drain()
                dve.tensor_tensor(k.x[:, here, :], k.x[:, here, :], clean[:, :, :], ALU.add).then_inc(summed, 1)
                dve.drain()

        @block.sync
        def _(sp):
            for g in range(GROUPS):
                sp.wait_ge(summed, g + 1)
                full = SLOTS if g < GROUPS - 1 else SLOTS - 1
                first, n = g * SLOTS, full * P
                sp.dma_start(out[first * P:first * P + n, :].rearrange("(j p) d -> p j d", p=P), k.x[:, first:first + full, :]).then_inc(stored, 16)
            sp.dma_start(out[(T - 1) * P:NODES, :], k.x[0:LAST, T - 1, :]).then_inc(stored, 16)
            sp.wait_ge(stored, 16 * (GROUPS + 1))
    k.end_stage()


class Program:
    pass


def build(nc, io, out, upto=99, dbg=None):
    with ExitStack() as program:
        k = Program()
        k.io = io
        k.sb = lambda name, shape, dt: program.enter_context(nc.sbuf_tensor(name, shape, dt))
        k.lasting_sem = lambda name: program.enter_context(nc.semaphore(name))
        k.stage_sems = []

        def stage_sem(name):
            k.stage_sems.append(nc.alloc_semaphore(name))
            return k.stage_sems[-1]

        def end_stage():
            k.stage.close()
            nc.clear_and_free_semaphores(k.stage_sems)
            k.stage_sems = []
            nc.all_engine_barrier()

        k.sem = stage_sem
        k.stage = ExitStack()
        k.stage_sb = lambda name, shape, dt: k.stage.enter_context(nc.sbuf_tensor(name, shape, dt))
        k.end_stage = end_stage
        k.ps = [program.enter_context(nc.psum_tensor(f"bank{i}", [P, 512], F32)) for i in range(8)]
        k.x = k.sb("x", [P, T, D], F32)
        k.ident, k.below = k.sb("ident", [P, P], F32), k.sb("below", [P, P], F32)
        k.dump, k.eps, k.zero = k.sb("dump", [P, 1], F32), k.sb("eps", [P, 1], F32), k.sb("zero", [P, 1], F32)
        k.ones = k.sb("ones", [P, P], F32)
        k.noise, k.own = k.sb("noise", [P, T], F32), k.sb("own", [P, 1], F32)
        k.rank_i = k.sb("rank_i", [P, T], I32)
        k.before = k.sb("before", [P, P], F32)
        k.lane8, k.lane32 = k.sb("lane8", [P, EXPERTS], F32), k.sb("lane32", [P, 32], F32)
        k.degree, k.prb = k.sb("degree", [P, T], F32), k.sb("prb", [P, T], F32)
        k.place_i, k.send_i = k.sb("place_i", [P, T], I32), k.sb("send_i", [P, T], I32)
        k.owner_i, k.hot = k.sb("owner_i", [P, SORTED], I32), k.sb("hot", [P, T, EXPERTS], F32)
        k.wide_zero = k.sb("wide_zero", [P, ROW], F32)
        k.stats = k.sb("stats", [P, T * 6], F32)
        k.a_mat, k.d_mat, k.d_col = k.sb("a_mat", [P, 2, STATES], F32), k.sb("d_mat", [P, 2, P], F32), k.sb("d_col", [P, 2], F32)
        k.edges = ExitStack()
        program.callback(k.edges.close)
        edge_sb = lambda name, shape, dt: k.edges.enter_context(nc.sbuf_tensor(name, shape, dt))
        k.src_col, k.dst_col, k.w_col, k.src_off, k.dst_off = (edge_sb(n, [P, C], F32) for n in ("src_col", "dst_col", "w_col", "src_off", "dst_off"))
        k.src_i, k.dst_i = (edge_sb(n, [P, C + 8], I32) for n in ("src_i", "dst_i"))
        k.src_to, k.dst_to = (edge_sb(n, [P, C], I32) for n in ("src_to", "dst_to"))
        k.high = edge_sb("high", [P, 2, C], F32)

        def dram(name, shape, dt=F32):
            return nc.dram_tensor(name, shape, dt, kind="Internal").ap()

        k.src_row, k.dst_row = dram("src_row", (EP,)), dram("dst_row", (EP,))
        k.low_row = [dram("src_low_row", (EP,)), dram("dst_low_row", (EP,))]
        k.order_row, k.by_rank_dram = dram("order_row", (NP,)), dram("by_rank_dram", (NP, D))
        k.bc_dram, k.scan_dram = dram("bc_dram", (2 * STATES, NP)), dram("scan_dram", (NP, D))
        k.nodes_dram = dram("nodes_dram", (NP, D))
        k.sorted_dram, k.result_dram = dram("sorted_dram", (SORTED * P, D)), dram("result_dram", (SORTED * P, D))
        k.tables = [[dram(f"table{layer}_{a}", (TROWS, ROW)) for a in range(TABLES)] for layer in range(2)]
        k.all_scattered = [[k.lasting_sem(f"scattered{layer}_{a}") for a in range(TABLES)] for layer in range(2)]
        setup_stage(nc, k)
        if upto >= 1:
            support_stage(nc, k)
        if upto >= 2:
            edges_stage(nc, k, "e0", 0, k.src_row, k.src_col, k.src_off, k.dst_i, scale_by_weight(k),
                        [(k.src_row, k.src_col, k.src_off, k.src_to), (k.dst_row, k.dst_col, k.dst_off, k.dst_to)], k.src_to)
        if upto >= 3:
            combine_stage(nc, k)
        if upto >= 4:
            ffn0_route_stage(nc, k)
        if upto >= 5:
            ffn0_experts_stage(nc, k)
            ffn0_return_stage(nc, k)
        if upto >= 6:
            k.score = edge_sb("score", [P, T, 2 * HEADS], F32)
            l1_pre_stage(nc, k)
        if upto >= 7:
            k.attn = edge_sb("attn", [P, C, HEADS], F32)
            attention_stage(nc, k)
        if upto >= 8:
            edges_stage(nc, k, "e1", 1, k.dst_row, k.dst_col, k.dst_off, k.src_i, scale_by_attention(k), [], k.dst_to)
        if upto >= 9:
            k.edges.close()
            k.late, k.scan = ExitStack(), ExitStack()
            program.callback(k.late.close)
            program.callback(k.scan.close)
            k.u, k.dt = (k.late.enter_context(nc.sbuf_tensor(name, [P, 2, NP], F32)) for name in ("u", "dt"))
            k.zs, k.dtx = (k.scan.enter_context(nc.sbuf_tensor(name, [P, 2, NP], F32)) for name in ("zs", "dtx"))
            mamba_in_stage(nc, k)
        if upto >= 10:
            scan_stage(nc, k)
        if upto >= 11:
            k.ha = by_tile(k.u)
            mamba_out_stage(nc, k)
            k.scan.close()
            k.hl = by_tile(k.dt)
        if upto >= 12:
            l1_post_stage(nc, k)
            k.late.close()
        if upto >= 13:
            ffn1_route_stage(nc, k)
        if upto >= 14:
            ffn1_experts_stage(nc, k)
            ffn1_return_stage(nc, k, out)
        if dbg:
            dbg(nc, k)


def host_arrays(inputs):
    import numpy as np
    arrays = {name: np.ascontiguousarray(inputs[name]) for name in _INS}
    for name in ("gat_w", "in_proj_w", "x_proj_w", "dt_proj_w", "out_proj_w", "wl", "wg", "ff1_w", "ff2_w"):
        arrays[f"{name}_t"] = np.ascontiguousarray(arrays.pop(f"L1_gnn_{name}").T)
    arrays["gat_w"] = np.ascontiguousarray(inputs["L1_gnn_gat_w"])
    return arrays


_INS = ['x', 'src', 'dst', 'edge_weight', 'node_vec', 'L0_gnn_weight', 'L0_gnn_b', 'L0_ffn_W1', 'L0_ffn_b1', 'L0_ffn_Wg', 'L0_ffn_bg', 'L0_ffn_Wd', 'L0_ffn_bd', 'L1_gnn_gat_w', 'L1_gnn_gat_a_src', 'L1_gnn_gat_a_tgt', 'L1_gnn_gat_b', 'L1_gnn_ln_local_g', 'L1_gnn_ln_local_b', 'L1_gnn_ln_global_g', 'L1_gnn_ln_global_b', 'L1_gnn_ln2_g', 'L1_gnn_ln2_b', 'L1_gnn_in_proj_w', 'L1_gnn_conv_w', 'L1_gnn_conv_b', 'L1_gnn_x_proj_w', 'L1_gnn_dt_proj_w', 'L1_gnn_dt_proj_b', 'L1_gnn_A_log', 'L1_gnn_D_param', 'L1_gnn_out_proj_w', 'L1_gnn_wl', 'L1_gnn_wg', 'L1_gnn_ff1_w', 'L1_gnn_ff1_b', 'L1_gnn_ff2_w', 'L1_gnn_ff2_b', 'L1_ffn_gate_w', 'L1_ffn_gate_b', 'L1_ffn_w1', 'L1_ffn_b1', 'L1_ffn_w2', 'L1_ffn_b2']

_OUTS = [((NODES, D), "float32")]


def kernel(**inputs):
    import numpy as _np
    import concourse.bacc as _bacc
    from concourse import mybir as _mybir
    from concourse.bass_utils import run_bass_kernel_spmd as _run

    nc = _bacc.Bacc("TRN2", target_bir_lowering=False, num_devices=1)
    arrays, io = {}, {}
    for name, a in host_arrays(inputs).items():
        arrays[f"in_{name}_dram"] = a
        io[name] = nc.dram_tensor(f"in_{name}_dram", a.shape, _mybir.dt.from_np(a.dtype), kind="ExternalInput").ap()
    shape, dtype = _OUTS[0]
    out = nc.dram_tensor("out_0_dram", shape, _mybir.dt.from_np(_np.dtype(dtype)), kind="ExternalOutput").ap()
    build(nc, io, out)
    return _run(nc, [arrays], core_ids=[0]).results[0]["out_0_dram"]
```

```python
from contextlib import ExitStack

import concourse.bass as bass
from concourse import mybir

F32 = mybir.dt.float32
I32 = mybir.dt.int32
ALU = mybir.AluOpType
ACT = mybir.ActivationFunctionType
AX = mybir.AxisListType.X

P = 128
NODES, D = 3125, 256
T = -(-NODES // P)
NP = T * P
LAST = NODES - (T - 1) * P
SLOTS = 5
GROUPS = T // SLOTS
EDGES = 53125
C = 416
EP = C * P
ER, EC = 104, 512
PADNODE = NP - 1
ROW = D + 4
TABLES = 4
TROWS = NP + P
HEADS, HD = 4, 64
EPS = 1e-5
assert T == SLOTS * GROUPS and ER * EC == EP and (ER - 1) * EC < EDGES <= EP


def rounds(engine, n, body):
    body(0, True)
    with engine.Fori(1, n) as g:
        body(g, False)


def after_earlier(engine, sem, first, value):
    if not first:
        engine.wait_ge(sem, value)


def row_view(ap, n):
    return ap.rearrange("(a n) -> a n", a=1)


def setup_stage(nc, k):
    with nc.Block() as block:
        filled, loaded, rows_in = k.sem("setup_filled"), k.sem("setup_loaded"), k.sem("setup_rows_in")
        floats, rows_out = k.sem("setup_floats"), k.sem("setup_rows_out")
        turned, cols = k.sem("setup_turned"), k.sem("setup_cols")
        built, dumps = k.sem("setup_built"), k.sem("setup_dumps")
        src_i = k.stage_sb("setup_src_i", [ER, EC], I32)
        dst_i = k.stage_sb("setup_dst_i", [ER, EC], I32)
        src_r = k.stage_sb("src_r", [ER, EC], F32)
        dst_r = k.stage_sb("dst_r", [ER, EC], F32)
        w_r = k.stage_sb("w_r", [ER, EC], F32)
        dump_i = k.stage_sb("dump_i", [P, 1], I32)
        lane_i, lane_p = k.stage_sb("lane_i", [P, 32], I32), k.stage_sb("lane_p", [P, 1], I32)
        low_i = k.stage_sb("low_i", [ER, 2, EC], I32)
        low_r = k.stage_sb("low_r", [ER, 2, EC], F32)
        high_i = k.stage_sb("high_i", [P, 2, C], I32)
        tail = EDGES - (ER - 1) * EC

        @block.sync
        def _(sp):
            sp.wait_ge(filled, 5)
            sp.dma_start(k.x[:, 0:T - 1, :], k.io["x"][0:(T - 1) * P, :].rearrange("(t p) d -> p t d", p=P)).then_inc(loaded, 16)
            sp.dma_start(k.x[0:LAST, T - 1, :], k.io["x"][(T - 1) * P:NODES, :]).then_inc(loaded, 16)
            for tile, dram in ((src_i, k.io["src"]), (dst_i, k.io["dst"]), (w_r, k.io["edge_weight"])):
                sp.dma_start(tile[0:ER - 1, :], dram[0:(ER - 1) * EC].rearrange("(r c) -> r c", c=EC)).then_inc(rows_in, 16)
                sp.dma_start(tile[ER - 1:ER, 0:tail], row_view(dram[(ER - 1) * EC:EDGES], tail)).then_inc(rows_in, 16)
            sp.wait_ge(floats, 2)
            sp.dma_start(k.src_row.rearrange("(r c) -> r c", c=EC), src_r[:, :]).then_inc(rows_out, 16)
            sp.dma_start(k.dst_row.rearrange("(r c) -> r c", c=EC), dst_r[:, :]).then_inc(rows_out, 16)
            sp.wait_ge(floats, 3)
            for a in range(2):
                sp.dma_start(k.low_row[a].rearrange("(r c) -> r c", c=EC), low_r[:, a, :]).then_inc(rows_out, 16)
            with nc.allow_non_contiguous_dma(reason="12 KB as columns"):
                sp.dma_start(k.noise[:, 0:T - 1], k.io["node_vec"][0:(T - 1) * P].rearrange("(t p) -> p t", p=P)).then_inc(loaded, 16)
                sp.dma_start(k.noise[0:LAST, T - 1:T], k.io["node_vec"][(T - 1) * P:NODES].rearrange("(p a) -> p a", a=1)).then_inc(loaded, 16)
            sp.wait_ge(loaded, 64)
            sp.wait_ge(rows_out, 64)

        @block.gpsimd
        def _(pool):
            pool.memset(k.ident[:, :], 0.0).then_inc(built, 1)
            pool.memset(k.below[:, :], 1.0).then_inc(built, 1)
            pool.iota(dump_i[:, :], [[1, 1]], base=NP, channel_multiplier=1).then_inc(dumps, 1)
            pool.iota(lane_p[:, :], [[1, 1]], base=0, channel_multiplier=1).then_inc(dumps, 1)
            pool.iota(lane_i[:, :], [[1, 32]], base=0, channel_multiplier=0).then_inc(dumps, 1)
            pool.memset(k.before[:, :], 1.0).then_inc(built, 1)
            pool.wait_ge(built, 3)
            pool.affine_select(out=k.ident[:, :], in_=k.ident[:, :], compare_op=ALU.not_equal, fill=1.0, base=0,
                               pattern=[[-1, P]], channel_multiplier=1).then_inc(built, 1)
            pool.affine_select(out=k.below[:, :], in_=k.below[:, :], compare_op=ALU.is_gt, fill=0.0, base=0,
                               pattern=[[-1, P]], channel_multiplier=1).then_inc(built, 1)
            pool.affine_select(out=k.before[:, :], in_=k.before[:, :], compare_op=ALU.is_gt, fill=0.0, base=0,
                               pattern=[[1, P]], channel_multiplier=-1).then_inc(built, 1)

        @block.vector
        def _(dve):
            dve.memset(k.x[:, T - 1, :], 0.0).then_inc(filled, 1)
            dve.memset(src_i[:, :], PADNODE).then_inc(filled, 1)
            dve.memset(dst_i[:, :], PADNODE).then_inc(filled, 1)
            dve.memset(w_r[:, :], 0.0).then_inc(filled, 1)
            dve.memset(k.eps[:, :], EPS)
            dve.memset(k.dst_i[:, C:C + 8], 0)
            dve.memset(k.src_i[:, C:C + 8], 0)
            dve.memset(k.zero[:, :], 0.0)
            dve.memset(k.ones[:, :], 1.0)
            dve.memset(k.noise[:, :], 0.0).then_inc(filled, 1)
            dve.wait_ge(dumps, 3)
            dve.tensor_copy(k.own[:, :], lane_p[:, :])
            dve.tensor_copy(k.dump[:, :], dump_i[:, :])
            dve.tensor_copy(k.lane8[:, :], lane_i[:, 0:EXPERTS])
            dve.tensor_copy(k.lane32[:, :], lane_i[:, :])
            dve.wait_ge(rows_in, 96)
            dve.tensor_copy(src_r[:, :], src_i[:, :]).then_inc(floats, 1)
            dve.tensor_copy(dst_r[:, :], dst_i[:, :]).then_inc(floats, 1)
            dve.tensor_scalar(low_i[:, 0, :], src_i[:, :], P - 1, None, ALU.bitwise_and)
            dve.tensor_scalar(low_i[:, 1, :], dst_i[:, :], P - 1, None, ALU.bitwise_and)
            dve.drain()
            dve.tensor_copy(low_r[:, :, :], low_i[:, :, :]).then_inc(floats, 1)
            for a, col in enumerate((k.src_col, k.dst_col, k.w_col)):
                dve.wait_ge(turned, a + 1)
                by_row = col[:, 0:C].rearrange("p (r q) -> p q r", q=EC // P)
                dve.tensor_copy(by_row, k.ps[a][:, 0:EC // P * ER].rearrange("p (q r) -> p q r", r=ER)).then_inc(cols, 1)
            dve.drain()
            dve.tensor_copy(k.src_i[:, 0:C], k.src_col[:, 0:C])
            dve.tensor_copy(k.dst_i[:, 0:C], k.dst_col[:, 0:C])
            dve.drain()
            dve.tensor_scalar(high_i[:, 0, :], k.src_i[:, 0:C], 7, None, ALU.arith_shift_right)
            dve.tensor_scalar(high_i[:, 1, :], k.dst_i[:, 0:C], 7, None, ALU.arith_shift_right)
            dve.drain()
            dve.tensor_copy(k.high[:, :, :], high_i[:, :, :])
            dve.tensor_scalar(k.src_off[:, :], k.src_col[:, :], -1.0, k.dump[:, :], ALU.mult, ALU.add)
            dve.tensor_scalar(k.dst_off[:, :], k.dst_col[:, :], -1.0, k.dump[:, :], ALU.mult, ALU.add)

        @block.tensor
        def _(pe):
            pe.wait_ge(built, 6)
            pe.wait_ge(floats, 2)
            for a, rows in enumerate((src_r, dst_r, w_r)):
                for q in range(EC // P):
                    last = pe.transpose(k.ps[a][:, q * ER:(q + 1) * ER], rows[:, q * P:(q + 1) * P], k.ident[0:ER, 0:ER])
                last.then_inc(turned, 1)
    k.end_stage()


def norm_stats(nc, k, dve, src, sums, inv, wait_sqrt, need_sqrt):
    st = k.stats
    with dve.Fori(0, T) as t:
        dve.bn_stats(st[:, bass.ds(t * 6, 6)], src[:, t, :])
    dve.drain()
    s = st[:, :].rearrange("p (t s) -> p s t", s=6)
    dve.tensor_tensor(sums[:, 0, :], s[:, 1, :], s[:, 4, :], ALU.add)
    dve.tensor_tensor(sums[:, 1, :], s[:, 1, :], s[:, 4, :], ALU.subtract)
    dve.tensor_tensor(sums[:, 2, :], s[:, 2, :], s[:, 5, :], ALU.add)
    dve.drain()
    dve.tensor_scalar(sums[:, 0, :], sums[:, 0, :], 0.5, None, ALU.mult)
    dve.tensor_tensor(sums[:, 1, :], sums[:, 1, :], sums[:, 1, :], ALU.mult)
    dve.tensor_scalar(sums[:, 2, :], sums[:, 2, :], 1.0 / D, None, ALU.mult)
    dve.drain()
    dve.scalar_tensor_tensor(out=sums[:, 3, :], in0=sums[:, 1, :], scalar=0.25, in1=sums[:, 2, :],
                             op0=ALU.mult, op1=ALU.add).then_inc(need_sqrt, 1)
    dve.wait_ge(wait_sqrt, 1)
    dve.reciprocal(inv[:, :], sums[:, 4, :])
    dve.drain()


def support_stage(nc, k):
    with nc.Block() as block:
        weights, var_ready, dev_ready = k.sem("l0_weights"), k.sem("l0_var_ready"), k.sem("l0_dev_ready")
        normed, turned, turned_sb = k.sem("l0_normed"), k.sem("l0_turned"), k.sem("l0_turned_sb")
        multiplied, out_ready = k.sem("l0_multiplied"), k.sem("l0_out_ready")
        stored = [k.sem(f"l0_stored{j}") for j in range(SLOTS)]
        zeroed = k.sem("l0_zero_tile")
        w = k.stage_sb("l0_w", [P, 2, D], F32)
        sums = k.stage_sb("l0_sums", [P, 5, T], F32)
        inv = k.stage_sb("l0_inv", [P, T], F32)
        xn = k.stage_sb("l0_xn", [P, SLOTS, D], F32)
        xt = k.stage_sb("l0_xt", [P, SLOTS, 2, P], F32)
        out = k.stage_sb("l0_out", [P, SLOTS, D], F32)
        zeros = k.stage_sb("l0_zeros", [P, TROWS // P * ROW], F32)

        @block.sync
        def _(sp):
            sp.dma_start(w[:, :, :], k.io["L0_gnn_weight"].rearrange("(c p) n -> p c n", p=P)).then_inc(weights, 16)

            def store(g, first):
                for j in range(SLOTS):
                    sp.wait_ge(out_ready, g * SLOTS + (j + 1))
                    sp.dma_start(k.nodes_dram[bass.ds((g * SLOTS + j) * P, P), 0:D], out[:, j, :]).then_inc(stored[j], 16)

            rounds(sp, GROUPS, store)
            for j in range(SLOTS):
                sp.wait_ge(stored[j], 16 * GROUPS)

        @block.gpsimd
        def _(pool):
            pool.wait_ge(zeroed, 1)
            for a in range(TABLES):
                pool.dma_start(k.tables[0][a].rearrange("(p r) c -> p (r c)", p=P), zeros[:, :]).then_inc(k.all_scattered[0][a], 16)
            for a in range(TABLES):
                pool.wait_ge(k.all_scattered[0][a], 16)

        @block.vector
        def _(dve):
            dve.memset(zeros[:, :], 0.0).then_inc(zeroed, 1)
            norm_stats(nc, k, dve, k.x, sums, inv, dev_ready, var_ready)

            def tiles(g, first):
                for j in range(SLOTS):
                    t = g * SLOTS + j
                    after_earlier(dve, turned, first, t - (SLOTS - 1))
                    dve.tensor_scalar(xn[:, j, :], k.x[:, t, :], sums[:, 0, bass.ds(t, 1)], inv[:, bass.ds(t, 1)],
                                      ALU.subtract, ALU.mult).then_inc(normed, 1)
                for j in range(SLOTS):
                    t = g * SLOTS + j
                    dve.wait_ge(multiplied, t + 1)
                    after_earlier(dve, stored[j], first, g * 16)
                    dve.tensor_copy(out[:, j, :], k.ps[j][:, D:2 * D]).then_inc(out_ready, 1)

            rounds(dve, GROUPS, tiles)

        @block.scalar
        def _(act):
            act.preload_act_table(ACT.Sqrt)
            act.wait_ge(var_ready, 1)
            act.activation(sums[:, 4, :], sums[:, 3, :], ACT.Sqrt, bias=k.eps[:, :]).then_inc(dev_ready, 1)

            def tiles(g, first):
                for j in range(SLOTS):
                    act.wait_ge(turned, g * SLOTS + (j + 1))
                    act.activation(xt[:, j, :, :], k.ps[j][:, 0:D].rearrange("p (c n) -> p c n", c=2), ACT.Copy).then_inc(turned_sb, 1)

            rounds(act, GROUPS, tiles)

        @block.tensor
        def _(pe):
            pe.wait_ge(weights, 16)

            def tiles(g, first):
                for j in range(SLOTS):
                    t = g * SLOTS + j
                    pe.wait_ge(normed, t + 1)
                    pe.transpose(k.ps[j][:, 0:P], xn[:, j, 0:P], k.ident[:, :])
                    pe.transpose(k.ps[j][:, P:D], xn[:, j, P:D], k.ident[:, :]).then_inc(turned, 1)
                for j in range(SLOTS):
                    t = g * SLOTS + j
                    pe.wait_ge(turned_sb, t + 1)
                    for c in range(2):
                        mm = pe.matmul(k.ps[j][:, D:2 * D], xt[:, j, c, :], w[:, c, :], start=c == 0, stop=c == 1)
                    mm.then_inc(multiplied, 1)

            rounds(pe, GROUPS, tiles)
    k.end_stage()


UNROLL = 2 * TABLES
ROUNDS = C // UNROLL


def edges_stage(nc, k, name, layer, key_row, key_col, key_off, other_i, scale, ranks, scatter_i):
    H = TABLES
    table, scattered = k.tables[layer], k.all_scattered[layer]
    with nc.Block() as block:
        keys_in = [k.sem(f"{name}_keys_in{h}") for h in range(2)]
        gathered = [k.sem(f"{name}_gathered{s}") for s in range(H)]
        gather_i_ready, scatter_i_ready = k.sem(f"{name}_gather_i"), k.sem(f"{name}_scatter_i")
        scaled, summed, out_ready = k.sem(f"{name}_scaled"), k.sem(f"{name}_summed"), k.sem(f"{name}_out_ready")
        pool_step = k.sem(f"{name}_pool_step")
        half_scattered = k.sem(f"{name}_half_scattered")
        lists = [r[0] for r in ranks] or [key_row]
        keys = k.stage_sb(f"{name}_keys", [P, 2, len(lists), H * P], F32)
        gi = k.stage_sb(f"{name}_gi", [P, 2, H], I32)
        si = k.stage_sb(f"{name}_si", [P, 2, H], I32)
        rank = k.stage_sb(f"{name}_rank", [P, len(lists), H], F32)
        shift = k.stage_sb(f"{name}_shift", [P, len(lists), H], F32)
        junk = k.stage_sb(f"{name}_junk", [P, len(lists), H, P], F32)
        same = k.stage_sb(f"{name}_same", [P, H, P], F32)
        rows = k.stage_sb(f"{name}_rows", [P, H, D], F32)
        vals = k.stage_sb(f"{name}_vals", [P, H, ROW], F32)
        out = k.stage_sb(f"{name}_out", [P, H, ROW], F32)

        @block.sync
        def _(sp):
            def load(g, h, first):
                if not first:
                    sp.wait_ge(scaled, g * UNROLL + (h * H + H - UNROLL))
                for a, row in enumerate(lists):
                    sp.dma_start(keys[:, h, a, :], row[bass.ds(g * UNROLL * P + h * H * P, H * P)].partition_broadcast(P)).then_inc(keys_in[h], 16)

            rounds(sp, ROUNDS, lambda g, first: (load(g, 0, first), load(g, 1, first)))

        @block.gpsimd
        def _(pool):
            def gather(h, s):
                pool.indirect_dma_start(out=rows[:, s, :], out_offset=None, in_=k.nodes_dram,
                                        in_offset=bass.IndirectOffsetOnAxis(ap=gi[:, h, s:s + 1], axis=0)).then_inc(gathered[s], 16)

            def body(g, last):
                for h in range(2):
                    for s in range(H):
                        pool.wait_ge(out_ready, g * UNROLL + (h * H + s + 1))
                        pool.wait_ge(scattered[s], g * 32 + (h * 16 + 16))
                        pool.sem_inc(pool_step, 1)
                        pool.indirect_dma_start(out=table[s], out_offset=bass.IndirectOffsetOnAxis(ap=si[:, h, s:s + 1], axis=0),
                                                in_=out[:, s, :], in_offset=None, compute_op=ALU.add).then_inc(scattered[s], 16)
                        if s == H - 1:
                            pool.sem_inc(half_scattered, 1)
                        if not (last and h == 1):
                            pool.wait_ge(scaled, g * UNROLL + (h * H + s + 1))
                            pool.wait_ge(gather_i_ready, g * 2 + (h + 2))
                            pool.sem_inc(pool_step, 1)
                            gather(1 - h, s)

            pool.wait_ge(gather_i_ready, 1)
            for s in range(H):
                gather(0, s)
            with pool.Fori(0, ROUNDS - 1) as g:
                body(g, False)
            body(ROUNDS - 1, True)
            for s in range(H):
                pool.wait_ge(scattered[s], (2 * ROUNDS + 1) * 16)

        @block.vector
        def _(dve):
            def indices(g, h):
                dve.tensor_scalar(gi[:, h, :], other_i[:, bass.ds(g * UNROLL + h * H, H)], 0.0, None, ALU.add).then_inc(gather_i_ready, 1)

            for s in range(H):
                scale(dve, vals[:, s, :], None, None)
            dve.drain()
            indices(0, 0)

            def body(g, first):
                for h in range(2):
                    at = g * UNROLL + h * H
                    dve.wait_ge(keys_in[h], (g + 1) * (16 * len(lists)))
                    for a, (row, col, off, idx) in enumerate(ranks):
                        for s in range(H):
                            dve.scalar_tensor_tensor(out=junk[:, a, s, :], in0=keys[:, h, a, s * P:(s + 1) * P], scalar=col[:, bass.ds(at + s, 1)],
                                                     in1=k.below[:, :], op0=ALU.is_equal, op1=ALU.mult, accum_out=rank[:, a, s:s + 1])
                    if ranks:
                        dve.drain()
                        for a, (row, col, off, idx) in enumerate(ranks):
                            dve.scalar_tensor_tensor(out=shift[:, a, :], in0=rank[:, a, :], scalar=0.0, in1=off[:, bass.ds(at, H)],
                                                     op0=ALU.is_gt, op1=ALU.mult)
                        dve.drain()
                        for a, (row, col, off, idx) in enumerate(ranks):
                            dve.tensor_tensor(idx[:, bass.ds(at, H)], shift[:, a, :], col[:, bass.ds(at, H)], ALU.add)
                        dve.drain()
                    if not first:
                        dve.wait_ge(half_scattered, g * 2 + h)
                    dve.tensor_scalar(si[:, h, :], scatter_i[:, bass.ds(at, H)], 0.0, None, ALU.add).then_inc(scatter_i_ready, 1)
                    indices(g + h, 1 - h)
                    for s in range(H):
                        if not (first and h == 0):
                            dve.wait_ge(summed, at + (s + 1 - H))
                        dve.tensor_scalar(same[:, s, :], keys[:, h, 0, s * P:(s + 1) * P], key_col[:, bass.ds(at + s, 1)], None, ALU.is_equal)
                        dve.wait_ge(gathered[s], g * 32 + (h * 16 + 16))
                        scale(dve, vals[:, s, :], rows[:, s, :], at + s).then_inc(scaled, 1)

            rounds(dve, ROUNDS, body)

        @block.tensor
        def _(pe):
            def body(g, first):
                for h in range(2):
                    for s in range(H):
                        n = g * UNROLL + (h * H + s + 1)
                        pe.wait_ge(scaled, n)
                        if not (first and h == 0):
                            pe.wait_ge(out_ready, n - H)
                        pe.matmul(k.ps[s][:, 0:ROW], same[:, s, :], vals[:, s, :], start=True, stop=True).then_inc(summed, 1)

            rounds(pe, ROUNDS, body)

        @block.scalar
        def _(act):
            def body(g, first):
                for h in range(2):
                    for s in range(H):
                        if not (first and h == 0):
                            act.wait_ge(scattered[s], g * 32 + (h * 16 + 16))
                        act.wait_ge(summed, g * UNROLL + (h * H + s + 1))
                        act.activation(out[:, s, :], k.ps[s][:, 0:ROW], ACT.Copy).then_inc(out_ready, 1)

            act.wait_ge(scatter_i_ready, 1)
            act.preload_act_table(ACT.Copy)
            rounds(act, ROUNDS, body)
    k.end_stage()


def scale_by_weight(k):
    def scale(dve, vals, rows, chunk):
        if rows is None:
            dve.memset(vals[:, D + 1:ROW], 0.0)
            return dve.memset(vals[:, D:D + 1], 1.0)
        return dve.tensor_scalar(vals[:, 0:D], rows, k.w_col[:, bass.ds(chunk, 1)], None, ALU.mult)
    return scale


def combine_stage(nc, k):
    with nc.Block() as block:
        bias_in, summed, folded = k.sem("c0_bias_in"), k.sem("c0_summed"), k.sem("c0_folded")
        tables_in = [k.sem(f"c0_tables_in{h}") for h in range(2)]
        part = k.stage_sb("c0_part", [P, 2, TABLES, SLOTS, ROW], F32)
        bias = k.stage_sb("c0_bias", [P, D], F32)

        @block.sync
        def _(sp):
            sp.dma_start(bias[:, :], k.io["L0_gnn_b"].partition_broadcast(P)).then_inc(bias_in, 16)
            for g in range(GROUPS):
                if g >= 2:
                    sp.wait_ge(summed, g - 1)
                for a in range(TABLES):
                    rows = k.tables[0][a][g * SLOTS * P:(g + 1) * SLOTS * P, :].rearrange("(j p) c -> p j c", p=P)
                    sp.dma_start(part[:, g % 2, a, :, :], rows).then_inc(tables_in[g % 2], 16)

        @block.vector
        def _(dve):
            dve.wait_ge(bias_in, 16)
            for g in range(GROUPS):
                t, pt = part[:, g % 2, :, :, :], slice(g * SLOTS, (g + 1) * SLOTS)
                dve.wait_ge(tables_in[g % 2], 16 * TABLES * (g // 2 + 1))
                dve.tensor_tensor(t[:, 0:2, :, :], t[:, 0:2, :, :], t[:, 2:4, :, :], ALU.add)
                dve.tensor_tensor(k.x[:, pt, :], k.x[:, pt, :], bias[:, :].unsqueeze(1).to_broadcast([P, SLOTS, D]), ALU.add)
                dve.drain()
                dve.tensor_tensor(t[:, 0, :, :], t[:, 0, :, :], t[:, 1, :, :], ALU.add)
                dve.drain()
                dve.tensor_tensor(k.x[:, pt, :], k.x[:, pt, :], t[:, 0, :, 0:D], ALU.add)
                dve.tensor_copy(k.degree[:, pt], t[:, 0, :, D]).then_inc(summed, 1)
    k.end_stage()


EXPERTS, HID = 8, 1024
CAPACITY = -(-5 * NODES // (4 * EXPERTS))
BUF = 512
HC = HID // P
SORTED = T + EXPERTS - 1
QUAD = 4
assert SORTED % QUAD == 0


def transposer(nc, k, name, normed, turned, turned_sb, xn, xt):
    def on_pe(pe, g):
        for j in range(SLOTS):
            pe.wait_ge(normed, g * SLOTS + (j + 1))
            pe.transpose(k.ps[j][:, 0:P], xn[:, j, 0:P], k.ident[:, :])
            pe.transpose(k.ps[j][:, P:D], xn[:, j, P:D], k.ident[:, :]).then_inc(turned, 1)

    def on_act(act, g):
        for j in range(SLOTS):
            act.wait_ge(turned, g * SLOTS + (j + 1))
            act.activation(xt[:, :, j * P:(j + 1) * P], k.ps[j][:, 0:D].rearrange("p (c n) -> p c n", c=2), ACT.Copy).then_inc(turned_sb, 1)

    return on_pe, on_act


def route(nc, k, dve, name, logits, exp_ready, exp_done, mask_ready, counted, padded):
    def tile3(n):
        return k.stage_sb(f"{name}_{n}", [P, T, EXPERTS], F32)

    def tile2(n):
        return k.stage_sb(f"{name}_{n}", [P, T], F32)

    over = lambda a: a[:, :].unsqueeze(2).to_broadcast([P, T, EXPERTS])
    lane = k.lane8[:, :].unsqueeze(1).to_broadcast([P, T, EXPERTS])
    top, total, inv, first = tile2("top"), tile2("total"), tile2("total_inv"), tile2("first")
    prob, tie, hot, place = k.prob_of[name], tile3("tie"), k.hot, tile3("place")
    dve.tensor_reduce(top[:, :], logits[:, :, :], AX, ALU.max)
    dve.drain()
    dve.tensor_tensor(prob[:, :, :], logits[:, :, :], over(top), ALU.subtract).then_inc(exp_ready, 1)
    dve.wait_ge(exp_done, 1)
    dve.tensor_reduce(total[:, :], prob[:, :, :], AX, ALU.add)
    dve.drain()
    dve.reciprocal(inv[:, :], total[:, :])
    dve.drain()
    dve.tensor_tensor(prob[:, :, :], prob[:, :, :], over(inv), ALU.mult)
    dve.drain()
    dve.tensor_reduce(k.prb[:, :], prob[:, :, :], AX, ALU.max)
    dve.drain()
    dve.tensor_tensor(tie[:, :, :], prob[:, :, :], over(k.prb), ALU.is_lt)
    dve.drain()
    dve.scalar_tensor_tensor(out=tie[:, :, :], in0=tie[:, :, :], scalar=float(EXPERTS), in1=lane, op0=ALU.mult, op1=ALU.add)
    dve.drain()
    dve.tensor_reduce(first[:, :], tie[:, :, :], AX, ALU.min)
    dve.drain()
    dve.tensor_tensor(hot[:, :, :], lane, over(first), ALU.is_equal).then_inc(mask_ready, 1)
    n = T * EXPERTS
    dve.wait_ge(counted, 1)
    total8 = tile3("total8")
    run = tile3("run")
    dve.tensor_copy(total8[:, :, :], k.ps[0][:, n:2 * n].rearrange("p (t e) -> p t e", e=EXPERTS))
    dve.drain()
    for e in range(EXPERTS):
        dve.tensor_tensor_scan(run[:, :, e], total8[:, :, e], k.zero[:, :].to_broadcast([P, T]), 0.0, ALU.add, ALU.add)
    dve.drain()
    dve.tensor_tensor(place[:, :, :], run[:, :, :], total8[:, :, :], ALU.subtract)
    dve.drain()
    dve.tensor_tensor(place[:, :, :], place[:, :, :], k.ps[0][:, 0:n].rearrange("p (t e) -> p t e", e=EXPERTS), ALU.add)
    counts = run[:, T - 1, :]
    start = k.stage_sb(f"{name}_start", [P, EXPERTS], F32)
    if padded:
        tiles_i = k.stage_sb(f"{name}_tiles_i", [P, EXPERTS], I32)
        tiles_f = k.stage_sb(f"{name}_tiles_f", [P, EXPERTS], F32)
        ends = k.stage_sb(f"{name}_ends", [P, EXPERTS], F32)
        past = k.stage_sb(f"{name}_past", [P, SORTED, EXPERTS - 1], F32)
        owner = k.stage_sb(f"{name}_owner", [P, SORTED], F32)
        dve.tensor_scalar(tiles_i[:, :], counts, float(P - 1), None, ALU.add)
        dve.drain()
        dve.tensor_scalar(tiles_i[:, :], tiles_i[:, :], 7, None, ALU.arith_shift_right)
        dve.drain()
        dve.tensor_copy(tiles_f[:, :], tiles_i[:, :])
        dve.drain()
        dve.tensor_tensor_scan(ends[:, :], tiles_f[:, :], k.zero[:, :].to_broadcast([P, EXPERTS]), 0.0, ALU.add, ALU.add)
        dve.drain()
        dve.tensor_tensor(start[:, :], ends[:, :], tiles_f[:, :], ALU.subtract)
        dve.tensor_tensor(past[:, :, :], k.lane32[:, 0:SORTED].unsqueeze(2).to_broadcast([P, SORTED, EXPERTS - 1]),
                          ends[:, 0:EXPERTS - 1].unsqueeze(1).to_broadcast([P, SORTED, EXPERTS - 1]), ALU.is_ge)
        dve.drain()
        dve.tensor_scalar(start[:, :], start[:, :], float(P), None, ALU.mult)
        dve.tensor_reduce(owner[:, :], past[:, :, :], AX, ALU.add)
        dve.drain()
        dve.tensor_copy(k.owner_i[:, :], owner[:, :])
    else:
        cap = k.stage_sb(f"{name}_cap", [P, T], F32)
        dve.drain()
        dve.tensor_tensor(tie[:, :, :], place[:, :, :], hot[:, :, :], ALU.mult)
        dve.drain()
        dve.tensor_reduce(cap[:, :], tie[:, :, :], AX, ALU.add)
        dve.drain()
        dve.tensor_scalar(cap[:, :], cap[:, :], float(CAPACITY), None, ALU.is_lt)
        dve.tensor_scalar(place[:, :, :], place[:, :, :], float(CAPACITY - 1), None, ALU.min)
        dve.tensor_scalar(start[:, :], k.lane8[:, :], float(BUF), None, ALU.mult)
        dve.drain()
        dve.tensor_tensor(k.prb[:, :], k.prb[:, :], cap[:, :], ALU.mult)
    dve.drain()
    dve.tensor_tensor(place[:, :, :], place[:, :, :], start[:, :].unsqueeze(1).to_broadcast([P, T, EXPERTS]), ALU.add)
    dve.drain()
    dve.tensor_tensor(place[:, :, :], place[:, :, :], hot[:, :, :], ALU.mult)
    dve.drain()
    dve.tensor_reduce(first[:, :], place[:, :, :], AX, ALU.add)
    dve.drain()
    dve.tensor_copy(k.place_i[:, :], first[:, :])
    if padded:
        dve.tensor_copy(k.send_i[:, :], first[:, :])
    else:
        dve.tensor_scalar(cap[:, :], cap[:, :], -float(1 << 20), float(1 << 20), ALU.mult, ALU.add)
        dve.drain()
        dve.tensor_tensor(k.send_i[:, :], cap[:, :], first[:, :], ALU.add)
    dve.drain()
    return prob


def count_tokens(k, pe):
    n = T * EXPERTS
    hot = k.hot[:, :, :].rearrange("p t e -> p (t e)")
    pe.matmul(k.ps[0][:, 0:n], k.before[:, :], hot, start=True, stop=True)
    return pe.matmul(k.ps[0][:, n:2 * n], k.ones[:, :], hot, start=True, stop=True)


def ffn0_route_stage(nc, k):
    with nc.Block() as block:
        weights, var_ready, dev_ready = k.sem("f0_weights"), k.sem("f0_var_ready"), k.sem("f0_dev_ready")
        normed, turned, turned_sb = k.sem("f0_normed"), k.sem("f0_turned"), k.sem("f0_turned_sb")
        hidden, hidden_sb, gated, logit_ready = k.sem("f0_hidden"), k.sem("f0_hidden_sb"), k.sem("f0_gated"), k.sem("f0_logit_ready")
        exp_ready, exp_done, mask_ready, counted = (k.sem(f"f0_{n}") for n in ("exp_ready", "exp_done", "mask_ready", "counted"))
        placed, sent, zero_sent = k.sem("f0_placed"), k.sem("f0_sent"), k.sem("f0_zero_sent")
        w1 = k.stage_sb("f0_w1", [P, 2, HID], F32)
        wg = k.stage_sb("f0_wg", [P, HC, EXPERTS], F32)
        b1 = k.stage_sb("f0_b1", [P, HC], F32)
        bg = k.stage_sb("f0_bg", [P, EXPERTS], F32)
        sums = k.stage_sb("f0_sums", [P, 5, T], F32)
        inv = k.stage_sb("f0_inv", [P, T], F32)
        xn = k.stage_sb("f0_xn", [P, T, D], F32)
        xs = k.stage_sb("f0_xs", [P, SLOTS, D], F32)
        xt = k.stage_sb("f0_xt", [P, 2, SLOTS * P], F32)
        ht = k.stage_sb("f0_ht", [P, HC, SLOTS * P], F32)
        logits = k.stage_sb("f0_logits", [P, T, EXPERTS], F32)
        half = SLOTS * P // 2
        pe_turn, act_turn = transposer(nc, k, "f0", normed, turned, turned_sb, xs, xt)
        hbank = [k.ps[5], k.ps[6]]
        k.prob_of = {"f0": k.stage_sb("f0_prob", [P, T, EXPERTS], F32)}

        @block.sync
        def _(sp):
            sp.dma_start(w1[:, :, :], k.io["L0_ffn_W1"].rearrange("(c p) n -> p c n", p=P)).then_inc(weights, 16)
            sp.dma_start(wg[:, :, :], k.io["L0_ffn_Wg"].rearrange("(f p) e -> p f e", p=P)).then_inc(weights, 16)
            with nc.allow_non_contiguous_dma(reason="a bias of 4 KB as columns"):
                sp.dma_start(b1[:, :], k.io["L0_ffn_b1"].rearrange("(f p) -> p f", p=P)).then_inc(weights, 16)
            sp.dma_start(bg[:, :], k.io["L0_ffn_bg"].partition_broadcast(P)).then_inc(weights, 16)

        @block.vector
        def _(dve):
            norm_stats(nc, k, dve, k.x, sums, inv, dev_ready, var_ready)
            dve.wait_ge(weights, 64)

            def tiles(g, first):
                for j in range(SLOTS):
                    t = g * SLOTS + j
                    after_earlier(dve, turned, first, t - (SLOTS - 1))
                    dve.tensor_scalar(xn[:, t, :], k.x[:, t, :], sums[:, 0, bass.ds(t, 1)], inv[:, bass.ds(t, 1)], ALU.subtract, ALU.mult)
                    dve.tensor_scalar(xs[:, j, :], k.x[:, t, :], sums[:, 0, bass.ds(t, 1)], inv[:, bass.ds(t, 1)],
                                      ALU.subtract, ALU.mult).then_inc(normed, 1)
                dve.wait_ge(gated, g + 1)
                dve.tensor_tensor(logits[:, bass.ds(g * SLOTS, SLOTS), :], k.ps[7][:, 0:SLOTS * EXPERTS].rearrange("p (j e) -> p j e", e=EXPERTS),
                                  bg[:, :].unsqueeze(1).to_broadcast([P, SLOTS, EXPERTS]), ALU.add).then_inc(logit_ready, 1)

            rounds(dve, GROUPS, tiles)
            dve.drain()
            route(nc, k, dve, "f0", logits, exp_ready, exp_done, mask_ready, counted, True)
            dve.sem_inc(placed, 1)

        @block.tensor
        def _(pe):
            pe.wait_ge(weights, 64)

            def tiles(g, first):
                pe_turn(pe, g)
                pe.wait_ge(turned_sb, (g + 1) * SLOTS)
                for f in range(HC):
                    for h in range(2):
                        n = 2 * f + h
                        if not (first and n < 2):
                            pe.wait_ge(hidden_sb, g * (2 * HC) + (n - 1))
                        for c in range(2):
                            mm = pe.matmul(hbank[h][:, 0:half], w1[:, c, f * P:(f + 1) * P], xt[:, c, h * half:(h + 1) * half], start=c == 0, stop=c == 1)
                        mm.then_inc(hidden, 1)
                pe.wait_ge(hidden_sb, (g + 1) * (2 * HC))
                after_earlier(pe, logit_ready, first, g)
                for j in range(SLOTS):
                    for f in range(HC):
                        mm = pe.matmul(k.ps[7][:, j * EXPERTS:(j + 1) * EXPERTS], ht[:, f, j * P:(j + 1) * P], wg[:, f, :], start=f == 0, stop=f == HC - 1)
                mm.then_inc(gated, 1)

            rounds(pe, GROUPS, tiles)
            pe.wait_ge(mask_ready, 1)
            count_tokens(k, pe).then_inc(counted, 1)

        @block.scalar
        def _(act):
            act.preload_act_table(ACT.Sqrt)
            act.wait_ge(var_ready, 1)
            act.activation(sums[:, 4, :], sums[:, 3, :], ACT.Sqrt, bias=k.eps[:, :]).then_inc(dev_ready, 1)
            act.wait_ge(weights, 64)
            act.preload_act_table(ACT.Gelu)

            def tiles(g, first):
                act_turn(act, g)
                after_earlier(act, gated, first, g)
                for f in range(HC):
                    for h in range(2):
                        act.wait_ge(hidden, g * (2 * HC) + (2 * f + h + 1))
                        act.activation(ht[:, f, h * half:(h + 1) * half], hbank[h][:, 0:half], ACT.Gelu, bias=b1[:, f:f + 1]).then_inc(hidden_sb, 1)

            rounds(act, GROUPS, tiles)
            act.wait_ge(exp_ready, 1)
            act.activation(k.prob_of["f0"][:, :, :], k.prob_of["f0"][:, :, :], ACT.Exp).then_inc(exp_done, 1)

        @block.gpsimd
        def _(pool):
            rows = k.sorted_dram.rearrange("(p r) d -> p r d", p=P)
            per = k.sorted_dram.shape[0] // P
            pool.wait_ge(normed, 1)
            pool.memset(k.wide_zero[:, :], 0.0).then_inc(zero_sent, 1)
            pool.wait_ge(zero_sent, 1)
            pool.dma_start(rows, k.wide_zero[:, 0:D].unsqueeze(1).to_broadcast([P, per, D])).then_inc(sent, 16)
            for a in range(TABLES):
                pool.dma_start(k.tables[1][a].rearrange("(p r) c -> p r c", p=P), k.wide_zero[:, :].unsqueeze(1).to_broadcast([P, TROWS // P, ROW]))\
                    .then_inc(k.all_scattered[1][a], 16)
            pool.wait_ge(sent, 16)
            pool.wait_ge(placed, 1)
            for t in range(T):
                pool.indirect_dma_start(out=k.sorted_dram, out_offset=bass.IndirectOffsetOnAxis(ap=k.send_i[:, t:t + 1], axis=0),
                                        in_=xn[:, t, :], in_offset=None).then_inc(sent, 16)
            pool.wait_ge(sent, 16 * (T + 1))
    k.end_stage()


def ffn0_experts_stage(nc, k):
    with nc.Block() as block:
        keyed, masked, key_turned, key_sb, key_out, key_in = (k.sem(f"x0_{n}") for n in ("keyed", "masked", "key_turned", "key_sb", "key_out", "key_in"))
        key = k.stage_sb("x0_key", [P, T], F32)
        key_t = k.stage_sb("x0_key_t", [T, P], F32)
        keys = k.stage_sb("x0_keys", [P, NP], F32)
        junk = k.stage_sb("x0_junk", [P, NP], F32)
        count = k.stage_sb("x0_count", [P, 4, T], F32)
        rank = k.stage_sb("x0_rank", [P, T], F32)
        weights, rows_in = k.sem("x0_weights"), k.sem("x0_rows_in")
        turned, turned_sb, hidden, hidden_sb = (k.sem(f"x0_{n}") for n in ("turned", "turned_sb", "hidden", "hidden_sb"))
        product, out_ready = k.sem("x0_product"), k.sem("x0_out_ready")
        stored = [k.sem(f"x0_stored{j}") for j in range(QUAD)]
        w1 = k.stage_sb("x0_w1", [P, 2, HID], F32)
        b1 = k.stage_sb("x0_b1", [P, HC], F32)
        wd = k.stage_sb("x0_wd", [P, EXPERTS, HC, D], F32)
        bd = k.stage_sb("x0_bd", [1, EXPERTS, D], F32)
        xs = k.stage_sb("x0_xs", [P, QUAD, D], F32)
        xt = k.stage_sb("x0_xt", [P, 2, QUAD * P], F32)
        ht = k.stage_sb("x0_ht", [P, HC, QUAD * P], F32)
        out = k.stage_sb("x0_out", [P, QUAD, D], F32)
        n_rounds = SORTED // QUAD

        @block.sync
        def _(sp):
            sp.dma_start(w1[:, :, :], k.io["L0_ffn_W1"].rearrange("(c p) n -> p c n", p=P)).then_inc(weights, 16)
            with nc.allow_non_contiguous_dma(reason="a bias of 4 KB as columns"):
                sp.dma_start(b1[:, :], k.io["L0_ffn_b1"].rearrange("(f p) -> p f", p=P)).then_inc(weights, 16)
            sp.dma_start(bd[:, :, :], k.io["L0_ffn_bd"].unsqueeze(0)).then_inc(weights, 16)
            for e in range(EXPERTS):
                sp.dma_start(wd[:, e, :, :], k.io["L0_ffn_Wd"][e].rearrange("(f p) n -> p f n", p=P)).then_inc(weights, 16)
            sp.wait_ge(key_sb, 1)
            sp.dma_start(k.order_row.rearrange("(t p) -> t p", p=P), key_t[:, :]).then_inc(key_out, 16)
            sp.wait_ge(key_out, 16)
            sp.dma_start(keys[:, :], k.order_row.partition_broadcast(P)).then_inc(key_in, 16)

            def tiles(g, first):
                after_earlier(sp, turned, first, g * QUAD)
                sp.dma_start(xs[:, :, :], k.sorted_dram[bass.ds(g * QUAD * P, QUAD * P), :].rearrange("(j p) d -> p j d", p=P)).then_inc(rows_in, 16)
                for j in range(QUAD):
                    sp.wait_ge(out_ready, g * QUAD + (j + 1))
                    sp.dma_start(k.result_dram[bass.ds((g * QUAD + j) * P, P), :], out[:, j, :]).then_inc(stored[j], 16)

            rounds(sp, n_rounds, tiles)
            for j in range(QUAD):
                sp.wait_ge(stored[j], 16 * n_rounds)

        @block.gpsimd
        def _(pool):
            pool.wait_ge(keyed, 1)
            pool.affine_select(out=key[:, :], in_=key[:, :], compare_op=ALU.is_ge, fill=1e30, base=NODES - 1,
                               pattern=[[-P, T]], channel_multiplier=-1).then_inc(masked, 1)

        @block.tensor
        def _(pe):
            pe.wait_ge(masked, 1)
            pe.transpose(k.ps[0][0:T, 0:P], key[:, :], k.ident[:, :]).then_inc(key_turned, 1)
            pe.wait_ge(key_sb, 1)
            pe.wait_ge(weights, (3 + EXPERTS) * 16)

            def tiles(g, first):
                pe.wait_ge(rows_in, g * 16 + 16)
                for j in range(QUAD):
                    pe.transpose(k.ps[j][:, 0:P], xs[:, j, 0:P], k.ident[:, :])
                    pe.transpose(k.ps[j][:, P:D], xs[:, j, P:D], k.ident[:, :]).then_inc(turned, 1)
                pe.wait_ge(turned_sb, g * QUAD + QUAD)
                for f in range(HC):
                    if not (first and f < 2):
                        pe.wait_ge(hidden_sb, g * HC + (f - 1))
                    for c in range(2):
                        mm = pe.matmul(k.ps[4 + f % 2][:, :], w1[:, c, f * P:(f + 1) * P], xt[:, c, :], start=c == 0, stop=c == 1)
                    mm.then_inc(hidden, 1)
                pe.wait_ge(hidden_sb, g * HC + HC)
                for j in range(QUAD):
                    e = pe.value_load(k.owner_i[0:1, bass.ds(g * QUAD + j, 1)], min_val=0, max_val=EXPERTS - 1)
                    if not (first and j < 2):
                        pe.wait_ge(out_ready, g * QUAD + (j - 1))
                    bank = k.ps[6 + j % 2]
                    for f in range(HC):
                        pe.matmul(bank[:, 0:D], ht[:, f, j * P:(j + 1) * P], wd[:, bass.ds(e, 1), f, :].rearrange("p a n -> p (a n)"), start=f == 0, stop=False)
                    pe.matmul(bank[:, 0:D], k.ones[0:1, :], bd[0:1, bass.ds(e, 1), :].rearrange("p a n -> p (a n)"), start=False, stop=True).then_inc(product, 1)

            rounds(pe, n_rounds, tiles)

        @block.scalar
        def _(act):
            act.wait_ge(key_turned, 1)
            act.activation(key_t[:, :], k.ps[0][0:T, 0:P], ACT.Copy).then_inc(key_sb, 1)
            act.wait_ge(weights, (3 + EXPERTS) * 16)
            act.preload_act_table(ACT.Gelu)

            def tiles(g, first):
                for j in range(QUAD):
                    act.wait_ge(turned, g * QUAD + (j + 1))
                    act.activation(xt[:, :, j * P:(j + 1) * P], k.ps[j][:, 0:D].rearrange("p (c n) -> p c n", c=2), ACT.Copy).then_inc(turned_sb, 1)
                after_earlier(act, product, first, g * QUAD)
                for f in range(HC):
                    act.wait_ge(hidden, g * HC + (f + 1))
                    act.activation(ht[:, f, :], k.ps[4 + f % 2][:, :], ACT.Gelu, bias=b1[:, f:f + 1]).then_inc(hidden_sb, 1)

            rounds(act, n_rounds, tiles)

        @block.vector
        def _(dve):
            def rank_tile(t):
                own, end = key[:, t:t + 1], (t + 1) * P
                if t > 0:
                    dve.tensor_scalar(junk[:, 0:t * P], keys[:, 0:t * P], own, 0.0, ALU.is_le, ALU.add, accum_out=count[:, 0, t:t + 1])
                dve.tensor_scalar(junk[:, t * P:NP], keys[:, t * P:NP], own, 0.0, ALU.is_lt, ALU.add, accum_out=count[:, 1, t:t + 1])
                dve.drain()
                dve.scalar_tensor_tensor(out=junk[:, 0:P], in0=keys[:, t * P:end], scalar=own, in1=k.below[:, :],
                                         op0=ALU.is_equal, op1=ALU.mult, accum_out=count[:, 2, t:t + 1])
                dve.drain()

            dve.tensor_tensor(key[:, :], k.degree[:, :], k.noise[:, :], ALU.add).then_inc(keyed, 1)
            dve.memset(count[:, :, :], 0.0)
            dve.drain()
            dve.wait_ge(key_in, 16)
            dve.wait_ge(masked, 1)
            for g in range(n_rounds):
                for j in range(QUAD):
                    if g > 0:
                        dve.wait_ge(stored[j], g * 16)
                    dve.wait_ge(product, g * QUAD + j + 1)
                    dve.tensor_copy(out[:, j, :], k.ps[6 + j % 2][:, 0:D]).then_inc(out_ready, 1)
                    if g * QUAD + j < T:
                        rank_tile(g * QUAD + j)
            dve.tensor_tensor(rank[:, :], count[:, 0, :], count[:, 1, :], ALU.add)
            dve.drain()
            dve.tensor_tensor(k.rank_i[:, :], rank[:, :], count[:, 2, :], ALU.add)
    k.end_stage()


def ffn0_return_stage(nc, k):
    with nc.Block() as block:
        back = [k.sem(f"r0_back{j}") for j in range(T)]
        rows = k.stage_sb("r0_rows", [P, T, D], F32)

        @block.gpsimd
        def _(pool):
            for t in range(T):
                pool.indirect_dma_start(out=rows[:, t, :], out_offset=None, in_=k.result_dram,
                                        in_offset=bass.IndirectOffsetOnAxis(ap=k.place_i[:, t:t + 1], axis=0)).then_inc(back[t], 16)

        @block.vector
        def _(dve):
            for t in range(T):
                dve.wait_ge(back[t], 16)
                dve.scalar_tensor_tensor(out=k.x[:, t, :], in0=rows[:, t, :], scalar=k.prb[:, t:t + 1], in1=k.x[:, t, :], op0=ALU.mult, op1=ALU.add)
    k.end_stage()


def by_tile(big):
    return big[:, :, :].rearrange("p c n -> p (c n)").rearrange("p (t d) -> p t d", d=D)


def l1_pre_stage(nc, k):
    with nc.Block() as block:
        x_saved = k.sem("p1_x_saved")
        weights, var_ready, dev_ready = k.sem("p1_weights"), k.sem("p1_var_ready"), k.sem("p1_dev_ready")
        normed, turned, turned_sb = k.sem("p1_normed"), k.sem("p1_turned"), k.sem("p1_turned_sb")
        product, out_ready = k.sem("p1_product"), k.sem("p1_out_ready")
        zeroed, spread, folded, folded_sb = (k.sem(f"p1_{n}") for n in ("zeroed", "spread", "folded", "folded_sb"))
        sent = k.sem("p1_sent")
        stored = [k.sem(f"p1_stored{j}") for j in range(SLOTS)]
        wn = k.stage_sb("p1_wn", [P, 2, D], F32)
        w = k.stage_sb("p1_w", [P, 2, D + 2 * HEADS], F32)
        acol = k.stage_sb("p1_acol", [P, 2, 2], F32)
        amat = k.stage_sb("p1_amat", [P, 2, 2 * HEADS], F32)
        sums = k.stage_sb("p1_sums", [P, 5, T], F32)
        inv = k.stage_sb("p1_inv", [P, T], F32)
        xn = k.stage_sb("p1_xn", [P, T, D], F32)
        xs = k.stage_sb("p1_xs", [P, SLOTS, D], F32)
        xt = k.stage_sb("p1_xt", [P, 2, SLOTS * P], F32)
        out = k.stage_sb("p1_out", [P, SLOTS, D], F32)
        pe_turn, act_turn = transposer(nc, k, "p1", normed, turned, turned_sb, xs, xt)

        @block.sync
        def _(sp):
            sp.dma_start(k.x_dram.rearrange("(t p) d -> p t d", p=P), k.x[:, :, :]).then_inc(x_saved, 16)
            sp.dma_start(wn[:, :, :], k.io["gat_w"].rearrange("(c p) n -> p c n", p=P)).then_inc(weights, 16)
            sp.dma_start(w[:, :, 0:D], k.io["gat_w_t"].rearrange("(c p) n -> p c n", p=P)).then_inc(weights, 16)
            with nc.allow_non_contiguous_dma(reason="2 KB as columns"):
                for a, v in enumerate((k.io["L1_gnn_gat_a_src"], k.io["L1_gnn_gat_a_tgt"])):
                    sp.dma_start(acol[:, a, :], v.rearrange("h f -> (h f)").rearrange("(c p) -> p c", p=P)).then_inc(weights, 16)
            def store(g, first):
                for j in range(SLOTS):
                    sp.wait_ge(out_ready, g * SLOTS + (j + 1))
                    sp.dma_start(k.nodes_dram[bass.ds((g * SLOTS + j) * P, P), :], out[:, j, :]).then_inc(stored[j], 16)

            rounds(sp, GROUPS, store)
            for j in range(SLOTS):
                sp.wait_ge(stored[j], 16 * GROUPS)
            sp.wait_ge(x_saved, 16)

        @block.gpsimd
        def _(pool):
            for t in range(T):
                pool.wait_ge(normed, t + 1)
                pool.indirect_dma_start(out=k.by_rank_dram, out_offset=bass.IndirectOffsetOnAxis(ap=k.rank_i[:, t:t + 1], axis=0),
                                        in_=xn[:, t, :], in_offset=None).then_inc(sent, 16)
            pool.wait_ge(sent, 16 * T)

        @block.vector
        def _(dve):
            dve.memset(amat[:, :, :], 0.0)
            dve.drain()
            dve.wait_ge(weights, 64)
            for a in range(2):
                for c in range(2):
                    for b in range(2):
                        lanes = slice(b * HD, (b + 1) * HD)
                        last = dve.tensor_copy(amat[lanes, c, a * HEADS + 2 * c + b:a * HEADS + 2 * c + b + 1], acol[lanes, a, c:c + 1])
            last.then_inc(spread, 1)
            dve.wait_ge(folded, 1)
            dve.tensor_copy(w[:, :, D:D + 2 * HEADS], k.ps[7][:, 0:4 * HEADS].rearrange("p (c a) -> p c a", c=2)).then_inc(folded_sb, 1)
            norm_stats(nc, k, dve, k.x, sums, inv, dev_ready, var_ready)

            def tiles(g, first):
                for j in range(SLOTS):
                    t = g * SLOTS + j
                    after_earlier(dve, turned, first, t - (SLOTS - 1))
                    dve.tensor_scalar(xn[:, t, :], k.x[:, t, :], sums[:, 0, bass.ds(t, 1)], inv[:, bass.ds(t, 1)], ALU.subtract, ALU.mult)
                    dve.tensor_scalar(xs[:, j, :], k.x[:, t, :], sums[:, 0, bass.ds(t, 1)], inv[:, bass.ds(t, 1)],
                                      ALU.subtract, ALU.mult).then_inc(normed, 1)
                for j in range(SLOTS):
                    t = g * SLOTS + j
                    bank = k.ps[5 + j % 3]
                    dve.wait_ge(product, t + 1)
                    after_earlier(dve, stored[j], first, g * 16)
                    dve.tensor_scalar(k.score[:, bass.ds(t, 1), :], bank[:, D:D + 2 * HEADS].unsqueeze(1), 0.0, None, ALU.add)
                    dve.tensor_copy(out[:, j, :], bank[:, 0:D]).then_inc(out_ready, 1)

            rounds(dve, GROUPS, tiles)

        @block.tensor
        def _(pe):
            pe.wait_ge(weights, 64)
            pe.wait_ge(spread, 1)
            for ci in range(2):
                for c in range(2):
                    mm = pe.matmul(k.ps[7][:, ci * 2 * HEADS:(ci + 1) * 2 * HEADS], wn[:, c, ci * P:(ci + 1) * P], amat[:, c, :], start=c == 0, stop=c == 1)
            mm.then_inc(folded, 1)
            pe.wait_ge(folded_sb, 1)

            def tiles(g, first):
                pe_turn(pe, g)
                pe.wait_ge(turned_sb, (g + 1) * SLOTS)
                for j in range(SLOTS):
                    if not (first and j < 2):
                        pe.wait_ge(out_ready, g * SLOTS + (j - 1))
                    for c in range(2):
                        mm = pe.matmul(k.ps[5 + j % 3][:, 0:D + 2 * HEADS], xt[:, c, j * P:(j + 1) * P], w[:, c, :], start=c == 0, stop=c == 1)
                    mm.then_inc(product, 1)

            rounds(pe, GROUPS, tiles)

        @block.scalar
        def _(act):
            act.preload_act_table(ACT.Sqrt)
            act.wait_ge(var_ready, 1)
            act.activation(sums[:, 4, :], sums[:, 3, :], ACT.Sqrt, bias=k.eps[:, :]).then_inc(dev_ready, 1)
            rounds(act, GROUPS, lambda g, first: act_turn(act, g))
    k.end_stage()


def attention_stage(nc, k):
    H = 4
    with nc.Block() as block:
        lows_in = [k.sem(f"a1_lows_in{h}") for h in range(2)]
        pool_step = k.sem("a1_pool_step")
        split, hot_ready, picked, taken = (k.sem(f"a1_{n}") for n in ("split", "hot_ready", "picked", "taken"))
        whole, masked, own_max, all_max, max_ready, done = (k.sem(f"a1_{n}") for n in ("whole", "masked", "own_max", "all_max", "max_ready", "done"))
        lows = k.stage_sb("a1_lows", [P, 2, 2, H * P], F32)
        hot = k.stage_sb("a1_hot", [P, 2, 2, H * P], F32)
        table = k.stage_sb("a1_table", [P, 2, T, HEADS], F32)
        tile = k.stage_sb("a1_tile", [P, 2, 2, H, T], F32)
        part = k.stage_sb("a1_part", [P, 2, H * HEADS, 2, T], F32)
        top = k.stage_sb("a1_top", [P, 1], F32)
        top_all = k.stage_sb("a1_top_all", [P, 1], F32)
        minus = k.stage_sb("a1_minus", [P, 1], F32)

        @block.sync
        def _(sp):
            def load(g, first):
                for h in range(2):
                    after_earlier(sp, hot_ready, first, g * 2 + (h - 1))
                    for a in range(2):
                        sp.dma_start(lows[:, h, a, :], k.low_row[a][bass.ds(g * UNROLL * P + h * H * P, H * P)].partition_broadcast(P)).then_inc(lows_in[h], 16)

            rounds(sp, ROUNDS, load)

        @block.vector
        def _(dve):
            for a in range(2):
                last = dve.tensor_copy(table[:, a, :, :], k.score[:, :, a * HEADS:(a + 1) * HEADS])
            last.then_inc(split, 1)
            lane = k.lane32[:, 0:T].unsqueeze(1).to_broadcast([P, H, T])

            def body(g, first):
                for h in range(2):
                    at = g * UNROLL + h * H
                    for a in range(2):
                        dve.tensor_tensor(tile[:, h, a, :, :], k.high[:, a, bass.ds(at, H)].unsqueeze(2).to_broadcast([P, H, T]), lane, ALU.is_equal)
                    dve.drain()
                    dve.wait_ge(picked, g * 2 + (h + 1))
                    for a in range(2):
                        got = k.ps[2 * h + a][:, 0:H * T * HEADS].rearrange("p (c a h) -> p c h a", c=H, a=T)
                        to = part[:, h, :, a, :].rearrange("p (c h) t -> p c h t", c=H)
                        last = dve.tensor_tensor(to, got, tile[:, h, a, :, :].unsqueeze(2).to_broadcast([P, H, HEADS, T]), ALU.mult)
                    last.then_inc(taken, 1)
                    dve.drain()
                    dve.tensor_reduce(k.attn[:, bass.ds(at, H), :], part[:, h, :, :, :].rearrange("p c a t -> p c (a t)"), AX, ALU.add)

            rounds(dve, ROUNDS, body)
            dve.drain()
            dve.scalar_tensor_tensor(out=k.attn[:, :, :], in0=k.attn[:, :, :], scalar=0.2, in1=k.attn[:, :, :], op0=ALU.mult, op1=ALU.max)\
               .then_inc(whole, 1)
            dve.wait_ge(masked, 1)
            dve.tensor_reduce(top[:, :], k.attn[:, :, :].rearrange("p c h -> p (c h)"), AX, ALU.max).then_inc(own_max, 1)
            dve.wait_ge(all_max, 1)
            dve.tensor_scalar(minus[:, :], top_all[:, :], -1.0, None, ALU.mult).then_inc(max_ready, 1)

        @block.tensor
        def _(pe):
            pe.wait_ge(split, 1)

            def body(g, first):
                for h in range(2):
                    pe.wait_ge(hot_ready, g * 2 + (h + 1))
                    after_earlier(pe, taken, first, g * 2 + (h - 1))
                    for a in range(2):
                        for c in range(H):
                            mm = pe.matmul(k.ps[2 * h + a][:, c * T * HEADS:(c + 1) * T * HEADS], hot[:, h, a, c * P:(c + 1) * P],
                                           table[:, a, :, :].rearrange("p t h -> p (t h)"), start=True, stop=True)
                    mm.then_inc(picked, 1)

            rounds(pe, ROUNDS, body)

        @block.gpsimd
        def _(pool):
            def body(g, first):
                for h in range(2):
                    pool.wait_ge(lows_in[h], (g + 1) * 32)
                    if not first:
                        pool.wait_ge(picked, g * 2 + (h - 1))
                    pool.sem_inc(pool_step, 1)
                    pool.tensor_scalar(hot[:, h, :, :], lows[:, h, :, :], k.own[:, :], None, ALU.is_equal).then_inc(hot_ready, 1)

            rounds(pool, ROUNDS, body)
            pool.wait_ge(whole, 1)
            pool.affine_select(out=k.attn[:, C - 1, :], in_=k.attn[:, C - 1, :], compare_op=ALU.is_ge, fill=-1e30,
                               base=EDGES - (C - 1) * P - 1, pattern=[[0, HEADS]], channel_multiplier=-1).then_inc(masked, 1)
            pool.wait_ge(own_max, 1)
            pool.partition_all_reduce(top_all[:, :], top[:, :], P, bass.bass_isa.ReduceOp.max).then_inc(all_max, 1)

        @block.scalar
        def _(act):
            act.wait_ge(max_ready, 1)
            act.activation(k.attn[:, :, :], k.attn[:, :, :], ACT.Exp, bias=minus[:, :]).then_inc(done, 1)
            act.wait_ge(done, 1)
    k.end_stage()


STATES, DT_RANK, TAPS = 16, 16, 4
HALF = SLOTS * P // 2
LOG1P = (1.0, -0.4999990463256836, 0.33330005407333374, -0.24954558908939362, 0.19678117334842682, -0.15311862528324127,
         0.10614264756441116, -0.057064201682806015, 0.019907161593437195, -0.003256378462538123)


SPAN = 640
SPANS = NP // SPAN
SBANK = SPAN // 2
PAIRS = STATES // 2
AHEAD = ROUNDS - SPANS * PAIRS
GN = SLOTS * P
assert AHEAD == 2 * GROUPS + 2


def edges_and_scan_stage(nc, k):
    H = TABLES
    table, scattered = k.tables[1], k.all_scattered[1]
    with nc.Block() as block:
        keys_in = [k.sem(f"es_keys_in{h}") for h in range(2)]
        gathered = [k.sem(f"es_gathered{s}") for s in range(H)]
        gather_i_ready, scatter_i_ready = k.sem("es_gather_i"), k.sem("es_scatter_i")
        scaled, summed, out_ready = k.sem("es_scaled"), k.sem("es_summed"), k.sem("es_out_ready")
        pool_step = k.sem("es_pool_step")
        bc_in = [k.sem(f"es_bc_in{b}") for b in range(2)]
        decayed, fed, scanned, weighed, added = (k.sem(f"es_{n}") for n in ("decayed", "fed", "scanned", "weighed", "added"))
        read_out = k.sem("es_read_out")
        weights, sp_step = k.sem("m1_weights"), k.sem("es_sp_step")
        rows_in, turned, turned_sb = k.sem("m1_rows_in"), k.sem("m1_turned"), k.sem("m1_turned_sb")
        product, evicted = k.sem("m1_product"), k.sem("m1_evicted")
        convolved, gated = k.sem("m1_convolved"), k.sem("m1_gated")
        low_rank, low_sb, low_out, stepped, step_sb = (k.sem(f"m1_{n}") for n in ("low_rank", "low_sb", "low_out", "stepped", "step_sb"))
        small, sized = k.sem("m1_small"), k.sem("m1_sized")
        a_ready, d_ready = k.sem("m1_a_ready"), k.sem("m1_d_ready")
        wi = k.stage_sb("m1_wi", [P, 2, 2 * D], F32)
        wx = k.stage_sb("m1_wx", [P, 2, DT_RANK + 2 * STATES], F32)
        wdt = k.stage_sb("m1_wdt", [DT_RANK, D], F32)
        cw = k.stage_sb("m1_cw", [P, 2, TAPS], F32)
        cb, db = k.stage_sb("m1_cb", [P, 2], F32), k.stage_sb("m1_db", [P, 2], F32)
        xs = k.stage_sb("m1_xs", [P, SLOTS, D], F32)
        xt = k.stage_sb("m1_xt", [P, 2, GN], F32)
        xc = k.stage_sb("m1_xc", [P, 2, TAPS - 1 + GN], F32)
        conv, poly = k.stage_sb("m1_conv", [P, 2, GN], F32), k.stage_sb("m1_poly", [P, 2, GN], F32)
        low = k.stage_sb("m1_low", [DT_RANK + 2 * STATES, GN], F32)
        keys = k.stage_sb("es_keys", [P, 2, H * P], F32)
        gi, si = k.stage_sb("es_gi", [P, 2, H], I32), k.stage_sb("es_si", [P, 2, H], I32)
        same = k.stage_sb("es_same", [P, H, P], F32)
        rows = k.stage_sb("es_rows", [P, H, D], F32)
        vals = k.stage_sb("es_vals", [P, H, ROW], F32)
        out = k.stage_sb("es_out", [P, H, ROW], F32)
        bc = k.stage_sb("es_bc", [P, 2, 2, SPAN], F32)
        decay = k.stage_sb("es_decay", [P, 2, 2, SPAN], F32)
        feed, state = poly, conv
        assert SPAN == GN
        weigh = k.stage_sb("es_weigh", [P, 2, 2, SPAN], F32)
        carry = k.stage_sb("es_carry", [P, 2, STATES], F32)

        def half_step(q, m, b, c):
            return (q * STATES + m * 2 + b) * 2 + c

        @block.sync
        def _(sp):
            def keys_load(g, h, first):
                if not first:
                    sp.wait_ge(scaled, g * UNROLL + (h * H + H - UNROLL))
                sp.dma_start(keys[:, h, :], k.dst_row[bass.ds(g * UNROLL * P + h * H * P, H * P)].partition_broadcast(P)).then_inc(keys_in[h], 16)

            def bc_load(q, m, b, first):
                if not first:
                    sp.wait_ge(weighed, half_step(q, m, b, 0) - 2)
                for a in range(2):
                    row = k.bc_dram[bass.ds(m * 2 + (a * STATES + b), 1), q * SPAN:(q + 1) * SPAN].rearrange("a n -> (a n)")
                    sp.dma_start(bc[:, b, a, :], row.partition_broadcast(P)).then_inc(bc_in[b], 16)

            def both(q, m, first):
                for b in range(2):
                    bc_load(q, m, b, first)
                    keys_load(AHEAD + q * PAIRS + m, b, False)

            def group(g, first):
                for b in range(2):
                    for h in range(2):
                        keys_load(g * 2 + b, h, first and b == 0)
                    if b == 0 and (first or not isinstance(g, int)):
                        sp.wait_ge(turned, g * SLOTS + SLOTS)
                        sp.sem_inc(sp_step, 1)
                        sp.dma_start(xs[:, :, :], k.by_rank_dram[bass.ds(g * GN + GN, GN), :].rearrange("(j p) d -> p j d", p=P)).then_inc(rows_in, 16)
                sp.wait_ge(low_sb, g * 2 + 2)
                sp.sem_inc(sp_step, 1)
                sp.dma_start(k.bc_dram[:, bass.ds(g * GN, GN)], low[DT_RANK:, :]).then_inc(low_out, 16)

            sp.dma_start(xs[:, :, :], k.by_rank_dram[0:GN, :].rearrange("(j p) d -> p j d", p=P)).then_inc(rows_in, 16)
            sp.dma_start(wi[:, :, :], k.io["in_proj_w_t"].rearrange("(c p) n -> p c n", p=P)).then_inc(weights, 16)
            sp.dma_start(wx[:, :, :], k.io["x_proj_w_t"].rearrange("(c p) n -> p c n", p=P)).then_inc(weights, 16)
            sp.dma_start(wdt[:, :], k.io["dt_proj_w_t"]).then_inc(weights, 16)
            sp.dma_start(cw[:, :, :], k.io["L1_gnn_conv_w"].rearrange("(c p) n -> p c n", p=P)).then_inc(weights, 16)
            with nc.allow_non_contiguous_dma(reason="biases of 1 KB as columns"):
                sp.dma_start(cb[:, :], k.io["L1_gnn_conv_b"].rearrange("(c p) -> p c", p=P)).then_inc(weights, 16)
                sp.dma_start(db[:, :], k.io["L1_gnn_dt_proj_b"].rearrange("(c p) -> p c", p=P)).then_inc(weights, 16)
                sp.dma_start(k.d_col[:, :], k.io["L1_gnn_D_param"].rearrange("(c p) -> p c", p=P)).then_inc(weights, 16)
            sp.dma_start(k.a_mat[:, :, :], k.io["L1_gnn_A_log"].rearrange("(c p) n -> p c n", p=P)).then_inc(weights, 16)
            group(0, True)
            with sp.Fori(1, GROUPS - 1) as g:
                group(g, False)
            group(GROUPS - 1, False)
            for g in range(2 * GROUPS, AHEAD):
                keys_load(g, 0, False)
                keys_load(g, 1, False)
            sp.wait_ge(low_out, 16 * GROUPS)
            for q in range(SPANS):
                both(q, 0, q == 0)
                with sp.Fori(1, PAIRS) as m:
                    both(q, m, False)

        @block.gpsimd
        def _(pool):
            def gather(h, s):
                pool.indirect_dma_start(out=rows[:, s, :], out_offset=None, in_=k.nodes_dram,
                                        in_offset=bass.IndirectOffsetOnAxis(ap=gi[:, h, s:s + 1], axis=0)).then_inc(gathered[s], 16)

            def body(g, last):
                for h in range(2):
                    for s in range(H):
                        pool.wait_ge(out_ready, g * UNROLL + (h * H + s + 1))
                        pool.wait_ge(scattered[s], g * 32 + (h * 16 + 16))
                        pool.sem_inc(pool_step, 1)
                        pool.indirect_dma_start(out=table[s], out_offset=bass.IndirectOffsetOnAxis(ap=si[:, h, s:s + 1], axis=0),
                                                in_=out[:, s, :], in_offset=None, compute_op=ALU.add).then_inc(scattered[s], 16)
                        if not (last and h == 1):
                            pool.wait_ge(scaled, g * UNROLL + (h * H + s + 1))
                            pool.wait_ge(gather_i_ready, g * 2 + (h + 2))
                            pool.sem_inc(pool_step, 1)
                            gather(1 - h, s)

            pool.wait_ge(gather_i_ready, 1)
            for s in range(H):
                gather(0, s)
            with pool.Fori(0, ROUNDS - 1) as g:
                body(g, False)
            body(ROUNDS - 1, True)
            for s in range(H):
                pool.wait_ge(scattered[s], (2 * ROUNDS + 1) * 16)

        @block.vector
        def _(dve):
            def indices(g, h):
                dve.tensor_scalar(gi[:, h, :], k.src_i[:, bass.ds(g * UNROLL + h * H, H)], 0.0, None, ALU.add).then_inc(gather_i_ready, 1)

            def start_half(g, h, first):
                dve.wait_ge(keys_in[h], (g + 1) * 16)
                if not first:
                    for s in range(H):
                        dve.wait_ge(scattered[s], g * 32 + h * 16)
                dve.tensor_scalar(si[:, h, :], k.dst_to[:, bass.ds(g * UNROLL + h * H, H)], 0.0, None, ALU.add).then_inc(scatter_i_ready, 1)
                indices(g + h, 1 - h)

            def chunk(g, h, s, first):
                at = g * UNROLL + (h * H + s)
                if not (first and h == 0):
                    dve.wait_ge(summed, at + (1 - H))
                dve.tensor_scalar(same[:, s, :], keys[:, h, s * P:(s + 1) * P], k.dst_col[:, bass.ds(at, 1)], None, ALU.is_equal)
                own = k.attn[:, bass.ds(at, 1), :].rearrange("p a h -> p (a h)")
                dve.tensor_scalar(vals[:, s, D:ROW], own, 0.0, None, ALU.add)
                dve.wait_ge(gathered[s], g * 32 + (h * 16 + 16))
                dve.tensor_tensor(vals[:, s, 0:D].rearrange("p (h f) -> p h f", f=HD), rows[:, s, :].rearrange("p (h f) -> p h f", f=HD),
                                  own.unsqueeze(2).to_broadcast([P, HEADS, HD]), ALU.mult).then_inc(scaled, 1)

            def feed_step(q, m, b, c, first):
                if not (first and b == 0):
                    dve.wait_ge(scanned, half_step(q, m, b, c) - 1)
                dve.tensor_tensor(feed[:, c, :], k.dtx[:, c, q * SPAN:(q + 1) * SPAN], bc[:, b, 0, :], ALU.mult).then_inc(fed, 1)

            def scan_step(q, m, b, c, first):
                n = half_step(q, m, b, c)
                dve.wait_ge(fed, n + 1)
                dve.wait_ge(decayed, n + 1)
                if not (first and b == 0):
                    dve.wait_ge(weighed, n - 1)
                dve.tensor_tensor_scan(state[:, c, :], decay[:, b, c, :], feed[:, c, :], carry[:, c, bass.ds(m * 2 + b, 1)],
                                       ALU.mult, ALU.add).then_inc(scanned, 1)

            def weigh_step(q, m, b, c, first):
                n = half_step(q, m, b, c)
                dve.wait_ge(scanned, n + 1)
                dve.tensor_scalar(carry[:, c, bass.ds(m * 2 + b, 1)], state[:, c, SPAN - 1:SPAN], 0.0, None, ALU.add)
                if not first:
                    dve.wait_ge(added, n - 3)
                dve.tensor_tensor(weigh[:, b, c, :], state[:, c, :], bc[:, b, 1, :], ALU.mult).then_inc(weighed, 1)

            def cols(big, g):
                return big[:, :, bass.ds(g * GN, GN)]

            def convolve(tap, last=False):
                for c in range(2):
                    if tap == 0:
                        op = dve.tensor_scalar(conv[:, c, :], xc[:, c, 0:GN], cw[:, c, 0:1], None, ALU.mult)
                    else:
                        op = dve.scalar_tensor_tensor(out=conv[:, c, :], in0=xc[:, c, tap:tap + GN], scalar=cw[:, c, tap:tap + 1], in1=conv[:, c, :],
                                                      op0=ALU.mult, op1=ALU.add)
                if last:
                    op.then_inc(convolved, 1)
                dve.drain()

            def size_step(g, n):
                if n == 0:
                    dve.wait_ge(small, g + 1)
                    dve.tensor_scalar(poly[:, :, :], cols(k.dtx, g), LOG1P[-1], None, ALU.mult)
                elif n < len(LOG1P):
                    dve.scalar_tensor_tensor(out=poly[:, :, :], in0=poly[:, :, :], scalar=LOG1P[-1 - n], in1=cols(k.dtx, g), op0=ALU.add, op1=ALU.mult)
                elif n == len(LOG1P):
                    dve.scalar_tensor_tensor(out=cols(k.dt, g), in0=cols(k.dt, g), scalar=0.0, in1=poly[:, :, :], op0=ALU.max, op1=ALU.add)
                else:
                    dve.tensor_tensor(cols(k.dtx, g), cols(k.dt, g), cols(k.u, g), ALU.mult).then_inc(sized, 1)
                dve.drain()

            def group(g, first):
                for b in range(2):
                    for h in range(2):
                        start_half(g * 2 + b, h, first and b == 0)
                        for s in range(H):
                            chunk(g * 2 + b, h, s, first and b == 0)
                            at = h * H + s
                            if not first and b == 0 and at < 5:
                                size_step(g - 1, at)
                            if not first and b == 1 and at < 7:
                                size_step(g - 1, 5 + at)
                            if b == 0 and at == 5:
                                dve.wait_ge(evicted, g * 8 + 4)
                                convolve(0)
                                convolve(1)
                            if b == 0 and at == 6:
                                convolve(2)
                            if b == 0 and at == 7:
                                convolve(3, True)

            def both(q, m, first):
                g = AHEAD + q * PAIRS + m
                for b in range(2):
                    start_half(g, b, False)
                    dve.wait_ge(bc_in[b], (q * PAIRS + m) * 32 + 32)
                    feed_step(q, m, b, 0, first)
                    chunk(g, b, 0, False)
                    scan_step(q, m, b, 0, first)
                    feed_step(q, m, b, 1, first)
                    chunk(g, b, 1, False)
                    scan_step(q, m, b, 1, first)
                    weigh_step(q, m, b, 0, first)
                    chunk(g, b, 2, False)
                    weigh_step(q, m, b, 1, first)
                    chunk(g, b, 3, False)

            dve.memset(carry[:, :, :], 0.0)
            dve.drain()
            indices(0, 0)
            dve.wait_ge(weights, 128)
            for c in range(2):
                dve.tensor_scalar(k.d_mat[:, c, :], k.ident[:, :], k.d_col[:, c:c + 1], None, ALU.mult).then_inc(d_ready, 1)
            dve.wait_ge(a_ready, 1)
            dve.tensor_scalar(k.a_mat[:, :, :], k.a_mat[:, :, :], -1.0, None, ALU.mult)
            rounds(dve, GROUPS, group)
            for b in range(2):
                for h in range(2):
                    start_half(2 * GROUPS + b, h, False)
                    for s in range(H):
                        chunk(2 * GROUPS + b, h, s, False)
                        if h * H + s < 6:
                            size_step(GROUPS - 1, b * 6 + h * H + s)
            for q in range(SPANS):
                both(q, 0, q == 0)
                with dve.Fori(1, PAIRS) as m:
                    both(q, m, False)
                dve.wait_ge(added, (q + 1) * 2 * STATES)
                for c in range(2):
                    for b in range(2):
                        at = q * SPAN + b * SBANK
                        dve.tensor_tensor(k.zs[:, c, at:at + SBANK], k.zs[:, c, at:at + SBANK], k.ps[4 + 2 * c + b][:, 0:SBANK], ALU.mult).then_inc(read_out, 1)
                dve.drain()

        @block.tensor
        def _(pe):
            def chunk(g, h, s, first):
                n = g * UNROLL + (h * H + s + 1)
                pe.wait_ge(scaled, n)
                if not (first and h == 0):
                    pe.wait_ge(out_ready, n - H)
                pe.matmul(k.ps[s][:, 0:ROW], same[:, s, :], vals[:, s, :], start=True, stop=True).then_inc(summed, 1)

            def add(q, m, b, c, last):
                pe.wait_ge(weighed, half_step(q, m, b, c) + 1)
                for a in range(2):
                    mm = pe.matmul(k.ps[4 + 2 * c + a][:, 0:SBANK], k.ident[:, :], weigh[:, b, c, a * SBANK:(a + 1) * SBANK],
                                   start=False, stop=last and b == 1)
                mm.then_inc(added, 1)

            def both(q, m, last):
                g = AHEAD + q * PAIRS + m
                for b in range(2):
                    chunk(g, b, 0, False)
                    chunk(g, b, 1, False)
                    add(q, m, b, 0, last)
                    chunk(g, b, 2, False)
                    add(q, m, b, 1, last)
                    chunk(g, b, 3, False)

            def project(g, n, first):
                if not (first and n < 4):
                    pe.wait_ge(evicted, g * 8 + (n - 3))
                for c in range(2):
                    mm = pe.matmul(k.ps[4 + n % 4][:, 0:HALF], wi[:, c, n // 2 * P:(n // 2 + 1) * P], xt[:, c, n % 2 * HALF:(n % 2 + 1) * HALF],
                                   start=c == 0, stop=c == 1)
                mm.then_inc(product, 1)

            def group_work(g, b, at, first):
                if b == 0 and at == 0:
                    pe.wait_ge(rows_in, (g + 1) * 16)
                    after_earlier(pe, step_sb, first, g * 4)
                    for j in range(SLOTS):
                        to = k.ps[4 + j // 2][:, j % 2 * D:(j % 2 + 1) * D]
                        pe.transpose(to[:, 0:P], xs[:, j, 0:P], k.ident[:, :])
                        pe.transpose(to[:, P:D], xs[:, j, P:D], k.ident[:, :]).then_inc(turned, 1)
                if b == 0 and 2 <= at <= 4:
                    if at == 2:
                        pe.wait_ge(turned_sb, g * 3 + 3)
                    project(g, 2 * at - 4, first)
                    project(g, 2 * at - 3, first)
                if b == 1 and at == 0:
                    project(g, 6, first)
                    project(g, 7, first)
                if b == 1 and at == 1:
                    pe.wait_ge(gated, g + 1)
                    pe.wait_ge(evicted, g * 8 + 6)
                    for h in range(2):
                        for c in range(2):
                            mm = pe.matmul(k.ps[4 + h][0:DT_RANK + 2 * STATES, 0:HALF], wx[:, c, :], k.u[:, c, bass.ds(g * GN + h * HALF, HALF)],
                                           start=c == 0, stop=c == 1)
                        mm.then_inc(low_rank, 1)
                if b == 1 and at == 3:
                    pe.wait_ge(evicted, g * 8 + 8)
                    pe.wait_ge(low_sb, g * 2 + 2)
                    for h in range(2):
                        for o in range(2):
                            pe.matmul(k.ps[(6, 7, 4, 5)[2 * h + o]][:, 0:HALF], wdt[:, o * P:(o + 1) * P], low[0:DT_RANK, h * HALF:(h + 1) * HALF],
                                      start=True, stop=True).then_inc(stepped, 1)

            def group(g, first):
                for b in range(2):
                    for h in range(2):
                        for s in range(H):
                            chunk(g * 2 + b, h, s, first and b == 0)
                            group_work(g, b, h * H + s, first)

            pe.wait_ge(weights, 128)
            rounds(pe, GROUPS, group)
            for g in range(2 * GROUPS, AHEAD):
                for h in range(2):
                    for s in range(H):
                        chunk(g, h, s, False)
            pe.wait_ge(step_sb, GROUPS * 4)
            pe.wait_ge(d_ready, 2)
            for q in range(SPANS):
                if q > 0:
                    pe.wait_ge(read_out, 4 * q)
                for c in range(2):
                    for a in range(2):
                        at = q * SPAN + a * SBANK
                        pe.matmul(k.ps[4 + 2 * c + a][:, 0:SBANK], k.d_mat[:, c, :], k.u[:, c, at:at + SBANK], start=True, stop=False)
                with pe.Fori(0, PAIRS - 1) as m:
                    both(q, m, False)
                both(q, PAIRS - 1, True)

        @block.scalar
        def _(act):
            def chunk(g, h, s, first):
                if not (first and h == 0):
                    act.wait_ge(scattered[s], g * 32 + (h * 16 + 16))
                act.wait_ge(summed, g * UNROLL + (h * H + s + 1))
                act.activation(out[:, s, :], k.ps[s][:, 0:ROW], ACT.Copy).then_inc(out_ready, 1)

            def decay_step(q, m, b, c, first):
                if not first:
                    act.wait_ge(scanned, half_step(q, m, b, c) - 3)
                act.activation(decay[:, b, c, :], k.dt[:, c, q * SPAN:(q + 1) * SPAN], ACT.Exp,
                               scale=k.a_mat[:, c, bass.ds(m * 2 + b, 1)]).then_inc(decayed, 1)

            def both(q, m, first, end=False):
                g = AHEAD + q * PAIRS + m
                for b in range(2):
                    later = (q, m, 1) if b == 0 else (q, m + 1, 0) if not end else (q + 1, 0, 0)
                    chunk(g, b, 0, False)
                    if later[0] < SPANS:
                        decay_step(*later, 0, first and b == 0)
                    chunk(g, b, 1, False)
                    chunk(g, b, 2, False)
                    if later[0] < SPANS:
                        decay_step(*later, 1, first and b == 0)
                    chunk(g, b, 3, False)

            def evict(g, n):
                h = n % 2
                act.wait_ge(product, g * 8 + (n + 1))
                if n < 4:
                    act.activation(xc[:, n // 2, TAPS - 1 + h * HALF:TAPS - 1 + (h + 1) * HALF], k.ps[4 + n % 4][:, 0:HALF], ACT.Copy).then_inc(evicted, 1)
                else:
                    act.activation(k.zs[:, n // 2 - 2, bass.ds(g * GN + h * HALF, HALF)], k.ps[4 + n % 4][:, 0:HALF], ACT.Silu).then_inc(evicted, 1)

            def group_work(g, b, at, first):
                if b == 0 and at == 0:
                    act.preload_act_table(ACT.Silu)
                    if not first:
                        act.wait_ge(convolved, g)
                        act.activation(xc[:, :, 0:TAPS - 1], xc[:, :, GN:GN + TAPS - 1], ACT.Copy)
                if b == 0 and at == 1:
                    for i in range(3):
                        n = min(2, SLOTS - 2 * i)
                        act.wait_ge(turned, g * SLOTS + (2 * i + n))
                        act.activation(xt[:, :, 2 * i * P:(2 * i + n) * P].rearrange("p c (j n) -> p j c n", n=P),
                                       k.ps[4 + i][:, 0:n * D].rearrange("p (j c n) -> p j c n", c=2, n=P), ACT.Copy).then_inc(turned_sb, 1)
                if b == 0 and 3 <= at <= 5:
                    evict(g, 2 * at - 6)
                    evict(g, 2 * at - 5)
                if b == 1 and at == 0:
                    act.wait_ge(convolved, g + 1)
                    for c in range(2):
                        last = act.activation(k.u[:, c, bass.ds(g * GN, GN)], conv[:, c, :], ACT.Silu, bias=cb[:, c:c + 1])
                    last.then_inc(gated, 1)
                if b == 1 and at == 1:
                    evict(g, 6)
                    evict(g, 7)
                if b == 1 and at == 2:
                    after_earlier(act, low_out, first, g * 16)
                    for h in range(2):
                        act.wait_ge(low_rank, g * 2 + (h + 1))
                        act.activation(low[:, h * HALF:(h + 1) * HALF], k.ps[4 + h][0:DT_RANK + 2 * STATES, 0:HALF], ACT.Copy).then_inc(low_sb, 1)
                if b == 1 and at == 4:
                    for h in range(2):
                        for o in range(2):
                            act.wait_ge(stepped, g * 4 + (2 * h + o + 1))
                            act.activation(k.dt[:, o, bass.ds(g * GN + h * HALF, HALF)], k.ps[(6, 7, 4, 5)[2 * h + o]][:, 0:HALF], ACT.Identity,
                                           bias=db[:, o:o + 1]).then_inc(step_sb, 1)
                    act.drain()
                    act.preload_act_table(ACT.Exp)
                if b == 1 and at == 5:
                    act.activation(k.dtx[:, :, bass.ds(g * GN, GN)], k.dt[:, :, bass.ds(g * GN, GN)], ACT.Abs)
                    act.drain()
                if b == 1 and at == 6:
                    act.activation(k.dtx[:, :, bass.ds(g * GN, GN)], k.dtx[:, :, bass.ds(g * GN, GN)], ACT.Exp, scale=-1.0).then_inc(small, 1)

            def group(g, first):
                for b in range(2):
                    for h in range(2):
                        for s in range(H):
                            chunk(g * 2 + b, h, s, first and b == 0)
                            group_work(g, b, h * H + s, first)

            act.activation(xc[:, :, 0:TAPS - 1], k.zero[:, :].unsqueeze(2).to_broadcast([P, 2, TAPS - 1]), ACT.Copy)
            act.wait_ge(weights, 128)
            act.activation(k.a_mat[:, :, :], k.a_mat[:, :, :], ACT.Exp).then_inc(a_ready, 1)
            act.wait_ge(scatter_i_ready, 1)
            rounds(act, GROUPS, group)
            for g in range(2 * GROUPS, AHEAD):
                for h in range(2):
                    for s in range(H):
                        chunk(g, h, s, False)
            act.wait_ge(sized, GROUPS)
            decay_step(0, 0, 0, 0, True)
            decay_step(0, 0, 0, 1, True)
            for q in range(SPANS):
                both(q, 0, q == 0)
                with act.Fori(1, PAIRS - 1) as m:
                    both(q, m, False)
                both(q, PAIRS - 1, False, True)
    k.end_stage()


def mamba_out_stage(nc, k):
    with nc.Block() as block:
        weights, copied, product, out_ready = (k.sem(f"o1_{n}") for n in ("weights", "copied", "product", "out_ready"))
        stored = [k.sem(f"o1_stored{j}") for j in range(SLOTS)]
        all_stored, back = k.sem("o1_all_stored"), k.sem("o1_back")
        w = k.stage_sb("o1_w", [P, 2, D], F32)
        yg = k.stage_sb("o1_yg", [P, 2, SLOTS * P], F32)
        out = k.stage_sb("o1_out", [P, SLOTS, D], F32)

        @block.sync
        def _(sp):
            sp.dma_start(w[:, :, :], k.io["out_proj_w_t"].rearrange("(c p) n -> p c n", p=P)).then_inc(weights, 16)

            def store(g, first):
                for j in range(SLOTS):
                    sp.wait_ge(out_ready, g * SLOTS + (j + 1))
                    sp.dma_start(k.scan_dram[bass.ds((g * SLOTS + j) * P, P), :], out[:, j, :]).then_inc(stored[j], 16)

            rounds(sp, GROUPS, store)
            for j in range(SLOTS):
                sp.wait_ge(stored[j], 16 * GROUPS)
            sp.sem_inc(all_stored, 1)

        @block.gpsimd
        def _(pool):
            pool.wait_ge(all_stored, 1)
            for t in range(T):
                pool.indirect_dma_start(out=k.ha[:, t, :], out_offset=None, in_=k.scan_dram,
                                        in_offset=bass.IndirectOffsetOnAxis(ap=k.rank_i[:, t:t + 1], axis=0)).then_inc(back, 16)
            pool.wait_ge(back, 16 * T)

        @block.scalar
        def _(act):
            act.preload_act_table(ACT.Copy)

            def copy(g, first):
                after_earlier(act, product, first, g * SLOTS)
                act.activation(yg[:, :, :], k.zs[:, :, bass.ds(g * SLOTS * P, SLOTS * P)], ACT.Copy).then_inc(copied, 1)

            rounds(act, GROUPS, copy)

        @block.tensor
        def _(pe):
            pe.wait_ge(weights, 16)

            def tiles(g, first):
                pe.wait_ge(copied, g + 1)
                for j in range(SLOTS):
                    after_earlier(pe, out_ready, first, g * SLOTS + (j + 1 - SLOTS))
                    for c in range(2):
                        mm = pe.matmul(k.ps[j][:, 0:D], yg[:, c, j * P:(j + 1) * P], w[:, c, :], start=c == 0, stop=c == 1)
                    mm.then_inc(product, 1)

            rounds(pe, GROUPS, tiles)

        @block.vector
        def _(dve):
            def tiles(g, first):
                for j in range(SLOTS):
                    after_earlier(dve, stored[j], first, g * 16)
                    dve.wait_ge(product, g * SLOTS + (j + 1))
                    dve.tensor_copy(out[:, j, :], k.ps[j][:, 0:D]).then_inc(out_ready, 1)

            rounds(dve, GROUPS, tiles)
    k.end_stage()


def l1_post_stage(nc, k):
    with nc.Block() as block:
        x_back = k.sem("q1_x_back")
        weights, tables_in, folded = k.sem("q1_weights"), k.sem("q1_tables_in"), k.sem("q1_folded")
        var = [k.sem(f"q1_var{i}") for i in range(4)]
        dev = [k.sem(f"q1_dev{i}") for i in range(4)]
        raw, expd = k.sem("q1_raw"), k.sem("q1_expd")
        normed, turned, turned_sb, gate_mm, gated = (k.sem(f"q1_{n}") for n in ("normed", "turned", "turned_sb", "gate_mm", "gated"))
        mixed, h_turned, h_turned_sb, hidden, hidden_sb, ff_mm = (k.sem(f"q1_{n}") for n in ("mixed", "h_turned", "h_turned_sb", "hidden", "hidden_sb", "ff_mm"))
        FF = 2 * D
        FC = FF // P
        wl, wg = k.stage_sb("q1_wl", [P, 2, D], F32), k.stage_sb("q1_wg", [P, 2, D], F32)
        f1w, f2w = k.stage_sb("q1_f1w", [P, 2, FF], F32), k.stage_sb("q1_f2w", [P, FC, D], F32)
        f1b, f2b = k.stage_sb("q1_f1b", [P, FC], F32), k.stage_sb("q1_f2b", [1, D], F32)
        gat_b = k.stage_sb("q1_gat_b", [P, D], F32)
        gains = k.stage_sb("q1_gains", [P, 3, D], F32)
        shifts = k.stage_sb("q1_shifts", [P, 3, D], F32)
        part = k.stage_sb("q1_part", [P, TABLES, SLOTS, ROW], F32)
        total = k.stage_sb("q1_total", [P, SLOTS, ROW], F32)
        den = k.stage_sb("q1_den", [P, SLOTS, HEADS], F32)
        sums = [k.stage_sb(f"q1_sums{i}", [P, 5, T], F32) for i in range(4)]
        inv = [k.stage_sb(f"q1_inv{i}", [P, T], F32) for i in range(4)]
        xg = k.stage_sb("q1_xg", [P, SLOTS, D], F32)
        ls, gs = k.stage_sb("q1_ls", [P, SLOTS, D], F32), k.stage_sb("q1_gs", [P, SLOTS, D], F32)
        gate = k.stage_sb("q1_gate", [P, SLOTS, D], F32)
        both_t = k.stage_sb("q1_both_t", [P, 4, SLOTS * P], F32)
        h_t = k.stage_sb("q1_h_t", [P, 2, SLOTS * P], F32)
        f1 = k.stage_sb("q1_f1", [P, FC, SLOTS * P], F32)
        over = lambda a: a.unsqueeze(1).to_broadcast([P, SLOTS, D])
        heads = lambda a: a.rearrange("p j (h f) -> p j h f", f=HD)

        @block.sync
        def _(sp):
            sp.dma_start(k.x[:, :, :], k.x_dram.rearrange("(t p) d -> p t d", p=P)).then_inc(x_back, 16)
            for dst, src in ((wl, k.io["wl_t"]), (wg, k.io["wg_t"]), (f1w, k.io["ff1_w_t"]), (f2w, k.io["ff2_w_t"])):
                sp.dma_start(dst[:, :, :], src.rearrange("(c p) n -> p c n", p=P)).then_inc(weights, 16)
            with nc.allow_non_contiguous_dma(reason="a bias of 2 KB as columns"):
                sp.dma_start(f1b[:, :], k.io["L1_gnn_ff1_b"].rearrange("(c p) -> p c", p=P)).then_inc(weights, 16)
            sp.dma_start(f2b[:, :], row_view(k.io["L1_gnn_ff2_b"], D)).then_inc(weights, 16)
            sp.dma_start(gat_b[:, :], k.io["L1_gnn_gat_b"].partition_broadcast(P)).then_inc(weights, 16)
            for i, (g, b) in enumerate(((k.io["L1_gnn_ln_local_g"], k.io["L1_gnn_ln_local_b"]), (k.io["L1_gnn_ln_global_g"], k.io["L1_gnn_ln_global_b"]),
                                        (k.io["L1_gnn_ln2_g"], k.io["L1_gnn_ln2_b"]))):
                sp.dma_start(gains[:, i, :], g.partition_broadcast(P)).then_inc(weights, 16)
                sp.dma_start(shifts[:, i, :], b.partition_broadcast(P)).then_inc(weights, 16)

            def load(g, first):
                after_earlier(sp, folded, first, g)
                for a in range(TABLES):
                    rows = k.tables[1][a][bass.ds(g * SLOTS * P, SLOTS * P), :].rearrange("(j p) c -> p j c", p=P)
                    sp.dma_start(part[:, a, :, :], rows).then_inc(tables_in, 16)

            rounds(sp, GROUPS, load)

        @block.vector
        def _(dve):
            dve.wait_ge(x_back, 16)
            norm_stats(nc, k, dve, k.x, sums[0], inv[0], dev[0], var[0])
            dve.wait_ge(weights, 13 * 16)

            def branches(g, first):
                here = bass.ds(g * SLOTS, SLOTS)
                dve.wait_ge(tables_in, (g + 1) * (16 * TABLES))
                dve.tensor_tensor(part[:, 0:2, :, :], part[:, 0:2, :, :], part[:, 2:4, :, :], ALU.add)
                for j in range(SLOTS):
                    t = g * SLOTS + j
                    dve.tensor_scalar(xg[:, j, :], k.x[:, t, :], sums[0][:, 0, bass.ds(t, 1)], inv[0][:, bass.ds(t, 1)], ALU.subtract, ALU.mult)
                dve.drain()
                dve.tensor_tensor(total[:, :, :], part[:, 0, :, :], part[:, 1, :, :], ALU.add).then_inc(folded, 1)
                dve.tensor_tensor(k.ha[:, here, :], k.ha[:, here, :], xg[:, :, :], ALU.add)
                dve.drain()
                dve.tensor_tensor(xg[:, :, :], xg[:, :, :], over(gat_b[:, :]), ALU.add)
                dve.tensor_scalar(den[:, :, :], total[:, :, D:ROW], 1e-16, None, ALU.add)
                dve.drain()
                dve.reciprocal(den[:, :, :], den[:, :, :])
                dve.drain()
                dve.tensor_tensor(heads(total[:, :, 0:D]), heads(total[:, :, 0:D]), den[:, :, :].unsqueeze(3).to_broadcast([P, SLOTS, HEADS, HD]), ALU.mult)
                dve.drain()
                dve.tensor_tensor(xg[:, :, :], xg[:, :, :], total[:, :, 0:D], ALU.add)
                dve.drain()
                dve.tensor_scalar(gate[:, :, :], xg[:, :, :], 0.0, None, ALU.min).then_inc(raw, 1)
                dve.wait_ge(expd, g + 1)
                dve.scalar_tensor_tensor(out=xg[:, :, :], in0=xg[:, :, :], scalar=0.0, in1=gate[:, :, :], op0=ALU.max, op1=ALU.add)
                dve.drain()
                dve.tensor_scalar(k.hl[:, here, :], xg[:, :, :], -1.0, None, ALU.add)
                dve.drain()

            rounds(dve, GROUPS, branches)
            norm_stats(nc, k, dve, k.hl, sums[1], inv[1], dev[1], var[1])
            norm_stats(nc, k, dve, k.ha, sums[2], inv[2], dev[2], var[2])

            def mix(g, first):
                here = bass.ds(g * SLOTS, SLOTS)
                for j in range(SLOTS):
                    t = g * SLOTS + j
                    for i, (dst, src) in enumerate(((ls, k.hl), (gs, k.ha))):
                        dve.tensor_scalar(dst[:, j, :], src[:, t, :], sums[1 + i][:, 0, bass.ds(t, 1)], inv[1 + i][:, bass.ds(t, 1)], ALU.subtract, ALU.mult)
                dve.drain()
                for i, dst in enumerate((ls, gs)):
                    dve.tensor_tensor(dst[:, :, :], dst[:, :, :], over(gains[:, i, :]), ALU.mult)
                dve.drain()
                for i, dst in enumerate((ls, gs)):
                    last = dve.tensor_tensor(dst[:, :, :], dst[:, :, :], over(shifts[:, i, :]), ALU.add)
                last.then_inc(normed, 1)
                dve.drain()
                dve.wait_ge(turned, (g + 1) * SLOTS)
                dve.tensor_tensor(ls[:, :, :], ls[:, :, :], gs[:, :, :], ALU.subtract)
                dve.drain()
                dve.wait_ge(gated, (g + 1) * SLOTS)
                dve.tensor_tensor(ls[:, :, :], ls[:, :, :], gate[:, :, :], ALU.mult)
                dve.drain()
                dve.tensor_tensor(gs[:, :, :], gs[:, :, :], ls[:, :, :], ALU.add).then_inc(mixed, 1)
                for j in range(SLOTS):
                    dve.wait_ge(ff_mm, g * SLOTS + (j + 1))
                    dve.tensor_tensor(k.hl[:, bass.ds(g * SLOTS + j, 1), :], gs[:, j:j + 1, :], k.ps[j][:, 0:D].unsqueeze(1), ALU.add)
                dve.drain()

            rounds(dve, GROUPS, mix)
            norm_stats(nc, k, dve, k.hl, sums[3], inv[3], dev[3], var[3])

            def add(g, first):
                here = bass.ds(g * SLOTS, SLOTS)
                for j in range(SLOTS):
                    t = g * SLOTS + j
                    dve.tensor_scalar(ls[:, j, :], k.hl[:, t, :], sums[3][:, 0, bass.ds(t, 1)], inv[3][:, bass.ds(t, 1)], ALU.subtract, ALU.mult)
                dve.drain()
                dve.tensor_tensor(ls[:, :, :], ls[:, :, :], over(gains[:, 2, :]), ALU.mult)
                dve.tensor_tensor(k.x[:, here, :], k.x[:, here, :], over(shifts[:, 2, :]), ALU.add)
                dve.drain()
                dve.tensor_tensor(k.x[:, here, :], k.x[:, here, :], ls[:, :, :], ALU.add)
                dve.drain()

            rounds(dve, GROUPS, add)

        @block.scalar
        def _(act):
            def root(i):
                act.wait_ge(var[i], 1)
                act.activation(sums[i][:, 4, :], sums[i][:, 3, :], ACT.Sqrt, bias=k.eps[:, :]).then_inc(dev[i], 1)

            act.preload_act_table(ACT.Sqrt)
            root(0)
            act.preload_act_table(ACT.Exp)

            def branches(g, first):
                act.wait_ge(raw, g + 1)
                act.activation(gate[:, :, :], gate[:, :, :], ACT.Exp).then_inc(expd, 1)

            rounds(act, GROUPS, branches)
            act.preload_act_table(ACT.Sqrt)
            root(1)
            root(2)
            act.wait_ge(weights, 13 * 16)
            act.preload_act_table(ACT.Sigmoid)

            def mix(g, first):
                for j in range(SLOTS):
                    act.wait_ge(turned, g * SLOTS + (j + 1))
                    act.activation(both_t[:, :, j * P:(j + 1) * P], k.ps[j][:, :].rearrange("p (c n) -> p c n", c=4), ACT.Copy).then_inc(turned_sb, 1)
                for j in range(SLOTS):
                    act.wait_ge(gate_mm, g * SLOTS + (j + 1))
                    act.activation(gate[:, j, :], k.ps[5 + j % 3][:, 0:D], ACT.Sigmoid).then_inc(gated, 1)
                for j in range(SLOTS):
                    act.wait_ge(h_turned, g * SLOTS + (j + 1))
                    act.activation(h_t[:, :, j * P:(j + 1) * P], k.ps[j][:, 0:D].rearrange("p (c n) -> p c n", c=2), ACT.Copy).then_inc(h_turned_sb, 1)
                for f in range(FC):
                    for h in range(2):
                        act.wait_ge(hidden, g * (2 * FC) + (2 * f + h + 1))
                        act.activation(f1[:, f, h * HALF:(h + 1) * HALF], k.ps[5 + h][:, 0:HALF], ACT.Relu, bias=f1b[:, f:f + 1]).then_inc(hidden_sb, 1)

            rounds(act, GROUPS, mix)
            act.preload_act_table(ACT.Sqrt)
            root(3)

        @block.tensor
        def _(pe):
            pe.wait_ge(weights, 13 * 16)

            def mix(g, first):
                pe.wait_ge(normed, g + 1)
                for j in range(SLOTS):
                    for c in range(4):
                        mm = pe.transpose(k.ps[j][:, c * P:(c + 1) * P], (ls, gs)[c // 2][:, j, (c % 2) * P:(c % 2 + 1) * P], k.ident[:, :])
                    mm.then_inc(turned, 1)
                for j in range(SLOTS):
                    pe.wait_ge(turned_sb, g * SLOTS + (j + 1))
                    if j >= 3:
                        pe.wait_ge(gated, g * SLOTS + (j - 2))
                    for c in range(4):
                        mm = pe.matmul(k.ps[5 + j % 3][:, 0:D], both_t[:, c, j * P:(j + 1) * P], (wl, wg)[c // 2][:, c % 2, :], start=c == 0, stop=c == 3)
                    mm.then_inc(gate_mm, 1)
                pe.wait_ge(mixed, g + 1)
                for j in range(SLOTS):
                    pe.transpose(k.ps[j][:, 0:P], gs[:, j, 0:P], k.ident[:, :])
                    pe.transpose(k.ps[j][:, P:D], gs[:, j, P:D], k.ident[:, :]).then_inc(h_turned, 1)
                pe.wait_ge(h_turned_sb, (g + 1) * SLOTS)
                for f in range(FC):
                    for h in range(2):
                        n = 2 * f + h
                        if n >= 2:
                            pe.wait_ge(hidden_sb, g * (2 * FC) + (n - 1))
                        for c in range(2):
                            mm = pe.matmul(k.ps[5 + h][:, 0:HALF], f1w[:, c, f * P:(f + 1) * P], h_t[:, c, h * HALF:(h + 1) * HALF], start=c == 0, stop=c == 1)
                        mm.then_inc(hidden, 1)
                pe.wait_ge(hidden_sb, (g + 1) * (2 * FC))
                for j in range(SLOTS):
                    for f in range(FC):
                        pe.matmul(k.ps[j][:, 0:D], f1[:, f, j * P:(j + 1) * P], f2w[:, f, :], start=f == 0, stop=False)
                    pe.matmul(k.ps[j][:, 0:D], k.ones[0:1, :], f2b[0:1, :], start=False, stop=True).then_inc(ff_mm, 1)

            rounds(pe, GROUPS, mix)
    k.end_stage()


def ffn1_route_stage(nc, k):
    with nc.Block() as block:
        weights, var_ready, dev_ready = k.sem("g1_weights"), k.sem("g1_var_ready"), k.sem("g1_dev_ready")
        normed, turned, turned_sb = k.sem("g1_normed"), k.sem("g1_turned"), k.sem("g1_turned_sb")
        gated, logit_ready = k.sem("g1_gated"), k.sem("g1_logit_ready")
        exp_ready, exp_done, mask_ready, counted = (k.sem(f"g1_{n}") for n in ("exp_ready", "exp_done", "mask_ready", "counted"))
        placed, sent = k.sem("g1_placed"), k.sem("g1_sent")
        wg = k.stage_sb("g1_wg", [P, 2, EXPERTS], F32)
        bg = k.stage_sb("g1_bg", [P, EXPERTS], F32)
        sums = k.stage_sb("g1_sums", [P, 5, T], F32)
        inv = k.stage_sb("g1_inv", [P, T], F32)
        xn = k.stage_sb("g1_xn", [P, T, D], F32)
        xs = k.stage_sb("g1_xs", [P, SLOTS, D], F32)
        xt = k.stage_sb("g1_xt", [P, 2, SLOTS * P], F32)
        logits = k.stage_sb("g1_logits", [P, T, EXPERTS], F32)
        pe_turn, act_turn = transposer(nc, k, "g1", normed, turned, turned_sb, xs, xt)
        k.prob_of["g1"] = k.stage_sb("g1_prob", [P, T, EXPERTS], F32)

        @block.sync
        def _(sp):
            sp.dma_start(wg[:, :, :], k.io["L1_ffn_gate_w"].rearrange("(c p) e -> p c e", p=P)).then_inc(weights, 16)
            sp.dma_start(bg[:, :], k.io["L1_ffn_gate_b"].partition_broadcast(P)).then_inc(weights, 16)

        @block.vector
        def _(dve):
            norm_stats(nc, k, dve, k.x, sums, inv, dev_ready, var_ready)
            dve.wait_ge(weights, 32)

            def tiles(g, first):
                for j in range(SLOTS):
                    t = g * SLOTS + j
                    after_earlier(dve, turned, first, t - (SLOTS - 1))
                    dve.tensor_scalar(xn[:, t, :], k.x[:, t, :], sums[:, 0, bass.ds(t, 1)], inv[:, bass.ds(t, 1)], ALU.subtract, ALU.mult)
                    dve.tensor_scalar(xs[:, j, :], k.x[:, t, :], sums[:, 0, bass.ds(t, 1)], inv[:, bass.ds(t, 1)],
                                      ALU.subtract, ALU.mult).then_inc(normed, 1)
                dve.wait_ge(gated, g + 1)
                dve.tensor_tensor(logits[:, bass.ds(g * SLOTS, SLOTS), :], k.ps[7][:, 0:SLOTS * EXPERTS].rearrange("p (j e) -> p j e", e=EXPERTS),
                                  bg[:, :].unsqueeze(1).to_broadcast([P, SLOTS, EXPERTS]), ALU.add).then_inc(logit_ready, 1)

            rounds(dve, GROUPS, tiles)
            dve.drain()
            route(nc, k, dve, "g1", logits, exp_ready, exp_done, mask_ready, counted, False)
            dve.sem_inc(placed, 1)

        @block.tensor
        def _(pe):
            pe.wait_ge(weights, 32)

            def tiles(g, first):
                pe_turn(pe, g)
                pe.wait_ge(turned_sb, (g + 1) * SLOTS)
                after_earlier(pe, logit_ready, first, g)
                for j in range(SLOTS):
                    for c in range(2):
                        mm = pe.matmul(k.ps[7][:, j * EXPERTS:(j + 1) * EXPERTS], xt[:, c, j * P:(j + 1) * P], wg[:, c, :], start=c == 0, stop=c == 1)
                mm.then_inc(gated, 1)

            rounds(pe, GROUPS, tiles)
            pe.wait_ge(mask_ready, 1)
            count_tokens(k, pe).then_inc(counted, 1)

        @block.scalar
        def _(act):
            act.preload_act_table(ACT.Sqrt)
            act.wait_ge(var_ready, 1)
            act.activation(sums[:, 4, :], sums[:, 3, :], ACT.Sqrt, bias=k.eps[:, :]).then_inc(dev_ready, 1)

            def tiles(g, first):
                after_earlier(act, gated, first, g)
                act_turn(act, g)

            rounds(act, GROUPS, tiles)
            act.wait_ge(exp_ready, 1)
            act.activation(k.prob_of["g1"][:, :, :], k.prob_of["g1"][:, :, :], ACT.Exp).then_inc(exp_done, 1)

        @block.gpsimd
        def _(pool):
            rows = k.sorted_dram.rearrange("(p r) d -> p r d", p=P)
            per = k.sorted_dram.shape[0] // P
            pool.dma_start(rows, k.wide_zero[:, 0:D].unsqueeze(1).to_broadcast([P, per, D])).then_inc(sent, 16)
            pool.wait_ge(sent, 16)
            pool.wait_ge(placed, 1)
            for t in range(T):
                pool.indirect_dma_start(out=k.sorted_dram, out_offset=bass.IndirectOffsetOnAxis(ap=k.send_i[:, t:t + 1], axis=0),
                                        in_=xn[:, t, :], in_offset=None, bounds_check=EXPERTS * BUF - 1, oob_is_err=False).then_inc(sent, 16)
            pool.wait_ge(sent, 16 * (T + 1))
    k.end_stage()


BT = BUF // P
assert EXPERTS * BUF == SORTED * P and CAPACITY <= BUF


def ffn1_experts_stage(nc, k):
    with nc.Block() as block:
        loaded = [k.sem(f"y1_loaded{s}") for s in range(2)]
        turned, turned_sb, hidden, hidden_sb = (k.sem(f"y1_{n}") for n in ("turned", "turned_sb", "hidden", "hidden_sb"))
        product, out_ready = k.sem("y1_product"), k.sem("y1_out_ready")
        stored = [k.sem(f"y1_stored{j}") for j in range(BT)]
        w1 = k.stage_sb("y1_w1", [P, 2, 2, HID], F32)
        w2 = k.stage_sb("y1_w2", [P, 2, HC, D], F32)
        b1, b2 = k.stage_sb("y1_b1", [P, 2, HC], F32), k.stage_sb("y1_b2", [1, 2, D], F32)
        xs = k.stage_sb("y1_xs", [P, 2, BT, D], F32)
        xt = k.stage_sb("y1_xt", [P, 2, BUF], F32)
        ht = k.stage_sb("y1_ht", [P, HC, BUF], F32)
        out = k.stage_sb("y1_out", [P, BT, D], F32)
        n_rounds = EXPERTS // 2

        @block.sync
        def _(sp):
            def load(r, s, first):
                e = r * 2 + s
                after_earlier(sp, product, first, e * BT - BT)
                sp.dma_start(xs[:, s, :, :], k.sorted_dram[bass.ds(e * BUF, BUF), :].rearrange("(j p) d -> p j d", p=P)).then_inc(loaded[s], 16)
                sp.dma_start(w1[:, s, :, :], k.io["L1_ffn_w1"][bass.ds(e, 1)].rearrange("a (c p) n -> p (a c) n", p=P)).then_inc(loaded[s], 16)
                sp.dma_start(w2[:, s, :, :], k.io["L1_ffn_w2"][bass.ds(e, 1)].rearrange("a (f p) n -> p (a f) n", p=P)).then_inc(loaded[s], 16)
                with nc.allow_non_contiguous_dma(reason="a bias of 4 KB as columns"):
                    sp.dma_start(b1[:, s, :], k.io["L1_ffn_b1"][bass.ds(e, 1)].rearrange("a (f p) -> p (a f)", p=P)).then_inc(loaded[s], 16)
                sp.dma_start(b2[:, s, :], k.io["L1_ffn_b2"][bass.ds(e, 1)]).then_inc(loaded[s], 16)

            load(0, 0, True)

            def tiles(r, last):
                load(r, 1, isinstance(r, int))
                for s in range(2):
                    e = r * 2 + s
                    for j in range(BT):
                        sp.wait_ge(out_ready, e * BT + (j + 1))
                        sp.dma_start(k.result_dram[bass.ds(e * BUF + j * P, P), :], out[:, j, :]).then_inc(stored[j], 16)
                    if s == 0 and not last:
                        load(r + 1, 0, False)

            tiles(0, False)
            with sp.Fori(1, n_rounds - 1) as r:
                tiles(r, False)
            tiles(n_rounds - 1, True)
            for j in range(BT):
                sp.wait_ge(stored[j], 16 * EXPERTS)

        @block.tensor
        def _(pe):
            def tiles(r, first):
                for s in range(2):
                    e = r * 2 + s
                    pe.wait_ge(loaded[s], (r + 1) * (5 * 16))
                    for j in range(BT):
                        pe.transpose(k.ps[j][:, 0:P], xs[:, s, j, 0:P], k.ident[:, :])
                        pe.transpose(k.ps[j][:, P:D], xs[:, s, j, P:D], k.ident[:, :]).then_inc(turned, 1)
                    pe.wait_ge(turned_sb, e * BT + BT)
                    for f in range(HC):
                        if not (first and s == 0 and f < 2):
                            pe.wait_ge(hidden_sb, e * HC + (f - 1))
                        for c in range(2):
                            mm = pe.matmul(k.ps[4 + f % 2][:, :], w1[:, s, c, f * P:(f + 1) * P], xt[:, c, :], start=c == 0, stop=c == 1)
                        mm.then_inc(hidden, 1)
                    pe.wait_ge(hidden_sb, e * HC + HC)
                    for j in range(BT):
                        if not (first and s == 0 and j < 2):
                            pe.wait_ge(out_ready, e * BT + (j - 1))
                        bank = k.ps[6 + j % 2]
                        for f in range(HC):
                            pe.matmul(bank[:, 0:D], ht[:, f, j * P:(j + 1) * P], w2[:, s, f, :], start=f == 0, stop=False)
                        pe.matmul(bank[:, 0:D], k.ones[0:1, :], b2[0:1, s, :], start=False, stop=True).then_inc(product, 1)

            rounds(pe, n_rounds, tiles)

        @block.scalar
        def _(act):
            act.preload_act_table(ACT.Relu)

            def tiles(r, first):
                for s in range(2):
                    e = r * 2 + s
                    act.wait_ge(loaded[s], (r + 1) * (5 * 16))
                    for j in range(BT):
                        act.wait_ge(turned, e * BT + (j + 1))
                        act.activation(xt[:, :, j * P:(j + 1) * P], k.ps[j][:, 0:D].rearrange("p (c n) -> p c n", c=2), ACT.Copy).then_inc(turned_sb, 1)
                    if not (first and s == 0):
                        act.wait_ge(product, e * BT)
                    for f in range(HC):
                        act.wait_ge(hidden, e * HC + (f + 1))
                        act.activation(ht[:, f, :], k.ps[4 + f % 2][:, :], ACT.Relu, bias=b1[:, s, f:f + 1]).then_inc(hidden_sb, 1)

            rounds(act, n_rounds, tiles)

        @block.vector
        def _(dve):
            def tiles(r, first):
                for s in range(2):
                    e = r * 2 + s
                    for j in range(BT):
                        if not (first and s == 0):
                            dve.wait_ge(stored[j], e * 16)
                        dve.wait_ge(product, e * BT + (j + 1))
                        dve.tensor_copy(out[:, j, :], k.ps[6 + j % 2][:, 0:D]).then_inc(out_ready, 1)

            rounds(dve, n_rounds, tiles)
    k.end_stage()


BIG = 3.4028234663852886e38


def ffn1_return_stage(nc, k, out):
    with nc.Block() as block:
        back = [k.sem(f"z1_back{g}") for g in range(GROUPS)]
        summed, stored = k.sem("z1_summed"), k.sem("z1_stored")
        rows = k.stage_sb("z1_rows", [P, T, D], F32)
        clamped = k.stage_sb("z1_clamped", [P, SLOTS, D], F32)
        clean = k.stage_sb("z1_clean", [P, SLOTS, D], F32)
        number = k.stage_sb("z1_number", [P, SLOTS, D], I32)
        finite = k.stage_sb("z1_finite", [P, SLOTS, D], I32)

        @block.gpsimd
        def _(pool):
            for t in range(T):
                pool.indirect_dma_start(out=rows[:, t, :], out_offset=None, in_=k.result_dram,
                                        in_offset=bass.IndirectOffsetOnAxis(ap=k.place_i[:, t:t + 1], axis=0)).then_inc(back[t // SLOTS], 16)

        @block.vector
        def _(dve):
            for g in range(GROUPS):
                here = slice(g * SLOTS, (g + 1) * SLOTS)
                z = rows[:, here, :]
                dve.wait_ge(back[g], 16 * SLOTS)
                dve.memset(clean[:, :, :], 0.0)
                dve.tensor_tensor(z, z, k.prb[:, here].unsqueeze(2).to_broadcast([P, SLOTS, D]), ALU.mult)
                dve.drain()
                dve.tensor_scalar(clamped[:, :, :], z, -1e4, 1e4, ALU.max, ALU.min)
                dve.tensor_tensor(number[:, :, :], z, z, ALU.is_equal)
                dve.tensor_scalar(finite[:, :, :], z, 0.0, 0.0, ALU.mult, ALU.is_equal)
                dve.drain()
                dve.copy_predicated(clean[:, :, :], number[:, :, :], clamped[:, :, :])
                dve.drain()
                dve.copy_predicated(clean[:, :, :], finite[:, :, :], z)
                dve.drain()
                dve.tensor_tensor(k.x[:, here, :], k.x[:, here, :], clean[:, :, :], ALU.add).then_inc(summed, 1)
                dve.drain()

        @block.sync
        def _(sp):
            for g in range(GROUPS):
                sp.wait_ge(summed, g + 1)
                full = SLOTS if g < GROUPS - 1 else SLOTS - 1
                first, n = g * SLOTS, full * P
                sp.dma_start(out[first * P:first * P + n, :].rearrange("(j p) d -> p j d", p=P), k.x[:, first:first + full, :]).then_inc(stored, 16)
            sp.dma_start(out[(T - 1) * P:NODES, :], k.x[0:LAST, T - 1, :]).then_inc(stored, 16)
            sp.wait_ge(stored, 16 * (GROUPS + 1))
    k.end_stage()


class Program:
    pass


def build(nc, io, out, upto=99, dbg=None):
    with ExitStack() as program:
        k = Program()
        k.io = io
        k.sb = lambda name, shape, dt: program.enter_context(nc.sbuf_tensor(name, shape, dt))
        k.lasting_sem = lambda name: program.enter_context(nc.semaphore(name))
        k.stage_sems = []

        def stage_sem(name):
            k.stage_sems.append(nc.alloc_semaphore(name))
            return k.stage_sems[-1]

        def end_stage():
            k.stage.close()
            nc.clear_and_free_semaphores(k.stage_sems)
            k.stage_sems = []
            nc.all_engine_barrier()

        k.sem = stage_sem
        k.stage = ExitStack()
        k.stage_sb = lambda name, shape, dt: k.stage.enter_context(nc.sbuf_tensor(name, shape, dt))
        k.end_stage = end_stage
        k.ps = [program.enter_context(nc.psum_tensor(f"bank{i}", [P, 512], F32)) for i in range(8)]
        k.x = k.sb("x", [P, T, D], F32)
        k.ident, k.below = k.sb("ident", [P, P], F32), k.sb("below", [P, P], F32)
        k.dump, k.eps, k.zero = k.sb("dump", [P, 1], F32), k.sb("eps", [P, 1], F32), k.sb("zero", [P, 1], F32)
        k.ones = k.sb("ones", [P, P], F32)
        k.noise, k.own = k.sb("noise", [P, T], F32), k.sb("own", [P, 1], F32)
        k.rank_i = k.sb("rank_i", [P, T], I32)
        k.before = k.sb("before", [P, P], F32)
        k.lane8, k.lane32 = k.sb("lane8", [P, EXPERTS], F32), k.sb("lane32", [P, 32], F32)
        k.degree, k.prb = k.sb("degree", [P, T], F32), k.sb("prb", [P, T], F32)
        k.place_i, k.send_i = k.sb("place_i", [P, T], I32), k.sb("send_i", [P, T], I32)
        k.owner_i, k.hot = k.sb("owner_i", [P, SORTED], I32), k.sb("hot", [P, T, EXPERTS], F32)
        k.wide_zero = k.sb("wide_zero", [P, ROW], F32)
        k.stats = k.sb("stats", [P, T * 6], F32)
        k.a_mat, k.d_mat, k.d_col = k.sb("a_mat", [P, 2, STATES], F32), k.sb("d_mat", [P, 2, P], F32), k.sb("d_col", [P, 2], F32)
        k.keys, k.edges = ExitStack(), ExitStack()
        program.callback(k.keys.close)
        program.callback(k.edges.close)
        key_sb = lambda name, shape, dt: k.keys.enter_context(nc.sbuf_tensor(name, shape, dt))
        edge_sb = lambda name, shape, dt: k.edges.enter_context(nc.sbuf_tensor(name, shape, dt))
        k.dst_col, k.src_i, k.dst_to = key_sb("dst_col", [P, C], F32), key_sb("src_i", [P, C + 8], I32), key_sb("dst_to", [P, C], I32)
        k.attn = key_sb("attn", [P, C, HEADS], F32)
        k.src_col, k.w_col, k.src_off, k.dst_off = (edge_sb(n, [P, C], F32) for n in ("src_col", "w_col", "src_off", "dst_off"))
        k.dst_i, k.src_to = edge_sb("dst_i", [P, C + 8], I32), edge_sb("src_to", [P, C], I32)
        k.high = edge_sb("high", [P, 2, C], F32)

        def dram(name, shape, dt=F32):
            return nc.dram_tensor(name, shape, dt, kind="Internal").ap()

        k.src_row, k.dst_row = dram("src_row", (EP,)), dram("dst_row", (EP,))
        k.low_row = [dram("src_low_row", (EP,)), dram("dst_low_row", (EP,))]
        k.order_row, k.by_rank_dram = dram("order_row", (NP,)), dram("by_rank_dram", (NP, D))
        k.bc_dram, k.scan_dram = dram("bc_dram", (2 * STATES, NP)), dram("scan_dram", (NP, D))
        k.x_dram = dram("x_dram", (NP, D))
        k.nodes_dram = dram("nodes_dram", (NP, D))
        k.sorted_dram, k.result_dram = dram("sorted_dram", (SORTED * P, D)), dram("result_dram", (SORTED * P, D))
        k.tables = [[dram(f"table{layer}_{a}", (TROWS, ROW)) for a in range(TABLES)] for layer in range(2)]
        k.all_scattered = [[k.lasting_sem(f"scattered{layer}_{a}") for a in range(TABLES)] for layer in range(2)]
        setup_stage(nc, k)
        if upto >= 1:
            support_stage(nc, k)
        if upto >= 2:
            edges_stage(nc, k, "e0", 0, k.src_row, k.src_col, k.src_off, k.dst_i, scale_by_weight(k),
                        [(k.src_row, k.src_col, k.src_off, k.src_to), (k.dst_row, k.dst_col, k.dst_off, k.dst_to)], k.src_to)
        if upto >= 3:
            combine_stage(nc, k)
        if upto >= 4:
            ffn0_route_stage(nc, k)
        if upto >= 5:
            ffn0_experts_stage(nc, k)
            ffn0_return_stage(nc, k)
        if upto >= 6:
            k.score = edge_sb("score", [P, T, 2 * HEADS], F32)
            l1_pre_stage(nc, k)
        if upto >= 7:
            attention_stage(nc, k)
        if upto >= 9:
            k.edges.close()
            k.late, k.scan = ExitStack(), ExitStack()
            program.callback(k.late.close)
            program.callback(k.scan.close)
            k.u, k.dt = (k.late.enter_context(nc.sbuf_tensor(name, [P, 2, NP], F32)) for name in ("u", "dt"))
            k.dtx = k.scan.enter_context(nc.sbuf_tensor("dtx", [P, 2, NP], F32))
            k.zs = k.x[:, :, :].rearrange("p t d -> p (t d)").rearrange("p (c n) -> p c n", c=2)
        if upto >= 10:
            edges_and_scan_stage(nc, k)
        if upto >= 11:
            k.ha = by_tile(k.u)
            mamba_out_stage(nc, k)
            k.scan.close()
            k.hl = by_tile(k.dt)
        if upto >= 12:
            l1_post_stage(nc, k)
            k.late.close()
        if upto >= 13:
            ffn1_route_stage(nc, k)
        if upto >= 14:
            ffn1_experts_stage(nc, k)
            ffn1_return_stage(nc, k, out)
        if dbg:
            dbg(nc, k)


def host_arrays(inputs):
    import numpy as np
    arrays = {name: np.ascontiguousarray(inputs[name]) for name in _INS}
    for name in ("gat_w", "in_proj_w", "x_proj_w", "dt_proj_w", "out_proj_w", "wl", "wg", "ff1_w", "ff2_w"):
        arrays[f"{name}_t"] = np.ascontiguousarray(arrays.pop(f"L1_gnn_{name}").T)
    arrays["gat_w"] = np.ascontiguousarray(inputs["L1_gnn_gat_w"])
    return arrays


_INS = ['x', 'src', 'dst', 'edge_weight', 'node_vec', 'L0_gnn_weight', 'L0_gnn_b', 'L0_ffn_W1', 'L0_ffn_b1', 'L0_ffn_Wg', 'L0_ffn_bg', 'L0_ffn_Wd', 'L0_ffn_bd', 'L1_gnn_gat_w', 'L1_gnn_gat_a_src', 'L1_gnn_gat_a_tgt', 'L1_gnn_gat_b', 'L1_gnn_ln_local_g', 'L1_gnn_ln_local_b', 'L1_gnn_ln_global_g', 'L1_gnn_ln_global_b', 'L1_gnn_ln2_g', 'L1_gnn_ln2_b', 'L1_gnn_in_proj_w', 'L1_gnn_conv_w', 'L1_gnn_conv_b', 'L1_gnn_x_proj_w', 'L1_gnn_dt_proj_w', 'L1_gnn_dt_proj_b', 'L1_gnn_A_log', 'L1_gnn_D_param', 'L1_gnn_out_proj_w', 'L1_gnn_wl', 'L1_gnn_wg', 'L1_gnn_ff1_w', 'L1_gnn_ff1_b', 'L1_gnn_ff2_w', 'L1_gnn_ff2_b', 'L1_ffn_gate_w', 'L1_ffn_gate_b', 'L1_ffn_w1', 'L1_ffn_b1', 'L1_ffn_w2', 'L1_ffn_b2']

_OUTS = [((NODES, D), "float32")]


def kernel(**inputs):
    import numpy as _np
    import concourse.bacc as _bacc
    from concourse import mybir as _mybir
    from concourse.bass_utils import run_bass_kernel_spmd as _run

    nc = _bacc.Bacc("TRN2", target_bir_lowering=False, num_devices=1)
    arrays, io = {}, {}
    for name, a in host_arrays(inputs).items():
        arrays[f"in_{name}_dram"] = a
        io[name] = nc.dram_tensor(f"in_{name}_dram", a.shape, _mybir.dt.from_np(a.dtype), kind="ExternalInput").ap()
    shape, dtype = _OUTS[0]
    out = nc.dram_tensor("out_0_dram", shape, _mybir.dt.from_np(_np.dtype(dtype)), kind="ExternalOutput").ap()
    build(nc, io, out)
    return _run(nc, [arrays], core_ids=[0]).results[0]["out_0_dram"]
```

```python
from contextlib import ExitStack

import concourse.bass as bass
from concourse import mybir

F32 = mybir.dt.float32
I32 = mybir.dt.int32
ALU = mybir.AluOpType
ACT = mybir.ActivationFunctionType
AX = mybir.AxisListType.X

P = 128
NODES, D = 3125, 256
T = -(-NODES // P)
NP = T * P
LAST = NODES - (T - 1) * P
SLOTS = 5
GROUPS = T // SLOTS
EDGES = 53125
C = 416
EP = C * P
ER, EC = 104, 512
PADNODE = NP - 1
ROW = D + 4
LANES = 4
TABLES = 2
TROWS = NP + P
HEADS, HD = 4, 64
EPS = 1e-5
assert T == SLOTS * GROUPS and ER * EC == EP and (ER - 1) * EC < EDGES <= EP


def rounds(engine, n, body):
    body(0, True)
    with engine.Fori(1, n) as g:
        body(g, False)


def after_earlier(engine, sem, first, value):
    if not first:
        engine.wait_ge(sem, value)


def skewed(engine, ahead, early, late):
    for j in range(ahead):
        early(0, j)

    def group(g, first):
        for j in range(SLOTS):
            after = j + ahead
            if not (isinstance(g, int) and g == GROUPS - 1 and after >= SLOTS):
                early(g + after // SLOTS, after % SLOTS)
            late(g, j)

    rounds(engine, GROUPS - 1, group)
    group(GROUPS - 1, False)


def wait_later(engine, sem, value):
    if not isinstance(value, int) or value > 0:
        engine.wait_ge(sem, value)


def row_view(ap, n):
    return ap.rearrange("(a n) -> a n", a=1)


def setup_stage(nc, k):
    with nc.Block() as block:
        zero_ready = k.sem("setup_zero_ready")
        filled, loaded, rows_in = k.sem("setup_filled"), k.sem("setup_loaded"), k.sem("setup_rows_in")
        floats, rows_out = k.sem("setup_floats"), k.sem("setup_rows_out")
        turned, cols = k.sem("setup_turned"), k.sem("setup_cols")
        built, dumps = k.sem("setup_built"), k.sem("setup_dumps")
        src_i = k.stage_sb("setup_src_i", [ER, EC], I32)
        dst_i = k.stage_sb("setup_dst_i", [ER, EC], I32)
        src_r = k.stage_sb("src_r", [ER, EC], F32)
        dst_r = k.stage_sb("dst_r", [ER, EC], F32)
        w_r = k.stage_sb("w_r", [ER, EC], F32)
        dump_i = k.stage_sb("dump_i", [P, 1], I32)
        lane_i, lane_p = k.stage_sb("lane_i", [P, 32], I32), k.stage_sb("lane_p", [P, 1], I32)
        low_i = k.stage_sb("low_i", [ER, 2, EC], I32)
        low_r = k.stage_sb("low_r", [ER, 2, EC], F32)
        high_i = k.stage_sb("high_i", [P, 2, C], I32)
        tail = EDGES - (ER - 1) * EC

        @block.sync
        def _(sp):
            sp.wait_ge(filled, 5)
            sp.dma_start(k.x[:, 0:T - 1, :], k.io["x"][0:(T - 1) * P, :].rearrange("(t p) d -> p t d", p=P)).then_inc(loaded, 16)
            sp.dma_start(k.x[0:LAST, T - 1, :], k.io["x"][(T - 1) * P:NODES, :]).then_inc(loaded, 16)
            for tile, dram in ((src_i, k.io["src"]), (dst_i, k.io["dst"]), (w_r, k.io["edge_weight"])):
                sp.dma_start(tile[0:ER - 1, :], dram[0:(ER - 1) * EC].rearrange("(r c) -> r c", c=EC)).then_inc(rows_in, 16)
                sp.dma_start(tile[ER - 1:ER, 0:tail], row_view(dram[(ER - 1) * EC:EDGES], tail)).then_inc(rows_in, 16)
            sp.wait_ge(floats, 2)
            sp.dma_start(k.src_row.rearrange("(r c) -> r c", c=EC), src_r[:, :]).then_inc(rows_out, 16)
            sp.dma_start(k.dst_row.rearrange("(r c) -> r c", c=EC), dst_r[:, :]).then_inc(rows_out, 16)
            sp.wait_ge(floats, 3)
            for a in range(2):
                sp.dma_start(k.low_row[a].rearrange("(r c) -> r c", c=EC), low_r[:, a, :]).then_inc(rows_out, 16)
            with nc.allow_non_contiguous_dma(reason="12 KB as columns"):
                sp.dma_start(k.noise[:, 0:T - 1], k.io["node_vec"][0:(T - 1) * P].rearrange("(t p) -> p t", p=P)).then_inc(loaded, 16)
                sp.dma_start(k.noise[0:LAST, T - 1:T], k.io["node_vec"][(T - 1) * P:NODES].rearrange("(p a) -> p a", a=1)).then_inc(loaded, 16)
            sp.wait_ge(loaded, 64)
            sp.wait_ge(rows_out, 64)
            sp.wait_ge(zero_ready, 1)
            zero_tables(k, sp, 0)

        @block.gpsimd
        def _(pool):
            pool.memset(k.wide_zero[:, :], 0.0).then_inc(zero_ready, 1)
            pool.memset(k.ident[:, :], 0.0).then_inc(built, 1)
            pool.memset(k.below[:, :], 1.0).then_inc(built, 1)
            pool.iota(dump_i[:, :], [[1, 1]], base=NP, channel_multiplier=1).then_inc(dumps, 1)
            pool.iota(lane_p[:, :], [[1, 1]], base=0, channel_multiplier=1).then_inc(dumps, 1)
            pool.iota(lane_i[:, :], [[1, 32]], base=0, channel_multiplier=0).then_inc(dumps, 1)
            pool.memset(k.before[:, :], 1.0).then_inc(built, 1)
            pool.wait_ge(built, 3)
            pool.affine_select(out=k.ident[:, :], in_=k.ident[:, :], compare_op=ALU.not_equal, fill=1.0, base=0,
                               pattern=[[-1, P]], channel_multiplier=1).then_inc(built, 1)
            pool.affine_select(out=k.below[:, :], in_=k.below[:, :], compare_op=ALU.is_gt, fill=0.0, base=0,
                               pattern=[[-1, P]], channel_multiplier=1).then_inc(built, 1)
            pool.affine_select(out=k.before[:, :], in_=k.before[:, :], compare_op=ALU.is_gt, fill=0.0, base=0,
                               pattern=[[1, P]], channel_multiplier=-1).then_inc(built, 1)

        @block.vector
        def _(dve):
            dve.memset(k.x[:, T - 1, :], 0.0).then_inc(filled, 1)
            dve.memset(src_i[:, :], PADNODE).then_inc(filled, 1)
            dve.memset(dst_i[:, :], PADNODE).then_inc(filled, 1)
            dve.memset(w_r[:, :], 0.0).then_inc(filled, 1)
            dve.memset(k.eps[:, :], EPS)
            dve.memset(k.dst_i[:, C:C + 8], 0)
            dve.memset(k.src_i[:, C:C + 8], 0)
            dve.memset(k.zero[:, :], 0.0)
            dve.memset(k.ones[:, :], 1.0)
            dve.memset(k.noise[:, :], 0.0).then_inc(filled, 1)
            dve.wait_ge(dumps, 3)
            dve.tensor_copy(k.own[:, :], lane_p[:, :])
            dve.tensor_copy(k.dump[:, :], dump_i[:, :])
            dve.tensor_copy(k.lane8[:, :], lane_i[:, 0:EXPERTS])
            dve.tensor_copy(k.lane32[:, :], lane_i[:, :])
            dve.wait_ge(rows_in, 96)
            dve.tensor_copy(src_r[:, :], src_i[:, :]).then_inc(floats, 1)
            dve.tensor_copy(dst_r[:, :], dst_i[:, :]).then_inc(floats, 1)
            dve.tensor_scalar(low_i[:, 0, :], src_i[:, :], P - 1, None, ALU.bitwise_and)
            dve.tensor_scalar(low_i[:, 1, :], dst_i[:, :], P - 1, None, ALU.bitwise_and)
            dve.drain()
            dve.tensor_copy(low_r[:, :, :], low_i[:, :, :]).then_inc(floats, 1)
            for a, col in enumerate((k.src_col, k.dst_col, k.w_col)):
                dve.wait_ge(turned, a + 1)
                by_row = col[:, 0:C].rearrange("p (r q) -> p q r", q=EC // P)
                dve.tensor_copy(by_row, k.ps[a][:, 0:EC // P * ER].rearrange("p (q r) -> p q r", r=ER)).then_inc(cols, 1)
            dve.drain()
            dve.tensor_copy(k.src_i[:, 0:C], k.src_col[:, 0:C])
            dve.tensor_copy(k.dst_i[:, 0:C], k.dst_col[:, 0:C])
            dve.drain()
            dve.tensor_scalar(high_i[:, 0, :], k.src_i[:, 0:C], 7, None, ALU.arith_shift_right)
            dve.tensor_scalar(high_i[:, 1, :], k.dst_i[:, 0:C], 7, None, ALU.arith_shift_right)
            dve.drain()
            dve.memset(k.high[:, :, C:], 0.0)
            dve.tensor_copy(k.high[:, :, 0:C], high_i[:, :, :])
            dve.tensor_scalar(k.src_off[:, :], k.src_col[:, :], -1.0, k.dump[:, :], ALU.mult, ALU.add)
            dve.tensor_scalar(k.dst_off[:, :], k.dst_col[:, :], -1.0, k.dump[:, :], ALU.mult, ALU.add)

        @block.tensor
        def _(pe):
            pe.wait_ge(built, 6)
            pe.wait_ge(floats, 2)
            for a, rows in enumerate((src_r, dst_r, w_r)):
                for q in range(EC // P):
                    last = pe.transpose(k.ps[a][:, q * ER:(q + 1) * ER], rows[:, q * P:(q + 1) * P], k.ident[0:ER, 0:ER])
                last.then_inc(turned, 1)
    k.end_stage()


def tile_stats(k, dve, t):
    dve.bn_stats(k.stats[:, bass.ds(t * 6, 6)], k.x[:, t, :])


def norm_stats(nc, k, dve, sums, inv, wait_sqrt, need_sqrt):
    st = k.stats
    s = st[:, :].rearrange("p (t s) -> p s t", s=6)
    dve.tensor_tensor(sums[:, 0, :], s[:, 1, :], s[:, 4, :], ALU.add)
    dve.tensor_tensor(sums[:, 1, :], s[:, 1, :], s[:, 4, :], ALU.subtract)
    dve.tensor_tensor(sums[:, 2, :], s[:, 2, :], s[:, 5, :], ALU.add)
    dve.drain()
    dve.tensor_scalar(sums[:, 0, :], sums[:, 0, :], 0.5, None, ALU.mult)
    dve.tensor_tensor(sums[:, 1, :], sums[:, 1, :], sums[:, 1, :], ALU.mult)
    dve.tensor_scalar(sums[:, 2, :], sums[:, 2, :], 1.0 / D, None, ALU.mult)
    dve.drain()
    dve.scalar_tensor_tensor(out=sums[:, 3, :], in0=sums[:, 1, :], scalar=0.25, in1=sums[:, 2, :],
                             op0=ALU.mult, op1=ALU.add).then_inc(need_sqrt, 1)
    dve.wait_ge(wait_sqrt, 1)
    dve.reciprocal(inv[:, :], sums[:, 4, :])
    dve.drain()


def support_stage(nc, k):
    with nc.Block() as block:
        weights, var_ready, dev_ready = k.sem("l0_weights"), k.sem("l0_var_ready"), k.sem("l0_dev_ready")
        normed, turned, turned_sb = k.sem("l0_normed"), k.sem("l0_turned"), k.sem("l0_turned_sb")
        multiplied, out_ready = k.sem("l0_multiplied"), k.sem("l0_out_ready")
        stored = [k.sem(f"l0_stored{j}") for j in range(SLOTS)]
        w = k.stage_sb("l0_w", [P, 2, D], F32)
        sums = k.stage_sb("l0_sums", [P, 5, T], F32)
        inv = k.stage_sb("l0_inv", [P, T], F32)
        xn = k.stage_sb("l0_xn", [P, SLOTS, D], F32)
        xt = k.stage_sb("l0_xt", [P, SLOTS, 2, P], F32)
        out = k.stage_sb("l0_out", [P, SLOTS, D], F32)

        @block.sync
        def _(sp):
            sp.dma_start(w[:, :, :], k.io["L0_gnn_weight"].rearrange("(c p) n -> p c n", p=P)).then_inc(weights, 16)

            def store(g, first):
                for j in range(SLOTS):
                    sp.wait_ge(out_ready, g * SLOTS + (j + 1))
                    sp.dma_start(k.nodes_dram[bass.ds((g * SLOTS + j) * P, P), 0:D], out[:, j, :]).then_inc(stored[j], 16)

            rounds(sp, GROUPS, store)
            for j in range(SLOTS):
                sp.wait_ge(stored[j], 16 * GROUPS)

        @block.vector
        def _(dve):
            with dve.Fori(0, GROUPS) as g:
                for j in range(SLOTS):
                    tile_stats(k, dve, g * SLOTS + j)
            dve.drain()
            norm_stats(nc, k, dve, sums, inv, dev_ready, var_ready)

            def normalise(g, j):
                t = g * SLOTS + j
                wait_later(dve, turned, t - (SLOTS - 1))
                dve.tensor_scalar(xn[:, j, :], k.x[:, t, :], sums[:, 0, bass.ds(t, 1)], inv[:, bass.ds(t, 1)],
                                  ALU.subtract, ALU.mult).then_inc(normed, 1)

            def take(g, j):
                dve.wait_ge(multiplied, g * SLOTS + (j + 1))
                wait_later(dve, stored[j], g * 16)
                dve.tensor_copy(out[:, j, :], k.ps[j][:, D:2 * D]).then_inc(out_ready, 1)

            skewed(dve, 3, normalise, take)

        @block.scalar
        def _(act):
            act.preload_act_table(ACT.Sqrt)
            act.wait_ge(var_ready, 1)
            act.activation(sums[:, 4, :], sums[:, 3, :], ACT.Sqrt, bias=k.eps[:, :]).then_inc(dev_ready, 1)

            def tiles(g, first):
                for j in range(SLOTS):
                    act.wait_ge(turned, g * SLOTS + (j + 1))
                    act.activation(xt[:, j, :, :], k.ps[j][:, 0:D].rearrange("p (c n) -> p c n", c=2), ACT.Copy).then_inc(turned_sb, 1)

            rounds(act, GROUPS, tiles)

        @block.tensor
        def _(pe):
            pe.wait_ge(weights, 16)

            def turn(g, j):
                t = g * SLOTS + j
                pe.wait_ge(normed, t + 1)
                pe.transpose(k.ps[j][:, 0:P], xn[:, j, 0:P], k.ident[:, :])
                pe.transpose(k.ps[j][:, P:D], xn[:, j, P:D], k.ident[:, :]).then_inc(turned, 1)

            def multiply(g, j):
                t = g * SLOTS + j
                pe.wait_ge(turned_sb, t + 1)
                wait_later(pe, out_ready, t - (SLOTS - 1))
                for c in range(2):
                    mm = pe.matmul(k.ps[j][:, D:2 * D], xt[:, j, c, :], w[:, c, :], start=c == 0, stop=c == 1)
                mm.then_inc(multiplied, 1)

            skewed(pe, 2, turn, multiply)
    k.end_stage()


UNROLL = 2 * LANES
ROUNDS = C // UNROLL


def scatters(g, h, s):
    per_half = LANES // TABLES
    return g * (2 * per_half * 16) + (h * per_half + s // TABLES) * 16


def zero_tables(k, engine, layer):
    for a in range(TABLES):
        engine.dma_start(k.tables[layer][a].rearrange("(p r) c -> p r c", p=P), k.wide_zero[:, :].unsqueeze(1).to_broadcast([P, TROWS // P, ROW]))\
              .then_inc(k.zeroed[layer], 16)


def edges_stage(nc, k, name, layer, key_row, key_col, key_off, other_i, scale, ranks, scatter_i):
    H = LANES
    table, scattered = k.tables[layer], k.all_scattered[layer]
    with nc.Block() as block:
        keys_in = [k.sem(f"{name}_keys_in{h}") for h in range(2)]
        gathered = [k.sem(f"{name}_gathered{s}") for s in range(H)]
        gather_i_ready, scatter_i_ready = k.sem(f"{name}_gather_i"), k.sem(f"{name}_scatter_i")
        scaled, summed, out_ready = k.sem(f"{name}_scaled"), k.sem(f"{name}_summed"), k.sem(f"{name}_out_ready")
        pool_step = k.sem(f"{name}_pool_step")
        lists = [r[0] for r in ranks] or [key_row]
        keys = k.stage_sb(f"{name}_keys", [P, 2, len(lists), H * P], F32)
        gi = k.stage_sb(f"{name}_gi", [P, 2, H], I32)
        si = k.stage_sb(f"{name}_si", [P, 2, H], I32)
        rank = k.stage_sb(f"{name}_rank", [P, len(lists), H], F32)
        shift = k.stage_sb(f"{name}_shift", [P, len(lists), H], F32)
        junk = k.stage_sb(f"{name}_junk", [P, len(lists), H, P], F32)
        same = k.stage_sb(f"{name}_same", [P, H, P], F32)
        rows = k.stage_sb(f"{name}_rows", [P, H, D], F32)
        vals = k.stage_sb(f"{name}_vals", [P, H, ROW], F32)
        out = k.stage_sb(f"{name}_out", [P, H, ROW], F32)

        @block.sync
        def _(sp):
            def load(g, h, first):
                if not first:
                    sp.wait_ge(scaled, g * UNROLL + (h * H + H - UNROLL))
                for a, row in enumerate(lists):
                    sp.dma_start(keys[:, h, a, :], row[bass.ds(g * UNROLL * P + h * H * P, H * P)].partition_broadcast(P)).then_inc(keys_in[h], 16)

            rounds(sp, ROUNDS, lambda g, first: (load(g, 0, first), load(g, 1, first)))

        @block.gpsimd
        def _(pool):
            def gather(h, s):
                pool.indirect_dma_start(out=rows[:, s, :], out_offset=None, in_=k.nodes_dram,
                                        in_offset=bass.IndirectOffsetOnAxis(ap=gi[:, h, s:s + 1], axis=0)).then_inc(gathered[s], 16)

            def body(g, last):
                for h in range(2):
                    for s in range(H):
                        pool.wait_ge(out_ready, g * UNROLL + (h * H + s + 1))
                        if not (isinstance(g, int) and g == h == 0 and s < TABLES):
                            pool.wait_ge(scattered[s % TABLES], scatters(g, h, s))
                        pool.sem_inc(pool_step, 1)
                        pool.indirect_dma_start(out=table[s % TABLES], out_offset=bass.IndirectOffsetOnAxis(ap=si[:, h, s:s + 1], axis=0),
                                                in_=out[:, s, :], in_offset=None, compute_op=ALU.add).then_inc(scattered[s % TABLES], 16)
                        if not (last and h == 1):
                            pool.wait_ge(scaled, g * UNROLL + (h * H + s + 1))
                            pool.wait_ge(gather_i_ready, g * 2 + (h + 2))
                            pool.sem_inc(pool_step, 1)
                            gather(1 - h, s)

            pool.wait_ge(gather_i_ready, 1)
            for s in range(H):
                gather(0, s)
            pool.wait_ge(k.zeroed[layer], 16 * TABLES)
            body(0, False)
            with pool.Fori(1, ROUNDS - 1) as g:
                body(g, False)
            body(ROUNDS - 1, True)
            for a in range(TABLES):
                pool.wait_ge(scattered[a], scatters(ROUNDS, 0, a))

        @block.vector
        def _(dve):
            def indices(g, h):
                dve.tensor_scalar(gi[:, h, :], other_i[:, bass.ds(g * UNROLL + h * H, H)], 0.0, None, ALU.add).then_inc(gather_i_ready, 1)

            for s in range(H):
                scale(dve, vals[:, s, :], None, None)
            dve.drain()
            indices(0, 0)

            def body(g, first):
                for h in range(2):
                    at = g * UNROLL + h * H
                    dve.wait_ge(keys_in[h], (g + 1) * (16 * len(lists)))
                    for a, (row, col, off, idx) in enumerate(ranks):
                        for s in range(H):
                            dve.scalar_tensor_tensor(out=junk[:, a, s, :], in0=keys[:, h, a, s * P:(s + 1) * P], scalar=col[:, bass.ds(at + s, 1)],
                                                     in1=k.below[:, :], op0=ALU.is_equal, op1=ALU.mult, accum_out=rank[:, a, s:s + 1])
                    if ranks:
                        dve.drain()
                        for a, (row, col, off, idx) in enumerate(ranks):
                            dve.scalar_tensor_tensor(out=shift[:, a, :], in0=rank[:, a, :], scalar=0.0, in1=off[:, bass.ds(at, H)],
                                                     op0=ALU.is_gt, op1=ALU.mult)
                        dve.drain()
                        for a, (row, col, off, idx) in enumerate(ranks):
                            dve.tensor_tensor(idx[:, bass.ds(at, H)], shift[:, a, :], col[:, bass.ds(at, H)], ALU.add)
                        dve.drain()
                    if not first:
                        for a in range(TABLES):
                            dve.wait_ge(scattered[a], scatters(g, h, a) - (LANES // TABLES) * 16)
                    dve.tensor_scalar(si[:, h, :], scatter_i[:, bass.ds(at, H)], 0.0, None, ALU.add).then_inc(scatter_i_ready, 1)
                    indices(g + h, 1 - h)
                    for s in range(H):
                        if not (first and h == 0):
                            dve.wait_ge(summed, at + (s + 1 - H))
                        dve.tensor_scalar(same[:, s, :], keys[:, h, 0, s * P:(s + 1) * P], key_col[:, bass.ds(at + s, 1)], None, ALU.is_equal)
                        dve.wait_ge(gathered[s], g * 32 + (h * 16 + 16))
                        scale(dve, vals[:, s, :], rows[:, s, :], at + s).then_inc(scaled, 1)

            rounds(dve, ROUNDS, body)

        @block.tensor
        def _(pe):
            def body(g, first):
                for h in range(2):
                    for s in range(H):
                        n = g * UNROLL + (h * H + s + 1)
                        pe.wait_ge(scaled, n)
                        if not (first and h == 0):
                            pe.wait_ge(out_ready, n - H)
                        pe.matmul(k.ps[s][:, 0:ROW], same[:, s, :], vals[:, s, :], start=True, stop=True).then_inc(summed, 1)

            rounds(pe, ROUNDS, body)

        @block.scalar
        def _(act):
            def body(g, first):
                for h in range(2):
                    for s in range(H):
                        if not (first and h == 0):
                            act.wait_ge(scattered[s % TABLES], scatters(g, h, s) - (LANES // TABLES - 1) * 16)
                        act.wait_ge(summed, g * UNROLL + (h * H + s + 1))
                        act.activation(out[:, s, :], k.ps[s][:, 0:ROW], ACT.Copy).then_inc(out_ready, 1)

            act.wait_ge(scatter_i_ready, 1)
            act.preload_act_table(ACT.Copy)
            rounds(act, ROUNDS, body)
    k.end_stage()


def scale_by_weight(k):
    def scale(dve, vals, rows, chunk):
        if rows is None:
            dve.memset(vals[:, D + 1:ROW], 0.0)
            return dve.memset(vals[:, D:D + 1], 1.0)
        return dve.tensor_scalar(vals[:, 0:D], rows, k.w_col[:, bass.ds(chunk, 1)], None, ALU.mult)
    return scale


def combine_stage(nc, k):
    with nc.Block() as block:
        bias_in, summed, folded = k.sem("c0_bias_in"), k.sem("c0_summed"), k.sem("c0_folded")
        tables_in = [k.sem(f"c0_tables_in{h}") for h in range(2)]
        part = k.stage_sb("c0_part", [P, 2, TABLES, SLOTS, ROW], F32)
        total = k.stage_sb("c0_total", [P, 2, SLOTS, ROW], F32)
        bias = k.stage_sb("c0_bias", [P, D], F32)

        @block.sync
        def _(sp):
            sp.dma_start(bias[:, :], k.io["L0_gnn_b"].partition_broadcast(P)).then_inc(bias_in, 16)
            for g in range(GROUPS):
                if g >= 2:
                    sp.wait_ge(folded, g - 1)
                for a in range(TABLES):
                    rows = k.tables[0][a][g * SLOTS * P:(g + 1) * SLOTS * P, :].rearrange("(j p) c -> p j c", p=P)
                    sp.dma_start(part[:, g % 2, a, :, :], rows).then_inc(tables_in[g % 2], 16)

        @block.gpsimd
        def _(pool):
            for g in range(GROUPS):
                pool.wait_ge(tables_in[g % 2], 16 * TABLES * (g // 2 + 1))
                if g >= 2:
                    pool.wait_ge(summed, g - 1)
                pool.tensor_tensor(total[:, g % 2, :, :], part[:, g % 2, 0, :, :], part[:, g % 2, 1, :, :], ALU.add).then_inc(folded, 1)

        @block.vector
        def _(dve):
            dve.wait_ge(bias_in, 16)
            for g in range(GROUPS):
                here = slice(g * SLOTS, (g + 1) * SLOTS)
                dve.tensor_tensor(k.x[:, here, :], k.x[:, here, :], bias[:, :].unsqueeze(1).to_broadcast([P, SLOTS, D]), ALU.add)
                dve.drain()
                dve.wait_ge(folded, g + 1)
                dve.tensor_copy(k.degree[:, here], total[:, g % 2, :, D])
                dve.tensor_tensor(k.x[:, here, :], k.x[:, here, :], total[:, g % 2, :, 0:D], ALU.add).then_inc(summed, 1)
                if g > 0:
                    for t in range((g - 1) * SLOTS, g * SLOTS):
                        tile_stats(k, dve, t)
            dve.drain()
            for t in range((GROUPS - 1) * SLOTS, T):
                tile_stats(k, dve, t)
    k.end_stage()


EXPERTS, HID = 8, 1024
CAPACITY = -(-5 * NODES // (4 * EXPERTS))
BUF = 512
HC = HID // P
SORTED = T + EXPERTS - 1
QUAD = 4
assert SORTED % QUAD == 0


def transposer(nc, k, name, normed, turned, turned_sb, xn, xt):
    def on_pe(pe, g):
        for j in range(SLOTS):
            pe.wait_ge(normed, g * SLOTS + (j + 1))
            pe.transpose(k.ps[j][:, 0:P], xn[:, j, 0:P], k.ident[:, :])
            pe.transpose(k.ps[j][:, P:D], xn[:, j, P:D], k.ident[:, :]).then_inc(turned, 1)

    def on_act(act, g):
        for j in range(SLOTS):
            act.wait_ge(turned, g * SLOTS + (j + 1))
            act.activation(xt[:, :, j * P:(j + 1) * P], k.ps[j][:, 0:D].rearrange("p (c n) -> p c n", c=2), ACT.Copy).then_inc(turned_sb, 1)

    return on_pe, on_act


def route(nc, k, dve, name, logits, exp_ready, exp_done, mask_ready, counted, padded):
    def tile3(n):
        return k.stage_sb(f"{name}_{n}", [P, T, EXPERTS], F32)

    def tile2(n):
        return k.stage_sb(f"{name}_{n}", [P, T], F32)

    over = lambda a: a[:, :].unsqueeze(2).to_broadcast([P, T, EXPERTS])
    lane = k.lane8[:, :].unsqueeze(1).to_broadcast([P, T, EXPERTS])
    top, total, inv, first = tile2("top"), tile2("total"), tile2("total_inv"), tile2("first")
    prob, tie, hot, place = k.prob_of[name], tile3("tie"), k.hot, tile3("place")
    dve.tensor_reduce(top[:, :], logits[:, :, :], AX, ALU.max)
    dve.drain()
    dve.tensor_tensor(prob[:, :, :], logits[:, :, :], over(top), ALU.subtract).then_inc(exp_ready, 1)
    dve.wait_ge(exp_done, 1)
    dve.tensor_reduce(total[:, :], prob[:, :, :], AX, ALU.add)
    dve.drain()
    dve.reciprocal(inv[:, :], total[:, :])
    dve.drain()
    dve.tensor_tensor(prob[:, :, :], prob[:, :, :], over(inv), ALU.mult)
    dve.drain()
    dve.tensor_reduce(k.prb[:, :], prob[:, :, :], AX, ALU.max)
    dve.drain()
    dve.tensor_tensor(tie[:, :, :], prob[:, :, :], over(k.prb), ALU.is_lt)
    dve.drain()
    dve.scalar_tensor_tensor(out=tie[:, :, :], in0=tie[:, :, :], scalar=float(EXPERTS), in1=lane, op0=ALU.mult, op1=ALU.add)
    dve.drain()
    dve.tensor_reduce(first[:, :], tie[:, :, :], AX, ALU.min)
    dve.drain()
    dve.tensor_tensor(hot[:, :, :], lane, over(first), ALU.is_equal).then_inc(mask_ready, 1)
    n = T * EXPERTS
    dve.wait_ge(counted, 1)
    total8 = tile3("total8")
    run = tile3("run")
    dve.tensor_copy(total8[:, :, :], k.ps[0][:, n:2 * n].rearrange("p (t e) -> p t e", e=EXPERTS))
    dve.drain()
    for e in range(EXPERTS):
        dve.tensor_tensor_scan(run[:, :, e], total8[:, :, e], k.zero[:, :].to_broadcast([P, T]), 0.0, ALU.add, ALU.add)
    dve.drain()
    dve.tensor_tensor(place[:, :, :], run[:, :, :], total8[:, :, :], ALU.subtract)
    dve.drain()
    dve.tensor_tensor(place[:, :, :], place[:, :, :], k.ps[0][:, 0:n].rearrange("p (t e) -> p t e", e=EXPERTS), ALU.add)
    counts = run[:, T - 1, :]
    start = k.stage_sb(f"{name}_start", [P, EXPERTS], F32)
    if padded:
        tiles_i = k.stage_sb(f"{name}_tiles_i", [P, EXPERTS], I32)
        tiles_f = k.stage_sb(f"{name}_tiles_f", [P, EXPERTS], F32)
        ends = k.stage_sb(f"{name}_ends", [P, EXPERTS], F32)
        past = k.stage_sb(f"{name}_past", [P, SORTED, EXPERTS - 1], F32)
        owner = k.stage_sb(f"{name}_owner", [P, SORTED], F32)
        dve.tensor_scalar(tiles_i[:, :], counts, float(P - 1), None, ALU.add)
        dve.drain()
        dve.tensor_scalar(tiles_i[:, :], tiles_i[:, :], 7, None, ALU.arith_shift_right)
        dve.drain()
        dve.tensor_copy(tiles_f[:, :], tiles_i[:, :])
        dve.drain()
        dve.tensor_tensor_scan(ends[:, :], tiles_f[:, :], k.zero[:, :].to_broadcast([P, EXPERTS]), 0.0, ALU.add, ALU.add)
        dve.drain()
        dve.tensor_tensor(start[:, :], ends[:, :], tiles_f[:, :], ALU.subtract)
        dve.tensor_tensor(past[:, :, :], k.lane32[:, 0:SORTED].unsqueeze(2).to_broadcast([P, SORTED, EXPERTS - 1]),
                          ends[:, 0:EXPERTS - 1].unsqueeze(1).to_broadcast([P, SORTED, EXPERTS - 1]), ALU.is_ge)
        dve.drain()
        dve.tensor_scalar(start[:, :], start[:, :], float(P), None, ALU.mult)
        dve.tensor_reduce(owner[:, :], past[:, :, :], AX, ALU.add)
        dve.drain()
        dve.tensor_copy(k.owner_i[:, :], owner[:, :])
    else:
        cap = k.stage_sb(f"{name}_cap", [P, T], F32)
        dve.drain()
        dve.tensor_tensor(tie[:, :, :], place[:, :, :], hot[:, :, :], ALU.mult)
        dve.drain()
        dve.tensor_reduce(cap[:, :], tie[:, :, :], AX, ALU.add)
        dve.drain()
        dve.tensor_scalar(cap[:, :], cap[:, :], float(CAPACITY), None, ALU.is_lt)
        dve.tensor_scalar(place[:, :, :], place[:, :, :], float(CAPACITY - 1), None, ALU.min)
        dve.tensor_scalar(start[:, :], k.lane8[:, :], float(BUF), None, ALU.mult)
        dve.drain()
        dve.tensor_tensor(k.prb[:, :], k.prb[:, :], cap[:, :], ALU.mult)
    dve.drain()
    dve.tensor_tensor(place[:, :, :], place[:, :, :], start[:, :].unsqueeze(1).to_broadcast([P, T, EXPERTS]), ALU.add)
    dve.drain()
    dve.tensor_tensor(place[:, :, :], place[:, :, :], hot[:, :, :], ALU.mult)
    dve.drain()
    dve.tensor_reduce(first[:, :], place[:, :, :], AX, ALU.add)
    dve.drain()
    dve.tensor_copy(k.place_i[:, :], first[:, :])
    if padded:
        dve.tensor_copy(k.send_i[:, :], first[:, :])
    else:
        dve.tensor_scalar(cap[:, :], cap[:, :], -float(1 << 20), float(1 << 20), ALU.mult, ALU.add)
        dve.drain()
        dve.tensor_tensor(k.send_i[:, :], cap[:, :], first[:, :], ALU.add)
    dve.drain()
    return prob


def count_tokens(k, pe):
    n = T * EXPERTS
    hot = k.hot[:, :, :].rearrange("p t e -> p (t e)")
    pe.matmul(k.ps[0][:, 0:n], k.before[:, :], hot, start=True, stop=True)
    return pe.matmul(k.ps[0][:, n:2 * n], k.ones[:, :], hot, start=True, stop=True)


def ffn0_route_stage(nc, k):
    with nc.Block() as block:
        weights, var_ready, dev_ready = k.sem("f0_weights"), k.sem("f0_var_ready"), k.sem("f0_dev_ready")
        normed, turned, turned_sb = k.sem("f0_normed"), k.sem("f0_turned"), k.sem("f0_turned_sb")
        hidden, hidden_sb, gate_step, gated, logit_ready = (k.sem(f"f0_{n}") for n in ("hidden", "hidden_sb", "gate_step", "gated", "logit_ready"))
        logits_sb, pe_step = k.sem("f0_logits_sb"), k.sem("f0_pe_step")
        exp_ready, exp_done, mask_ready, counted = (k.sem(f"f0_{n}") for n in ("exp_ready", "exp_done", "mask_ready", "counted"))
        placed, sent, zero_sent = k.sem("f0_placed"), k.sem("f0_sent"), k.sem("f0_zero_sent")
        w1, b1 = k.layer0_w1, k.layer0_b1
        wg = k.stage_sb("f0_wg", [P, HC, EXPERTS], F32)
        bg = k.stage_sb("f0_bg", [EXPERTS, 1], F32)
        sums = k.stage_sb("f0_sums", [P, 5, T], F32)
        inv = k.stage_sb("f0_inv", [P, T], F32)
        xn = k.stage_sb("f0_xn", [P, T, D], F32)
        xs = k.stage_sb("f0_xs", [P, SLOTS, D], F32)
        xt = k.stage_sb("f0_xt", [P, 2, SLOTS * P], F32)
        ht = k.stage_sb("f0_ht", [P, 4, SLOTS * P], F32)
        logits_t = k.stage_sb("f0_logits_t", [EXPERTS, SLOTS * P], F32)
        logits = k.stage_sb("f0_logits", [P, T, EXPERTS], F32)
        half = SLOTS * P // 2
        hbank, gbank = [k.ps[5], k.ps[6]], [k.ps[3], k.ps[4]]
        k.prob_of = {"f0": k.stage_sb("f0_prob", [P, T, EXPERTS], F32)}

        @block.sync
        def _(sp):
            sp.dma_start(w1[:, :, :], k.io["L0_ffn_W1"].rearrange("(c p) n -> p c n", p=P)).then_inc(weights, 16)
            sp.dma_start(wg[:, :, :], k.io["L0_ffn_Wg"].rearrange("(f p) e -> p f e", p=P)).then_inc(weights, 16)
            with nc.allow_non_contiguous_dma(reason="a bias of 4 KB as columns"):
                sp.dma_start(b1[:, :], k.io["L0_ffn_b1"].rearrange("(f p) -> p f", p=P)).then_inc(weights, 16)
            sp.dma_start(bg[:, :], k.io["L0_ffn_bg"].rearrange("(e a) -> e a", a=1)).then_inc(weights, 16)
            sp.dma_start(k.bd[:, :], k.io["L0_ffn_bd"].rearrange("e n -> (e n)").partition_broadcast(P)).then_inc(k.wd_in, 16)
            for e in range(EXPERTS):
                sp.dma_start(k.wd[:, e, :, :], k.io["L0_ffn_Wd"][e].rearrange("(f p) n -> p f n", p=P)).then_inc(k.wd_in, 16)
            per = k.sorted_dram.shape[0] // P
            sp.dma_start(k.sorted_dram.rearrange("(p r) d -> p r d", p=P), k.wide_zero[:, 0:D].unsqueeze(1).to_broadcast([P, per, D])).then_inc(zero_sent, 16)
            zero_tables(k, sp, 1)

        @block.vector
        def _(dve):
            norm_stats(nc, k, dve, sums, inv, dev_ready, var_ready)
            dve.wait_ge(weights, 64)

            def normalise(g, first):
                for j in range(SLOTS):
                    t = g * SLOTS + j
                    after_earlier(dve, turned, first, t - (SLOTS - 1))
                    dve.tensor_scalar(xn[:, t, :], k.x[:, t, :], sums[:, 0, bass.ds(t, 1)], inv[:, bass.ds(t, 1)], ALU.subtract, ALU.mult)
                    dve.tensor_scalar(xs[:, j, :], k.x[:, t, :], sums[:, 0, bass.ds(t, 1)], inv[:, bass.ds(t, 1)],
                                      ALU.subtract, ALU.mult).then_inc(normed, 1)

            def take_logits(g):
                dve.wait_ge(gated, g + 1)
                dve.tensor_scalar(logits[:, bass.ds(g * SLOTS, SLOTS), :], k.ps[7][:, 0:SLOTS * EXPERTS].rearrange("p (j e) -> p j e", e=EXPERTS),
                                  0.0, None, ALU.add).then_inc(logit_ready, 1)

            def group(g, first):
                normalise(g + 1, False)
                take_logits(g)

            normalise(0, True)
            rounds(dve, GROUPS - 1, group)
            take_logits(GROUPS - 1)
            dve.drain()
            route(nc, k, dve, "f0", logits, exp_ready, exp_done, mask_ready, counted, True)
            dve.sem_inc(placed, 1)

        @block.tensor
        def _(pe):
            pe.wait_ge(weights, 64)

            def turn(g):
                for j in range(SLOTS):
                    pe.wait_ge(normed, g * SLOTS + (j + 1))
                    to = k.ps[j // 2][:, j % 2 * D:(j % 2 + 1) * D]
                    pe.transpose(to[:, 0:P], xs[:, j, 0:P], k.ident[:, :])
                    pe.transpose(to[:, P:D], xs[:, j, P:D], k.ident[:, :]).then_inc(turned, 1)

            def gate(g, f):
                for h in range(2):
                    pe.wait_ge(hidden_sb, g * (2 * HC) + (2 * f + h + 1))
                    pe.matmul(gbank[h][0:EXPERTS, 0:half], wg[:, f, :], ht[:, f % 4, h * half:(h + 1) * half], start=f == 0, stop=f == HC - 1)\
                      .then_inc(gate_step, 1)

            def layers(g, first):
                pe.wait_ge(turned_sb, g * 3 + 3)
                after_earlier(pe, logits_sb, first, g * 2)
                for f in range(HC):
                    for h in range(2):
                        n = 2 * f + h
                        if not (first and n < 2):
                            pe.wait_ge(hidden_sb, g * (2 * HC) + (n - 1))
                        for c in range(2):
                            mm = pe.matmul(hbank[h][:, 0:half], w1[:, c, f * P:(f + 1) * P], xt[:, c, h * half:(h + 1) * half], start=c == 0, stop=c == 1)
                        mm.then_inc(hidden, 1)
                    if f > 0:
                        gate(g, f - 1)

            def finish(g, first):
                gate(g, HC - 1)
                pe.wait_ge(logits_sb, g * 2 + 2)
                after_earlier(pe, logit_ready, first, g)
                pe.sem_inc(pe_step, 1)
                for j in range(SLOTS):
                    mm = pe.transpose(k.ps[7][:, j * EXPERTS:(j + 1) * EXPERTS], logits_t[:, j * P:(j + 1) * P], k.ident[0:EXPERTS, 0:EXPERTS])
                mm.then_inc(gated, 1)

            def group(g, first):
                layers(g, first)
                turn(g + 1)
                finish(g, first)

            turn(0)
            rounds(pe, GROUPS - 1, group)
            layers(GROUPS - 1, False)
            finish(GROUPS - 1, False)
            pe.wait_ge(mask_ready, 1)
            count_tokens(k, pe).then_inc(counted, 1)

        @block.scalar
        def _(act):
            act.preload_act_table(ACT.Sqrt)
            act.wait_ge(var_ready, 1)
            act.activation(sums[:, 4, :], sums[:, 3, :], ACT.Sqrt, bias=k.eps[:, :]).then_inc(dev_ready, 1)
            act.wait_ge(weights, 64)
            act.preload_act_table(ACT.Gelu)

            def turn(g):
                for i in range(3):
                    n = min(2, SLOTS - 2 * i)
                    act.wait_ge(turned, g * SLOTS + (2 * i + n))
                    act.activation(xt[:, :, 2 * i * P:(2 * i + n) * P].rearrange("p c (j n) -> p j c n", n=P),
                                   k.ps[i][:, 0:n * D].rearrange("p (j c n) -> p j c n", c=2, n=P), ACT.Copy).then_inc(turned_sb, 1)

            def layers(g, first):
                for f in range(HC):
                    for h in range(2):
                        act.wait_ge(hidden, g * (2 * HC) + (2 * f + h + 1))
                        if not (first and f < 4):
                            act.wait_ge(gate_step, g * (2 * HC) + (2 * f + h - 7))
                        act.activation(ht[:, f % 4, h * half:(h + 1) * half], hbank[h][:, 0:half], ACT.Gelu, bias=b1[:, f:f + 1]).then_inc(hidden_sb, 1)

            def finish(g, first):
                after_earlier(act, gated, first, g)
                for h in range(2):
                    act.wait_ge(gate_step, g * (2 * HC) + (2 * HC - 1 + h))
                    act.activation(logits_t[:, h * half:(h + 1) * half], gbank[h][0:EXPERTS, 0:half], ACT.Identity, bias=bg[:, :]).then_inc(logits_sb, 1)

            def group(g, first):
                layers(g, first)
                turn(g + 1)
                finish(g, first)

            turn(0)
            rounds(act, GROUPS - 1, group)
            layers(GROUPS - 1, False)
            finish(GROUPS - 1, False)
            act.wait_ge(exp_ready, 1)
            act.activation(k.prob_of["f0"][:, :, :], k.prob_of["f0"][:, :, :], ACT.Exp).then_inc(exp_done, 1)

        @block.gpsimd
        def _(pool):
            pool.wait_ge(zero_sent, 16)
            pool.wait_ge(placed, 1)
            for t in range(T):
                pool.indirect_dma_start(out=k.sorted_dram, out_offset=bass.IndirectOffsetOnAxis(ap=k.send_i[:, t:t + 1], axis=0),
                                        in_=xn[:, t, :], in_offset=None).then_inc(sent, 16)
            pool.wait_ge(sent, 16 * T)
    k.end_stage()


def ffn0_experts_stage(nc, k):
    with nc.Block() as block:
        keyed, masked, key_turned, key_sb, key_out, key_in = (k.sem(f"x0_{n}") for n in ("keyed", "masked", "key_turned", "key_sb", "key_out", "key_in"))
        key = k.stage_sb("x0_key", [P, T], F32)
        key_t = k.stage_sb("x0_key_t", [T, P], F32)
        keys = k.stage_sb("x0_keys", [P, NP], F32)
        junk = k.stage_sb("x0_junk", [P, NP], F32)
        count = k.stage_sb("x0_count", [P, 4, T], F32)
        rank = k.stage_sb("x0_rank", [P, T], F32)
        rows_in, sp_step = k.sem("x0_rows_in"), k.sem("x0_sp_step")
        turned, turned_sb, hidden, hidden_sb = (k.sem(f"x0_{n}") for n in ("turned", "turned_sb", "hidden", "hidden_sb"))
        product, out_ready = k.sem("x0_product"), k.sem("x0_out_ready")
        stored = [k.sem(f"x0_stored{j}") for j in range(QUAD)]
        w1, b1, wd, bd = k.layer0_w1, k.layer0_b1, k.wd, k.bd
        xs = k.stage_sb("x0_xs", [P, QUAD, D], F32)
        xt = k.stage_sb("x0_xt", [P, 2, QUAD * P], F32)
        ht = k.stage_sb("x0_ht", [P, HC, QUAD * P], F32)
        out = k.stage_sb("x0_out", [P, QUAD, D], F32)
        n_rounds = SORTED // QUAD

        @block.sync
        def _(sp):
            def load(g):
                sp.dma_start(xs[:, :, :], k.sorted_dram[bass.ds(g * QUAD * P, QUAD * P), :].rearrange("(j p) d -> p j d", p=P)).then_inc(rows_in, 16)

            load(0)
            sp.wait_ge(key_sb, 1)
            sp.dma_start(k.order_row.rearrange("(t p) -> t p", p=P), key_t[:, :]).then_inc(key_out, 16)
            sp.wait_ge(key_out, 16)
            sp.dma_start(keys[:, :], k.order_row.partition_broadcast(P)).then_inc(key_in, 16)

            def tiles(g, first, last=False):
                if not last:
                    sp.wait_ge(turned, g * QUAD + QUAD)
                    sp.sem_inc(sp_step, 1)
                    load(g + 1)
                for j in range(QUAD):
                    sp.wait_ge(out_ready, g * QUAD + (j + 1))
                    sp.dma_start(k.result_dram[bass.ds((g * QUAD + j) * P, P), :], out[:, j, :]).then_inc(stored[j], 16)

            rounds(sp, n_rounds - 1, tiles)
            tiles(n_rounds - 1, False, True)
            for j in range(QUAD):
                sp.wait_ge(stored[j], 16 * n_rounds)

        @block.gpsimd
        def _(pool):
            pool.wait_ge(keyed, 1)
            pool.affine_select(out=key[:, :], in_=key[:, :], compare_op=ALU.is_ge, fill=1e30, base=NODES - 1,
                               pattern=[[-P, T]], channel_multiplier=-1).then_inc(masked, 1)

        @block.tensor
        def _(pe):
            pe.wait_ge(masked, 1)
            pe.transpose(k.ps[6][0:T, 0:P], key[:, :], k.ident[:, :]).then_inc(key_turned, 1)
            pe.wait_ge(k.wd_in, 16 * (EXPERTS + 1))

            def turn(g):
                pe.wait_ge(rows_in, g * 16 + 16)
                for j in range(QUAD):
                    pe.transpose(k.ps[j][:, 0:P], xs[:, j, 0:P], k.ident[:, :])
                    pe.transpose(k.ps[j][:, P:D], xs[:, j, P:D], k.ident[:, :]).then_inc(turned, 1)

            def layers(g, first, last=False):
                pe.wait_ge(turned_sb, g * QUAD + QUAD)
                for f in range(HC):
                    if not (first and f < 2):
                        pe.wait_ge(hidden_sb, g * HC + (f - 1))
                    for c in range(2):
                        mm = pe.matmul(k.ps[4 + f % 2][:, :], w1[:, c, f * P:(f + 1) * P], xt[:, c, :], start=c == 0, stop=c == 1)
                    mm.then_inc(hidden, 1)
                if not last:
                    turn(g + 1)
                pe.wait_ge(hidden_sb, g * HC + HC)
                for j in range(QUAD):
                    e = pe.value_load(k.owner_i[0:1, bass.ds(g * QUAD + j, 1)], min_val=0, max_val=EXPERTS - 1)
                    if not (first and j < 2):
                        pe.wait_ge(out_ready, g * QUAD + (j - 1))
                    elif j == 0:
                        pe.wait_ge(key_sb, 1)
                    bank = k.ps[6 + j % 2]
                    for f in range(HC):
                        mm = pe.matmul(bank[:, 0:D], ht[:, f, j * P:(j + 1) * P], wd[:, bass.ds(e, 1), f, :].rearrange("p a n -> p (a n)"), start=f == 0, stop=f == HC - 1)
                    mm.then_inc(product, 1)

            turn(0)
            rounds(pe, n_rounds - 1, layers)
            layers(n_rounds - 1, False, True)

        @block.scalar
        def _(act):
            act.wait_ge(key_turned, 1)
            act.activation(key_t[:, :], k.ps[6][0:T, 0:P], ACT.Copy).then_inc(key_sb, 1)
            act.preload_act_table(ACT.Gelu)

            def turn(g):
                for j in range(QUAD):
                    act.wait_ge(turned, g * QUAD + (j + 1))
                    act.activation(xt[:, :, j * P:(j + 1) * P], k.ps[j][:, 0:D].rearrange("p (c n) -> p c n", c=2), ACT.Copy).then_inc(turned_sb, 1)

            def layers(g, first, last=False):
                after_earlier(act, product, first, g * QUAD)
                for f in range(HC):
                    act.wait_ge(hidden, g * HC + (f + 1))
                    act.activation(ht[:, f, :], k.ps[4 + f % 2][:, :], ACT.Gelu, bias=b1[:, f:f + 1]).then_inc(hidden_sb, 1)
                if not last:
                    turn(g + 1)

            turn(0)
            rounds(act, n_rounds - 1, layers)
            layers(n_rounds - 1, False, True)

        @block.vector
        def _(dve):
            def rank_tile(t):
                own, end = key[:, t:t + 1], (t + 1) * P
                if t > 0:
                    dve.tensor_scalar(junk[:, 0:t * P], keys[:, 0:t * P], own, 0.0, ALU.is_le, ALU.add, accum_out=count[:, 0, t:t + 1])
                dve.tensor_scalar(junk[:, t * P:NP], keys[:, t * P:NP], own, 0.0, ALU.is_lt, ALU.add, accum_out=count[:, 1, t:t + 1])
                dve.drain()
                dve.scalar_tensor_tensor(out=junk[:, 0:P], in0=keys[:, t * P:end], scalar=own, in1=k.below[:, :],
                                         op0=ALU.is_equal, op1=ALU.mult, accum_out=count[:, 2, t:t + 1])
                dve.drain()

            dve.tensor_tensor(key[:, :], k.degree[:, :], k.noise[:, :], ALU.add).then_inc(keyed, 1)
            dve.memset(count[:, :, :], 0.0)
            dve.drain()
            dve.wait_ge(key_in, 16)
            dve.wait_ge(masked, 1)
            dve.wait_ge(k.wd_in, 16 * (EXPERTS + 1))
            for g in range(n_rounds):
                for j in range(QUAD):
                    if g > 0:
                        dve.wait_ge(stored[j], g * 16)
                    e = dve.value_load(k.owner_i[0:1, g * QUAD + j:g * QUAD + j + 1], min_val=0, max_val=EXPERTS - 1)
                    dve.wait_ge(product, g * QUAD + j + 1)
                    dve.tensor_tensor(out[:, j, :], k.ps[6 + j % 2][:, 0:D], bd[:, bass.ds(e * D, D)], ALU.add).then_inc(out_ready, 1)
                    if g * QUAD + j < T:
                        rank_tile(g * QUAD + j)
            dve.tensor_tensor(rank[:, :], count[:, 0, :], count[:, 1, :], ALU.add)
            dve.drain()
            dve.tensor_tensor(k.rank_i[:, :], rank[:, :], count[:, 2, :], ALU.add)
    k.end_stage()


def ffn0_return_stage(nc, k):
    with nc.Block() as block:
        back = [k.sem(f"r0_back{j}") for j in range(T)]
        rows = k.stage_sb("r0_rows", [P, T, D], F32)

        @block.gpsimd
        def _(pool):
            for t in range(T):
                pool.indirect_dma_start(out=rows[:, t, :], out_offset=None, in_=k.result_dram,
                                        in_offset=bass.IndirectOffsetOnAxis(ap=k.place_i[:, t:t + 1], axis=0)).then_inc(back[t], 16)

        @block.vector
        def _(dve):
            for t in range(T):
                dve.wait_ge(back[t], 16)
                dve.scalar_tensor_tensor(out=k.x[:, t, :], in0=rows[:, t, :], scalar=k.prb[:, t:t + 1], in1=k.x[:, t, :], op0=ALU.mult, op1=ALU.add)
                dve.drain()
                tile_stats(k, dve, t)
    k.end_stage()


def by_tile(big):
    return big[:, :, :].rearrange("p c n -> p (c n)").rearrange("p (t d) -> p t d", d=D)


def l1_pre_stage(nc, k):
    with nc.Block() as block:
        x_saved = k.sem("p1_x_saved")
        weights, var_ready, dev_ready = k.sem("p1_weights"), k.sem("p1_var_ready"), k.sem("p1_dev_ready")
        normed, turned, turned_sb = k.sem("p1_normed"), k.sem("p1_turned"), k.sem("p1_turned_sb")
        product, out_ready = k.sem("p1_product"), k.sem("p1_out_ready")
        zeroed, spread, folded, folded_sb = (k.sem(f"p1_{n}") for n in ("zeroed", "spread", "folded", "folded_sb"))
        sent, kept = k.sem("p1_sent"), k.sem("p1_kept")
        stored = [k.sem(f"p1_stored{j}") for j in range(SLOTS)]
        wn = k.stage_sb("p1_wn", [P, 2, D], F32)
        w = k.stage_sb("p1_w", [P, 2, D + 2 * HEADS], F32)
        acol = k.stage_sb("p1_acol", [P, 2, 2], F32)
        amat = k.stage_sb("p1_amat", [P, 2, 2 * HEADS], F32)
        sums = k.stage_sb("p1_sums", [P, 5, T], F32)
        inv = k.stage_sb("p1_inv", [P, T], F32)
        xn = k.stage_sb("p1_xn", [P, T, D], F32)
        xs = k.stage_sb("p1_xs", [P, SLOTS, D], F32)
        xt = k.stage_sb("p1_xt", [P, 2, SLOTS * P], F32)
        out = k.stage_sb("p1_out", [P, SLOTS, D], F32)
        pe_turn, act_turn = transposer(nc, k, "p1", normed, turned, turned_sb, xs, xt)

        @block.sync
        def _(sp):
            sp.dma_start(wn[:, :, :], k.io["gat_w"].rearrange("(c p) n -> p c n", p=P)).then_inc(weights, 16)
            sp.dma_start(w[:, :, 0:D], k.io["gat_w_t"].rearrange("(c p) n -> p c n", p=P)).then_inc(weights, 16)
            with nc.allow_non_contiguous_dma(reason="2 KB as columns"):
                for a, v in enumerate((k.io["L1_gnn_gat_a_src"], k.io["L1_gnn_gat_a_tgt"])):
                    sp.dma_start(acol[:, a, :], v.rearrange("h f -> (h f)").rearrange("(c p) -> p c", p=P)).then_inc(weights, 16)
            sp.dma_start(k.x_dram.rearrange("(t p) d -> p t d", p=P), k.x[:, :, :]).then_inc(x_saved, 16)

            def store(g, first):
                for j in range(SLOTS):
                    sp.wait_ge(out_ready, g * SLOTS + (j + 1))
                    sp.dma_start(k.nodes_dram[bass.ds((g * SLOTS + j) * P, P), :], out[:, j, :]).then_inc(stored[j], 16)

            rounds(sp, GROUPS, store)
            for j in range(SLOTS):
                sp.wait_ge(stored[j], 16 * GROUPS)
            sp.wait_ge(x_saved, 16)

        @block.gpsimd
        def _(pool):
            for t in range(T):
                pool.wait_ge(kept, t + 1)
                pool.indirect_dma_start(out=k.by_rank_dram, out_offset=bass.IndirectOffsetOnAxis(ap=k.rank_i[:, t:t + 1], axis=0),
                                        in_=xn[:, t, :], in_offset=None).then_inc(sent, 16)
            pool.wait_ge(sent, 16 * T)

        @block.vector
        def _(dve):
            norm_stats(nc, k, dve, sums, inv, dev_ready, var_ready)
            dve.tensor_copy(k.mean_x[:, :], sums[:, 0, :])
            dve.tensor_copy(k.inv_x[:, :], inv[:, :])
            dve.memset(amat[:, :, :], 0.0)
            dve.drain()
            dve.wait_ge(weights, 64)
            for a in range(2):
                for c in range(2):
                    for b in range(2):
                        lanes = slice(b * HD, (b + 1) * HD)
                        last = dve.tensor_copy(amat[lanes, c, a * HEADS + 2 * c + b:a * HEADS + 2 * c + b + 1], acol[lanes, a, c:c + 1])
            last.then_inc(spread, 1)
            dve.wait_ge(folded, 1)
            dve.tensor_copy(w[:, :, D:D + 2 * HEADS], k.ps[7][:, 0:4 * HEADS].rearrange("p (c a) -> p c a", c=2)).then_inc(folded_sb, 1)

            def normalise(g, j):
                t = g * SLOTS + j
                wait_later(dve, turned, t - (SLOTS - 1))
                dve.tensor_scalar(xs[:, j, :], k.x[:, t, :], sums[:, 0, bass.ds(t, 1)], inv[:, bass.ds(t, 1)], ALU.subtract, ALU.mult).then_inc(normed, 1)
                dve.tensor_scalar(xn[:, t, :], k.x[:, t, :], sums[:, 0, bass.ds(t, 1)], inv[:, bass.ds(t, 1)],
                                  ALU.subtract, ALU.mult).then_inc(kept, 1)

            def take(g, j):
                t = g * SLOTS + j
                bank = k.ps[5 + j % 3]
                dve.wait_ge(product, t + 1)
                wait_later(dve, stored[j], g * 16)
                dve.tensor_scalar(k.score[:, bass.ds(t, 1), :], bank[:, D:D + 2 * HEADS].unsqueeze(1), 0.0, None, ALU.add)
                dve.tensor_copy(out[:, j, :], bank[:, 0:D]).then_inc(out_ready, 1)

            skewed(dve, 3, normalise, take)

        @block.tensor
        def _(pe):
            pe.wait_ge(weights, 64)
            pe.wait_ge(spread, 1)
            for ci in range(2):
                for c in range(2):
                    mm = pe.matmul(k.ps[7][:, ci * 2 * HEADS:(ci + 1) * 2 * HEADS], wn[:, c, ci * P:(ci + 1) * P], amat[:, c, :], start=c == 0, stop=c == 1)
            mm.then_inc(folded, 1)
            pe.wait_ge(folded_sb, 1)

            def turn(g, j):
                pe.wait_ge(normed, g * SLOTS + (j + 1))
                pe.transpose(k.ps[j][:, 0:P], xs[:, j, 0:P], k.ident[:, :])
                pe.transpose(k.ps[j][:, P:D], xs[:, j, P:D], k.ident[:, :]).then_inc(turned, 1)

            def multiply(g, j):
                t = g * SLOTS + j
                pe.wait_ge(turned_sb, t + 1)
                wait_later(pe, out_ready, t - 1)
                for c in range(2):
                    mm = pe.matmul(k.ps[5 + j % 3][:, 0:D + 2 * HEADS], xt[:, c, j * P:(j + 1) * P], w[:, c, :], start=c == 0, stop=c == 1)
                mm.then_inc(product, 1)

            skewed(pe, 2, turn, multiply)

        @block.scalar
        def _(act):
            act.preload_act_table(ACT.Sqrt)
            act.wait_ge(var_ready, 1)
            act.activation(sums[:, 4, :], sums[:, 3, :], ACT.Sqrt, bias=k.eps[:, :]).then_inc(dev_ready, 1)
            rounds(act, GROUPS, lambda g, first: act_turn(act, g))
    k.end_stage()


def attention_stage(nc, k):
    H = 4
    Q = 4
    A_ROUNDS = C // (Q * H)
    assert A_ROUNDS * Q * H == C
    with nc.Block() as block:
        lows_in = [k.sem(f"a1_lows_in{h}") for h in range(Q)]
        pool_step = k.sem("a1_pool_step")
        split, picked, taken = (k.sem(f"a1_{n}") for n in ("split", "picked", "taken"))
        hot_ready = [k.sem(f"a1_hot_ready{a}") for a in range(2)]
        own_ready, masks_ready, reduced = k.sem("a1_own_ready"), k.sem("a1_masks_ready"), k.sem("a1_reduced")
        minus_own = k.stage_sb("a1_minus_own", [P, 1], F32)
        away = k.stage_sb("a1_away", [P, 2, H * P], F32)
        whole, masked, own_max, all_max, max_ready, done = (k.sem(f"a1_{n}") for n in ("whole", "masked", "own_max", "all_max", "max_ready", "done"))
        lows = k.stage_sb("a1_lows", [P, Q, 2, H * P], F32)
        hot = k.stage_sb("a1_hot", [P, 2, 2, H * P], F32)
        table = k.stage_sb("a1_table", [P, 2, T, HEADS], F32)
        tile = k.stage_sb("a1_tile", [P, 2, 2, H, T], F32)
        part = k.stage_sb("a1_part", [P, 2, H * HEADS, 2, T], F32)
        top = k.stage_sb("a1_top", [P, 1], F32)
        top_all = k.stage_sb("a1_top_all", [P, 1], F32)
        minus = k.stage_sb("a1_minus", [P, 1], F32)

        @block.sync
        def _(sp):
            def load(g, first):
                for h in range(Q):
                    for a in range(2):
                        if not first:
                            sp.wait_ge(hot_ready[a], g * Q + (h + 1 - Q))
                    for a in range(2):
                        sp.dma_start(lows[:, h, a, :], k.low_row[a][bass.ds(g * Q * H * P + h * H * P, H * P)].partition_broadcast(P)).then_inc(lows_in[h], 16)

            rounds(sp, A_ROUNDS, load)

        @block.vector
        def _(dve):
            for a in range(2):
                last = dve.tensor_copy(table[:, a, :, :], k.score[:, :, a * HEADS:(a + 1) * HEADS])
            last.then_inc(split, 1)
            dve.tensor_scalar(minus_own[:, :], k.own[:, :], -1.0, None, ALU.mult).then_inc(own_ready, 1)
            lane = k.lane32[:, 0:T].unsqueeze(1).unsqueeze(1).to_broadcast([P, 2, H, T])

            def mask(g, h):
                high = k.high[:, :, bass.ds(g * Q * H + h * H, H)].unsqueeze(3).to_broadcast([P, 2, H, T])
                dve.tensor_tensor(tile[:, h % 2, :, :, :], high, lane, ALU.is_equal).then_inc(masks_ready, 1)

            def take(g, h):
                dve.wait_ge(masks_ready, g * Q + (h + 1))
                dve.wait_ge(picked, g * Q + (h + 1))
                for a in range(2):
                    got = k.ps[2 * h + a][:, 0:H * T * HEADS].rearrange("p (c a h) -> p c h a", c=H, a=T)
                    to = part[:, h % 2, :, a, :].rearrange("p (c h) t -> p c h t", c=H)
                    last = dve.tensor_tensor(to, got, tile[:, h % 2, a, :, :].unsqueeze(2).to_broadcast([P, H, HEADS, T]), ALU.mult)
                last.then_inc(taken, 1)

            def reduce(g, h):
                dve.wait_ge(taken, g * Q + (h + 1))
                dve.tensor_reduce(k.attn[:, bass.ds(g * Q * H + h * H, H), :], part[:, h % 2, :, :, :].rearrange("p c a t -> p c (a t)"), AX, ALU.add)\
                   .then_inc(reduced, 1)

            def body(g, first):
                for h in range(Q):
                    if not (first and h < 2):
                        dve.wait_ge(reduced, g * Q + (h - 1))
                    take(g, h)
                    if not (first and h == 0):
                        reduce(g if h > 0 else g - 1, (h - 1) % Q)
                        dve.wait_ge(taken, g * Q + h)
                    mask(g if h < Q - 1 else g + 1, (h + 1) % Q)

            mask(0, 0)
            rounds(dve, A_ROUNDS, body)
            reduce(A_ROUNDS - 1, Q - 1)
            dve.drain()
            dve.scalar_tensor_tensor(out=k.attn[:, :, :], in0=k.attn[:, :, :], scalar=0.2, in1=k.attn[:, :, :], op0=ALU.mult, op1=ALU.max)\
               .then_inc(whole, 1)
            dve.wait_ge(masked, 1)
            dve.tensor_reduce(top[:, :], k.attn[:, :, :].rearrange("p c h -> p (c h)"), AX, ALU.max).then_inc(own_max, 1)
            dve.wait_ge(all_max, 1)
            dve.tensor_scalar(minus[:, :], top_all[:, :], -1.0, None, ALU.mult).then_inc(max_ready, 1)

        @block.tensor
        def _(pe):
            pe.wait_ge(split, 1)

            def body(g, first):
                for h in range(Q):
                    for a in range(2):
                        pe.wait_ge(hot_ready[a], g * Q + (h + 1))
                    if not first:
                        pe.wait_ge(taken, g * Q + (h + 1 - Q))
                    for a in range(2):
                        for c in range(H):
                            mm = pe.matmul(k.ps[2 * h + a][:, c * T * HEADS:(c + 1) * T * HEADS], hot[:, h % 2, a, c * P:(c + 1) * P],
                                           table[:, a, :, :].rearrange("p t h -> p (t h)"), start=True, stop=True)
                    mm.then_inc(picked, 1)

            rounds(pe, A_ROUNDS, body)

        @block.gpsimd
        def _(pool):
            def body(g, first):
                for h in range(Q):
                    pool.wait_ge(lows_in[h], g * 32 + 32)
                    if not (first and h < 2):
                        pool.wait_ge(picked, g * Q + (h - 1))
                    pool.sem_inc(pool_step, 1)
                    pool.tensor_scalar(hot[:, h % 2, 1, :], lows[:, h, 1, :], k.own[:, :], None, ALU.is_equal).then_inc(hot_ready[1], 1)

            rounds(pool, A_ROUNDS, body)
            pool.wait_ge(whole, 1)
            pool.affine_select(out=k.attn[:, C - 1, :], in_=k.attn[:, C - 1, :], compare_op=ALU.is_ge, fill=-1e30,
                               base=EDGES - (C - 1) * P - 1, pattern=[[0, HEADS]], channel_multiplier=-1).then_inc(masked, 1)
            pool.wait_ge(own_max, 1)
            pool.partition_all_reduce(top_all[:, :], top[:, :], P, bass.bass_isa.ReduceOp.max).then_inc(all_max, 1)

        @block.scalar
        def _(act):
            act.preload_act_table(ACT.Exp)
            act.wait_ge(own_ready, 1)

            def body(g, first):
                for h in range(Q):
                    act.wait_ge(lows_in[h], g * 32 + 32)
                    act.activation(away[:, h % 2, :], lows[:, h, 0, :], ACT.Abs, bias=minus_own[:, :])
                    act.drain()
                    if not (first and h < 2):
                        act.wait_ge(picked, g * Q + (h - 1))
                    act.activation(hot[:, h % 2, 0, :], away[:, h % 2, :], ACT.Relu, bias=k.ones[:, 0:1], scale=-1.0).then_inc(hot_ready[0], 1)

            rounds(act, A_ROUNDS, body)
            act.wait_ge(max_ready, 1)
            act.activation(k.attn[:, :, :], k.attn[:, :, :], ACT.Exp, bias=minus[:, :]).then_inc(done, 1)
            act.wait_ge(done, 1)
    k.end_stage()


STATES, DT_RANK, TAPS = 16, 16, 4
HALF = SLOTS * P // 2
LOG1P = (1.0, -0.4999990463256836, 0.33330005407333374, -0.24954558908939362, 0.19678117334842682, -0.15311862528324127,
         0.10614264756441116, -0.057064201682806015, 0.019907161593437195, -0.003256378462538123)


SPAN = 640
SPANS = NP // SPAN
SBANK = SPAN // 2
PAIRS = STATES // 2
AHEAD = ROUNDS - SPANS * PAIRS
GN = SLOTS * P
assert AHEAD == 2 * GROUPS + 2


def edges_and_scan_stage(nc, k):
    H = LANES
    table, scattered = k.tables[1], k.all_scattered[1]
    with nc.Block() as block:
        keys_in = [k.sem(f"es_keys_in{h}") for h in range(2)]
        gathered = [k.sem(f"es_gathered{s}") for s in range(H)]
        gather_i_ready, scatter_i_ready = k.sem("es_gather_i"), k.sem("es_scatter_i")
        scaled, summed, out_ready = k.sem("es_scaled"), k.sem("es_summed"), k.sem("es_out_ready")
        pool_step = k.sem("es_pool_step")
        bc_in = [k.sem(f"es_bc_in{b}") for b in range(2)]
        decayed, fed, scanned, weighed, added = (k.sem(f"es_{n}") for n in ("decayed", "fed", "scanned", "weighed", "added"))
        read_out = k.sem("es_read_out")
        weights, sp_step = k.sem("m1_weights"), k.sem("es_sp_step")
        rows_in, turned, turned_sb = k.sem("m1_rows_in"), k.sem("m1_turned"), k.sem("m1_turned_sb")
        product, evicted = k.sem("m1_product"), k.sem("m1_evicted")
        convolved, gated = k.sem("m1_convolved"), k.sem("m1_gated")
        low_rank, low_sb, low_out, stepped, step_sb = (k.sem(f"m1_{n}") for n in ("low_rank", "low_sb", "low_out", "stepped", "step_sb"))
        small, sized = k.sem("m1_small"), k.sem("m1_sized")
        a_ready, d_ready = k.sem("m1_a_ready"), k.sem("m1_d_ready")
        wi = k.stage_sb("m1_wi", [P, 2, 2 * D], F32)
        wx = k.stage_sb("m1_wx", [P, 2, DT_RANK + 2 * STATES], F32)
        wdt = k.stage_sb("m1_wdt", [DT_RANK, D], F32)
        cw = k.stage_sb("m1_cw", [P, 2, TAPS], F32)
        cb, db = k.stage_sb("m1_cb", [P, 2], F32), k.stage_sb("m1_db", [P, 2], F32)
        xs = k.stage_sb("m1_xs", [P, SLOTS, D], F32)
        xt = k.stage_sb("m1_xt", [P, 2, GN], F32)
        xc = k.stage_sb("m1_xc", [P, 2, TAPS - 1 + GN], F32)
        conv, poly = k.stage_sb("m1_conv", [P, 2, GN], F32), k.stage_sb("m1_poly", [P, 2, GN], F32)
        low = k.stage_sb("m1_low", [DT_RANK + 2 * STATES, GN], F32)
        keys = k.stage_sb("es_keys", [P, 2, H * P], F32)
        gi, si = k.stage_sb("es_gi", [P, 2, H], I32), k.stage_sb("es_si", [P, 2, H], I32)
        same = k.stage_sb("es_same", [P, H, P], F32)
        rows = k.stage_sb("es_rows", [P, H, D], F32)
        vals = k.stage_sb("es_vals", [P, H, ROW], F32)
        out = k.stage_sb("es_out", [P, H, ROW], F32)
        bc = k.stage_sb("es_bc", [P, 2, 2, SPAN], F32)
        decay = k.stage_sb("es_decay", [P, 2, 2, SPAN], F32)
        feed, state = poly, conv
        assert SPAN == GN
        weigh = k.stage_sb("es_weigh", [P, 2, 2, SPAN], F32)
        carry = k.stage_sb("es_carry", [P, 2, STATES], F32)

        def half_step(q, m, b, c):
            return (q * STATES + m * 2 + b) * 2 + c

        @block.sync
        def _(sp):
            def keys_load(g, h, first):
                if not first:
                    sp.wait_ge(scaled, g * UNROLL + (h * H + H - UNROLL))
                sp.dma_start(keys[:, h, :], k.dst_row[bass.ds(g * UNROLL * P + h * H * P, H * P)].partition_broadcast(P)).then_inc(keys_in[h], 16)

            def bc_load(q, m, b, first):
                if not first:
                    sp.wait_ge(weighed, half_step(q, m, b, 0) - 2)
                for a in range(2):
                    row = k.bc_dram[bass.ds(m * 2 + (a * STATES + b), 1), q * SPAN:(q + 1) * SPAN].rearrange("a n -> (a n)")
                    sp.dma_start(bc[:, b, a, :], row.partition_broadcast(P)).then_inc(bc_in[b], 16)

            def both(q, m, first):
                for b in range(2):
                    bc_load(q, m, b, first)
                    keys_load(AHEAD + q * PAIRS + m, b, False)

            def group(g, first):
                for b in range(2):
                    for h in range(2):
                        keys_load(g * 2 + b, h, first and b == 0)
                    if b == 0 and (first or not isinstance(g, int)):
                        sp.wait_ge(turned, g * SLOTS + SLOTS)
                        sp.sem_inc(sp_step, 1)
                        sp.dma_start(xs[:, :, :], k.by_rank_dram[bass.ds(g * GN + GN, GN), :].rearrange("(j p) d -> p j d", p=P)).then_inc(rows_in, 16)
                sp.wait_ge(low_sb, g * 2 + 2)
                sp.sem_inc(sp_step, 1)
                sp.dma_start(k.bc_dram[:, bass.ds(g * GN, GN)], low[DT_RANK:, :]).then_inc(low_out, 16)

            sp.dma_start(xs[:, :, :], k.by_rank_dram[0:GN, :].rearrange("(j p) d -> p j d", p=P)).then_inc(rows_in, 16)
            sp.dma_start(wi[:, :, :], k.io["in_proj_w_t"].rearrange("(c p) n -> p c n", p=P)).then_inc(weights, 16)
            sp.dma_start(wx[:, :, :], k.io["x_proj_w_t"].rearrange("(c p) n -> p c n", p=P)).then_inc(weights, 16)
            sp.dma_start(wdt[:, :], k.io["dt_proj_w_t"]).then_inc(weights, 16)
            sp.dma_start(cw[:, :, :], k.io["L1_gnn_conv_w"].rearrange("(c p) n -> p c n", p=P)).then_inc(weights, 16)
            with nc.allow_non_contiguous_dma(reason="biases of 1 KB as columns"):
                sp.dma_start(cb[:, :], k.io["L1_gnn_conv_b"].rearrange("(c p) -> p c", p=P)).then_inc(weights, 16)
                sp.dma_start(db[:, :], k.io["L1_gnn_dt_proj_b"].rearrange("(c p) -> p c", p=P)).then_inc(weights, 16)
                sp.dma_start(k.d_col[:, :], k.io["L1_gnn_D_param"].rearrange("(c p) -> p c", p=P)).then_inc(weights, 16)
            sp.dma_start(k.a_mat[:, :, :], k.io["L1_gnn_A_log"].rearrange("(c p) n -> p c n", p=P)).then_inc(weights, 16)
            group(0, True)
            with sp.Fori(1, GROUPS - 1) as g:
                group(g, False)
            group(GROUPS - 1, False)
            for g in range(2 * GROUPS, AHEAD):
                keys_load(g, 0, False)
                keys_load(g, 1, False)
            sp.wait_ge(low_out, 16 * GROUPS)
            for q in range(SPANS):
                both(q, 0, q == 0)
                with sp.Fori(1, PAIRS) as m:
                    both(q, m, False)

        @block.gpsimd
        def _(pool):
            def gather(h, s):
                pool.indirect_dma_start(out=rows[:, s, :], out_offset=None, in_=k.nodes_dram,
                                        in_offset=bass.IndirectOffsetOnAxis(ap=gi[:, h, s:s + 1], axis=0)).then_inc(gathered[s], 16)

            def body(g, last):
                for h in range(2):
                    for s in range(H):
                        pool.wait_ge(out_ready, g * UNROLL + (h * H + s + 1))
                        if not (isinstance(g, int) and g == h == 0 and s < TABLES):
                            pool.wait_ge(scattered[s % TABLES], scatters(g, h, s))
                        pool.sem_inc(pool_step, 1)
                        pool.indirect_dma_start(out=table[s % TABLES], out_offset=bass.IndirectOffsetOnAxis(ap=si[:, h, s:s + 1], axis=0),
                                                in_=out[:, s, :], in_offset=None, compute_op=ALU.add).then_inc(scattered[s % TABLES], 16)
                        if not (last and h == 1):
                            pool.wait_ge(scaled, g * UNROLL + (h * H + s + 1))
                            pool.wait_ge(gather_i_ready, g * 2 + (h + 2))
                            pool.sem_inc(pool_step, 1)
                            gather(1 - h, s)

            pool.wait_ge(gather_i_ready, 1)
            for s in range(H):
                gather(0, s)
            pool.wait_ge(k.zeroed[1], 16 * TABLES)
            body(0, False)
            with pool.Fori(1, ROUNDS - 1) as g:
                body(g, False)
            body(ROUNDS - 1, True)
            for a in range(TABLES):
                pool.wait_ge(scattered[a], scatters(ROUNDS, 0, a))

        @block.vector
        def _(dve):
            def indices(g, h):
                dve.tensor_scalar(gi[:, h, :], k.src_i[:, bass.ds(g * UNROLL + h * H, H)], 0.0, None, ALU.add).then_inc(gather_i_ready, 1)

            def start_half(g, h, first):
                dve.wait_ge(keys_in[h], (g + 1) * 16)
                if not first:
                    for a in range(TABLES):
                        dve.wait_ge(scattered[a], scatters(g, h, a) - (LANES // TABLES) * 16)
                dve.tensor_scalar(si[:, h, :], k.dst_to[:, bass.ds(g * UNROLL + h * H, H)], 0.0, None, ALU.add).then_inc(scatter_i_ready, 1)
                indices(g + h, 1 - h)

            def chunk(g, h, s, first):
                at = g * UNROLL + (h * H + s)
                if not (first and h == 0):
                    dve.wait_ge(summed, at + (1 - H))
                dve.tensor_scalar(same[:, s, :], keys[:, h, s * P:(s + 1) * P], k.dst_col[:, bass.ds(at, 1)], None, ALU.is_equal)
                own = k.attn[:, bass.ds(at, 1), :].rearrange("p a h -> p (a h)")
                dve.tensor_scalar(vals[:, s, D:ROW], own, 0.0, None, ALU.add)
                dve.wait_ge(gathered[s], g * 32 + (h * 16 + 16))
                dve.tensor_tensor(vals[:, s, 0:D].rearrange("p (h f) -> p h f", f=HD), rows[:, s, :].rearrange("p (h f) -> p h f", f=HD),
                                  own.unsqueeze(2).to_broadcast([P, HEADS, HD]), ALU.mult).then_inc(scaled, 1)

            def feed_step(q, m, b, c, first):
                if not (first and b == 0):
                    dve.wait_ge(scanned, half_step(q, m, b, c) - 1)
                dve.tensor_tensor(feed[:, c, :], k.dtx[:, c, q * SPAN:(q + 1) * SPAN], bc[:, b, 0, :], ALU.mult).then_inc(fed, 1)

            def scan_step(q, m, b, c, first):
                n = half_step(q, m, b, c)
                dve.wait_ge(fed, n + 1)
                dve.wait_ge(decayed, n + 1)
                if not (first and b == 0):
                    dve.wait_ge(weighed, n - 1)
                dve.tensor_tensor_scan(state[:, c, :], decay[:, b, c, :], feed[:, c, :], carry[:, c, bass.ds(m * 2 + b, 1)],
                                       ALU.mult, ALU.add).then_inc(scanned, 1)

            def weigh_step(q, m, b, c, first):
                n = half_step(q, m, b, c)
                dve.wait_ge(scanned, n + 1)
                dve.tensor_scalar(carry[:, c, bass.ds(m * 2 + b, 1)], state[:, c, SPAN - 1:SPAN], 0.0, None, ALU.add)
                if not first:
                    dve.wait_ge(added, n - 3)
                dve.tensor_tensor(weigh[:, b, c, :], state[:, c, :], bc[:, b, 1, :], ALU.mult).then_inc(weighed, 1)

            def cols(big, g):
                return big[:, :, bass.ds(g * GN, GN)]

            def convolve(tap, last=False):
                for c in range(2):
                    if tap == 0:
                        op = dve.tensor_scalar(conv[:, c, :], xc[:, c, 0:GN], cw[:, c, 0:1], None, ALU.mult)
                    else:
                        op = dve.scalar_tensor_tensor(out=conv[:, c, :], in0=xc[:, c, tap:tap + GN], scalar=cw[:, c, tap:tap + 1], in1=conv[:, c, :],
                                                      op0=ALU.mult, op1=ALU.add)
                if last:
                    op.then_inc(convolved, 1)
                dve.drain()

            def size_step(g, n):
                if n == 0:
                    dve.wait_ge(small, g + 1)
                    dve.tensor_scalar(poly[:, :, :], cols(k.dtx, g), LOG1P[-1], None, ALU.mult)
                elif n < len(LOG1P):
                    dve.scalar_tensor_tensor(out=poly[:, :, :], in0=poly[:, :, :], scalar=LOG1P[-1 - n], in1=cols(k.dtx, g), op0=ALU.add, op1=ALU.mult)
                elif n == len(LOG1P):
                    dve.scalar_tensor_tensor(out=cols(k.dt, g), in0=cols(k.dt, g), scalar=0.0, in1=poly[:, :, :], op0=ALU.max, op1=ALU.add)
                else:
                    dve.tensor_tensor(cols(k.dtx, g), cols(k.dt, g), cols(k.u, g), ALU.mult).then_inc(sized, 1)
                dve.drain()

            def group(g, first):
                for b in range(2):
                    for h in range(2):
                        start_half(g * 2 + b, h, first and b == 0)
                        for s in range(H):
                            chunk(g * 2 + b, h, s, first and b == 0)
                            at = h * H + s
                            if not first and b == 0 and at < 5:
                                size_step(g - 1, at)
                            if not first and b == 1 and at < 7:
                                size_step(g - 1, 5 + at)
                            if b == 0 and at == 5:
                                dve.wait_ge(evicted, g * 8 + 4)
                                convolve(0)
                                convolve(1)
                            if b == 0 and at == 6:
                                convolve(2)
                            if b == 0 and at == 7:
                                convolve(3, True)

            def both(q, m, first):
                g = AHEAD + q * PAIRS + m
                for b in range(2):
                    start_half(g, b, False)
                    dve.wait_ge(bc_in[b], (q * PAIRS + m) * 32 + 32)
                    feed_step(q, m, b, 0, first)
                    chunk(g, b, 0, False)
                    scan_step(q, m, b, 0, first)
                    feed_step(q, m, b, 1, first)
                    chunk(g, b, 1, False)
                    scan_step(q, m, b, 1, first)
                    weigh_step(q, m, b, 0, first)
                    chunk(g, b, 2, False)
                    weigh_step(q, m, b, 1, first)
                    chunk(g, b, 3, False)

            dve.memset(carry[:, :, :], 0.0)
            dve.drain()
            indices(0, 0)
            dve.wait_ge(weights, 128)
            for c in range(2):
                dve.tensor_scalar(k.d_mat[:, c, :], k.ident[:, :], k.d_col[:, c:c + 1], None, ALU.mult).then_inc(d_ready, 1)
            dve.wait_ge(a_ready, 1)
            dve.tensor_scalar(k.a_mat[:, :, :], k.a_mat[:, :, :], -1.0, None, ALU.mult)
            rounds(dve, GROUPS, group)
            for b in range(2):
                for h in range(2):
                    start_half(2 * GROUPS + b, h, False)
                    for s in range(H):
                        chunk(2 * GROUPS + b, h, s, False)
                        if h * H + s < 6:
                            size_step(GROUPS - 1, b * 6 + h * H + s)
            for q in range(SPANS):
                both(q, 0, q == 0)
                with dve.Fori(1, PAIRS) as m:
                    both(q, m, False)
                dve.wait_ge(added, (q + 1) * 2 * STATES)
                for c in range(2):
                    for b in range(2):
                        at = q * SPAN + b * SBANK
                        dve.tensor_tensor(k.zs[:, c, at:at + SBANK], k.zs[:, c, at:at + SBANK], k.ps[4 + 2 * c + b][:, 0:SBANK], ALU.mult).then_inc(read_out, 1)
                dve.drain()

        @block.tensor
        def _(pe):
            def chunk(g, h, s, first):
                n = g * UNROLL + (h * H + s + 1)
                pe.wait_ge(scaled, n)
                if not (first and h == 0):
                    pe.wait_ge(out_ready, n - H)
                pe.matmul(k.ps[s][:, 0:ROW], same[:, s, :], vals[:, s, :], start=True, stop=True).then_inc(summed, 1)

            def add(q, m, b, c, last):
                pe.wait_ge(weighed, half_step(q, m, b, c) + 1)
                for a in range(2):
                    mm = pe.matmul(k.ps[4 + 2 * c + a][:, 0:SBANK], k.ident[:, :], weigh[:, b, c, a * SBANK:(a + 1) * SBANK],
                                   start=False, stop=last and b == 1)
                mm.then_inc(added, 1)

            def both(q, m, last):
                g = AHEAD + q * PAIRS + m
                for b in range(2):
                    chunk(g, b, 0, False)
                    chunk(g, b, 1, False)
                    add(q, m, b, 0, last)
                    chunk(g, b, 2, False)
                    add(q, m, b, 1, last)
                    chunk(g, b, 3, False)

            def project(g, n, first):
                if not (first and n < 4):
                    pe.wait_ge(evicted, g * 8 + (n - 3))
                for c in range(2):
                    mm = pe.matmul(k.ps[4 + n % 4][:, 0:HALF], wi[:, c, n // 2 * P:(n // 2 + 1) * P], xt[:, c, n % 2 * HALF:(n % 2 + 1) * HALF],
                                   start=c == 0, stop=c == 1)
                mm.then_inc(product, 1)

            def group_work(g, b, at, first):
                if b == 0 and at == 0:
                    pe.wait_ge(rows_in, (g + 1) * 16)
                    after_earlier(pe, step_sb, first, g * 4)
                    for j in range(SLOTS):
                        to = k.ps[4 + j // 2][:, j % 2 * D:(j % 2 + 1) * D]
                        pe.transpose(to[:, 0:P], xs[:, j, 0:P], k.ident[:, :])
                        pe.transpose(to[:, P:D], xs[:, j, P:D], k.ident[:, :]).then_inc(turned, 1)
                if b == 0 and 2 <= at <= 4:
                    if at == 2:
                        pe.wait_ge(turned_sb, g * 3 + 3)
                    project(g, 2 * at - 4, first)
                    project(g, 2 * at - 3, first)
                if b == 1 and at == 0:
                    project(g, 6, first)
                    project(g, 7, first)
                if b == 1 and at == 1:
                    pe.wait_ge(gated, g + 1)
                    pe.wait_ge(evicted, g * 8 + 6)
                    for h in range(2):
                        for c in range(2):
                            mm = pe.matmul(k.ps[4 + h][0:DT_RANK + 2 * STATES, 0:HALF], wx[:, c, :], k.u[:, c, bass.ds(g * GN + h * HALF, HALF)],
                                           start=c == 0, stop=c == 1)
                        mm.then_inc(low_rank, 1)
                if b == 1 and at == 3:
                    pe.wait_ge(evicted, g * 8 + 8)
                    pe.wait_ge(low_sb, g * 2 + 2)
                    for h in range(2):
                        for o in range(2):
                            pe.matmul(k.ps[(6, 7, 4, 5)[2 * h + o]][:, 0:HALF], wdt[:, o * P:(o + 1) * P], low[0:DT_RANK, h * HALF:(h + 1) * HALF],
                                      start=True, stop=True).then_inc(stepped, 1)

            def group(g, first):
                for b in range(2):
                    for h in range(2):
                        for s in range(H):
                            chunk(g * 2 + b, h, s, first and b == 0)
                            group_work(g, b, h * H + s, first)

            pe.wait_ge(weights, 128)
            rounds(pe, GROUPS, group)
            for g in range(2 * GROUPS, AHEAD):
                for h in range(2):
                    for s in range(H):
                        chunk(g, h, s, False)
            pe.wait_ge(step_sb, GROUPS * 4)
            pe.wait_ge(d_ready, 2)
            for q in range(SPANS):
                if q > 0:
                    pe.wait_ge(read_out, 4 * q)
                for c in range(2):
                    for a in range(2):
                        at = q * SPAN + a * SBANK
                        pe.matmul(k.ps[4 + 2 * c + a][:, 0:SBANK], k.d_mat[:, c, :], k.u[:, c, at:at + SBANK], start=True, stop=False)
                with pe.Fori(0, PAIRS - 1) as m:
                    both(q, m, False)
                both(q, PAIRS - 1, True)

        @block.scalar
        def _(act):
            def chunk(g, h, s, first):
                if not (first and h == 0):
                    act.wait_ge(scattered[s % TABLES], scatters(g, h, s) - (LANES // TABLES - 1) * 16)
                act.wait_ge(summed, g * UNROLL + (h * H + s + 1))
                act.activation(out[:, s, :], k.ps[s][:, 0:ROW], ACT.Copy).then_inc(out_ready, 1)

            def decay_step(q, m, b, c, first):
                if not first:
                    act.wait_ge(scanned, half_step(q, m, b, c) - 3)
                act.activation(decay[:, b, c, :], k.dt[:, c, q * SPAN:(q + 1) * SPAN], ACT.Exp,
                               scale=k.a_mat[:, c, bass.ds(m * 2 + b, 1)]).then_inc(decayed, 1)

            def both(q, m, first, end=False):
                g = AHEAD + q * PAIRS + m
                for b in range(2):
                    later = (q, m, 1) if b == 0 else (q, m + 1, 0) if not end else (q + 1, 0, 0)
                    chunk(g, b, 0, False)
                    if later[0] < SPANS:
                        decay_step(*later, 0, first and b == 0)
                    chunk(g, b, 1, False)
                    chunk(g, b, 2, False)
                    if later[0] < SPANS:
                        decay_step(*later, 1, first and b == 0)
                    chunk(g, b, 3, False)

            def evict(g, n):
                h = n % 2
                act.wait_ge(product, g * 8 + (n + 1))
                if n < 4:
                    act.activation(xc[:, n // 2, TAPS - 1 + h * HALF:TAPS - 1 + (h + 1) * HALF], k.ps[4 + n % 4][:, 0:HALF], ACT.Copy).then_inc(evicted, 1)
                else:
                    act.activation(k.zs[:, n // 2 - 2, bass.ds(g * GN + h * HALF, HALF)], k.ps[4 + n % 4][:, 0:HALF], ACT.Silu).then_inc(evicted, 1)

            def group_work(g, b, at, first):
                if b == 0 and at == 0:
                    act.preload_act_table(ACT.Silu)
                    if not first:
                        act.wait_ge(convolved, g)
                        act.activation(xc[:, :, 0:TAPS - 1], xc[:, :, GN:GN + TAPS - 1], ACT.Copy)
                if b == 0 and at == 1:
                    for i in range(3):
                        n = min(2, SLOTS - 2 * i)
                        act.wait_ge(turned, g * SLOTS + (2 * i + n))
                        act.activation(xt[:, :, 2 * i * P:(2 * i + n) * P].rearrange("p c (j n) -> p j c n", n=P),
                                       k.ps[4 + i][:, 0:n * D].rearrange("p (j c n) -> p j c n", c=2, n=P), ACT.Copy).then_inc(turned_sb, 1)
                if b == 0 and 3 <= at <= 5:
                    evict(g, 2 * at - 6)
                    evict(g, 2 * at - 5)
                if b == 1 and at == 0:
                    act.wait_ge(convolved, g + 1)
                    for c in range(2):
                        last = act.activation(k.u[:, c, bass.ds(g * GN, GN)], conv[:, c, :], ACT.Silu, bias=cb[:, c:c + 1])
                    last.then_inc(gated, 1)
                if b == 1 and at == 1:
                    evict(g, 6)
                    evict(g, 7)
                if b == 1 and at == 2:
                    after_earlier(act, low_out, first, g * 16)
                    for h in range(2):
                        act.wait_ge(low_rank, g * 2 + (h + 1))
                        act.activation(low[:, h * HALF:(h + 1) * HALF], k.ps[4 + h][0:DT_RANK + 2 * STATES, 0:HALF], ACT.Copy).then_inc(low_sb, 1)
                if b == 1 and at == 4:
                    for h in range(2):
                        for o in range(2):
                            act.wait_ge(stepped, g * 4 + (2 * h + o + 1))
                            act.activation(k.dt[:, o, bass.ds(g * GN + h * HALF, HALF)], k.ps[(6, 7, 4, 5)[2 * h + o]][:, 0:HALF], ACT.Identity,
                                           bias=db[:, o:o + 1]).then_inc(step_sb, 1)
                    act.drain()
                    act.preload_act_table(ACT.Exp)
                if b == 1 and at == 5:
                    act.activation(k.dtx[:, :, bass.ds(g * GN, GN)], k.dt[:, :, bass.ds(g * GN, GN)], ACT.Abs)
                    act.drain()
                if b == 1 and at == 6:
                    act.activation(k.dtx[:, :, bass.ds(g * GN, GN)], k.dtx[:, :, bass.ds(g * GN, GN)], ACT.Exp, scale=-1.0).then_inc(small, 1)

            def group(g, first):
                for b in range(2):
                    for h in range(2):
                        for s in range(H):
                            chunk(g * 2 + b, h, s, first and b == 0)
                            group_work(g, b, h * H + s, first)

            act.activation(xc[:, :, 0:TAPS - 1], k.zero[:, :].unsqueeze(2).to_broadcast([P, 2, TAPS - 1]), ACT.Copy)
            act.wait_ge(weights, 128)
            act.activation(k.a_mat[:, :, :], k.a_mat[:, :, :], ACT.Exp).then_inc(a_ready, 1)
            act.wait_ge(scatter_i_ready, 1)
            rounds(act, GROUPS, group)
            for g in range(2 * GROUPS, AHEAD):
                for h in range(2):
                    for s in range(H):
                        chunk(g, h, s, False)
            act.wait_ge(sized, GROUPS)
            decay_step(0, 0, 0, 0, True)
            decay_step(0, 0, 0, 1, True)
            for q in range(SPANS):
                both(q, 0, q == 0)
                with act.Fori(1, PAIRS - 1) as m:
                    both(q, m, False)
                both(q, PAIRS - 1, False, True)
    k.end_stage()


def mamba_out_stage(nc, k):
    with nc.Block() as block:
        weights, copied, product, out_ready = (k.sem(f"o1_{n}") for n in ("weights", "copied", "product", "out_ready"))
        stored = [k.sem(f"o1_stored{j}") for j in range(SLOTS)]
        w = k.stage_sb("o1_w", [P, 2, D], F32)
        yg = k.stage_sb("o1_yg", [P, 2, SLOTS * P], F32)
        out = k.stage_sb("o1_out", [P, SLOTS, D], F32)

        @block.sync
        def _(sp):
            sp.dma_start(w[:, :, :], k.io["out_proj_w_t"].rearrange("(c p) n -> p c n", p=P)).then_inc(weights, 16)
            sp.wait_ge(copied, 2 * SLOTS)
            sp.dma_start(k.x[:, 0:SLOTS, :], k.x_dram[0:SLOTS * P, :].rearrange("(t p) d -> p t d", p=P)).then_inc(k.x_back[0], 16)

            def store(g, first):
                for j in range(SLOTS):
                    sp.wait_ge(out_ready, g * SLOTS + (j + 1))
                    sp.dma_start(k.scan_dram[bass.ds((g * SLOTS + j) * P, P), :], out[:, j, :]).then_inc(stored[j], 16)

            load_tables(k, sp, 0)
            store(0, True)
            load_post_vectors(k, sp)
            store(1, False)
            load_post_weights(nc, k, sp)
            with sp.Fori(2, GROUPS) as g:
                store(g, False)
            for j in range(SLOTS):
                sp.wait_ge(stored[j], 16 * GROUPS)

        @block.scalar
        def _(act):
            act.preload_act_table(ACT.Copy)

            def copy(g, first):
                for j in range(SLOTS):
                    after_earlier(act, product, first, g * SLOTS + (j + 1 - SLOTS))
                    act.activation(yg[:, :, j * P:(j + 1) * P], k.zs[:, :, bass.ds((g * SLOTS + j) * P, P)], ACT.Copy).then_inc(copied, 1)

            rounds(act, GROUPS, copy)

        @block.tensor
        def _(pe):
            pe.wait_ge(weights, 16)

            def tiles(g, first):
                for j in range(SLOTS):
                    pe.wait_ge(copied, g * SLOTS + (j + 1))
                    after_earlier(pe, out_ready, first, g * SLOTS + (j + 1 - SLOTS))
                    for c in range(2):
                        mm = pe.matmul(k.ps[j][:, 0:D], yg[:, c, j * P:(j + 1) * P], w[:, c, :], start=c == 0, stop=c == 1)
                    mm.then_inc(product, 1)

            rounds(pe, GROUPS, tiles)

        @block.vector
        def _(dve):
            def tiles(g, first):
                for j in range(SLOTS):
                    after_earlier(dve, stored[j], first, g * 16)
                    dve.wait_ge(product, g * SLOTS + (j + 1))
                    dve.tensor_copy(out[:, j, :], k.ps[j][:, 0:D]).then_inc(out_ready, 1)

            rounds(dve, GROUPS, tiles)
    k.end_stage()


FF = 2 * D
FC = FF // P


def load_tables(k, sp, g):
    for a in range(TABLES):
        rows = k.tables[1][a][bass.ds(g * GN, GN), :].rearrange("(j p) c -> p j c", p=P)
        sp.dma_start(k.part[:, a, :, :], rows).then_inc(k.post_tables_in, 16)


def load_post_vectors(k, sp):
    sp.dma_start(k.gat_b[:, :], k.io["L1_gnn_gat_b"].partition_broadcast(P)).then_inc(k.post_vectors_in, 16)
    for i, (g, b) in enumerate((("ln_local_g", "ln_local_b"), ("ln_global_g", "ln_global_b"), ("ln2_g", "ln2_b"))):
        sp.dma_start(k.gains[:, i, :], k.io[f"L1_gnn_{g}"].partition_broadcast(P)).then_inc(k.post_vectors_in, 16)
        sp.dma_start(k.shifts[:, i, :], k.io[f"L1_gnn_{b}"].partition_broadcast(P)).then_inc(k.post_vectors_in, 16)


def load_post_weights(nc, k, sp):
    for dst, src in ((k.wl, k.io["wl_t"]), (k.wg, k.io["wg_t"]), (k.f1w, k.io["ff1_w_t"]), (k.f2w, k.io["ff2_w_t"])):
        sp.dma_start(dst[:, :, :], src.rearrange("(c p) n -> p c n", p=P)).then_inc(k.post_weights_in, 16)
    with nc.allow_non_contiguous_dma(reason="a bias of 2 KB as columns"):
        sp.dma_start(k.f1b[:, :], k.io["L1_gnn_ff1_b"].rearrange("(c p) -> p c", p=P)).then_inc(k.post_weights_in, 16)
    sp.dma_start(k.f2b[:, :], row_view(k.io["L1_gnn_ff2_b"], D)).then_inc(k.post_weights_in, 16)


def l1_post_stage(nc, k):
    with nc.Block() as block:
        vectors, weights, tables_in = k.post_vectors_in, k.post_weights_in, k.post_tables_in
        back = [k.sem(f"q1_back{i}") for i in range(2)]
        folded, total_used = k.sem("q1_folded"), k.sem("q1_total_used")
        moment_ready, inv_ready = ([k.sem(f"q1_{n}{end}") for end in range(2)] for n in ("moment_ready", "inv_ready"))
        pool_step, sp_step = k.sem("q1_pool_step"), k.sem("q1_sp_step")
        above_ready = k.sem("q1_above_ready")
        raw, expd, shifted = k.sem("q1_raw"), k.sem("q1_expd"), k.sem("q1_shifted")
        normed, turned, turned_sb, gate_mm, gated = (k.sem(f"q1_{n}") for n in ("normed", "turned", "turned_sb", "gate_mm", "gated"))
        mixed, h_turned, h_turned_sb, hidden, hidden_sb, ff_mm, joined = (
            k.sem(f"q1_{n}") for n in ("mixed", "h_turned", "h_turned_sb", "hidden", "hidden_sb", "ff_mm", "joined"))
        wl, wg, f1w, f2w, f1b, f2b = k.wl, k.wg, k.f1w, k.f2w, k.f1b, k.f2b
        gat_b, gains, shifts, part = k.gat_b, k.gains, k.shifts, k.part
        total = k.stage_sb("q1_total", [P, SLOTS, ROW], F32)
        den = k.stage_sb("q1_den", [P, SLOTS, HEADS], F32)
        stats = k.stage_sb("q1_stats", [P, 2, SLOTS, 6], F32)
        moments = k.stage_sb("q1_moments", [P, 2, SLOTS, 2], F32)
        inv, minus_half = k.stage_sb("q1_inv", [P, 2, SLOTS], F32), k.stage_sb("q1_minus_half", [P, 2, SLOTS], F32)
        xg = k.stage_sb("q1_xg", [P, SLOTS, D], F32)
        above, below = k.stage_sb("q1_above", [P, SLOTS, D], F32), k.stage_sb("q1_below", [P, SLOTS, D], F32)
        ls, gs = k.stage_sb("q1_ls", [P, SLOTS, D], F32), k.stage_sb("q1_gs", [P, SLOTS, D], F32)
        mix = k.stage_sb("q1_mix", [P, SLOTS, D], F32)
        gate = k.stage_sb("q1_gate", [P, SLOTS, D], F32)
        both_t = k.stage_sb("q1_both_t", [P, 4, SLOTS * P], F32)
        h_t = k.stage_sb("q1_h_t", [P, 2, SLOTS * P], F32)
        f1 = k.stage_sb("q1_f1", [P, FC, SLOTS * P], F32)
        over = lambda a: a.unsqueeze(1).to_broadcast([P, SLOTS, D])
        heads = lambda a: a.rearrange("p j (h f) -> p j h f", f=HD)

        @block.sync
        def _(sp):
            sp.wait_ge(back[0], 16 * SLOTS)
            sp.sem_inc(sp_step, 1)
            sp.dma_start(k.x[:, SLOTS:, :], k.x_dram[SLOTS * P:, :].rearrange("(t p) d -> p t d", p=P)).then_inc(k.x_back[1], 16)
            with sp.Fori(1, GROUPS) as g:
                sp.wait_ge(folded, g)
                sp.sem_inc(sp_step, 1)
                load_tables(k, sp, g)

        @block.gpsimd
        def _(pool):
            def gather(start, end):
                for t in range(start, end):
                    pool.indirect_dma_start(out=k.ha[:, t, :], out_offset=None, in_=k.scan_dram,
                                            in_offset=bass.IndirectOffsetOnAxis(ap=k.rank_i[:, t:t + 1], axis=0)).then_inc(back[t >= SLOTS], 16)

            def add_tables(g, first):
                pool.wait_ge(tables_in, (g + 1) * (16 * TABLES))
                after_earlier(pool, total_used, first, g)
                pool.tensor_tensor(total[:, :, :], part[:, 0, :, :], part[:, 1, :, :], ALU.add).then_inc(folded, 1)

            def reciprocal_deviations(g, end):
                n = 1 if end else 2
                pool.wait_ge(moment_ready[end], g + 1)
                pool.sem_inc(pool_step, 1)
                pool.tensor_scalar(inv[:, 0:n, :], moments[:, 0:n, :, 1], EPS, None, ALU.add)
                pool.drain()
                pool.tensor_tensor(inv[:, 0:n, :], inv[:, 0:n, :], minus_half[:, 0:n, :], ALU.pow).then_inc(inv_ready[end], 1)

            def positive_part(g):
                pool.wait_ge(raw, g + 1)
                pool.sem_inc(pool_step, 1)
                pool.tensor_scalar(above[:, :, :], ls[:, :, :], 0.0, None, ALU.max).then_inc(above_ready, 1)

            def shift_x(g):
                here = bass.ds(g * SLOTS, SLOTS)
                pool.wait_ge(raw, g + 1)
                pool.tensor_tensor(k.x[:, here, :], k.x[:, here, :], over(shifts[:, 2, :]), ALU.add).then_inc(shifted, 1)

            def group(g, first, last=False):
                positive_part(g + 1)
                shift_x(g + 1)
                reciprocal_deviations(g + 1, 0)
                if not last:
                    add_tables(g + 2, False)
                reciprocal_deviations(g, 1)

            pool.memset(minus_half[:, :, :], -0.5)
            gather(0, SLOTS)
            add_tables(0, True)
            gather(SLOTS, 2 * SLOTS)
            positive_part(0)
            shift_x(0)
            reciprocal_deviations(0, 0)
            gather(2 * SLOTS, T)
            add_tables(1, False)
            rounds(pool, GROUPS - 2, group)
            group(GROUPS - 2, False, True)
            reciprocal_deviations(GROUPS - 1, 1)

        @block.vector
        def _(dve):
            def front(g, first):
                here = bass.ds(g * SLOTS, SLOTS)
                for j in range(SLOTS):
                    t = g * SLOTS + j
                    dve.tensor_scalar(xg[:, j, :], k.x[:, t, :], k.mean_x[:, bass.ds(t, 1)], k.inv_x[:, bass.ds(t, 1)], ALU.subtract, ALU.mult)
                dve.drain()
                dve.tensor_tensor(gs[:, :, :], k.ha[:, here, :], xg[:, :, :], ALU.add)
                dve.tensor_tensor(xg[:, :, :], xg[:, :, :], over(gat_b[:, :]), ALU.add)
                dve.wait_ge(folded, g + 1)
                dve.tensor_scalar(den[:, :, :], total[:, :, D:ROW], 1e-16, None, ALU.add)
                dve.drain()
                dve.reciprocal(den[:, :, :], den[:, :, :])
                dve.drain()
                dve.tensor_tensor(heads(ls[:, :, :]), heads(total[:, :, 0:D]), den[:, :, :].unsqueeze(3).to_broadcast([P, SLOTS, HEADS, HD]), ALU.mult)\
                   .then_inc(total_used, 1)
                dve.drain()
                dve.tensor_tensor(ls[:, :, :], ls[:, :, :], xg[:, :, :], ALU.add).then_inc(raw, 1)
                for j in range(SLOTS):
                    dve.bn_stats(stats[:, 1, j, :], gs[:, j, :])
                dve.wait_ge(above_ready, g + 1)
                dve.wait_ge(expd, g + 1)
                dve.scalar_tensor_tensor(out=ls[:, :, :], in0=below[:, :, :], scalar=-1.0, in1=above[:, :, :], op0=ALU.add, op1=ALU.add)
                dve.drain()
                for j in range(SLOTS):
                    dve.bn_stats(stats[:, 0, j, :], ls[:, j, :])
                dve.drain()
                normalise(g, (ls, gs), (gains[:, 0, :], gains[:, 1, :]), [lambda j: shifts[:, 0, :], lambda j: shifts[:, 1, :]], (ls, gs), None)

            def normalise(g, sources, gain, shift, to, done):
                n = len(sources)
                for i in range(n):
                    for j in range(SLOTS):
                        last = dve.bn_aggr(moments[:, i, j, :], stats[:, i, j, :])
                last.then_inc(moment_ready[done is not None], 1)
                dve.drain()
                for i in range(n):
                    for j in range(SLOTS):
                        dve.scalar_tensor_tensor(out=sources[i][:, j, :], in0=sources[i][:, j, :], scalar=moments[:, i, j, 0:1], in1=gain[i],
                                                 op0=ALU.subtract, op1=ALU.mult)
                dve.drain()
                if done is not None:
                    dve.wait_ge(shifted, g + 1)
                dve.wait_ge(inv_ready[done is not None], g + 1)
                for i in range(n):
                    for j in range(SLOTS):
                        out = to[i][:, j, :] if done is None else done(j)
                        last = dve.scalar_tensor_tensor(out=out, in0=sources[i][:, j, :], scalar=inv[:, i, j:j + 1], in1=shift[i](j),
                                                        op0=ALU.mult, op1=ALU.add)
                if done is None:
                    last.then_inc(normed, 1)
                dve.drain()

            def mix_step(g):
                dve.wait_ge(turned, (g + 1) * SLOTS)
                dve.tensor_tensor(mix[:, :, :], ls[:, :, :], gs[:, :, :], ALU.subtract)
                dve.drain()
                dve.wait_ge(gated, (g + 1) * SLOTS)
                dve.tensor_tensor(mix[:, :, :], mix[:, :, :], gate[:, :, :], ALU.mult)
                dve.drain()
                dve.tensor_tensor(mix[:, :, :], mix[:, :, :], gs[:, :, :], ALU.add).then_inc(mixed, 1)
                dve.drain()

            def finish(g):
                for j in range(SLOTS):
                    dve.wait_ge(ff_mm, g * SLOTS + (j + 1))
                    dve.tensor_tensor(mix[:, j, :], mix[:, j, :], k.ps[j][:, 0:D], ALU.add).then_inc(joined, 1)
                dve.drain()
                for j in range(SLOTS):
                    dve.bn_stats(stats[:, 0, j, :], mix[:, j, :])
                dve.drain()
                x_tile = lambda j: k.x[:, g * SLOTS + j, :]
                normalise(g, (mix,), (gains[:, 2, :],), (x_tile,), None, x_tile)
                for j in range(SLOTS):
                    tile_stats(k, dve, g * SLOTS + j)

            dve.wait_ge(k.x_back[0], 16)
            dve.wait_ge(vectors, 7 * 16)
            dve.wait_ge(back[0], 16 * SLOTS)
            front(0, True)
            dve.wait_ge(back[1], 16 * (T - SLOTS))
            dve.wait_ge(k.x_back[1], 16)

            def group(g, first):
                mix_step(g)
                front(g + 1, False)
                finish(g)

            rounds(dve, GROUPS - 1, group)
            mix_step(GROUPS - 1)
            finish(GROUPS - 1)

        @block.scalar
        def _(act):
            def elu(g, first):
                act.wait_ge(raw, g + 1)
                act.activation(below[:, :, :], ls[:, :, :], ACT.Relu, scale=-1.0)
                act.drain()
                act.activation(below[:, :, :], below[:, :, :], ACT.Exp, scale=-1.0).then_inc(expd, 1)

            def gates(g, first):
                for j in range(SLOTS):
                    act.wait_ge(turned, g * SLOTS + (j + 1))
                    act.activation(both_t[:, :, j * P:(j + 1) * P], k.ps[j][:, :].rearrange("p (c n) -> p c n", c=4), ACT.Copy).then_inc(turned_sb, 1)
                for j in range(SLOTS):
                    act.wait_ge(gate_mm, g * SLOTS + (j + 1))
                    act.activation(gate[:, j, :], k.ps[5 + j % 3][:, 0:D], ACT.Sigmoid).then_inc(gated, 1)

            def feed_forward(g, last=False):
                for j in range(SLOTS):
                    act.wait_ge(h_turned, g * SLOTS + (j + 1))
                    act.activation(h_t[:, :, j * P:(j + 1) * P], k.ps[j][:, 0:D].rearrange("p (c n) -> p c n", c=2), ACT.Copy).then_inc(h_turned_sb, 1)
                for f in range(FC):
                    for h in range(2):
                        act.wait_ge(hidden, g * (2 * FC) + (2 * f + h + 1))
                        act.activation(f1[:, f, h * HALF:(h + 1) * HALF], k.ps[5 + (2 * f + h) % 3][:, 0:HALF], ACT.Relu, bias=f1b[:, f:f + 1]).then_inc(hidden_sb, 1)
                    if f == 1 and not last:
                        elu(g + 1, False)

            def group(g, first):
                act.preload_act_table(ACT.Exp)
                feed_forward(g)
                act.preload_act_table(ACT.Sigmoid)
                gates(g + 1, False)

            act.preload_act_table(ACT.Exp)
            act.wait_ge(weights, 6 * 16)
            elu(0, True)
            act.preload_act_table(ACT.Sigmoid)
            gates(0, True)
            rounds(act, GROUPS - 1, group)
            feed_forward(GROUPS - 1, True)

        @block.tensor
        def _(pe):
            def gates(g, first):
                pe.wait_ge(normed, g + 1)
                for j in range(SLOTS):
                    if not first:
                        pe.wait_ge(joined, g * SLOTS + (j + 1 - SLOTS))
                    for c in range(4):
                        mm = pe.transpose(k.ps[j][:, c * P:(c + 1) * P], (ls, gs)[c // 2][:, j, (c % 2) * P:(c % 2 + 1) * P], k.ident[:, :])
                    mm.then_inc(turned, 1)
                for j in range(SLOTS):
                    pe.wait_ge(turned_sb, g * SLOTS + (j + 1))
                    if j >= 3:
                        pe.wait_ge(gated, g * SLOTS + (j - 2))
                    for c in range(4):
                        mm = pe.matmul(k.ps[5 + j % 3][:, 0:D], both_t[:, c, j * P:(j + 1) * P], (wl, wg)[c // 2][:, c % 2, :], start=c == 0, stop=c == 3)
                    mm.then_inc(gate_mm, 1)

            def feed_forward(g):
                pe.wait_ge(mixed, g + 1)
                for j in range(SLOTS):
                    pe.transpose(k.ps[j][:, 0:P], mix[:, j, 0:P], k.ident[:, :])
                    pe.transpose(k.ps[j][:, P:D], mix[:, j, P:D], k.ident[:, :]).then_inc(h_turned, 1)
                pe.wait_ge(h_turned_sb, (g + 1) * SLOTS)
                for f in range(FC):
                    for h in range(2):
                        n = 2 * f + h
                        if n >= 3:
                            pe.wait_ge(hidden_sb, g * (2 * FC) + (n - 2))
                        for c in range(2):
                            mm = pe.matmul(k.ps[5 + n % 3][:, 0:HALF], f1w[:, c, f * P:(f + 1) * P], h_t[:, c, h * HALF:(h + 1) * HALF], start=c == 0, stop=c == 1)
                        mm.then_inc(hidden, 1)
                pe.wait_ge(hidden_sb, (g + 1) * (2 * FC))
                for j in range(SLOTS):
                    for f in range(FC):
                        pe.matmul(k.ps[j][:, 0:D], f1[:, f, j * P:(j + 1) * P], f2w[:, f, :], start=f == 0, stop=False)
                    pe.matmul(k.ps[j][:, 0:D], k.ones[0:1, :], f2b[0:1, :], start=False, stop=True).then_inc(ff_mm, 1)

            def group(g, first):
                feed_forward(g)
                gates(g + 1, False)

            pe.wait_ge(weights, 6 * 16)
            gates(0, True)
            rounds(pe, GROUPS - 1, group)
            feed_forward(GROUPS - 1)
    k.end_stage()


def load_expert(nc, k, sp, e, s):
    sp.dma_start(k.w1[:, s, :, :], k.io["L1_ffn_w1"][bass.ds(e, 1)].rearrange("a (c p) n -> p (a c) n", p=P)).then_inc(k.expert_in[s], 16)
    sp.dma_start(k.w2[:, s, :, :], k.io["L1_ffn_w2"][bass.ds(e, 1)].rearrange("a (f p) n -> p (a f) n", p=P)).then_inc(k.expert_in[s], 16)
    with nc.allow_non_contiguous_dma(reason="a bias of 4 KB as columns"):
        sp.dma_start(k.b1[:, s, :], k.io["L1_ffn_b1"][bass.ds(e, 1)].rearrange("a (f p) -> p (a f)", p=P)).then_inc(k.expert_in[s], 16)
    sp.dma_start(k.b2[:, s, :], k.io["L1_ffn_b2"].rearrange("e n -> (e n)")[bass.ds(e * D, D)].partition_broadcast(P)).then_inc(k.expert_in[s], 16)


def ffn1_route_stage(nc, k):
    with nc.Block() as block:
        weights, var_ready, dev_ready = k.sem("g1_weights"), k.sem("g1_var_ready"), k.sem("g1_dev_ready")
        normed, turned, turned_sb = k.sem("g1_normed"), k.sem("g1_turned"), k.sem("g1_turned_sb")
        gated, logit_ready = k.sem("g1_gated"), k.sem("g1_logit_ready")
        exp_ready, exp_done, mask_ready, counted = (k.sem(f"g1_{n}") for n in ("exp_ready", "exp_done", "mask_ready", "counted"))
        placed, sent = k.sem("g1_placed"), k.sem("g1_sent")
        wg = k.stage_sb("g1_wg", [P, 2, EXPERTS], F32)
        bg = k.stage_sb("g1_bg", [P, EXPERTS], F32)
        sums = k.stage_sb("g1_sums", [P, 5, T], F32)
        inv = k.stage_sb("g1_inv", [P, T], F32)
        xn = k.stage_sb("g1_xn", [P, T, D], F32)
        xs = k.stage_sb("g1_xs", [P, SLOTS, D], F32)
        xt = k.stage_sb("g1_xt", [P, 2, SLOTS * P], F32)
        logits = k.stage_sb("g1_logits", [P, T, EXPERTS], F32)
        pe_turn, act_turn = transposer(nc, k, "g1", normed, turned, turned_sb, xs, xt)
        k.prob_of["g1"] = k.stage_sb("g1_prob", [P, T, EXPERTS], F32)

        @block.sync
        def _(sp):
            sp.dma_start(wg[:, :, :], k.io["L1_ffn_gate_w"].rearrange("(c p) e -> p c e", p=P)).then_inc(weights, 16)
            sp.dma_start(bg[:, :], k.io["L1_ffn_gate_b"].partition_broadcast(P)).then_inc(weights, 16)
            for e in range(2):
                load_expert(nc, k, sp, e, e)

        @block.vector
        def _(dve):
            norm_stats(nc, k, dve, sums, inv, dev_ready, var_ready)
            dve.wait_ge(weights, 32)

            def normalise(g, j):
                t = g * SLOTS + j
                wait_later(dve, turned, t - (SLOTS - 1))
                dve.tensor_scalar(xs[:, j, :], k.x[:, t, :], sums[:, 0, bass.ds(t, 1)], inv[:, bass.ds(t, 1)],
                                  ALU.subtract, ALU.mult).then_inc(normed, 1)
                dve.tensor_scalar(xn[:, t, :], k.x[:, t, :], sums[:, 0, bass.ds(t, 1)], inv[:, bass.ds(t, 1)], ALU.subtract, ALU.mult)

            def take(g, j):
                t = g * SLOTS + j
                dve.wait_ge(gated, t + 1)
                dve.tensor_tensor(logits[:, bass.ds(t, 1), :], k.ps[5 + j % 3][:, 0:EXPERTS].unsqueeze(1), bg[:, :].unsqueeze(1), ALU.add).then_inc(logit_ready, 1)

            skewed(dve, 3, normalise, take)
            dve.drain()
            route(nc, k, dve, "g1", logits, exp_ready, exp_done, mask_ready, counted, False)
            dve.sem_inc(placed, 1)

        @block.tensor
        def _(pe):
            pe.wait_ge(weights, 32)

            def turn(g, j):
                pe.wait_ge(normed, g * SLOTS + (j + 1))
                pe.transpose(k.ps[j][:, 0:P], xs[:, j, 0:P], k.ident[:, :])
                pe.transpose(k.ps[j][:, P:D], xs[:, j, P:D], k.ident[:, :]).then_inc(turned, 1)

            def gate(g, j):
                t = g * SLOTS + j
                pe.wait_ge(turned_sb, t + 1)
                wait_later(pe, logit_ready, t - 1)
                for c in range(2):
                    mm = pe.matmul(k.ps[5 + j % 3][:, 0:EXPERTS], xt[:, c, j * P:(j + 1) * P], wg[:, c, :], start=c == 0, stop=c == 1)
                mm.then_inc(gated, 1)

            skewed(pe, 2, turn, gate)
            pe.wait_ge(mask_ready, 1)
            count_tokens(k, pe).then_inc(counted, 1)

        @block.scalar
        def _(act):
            act.preload_act_table(ACT.Sqrt)
            act.wait_ge(var_ready, 1)
            act.activation(sums[:, 4, :], sums[:, 3, :], ACT.Sqrt, bias=k.eps[:, :]).then_inc(dev_ready, 1)

            rounds(act, GROUPS, lambda g, first: act_turn(act, g))
            act.wait_ge(exp_ready, 1)
            act.activation(k.prob_of["g1"][:, :, :], k.prob_of["g1"][:, :, :], ACT.Exp).then_inc(exp_done, 1)

        @block.gpsimd
        def _(pool):
            pool.wait_ge(placed, 1)
            for t in range(T):
                pool.indirect_dma_start(out=k.sorted_dram, out_offset=bass.IndirectOffsetOnAxis(ap=k.send_i[:, t:t + 1], axis=0),
                                        in_=xn[:, t, :], in_offset=None, bounds_check=EXPERTS * BUF - 1, oob_is_err=False).then_inc(sent, 16)
            pool.wait_ge(sent, 16 * T)
    k.end_stage()


BT = BUF // P
assert EXPERTS * BUF == SORTED * P and CAPACITY <= BUF


def ffn1_experts_stage(nc, k):
    with nc.Block() as block:
        loaded, rows_in = k.expert_in, [k.sem(f"y1_rows_in{s}") for s in range(2)]
        turned, turned_sb, hidden, hidden_sb = (k.sem(f"y1_{n}") for n in ("turned", "turned_sb", "hidden", "hidden_sb"))
        product, out_ready = k.sem("y1_product"), k.sem("y1_out_ready")
        stored = [k.sem(f"y1_stored{j}") for j in range(BT)]
        w1, w2, b1, b2 = k.w1, k.w2, k.b1, k.b2
        xs = k.stage_sb("y1_xs", [P, 2, BT, D], F32)
        xt = k.stage_sb("y1_xt", [P, 2, BUF], F32)
        ht = k.stage_sb("y1_ht", [P, HC, BUF], F32)
        out = k.stage_sb("y1_out", [P, BT, D], F32)
        n_rounds = EXPERTS // 2
        places = [min(P, CAPACITY - j * P) for j in range(BT)]

        @block.sync
        def _(sp):
            def load(r, s, first):
                e = r * 2 + s
                if not first:
                    sp.wait_ge(out_ready, e * BT - BT)
                sp.dma_start(xs[:, s, :, :], k.sorted_dram[bass.ds(e * BUF, BUF), :].rearrange("(j p) d -> p j d", p=P)).then_inc(rows_in[s], 16)
                if not first:
                    load_expert(nc, k, sp, e, s)

            load(0, 0, True)

            def tiles(r, last):
                load(r, 1, isinstance(r, int) and r == 0)
                for s in range(2):
                    e = r * 2 + s
                    for j in range(BT):
                        sp.wait_ge(out_ready, e * BT + (j + 1))
                        sp.dma_start(k.result_dram[bass.ds(e * BUF + j * P, places[j]), :], out[0:places[j], j, :]).then_inc(stored[j], 16)
                    if s == 0 and not last:
                        load(r + 1, 0, False)

            tiles(0, False)
            with sp.Fori(1, n_rounds - 1) as r:
                tiles(r, False)
            tiles(n_rounds - 1, True)
            for j in range(BT):
                sp.wait_ge(stored[j], 16 * EXPERTS)

        @block.tensor
        def _(pe):
            def turn(r, s):
                pe.wait_ge(rows_in[s], r * 16 + 16)
                for j in range(BT):
                    pe.transpose(k.ps[j][:, 0:P], xs[:, s, j, 0:P], k.ident[:, :])
                    pe.transpose(k.ps[j][:, P:D], xs[:, s, j, P:D], k.ident[:, :]).then_inc(turned, 1)

            def layers(r, s, first, last=False):
                e = r * 2 + s
                pe.wait_ge(turned_sb, e * BT + BT)
                pe.wait_ge(loaded[s], (r + 1) * (4 * 16))
                for f in range(HC):
                    if not (first and f < 2):
                        pe.wait_ge(hidden_sb, e * HC + (f - 1))
                    for c in range(2):
                        mm = pe.matmul(k.ps[4 + f % 2][:, 0:CAPACITY], w1[:, s, c, f * P:(f + 1) * P], xt[:, c, 0:CAPACITY], start=c == 0, stop=c == 1)
                    mm.then_inc(hidden, 1)
                if not last:
                    turn(r + s, 1 - s)
                pe.wait_ge(hidden_sb, e * HC + HC)
                for j in range(BT):
                    if not (first and j < 2):
                        pe.wait_ge(out_ready, e * BT + (j - 1))
                    bank = k.ps[6 + j % 2]
                    for f in range(HC):
                        mm = pe.matmul(bank[0:places[j], 0:D], ht[:, f, j * P:j * P + places[j]], w2[:, s, f, :], start=f == 0, stop=f == HC - 1)
                    mm.then_inc(product, 1)

            def both(r, first):
                layers(r, 0, first)
                layers(r, 1, False)

            turn(0, 0)
            rounds(pe, n_rounds - 1, both)
            layers(n_rounds - 1, 0, False)
            layers(n_rounds - 1, 1, False, True)

        @block.scalar
        def _(act):
            act.preload_act_table(ACT.Relu)

            def turn(e):
                for j in range(BT):
                    act.wait_ge(turned, e * BT + (j + 1))
                    act.activation(xt[:, :, j * P:(j + 1) * P], k.ps[j][:, 0:D].rearrange("p (c n) -> p c n", c=2), ACT.Copy).then_inc(turned_sb, 1)

            def layers(r, s, first, last=False):
                e = r * 2 + s
                act.wait_ge(loaded[s], (r + 1) * (4 * 16))
                after_earlier(act, product, first, e * BT)
                for f in range(HC):
                    act.wait_ge(hidden, e * HC + (f + 1))
                    act.activation(ht[:, f, 0:CAPACITY], k.ps[4 + f % 2][:, 0:CAPACITY], ACT.Relu, bias=b1[:, s, f:f + 1]).then_inc(hidden_sb, 1)
                if not last:
                    turn(e + 1)

            def both(r, first):
                layers(r, 0, first)
                layers(r, 1, False)

            turn(0)
            rounds(act, n_rounds - 1, both)
            layers(n_rounds - 1, 0, False)
            layers(n_rounds - 1, 1, False, True)

        @block.vector
        def _(dve):
            def tiles(r, first):
                for s in range(2):
                    e = r * 2 + s
                    for j in range(BT):
                        if not (first and s == 0):
                            dve.wait_ge(stored[j], e * 16)
                        dve.wait_ge(product, e * BT + (j + 1))
                        n = places[j]
                        dve.tensor_tensor(out[0:n, j, :], k.ps[6 + j % 2][0:n, 0:D], b2[0:n, s, :], ALU.add).then_inc(out_ready, 1)

            rounds(dve, n_rounds, tiles)
    k.end_stage()


BIG = 3.4028234663852886e38


def ffn1_return_stage(nc, k, out):
    with nc.Block() as block:
        back = [k.sem(f"z1_back{g}") for g in range(GROUPS)]
        summed, stored = [k.sem(f"z1_summed{g}") for g in range(GROUPS)], k.sem("z1_stored")
        rows = k.stage_sb("z1_rows", [P, T, D], F32)
        weighted = k.sem("z1_weighted")
        zeros = k.stage_sb("z1_zeros", [P, SLOTS, D], F32)
        clean = k.stage_sb("z1_clean", [P, T, D], F32)
        not_number = k.stage_sb("z1_not_number", [P, 2, SLOTS, D], I32)
        finite = k.stage_sb("z1_finite", [P, 2, SLOTS, D], I32)
        cleaned = k.sem("z1_cleaned")

        @block.gpsimd
        def _(pool):
            for t in range(T):
                pool.indirect_dma_start(out=rows[:, t, :], out_offset=None, in_=k.result_dram,
                                        in_offset=bass.IndirectOffsetOnAxis(ap=k.place_i[:, t:t + 1], axis=0)).then_inc(back[t // SLOTS], 16)
            for g in range(GROUPS - 1):
                here = slice(g * SLOTS, (g + 1) * SLOTS)
                pool.wait_ge(cleaned, g + 1)
                pool.tensor_tensor(k.x[:, here, :], k.x[:, here, :], clean[:, here, :], ALU.add).then_inc(summed[g], 1)

        @block.scalar
        def _(act):
            act.preload_act_table(ACT.Copy)
            for t in range(T):
                if t % SLOTS == 0:
                    act.wait_ge(back[t // SLOTS], 16 * SLOTS)
                act.activation(rows[:, t, :], rows[:, t, :], ACT.Copy, scale=k.prb[:, t:t + 1]).then_inc(weighted, 1)

        @block.vector
        def _(dve):
            dve.memset(zeros[:, :, :], 0.0)
            for g in range(GROUPS):
                here = slice(g * SLOTS, (g + 1) * SLOTS)
                z = rows[:, here, :]
                dve.wait_ge(weighted, (g + 1) * SLOTS)
                dve.tensor_scalar(clean[:, here, :], z, -1e4, 1e4, ALU.max, ALU.min)
                dve.tensor_tensor(not_number[:, g % 2, :, :], z, z, ALU.not_equal)
                dve.tensor_scalar(finite[:, g % 2, :, :], z, 0.0, 0.0, ALU.mult, ALU.is_equal)
                dve.drain()
                dve.copy_predicated(clean[:, here, :], not_number[:, g % 2, :, :], zeros[:, :, :])
                dve.drain()
                dve.copy_predicated(clean[:, here, :], finite[:, g % 2, :, :], z).then_inc(cleaned, 1)
            dve.drain()
            dve.tensor_tensor(k.x[:, here, :], k.x[:, here, :], clean[:, here, :], ALU.add).then_inc(summed[GROUPS - 1], 1)

        @block.sync
        def _(sp):
            for g in range(GROUPS):
                sp.wait_ge(summed[g], 1)
                full = SLOTS if g < GROUPS - 1 else SLOTS - 1
                first, n = g * SLOTS, full * P
                sp.dma_start(out[first * P:first * P + n, :].rearrange("(j p) d -> p j d", p=P), k.x[:, first:first + full, :]).then_inc(stored, 16)
            sp.dma_start(out[(T - 1) * P:NODES, :], k.x[0:LAST, T - 1, :]).then_inc(stored, 16)
            sp.wait_ge(stored, 16 * (GROUPS + 1))
    k.end_stage()


class Program:
    pass


def build(nc, io, out, upto=99, dbg=None):
    with ExitStack() as program:
        k = Program()
        k.io = io
        k.sb = lambda name, shape, dt: program.enter_context(nc.sbuf_tensor(name, shape, dt))
        k.lasting_sem = lambda name: program.enter_context(nc.semaphore(name))
        k.stage_sems = []

        def stage_sem(name):
            k.stage_sems.append(nc.alloc_semaphore(name))
            return k.stage_sems[-1]

        def end_stage():
            k.stage.close()
            nc.clear_and_free_semaphores(k.stage_sems)
            k.stage_sems = []
            nc.all_engine_barrier()

        k.sem = stage_sem
        k.stage = ExitStack()
        k.stage_sb = lambda name, shape, dt: k.stage.enter_context(nc.sbuf_tensor(name, shape, dt))
        k.end_stage = end_stage
        k.ps = [program.enter_context(nc.psum_tensor(f"bank{i}", [P, 512], F32)) for i in range(8)]
        k.x = k.sb("x", [P, T, D], F32)
        k.ident, k.below = k.sb("ident", [P, P], F32), k.sb("below", [P, P], F32)
        k.dump, k.eps, k.zero = k.sb("dump", [P, 1], F32), k.sb("eps", [P, 1], F32), k.sb("zero", [P, 1], F32)
        k.ones = k.sb("ones", [P, P], F32)
        k.noise, k.own = k.sb("noise", [P, T], F32), k.sb("own", [P, 1], F32)
        k.rank_i = k.sb("rank_i", [P, T], I32)
        k.mean_x, k.inv_x = k.sb("mean_x", [P, T], F32), k.sb("inv_x", [P, T], F32)
        k.before = k.sb("before", [P, P], F32)
        k.lane8, k.lane32 = k.sb("lane8", [P, EXPERTS], F32), k.sb("lane32", [P, 32], F32)
        k.degree, k.prb = k.sb("degree", [P, T], F32), k.sb("prb", [P, T], F32)
        k.place_i, k.send_i = k.sb("place_i", [P, T], I32), k.sb("send_i", [P, T], I32)
        k.owner_i, k.hot = k.sb("owner_i", [P, SORTED], I32), k.sb("hot", [P, T, EXPERTS], F32)
        k.wide_zero = k.sb("wide_zero", [P, ROW], F32)
        k.x_back = [k.lasting_sem(f"x_back{i}") for i in range(2)]
        k.zeroed = [k.lasting_sem(f"zeroed{layer}") for layer in range(2)]
        k.stats = k.sb("stats", [P, T * 6], F32)
        k.a_mat, k.d_mat, k.d_col = k.sb("a_mat", [P, 2, STATES], F32), k.sb("d_mat", [P, 2, P], F32), k.sb("d_col", [P, 2], F32)
        k.keys, k.edges = ExitStack(), ExitStack()
        program.callback(k.keys.close)
        program.callback(k.edges.close)
        key_sb = lambda name, shape, dt: k.keys.enter_context(nc.sbuf_tensor(name, shape, dt))
        edge_sb = lambda name, shape, dt: k.edges.enter_context(nc.sbuf_tensor(name, shape, dt))
        k.dst_col, k.src_i, k.dst_to = key_sb("dst_col", [P, C], F32), key_sb("src_i", [P, C + 8], I32), key_sb("dst_to", [P, C], I32)
        k.attn = key_sb("attn", [P, C, HEADS], F32)
        k.src_col, k.w_col, k.src_off, k.dst_off = (edge_sb(n, [P, C], F32) for n in ("src_col", "w_col", "src_off", "dst_off"))
        k.dst_i, k.src_to = edge_sb("dst_i", [P, C + 8], I32), edge_sb("src_to", [P, C], I32)
        k.high = edge_sb("high", [P, 2, C + LANES], F32)

        def dram(name, shape, dt=F32):
            return nc.dram_tensor(name, shape, dt, kind="Internal").ap()

        k.src_row, k.dst_row = dram("src_row", (EP,)), dram("dst_row", (EP,))
        k.low_row = [dram("src_low_row", (EP,)), dram("dst_low_row", (EP,))]
        k.order_row, k.by_rank_dram = dram("order_row", (NP,)), dram("by_rank_dram", (NP, D))
        k.bc_dram, k.scan_dram = dram("bc_dram", (2 * STATES, NP)), dram("scan_dram", (NP, D))
        k.x_dram = dram("x_dram", (NP, D))
        k.nodes_dram = dram("nodes_dram", (NP, D))
        k.sorted_dram, k.result_dram = dram("sorted_dram", (SORTED * P, D)), dram("result_dram", (SORTED * P, D))
        k.tables = [[dram(f"table{layer}_{a}", (TROWS, ROW)) for a in range(TABLES)] for layer in range(2)]
        k.all_scattered = [[k.lasting_sem(f"scattered{layer}_{a}") for a in range(TABLES)] for layer in range(2)]
        setup_stage(nc, k)
        if upto >= 1:
            support_stage(nc, k)
        if upto >= 2:
            edges_stage(nc, k, "e0", 0, k.src_row, k.src_col, k.src_off, k.dst_i, scale_by_weight(k),
                        [(k.src_row, k.src_col, k.src_off, k.src_to), (k.dst_row, k.dst_col, k.dst_off, k.dst_to)], k.src_to)
        if upto >= 3:
            combine_stage(nc, k)
        if upto >= 4:
            k.experts = ExitStack()
            program.callback(k.experts.close)
            k.wd = k.experts.enter_context(nc.sbuf_tensor("expert_weights", [P, EXPERTS, HC, D], F32))
            k.bd = k.experts.enter_context(nc.sbuf_tensor("expert_biases", [P, EXPERTS * D], F32))
            k.layer0_w1 = k.experts.enter_context(nc.sbuf_tensor("layer0_w1", [P, 2, HID], F32))
            k.layer0_b1 = k.experts.enter_context(nc.sbuf_tensor("layer0_b1", [P, HC], F32))
            k.wd_in = k.lasting_sem("expert_weights_in")
            ffn0_route_stage(nc, k)
        if upto >= 5:
            ffn0_experts_stage(nc, k)
            k.experts.close()
            ffn0_return_stage(nc, k)
        if upto >= 6:
            k.score = edge_sb("score", [P, T, 2 * HEADS], F32)
            l1_pre_stage(nc, k)
        if upto >= 7:
            attention_stage(nc, k)
        if upto >= 9:
            k.edges.close()
            k.late, k.scan = ExitStack(), ExitStack()
            program.callback(k.late.close)
            program.callback(k.scan.close)
            k.u, k.dt = (k.late.enter_context(nc.sbuf_tensor(name, [P, 2, NP], F32)) for name in ("u", "dt"))
            k.dtx = k.scan.enter_context(nc.sbuf_tensor("dtx", [P, 2, NP], F32))
            k.zs = k.x[:, :, :].rearrange("p t d -> p (t d)").rearrange("p (c n) -> p c n", c=2)
        if upto >= 10:
            edges_and_scan_stage(nc, k)
        if upto >= 11:
            k.ha = by_tile(k.u)
            k.scan.close()
            late_sb = lambda name, shape: k.late.enter_context(nc.sbuf_tensor(f"post_{name}", shape, F32))
            k.wl, k.wg, k.f1w, k.f2w = late_sb("wl", [P, 2, D]), late_sb("wg", [P, 2, D]), late_sb("f1w", [P, 2, FF]), late_sb("f2w", [P, FC, D])
            k.f1b, k.f2b, k.gat_b = late_sb("f1b", [P, FC]), late_sb("f2b", [1, D]), late_sb("gat_b", [P, D])
            k.gains, k.shifts = late_sb("gains", [P, 3, D]), late_sb("shifts", [P, 3, D])
            k.part = late_sb("part", [P, TABLES, SLOTS, ROW])
            k.post_vectors_in, k.post_weights_in, k.post_tables_in = (k.lasting_sem(f"post_{n}_in") for n in ("vectors", "weights", "tables"))
            mamba_out_stage(nc, k)
            k.hl = by_tile(k.dt)
        if upto >= 12:
            l1_post_stage(nc, k)
            k.late.close()
        if upto >= 13:
            k.experts = ExitStack()
            program.callback(k.experts.close)
            expert_sb = lambda name, shape: k.experts.enter_context(nc.sbuf_tensor(name, shape, F32))
            k.w1, k.w2 = expert_sb("expert_w1", [P, 2, 2, HID]), expert_sb("expert_w2", [P, 2, HC, D])
            k.b1, k.b2 = expert_sb("expert_b1", [P, 2, HC]), expert_sb("expert_b2", [P, 2, D])
            k.expert_in = [k.lasting_sem(f"expert_in{s}") for s in range(2)]
            ffn1_route_stage(nc, k)
        if upto >= 14:
            ffn1_experts_stage(nc, k)
            ffn1_return_stage(nc, k, out)
        if dbg:
            dbg(nc, k)


def host_arrays(inputs):
    import numpy as np
    arrays = {name: np.ascontiguousarray(inputs[name]) for name in _INS}
    for name in ("gat_w", "in_proj_w", "x_proj_w", "dt_proj_w", "out_proj_w", "wl", "wg", "ff1_w", "ff2_w"):
        arrays[f"{name}_t"] = np.ascontiguousarray(arrays.pop(f"L1_gnn_{name}").T)
    arrays["gat_w"] = np.ascontiguousarray(inputs["L1_gnn_gat_w"])
    return arrays


_INS = ['x', 'src', 'dst', 'edge_weight', 'node_vec', 'L0_gnn_weight', 'L0_gnn_b', 'L0_ffn_W1', 'L0_ffn_b1', 'L0_ffn_Wg', 'L0_ffn_bg', 'L0_ffn_Wd', 'L0_ffn_bd', 'L1_gnn_gat_w', 'L1_gnn_gat_a_src', 'L1_gnn_gat_a_tgt', 'L1_gnn_gat_b', 'L1_gnn_ln_local_g', 'L1_gnn_ln_local_b', 'L1_gnn_ln_global_g', 'L1_gnn_ln_global_b', 'L1_gnn_ln2_g', 'L1_gnn_ln2_b', 'L1_gnn_in_proj_w', 'L1_gnn_conv_w', 'L1_gnn_conv_b', 'L1_gnn_x_proj_w', 'L1_gnn_dt_proj_w', 'L1_gnn_dt_proj_b', 'L1_gnn_A_log', 'L1_gnn_D_param', 'L1_gnn_out_proj_w', 'L1_gnn_wl', 'L1_gnn_wg', 'L1_gnn_ff1_w', 'L1_gnn_ff1_b', 'L1_gnn_ff2_w', 'L1_gnn_ff2_b', 'L1_ffn_gate_w', 'L1_ffn_gate_b', 'L1_ffn_w1', 'L1_ffn_b1', 'L1_ffn_w2', 'L1_ffn_b2']

_OUTS = [((NODES, D), "float32")]


def kernel(**inputs):
    import numpy as _np
    import concourse.bacc as _bacc
    from concourse import mybir as _mybir
    from concourse.bass_utils import run_bass_kernel_spmd as _run

    nc = _bacc.Bacc("TRN2", target_bir_lowering=False, num_devices=1)
    arrays, io = {}, {}
    for name, a in host_arrays(inputs).items():
        arrays[f"in_{name}_dram"] = a
        io[name] = nc.dram_tensor(f"in_{name}_dram", a.shape, _mybir.dt.from_np(a.dtype), kind="ExternalInput").ap()
    shape, dtype = _OUTS[0]
    out = nc.dram_tensor("out_0_dram", shape, _mybir.dt.from_np(_np.dtype(dtype)), kind="ExternalOutput").ap()
    build(nc, io, out)
    return _run(nc, [arrays], core_ids=[0]).results[0]["out_0_dram"]
```
